# Optimizing a Trainium2 kernel written in Bass

```python
import numpy as np
import jax
import jax.numpy as jnp

def _softmax(x, axis=-1):
    return jax.nn.softmax(x, axis=axis)

def _gelu(x):
    return jax.nn.gelu(x, approximate=True)

def _silu(x):
    return jax.nn.silu(x)

def _sigmoid(x):
    return jax.nn.sigmoid(x)

def _layernorm(x, axis=-1, eps=1e-05):
    m = jnp.mean(x, axis=axis, keepdims=True)
    v = jnp.var(x, axis=axis, keepdims=True)
    return (x - m) / jnp.sqrt(v + eps)

def _scatter_add(tgt, idx, src, axis=0):
    return tgt.at[idx].add(src)

def _segment_sum(src, seg, n):
    return jax.ops.segment_sum(src, seg, n)
kernel_name = 'mk_vit_tower_cls_d4_tok_img1024_r4_f51733'

def setup_inputs(seed: int=0):
    np.random.seed(seed)
    _w = jnp.asarray

    def _rec_inputs():
        import jax
        import jax.numpy as jnp
        _rk = jax.random.key(seed)
        x = -0.00016672 + 0.999947 * jax.random.normal(jax.random.fold_in(_rk, 1), (32, 3, 96, 96), jnp.float32)
        cls_tok = 0.02 * jax.random.normal(jax.random.fold_in(_rk, 5), (1, 1, 256), jnp.float32)
        return (x, cls_tok)
    x, cls_tok = _rec_inputs()

    def _L0_tok_setup():
        import jax, jax.numpy as jnp
        import numpy as np
        PATCH = 16
        EPS = 1e-05

        def _patchify(img, p):
            B, C, H, W = img.shape
            h, w = (H // p, W // p)
            x = img.reshape(B, C, h, p, w, p)
            x = x.transpose(0, 2, 4, 1, 3, 5)
            return x.reshape(B, h, w, C * p * p)

        def _layernorm(x, gamma):
            mu = x.mean(axis=-1, keepdims=True)
            var = ((x - mu) ** 2).mean(axis=-1, keepdims=True)
            return (x - mu) * jax.lax.rsqrt(var + EPS) * gamma

        def _posemb_sincos_2d(h, w, dim, temperature=10000.0, dtype=jnp.float32):
            y, x = jnp.meshgrid(jnp.arange(h, dtype=dtype), jnp.arange(w, dtype=dtype), indexing='ij')
            omega = jnp.arange(dim // 4, dtype=dtype) / (dim // 4 - 1)
            omega = 1.0 / temperature ** omega
            y = y.reshape(-1)[:, None] * omega[None, :]
            x = x.reshape(-1)[:, None] * omega[None, :]
            return jnp.concatenate([jnp.sin(x), jnp.cos(x), jnp.sin(y), jnp.cos(y)], axis=1)
        key = jax.random.key(seed)
        k1, k2, k3, k4 = jax.random.split(key, 4)
        patch_dim = 3 * PATCH * PATCH
        dim = 256
        img = jax.random.normal(k1, (64, 3, 96, 96), dtype=jnp.float32)
        ln1_w = jax.random.uniform(k2, (patch_dim,), dtype=jnp.float32, minval=0.9, maxval=1.1)
        W = jax.random.normal(k3, (dim, patch_dim), dtype=jnp.float32) * 0.02
        ln2_w = jax.random.uniform(k4, (dim,), dtype=jnp.float32, minval=0.9, maxval=1.1)
        return {'img': img, 'ln1_w': ln1_w, 'W': W, 'ln2_w': ln2_w}
    _L0_tok_all = _L0_tok_setup()
    _L0_tok_in = {k: v for k, v in _L0_tok_all.items() if k in ('ln1_w', 'W', 'ln2_w')}
    del _L0_tok_all

    def _L0_attn_setup():
        import math
        import jax, jax.numpy as jnp
        import numpy as np
        H = 16

        def get_alibi_slopes(n):

            def pow2_slopes(n):
                start = 2 ** (-2 ** (-(math.log2(n) - 3)))
                return [start * start ** i for i in range(n)]
            if math.log2(n).is_integer():
                return pow2_slopes(n)
            c = 2 ** math.floor(math.log2(n))
            return pow2_slopes(c) + get_alibi_slopes(2 * c)[0::2][:n - c]

        def alibi_bias(num_heads, L, dtype=jnp.float32):
            slopes = jnp.asarray(get_alibi_slopes(num_heads), dtype=dtype)
            pos = jnp.arange(L)
            rel = (pos[None, :] - pos[:, None]).astype(dtype)
            bias = slopes[:, None, None] * rel[None, :, :]
            causal = pos[None, :] <= pos[:, None]
            return jnp.where(causal[None, :, :], bias, -jnp.inf)
        key = jax.random.key(seed)
        ks = jax.random.split(key, 4)
        D = 256
        B, L = (2, 512)
        s_in = 1.0 / math.sqrt(D)
        return {'x': jax.random.normal(ks[0], (B, L, D), dtype=jnp.float32), 'w_in': jax.random.normal(ks[1], (D, 3 * D), dtype=jnp.float32) * s_in, 'b_in': jnp.zeros((3 * D,), dtype=jnp.float32), 'w_out': jax.random.normal(ks[2], (D, D), dtype=jnp.float32) * s_in, 'b_out': jnp.zeros((D,), dtype=jnp.float32)}
    _L0_attn_all = _L0_attn_setup()
    _L0_attn_in = {k: v for k, v in _L0_attn_all.items() if k in ('w_in', 'b_in', 'w_out', 'b_out')}
    del _L0_attn_all

    def _L0_ffn_setup():
        import jax, jax.numpy as jnp
        import numpy as np
        B, S, D, E, F, TOP_K = (4, 512, 256, 8, 1024, 2)
        key = jax.random.key(seed)
        k0, k1, k2, k3 = jax.random.split(key, 4)
        init = lambda k, shape, fan: (jax.random.normal(k, shape, jnp.float32) / np.sqrt(fan)).astype(jnp.float32)
        return {'x': jax.random.normal(k0, (B, S, D), jnp.float32), 'gate_w': init(k1, (D, E), D), 'w1': init(k2, (E, D, F), D), 'b1': jnp.zeros((E, F), jnp.float32), 'w2': init(k3, (E, F, D), F), 'b2': jnp.zeros((E, D), jnp.float32)}
    _L0_ffn_all = _L0_ffn_setup()
    _L0_ffn_in = {k: v for k, v in _L0_ffn_all.items() if k in ('gate_w', 'w1', 'b1', 'w2', 'b2')}
    del _L0_ffn_all

    def _L1_attn_setup():
        import math
        import jax, jax.numpy as jnp
        import numpy as np
        EMBED_DIM = 256
        NUM_HEADS = 8
        HEAD_DIM = EMBED_DIM // NUM_HEADS // 2
        DEPTH = 12
        LAMBDA_INIT = 0.8 - 0.6 * math.exp(-0.3 * DEPTH)
        B, S = (2, 512)
        ROPE_THETA = 10000.0
        EPS = 1e-08

        def rope_rotate(x):
            d = x.shape[-1]
            inv_freq = 1.0 / ROPE_THETA ** (jnp.arange(0, d, 2, dtype=jnp.float32) / d)
            t = jnp.arange(x.shape[1], dtype=jnp.float32)
            freqs = t[:, None] * inv_freq[None, :]
            freqs = jnp.repeat(freqs, 2, axis=-1)
            cos = jnp.cos(freqs)[None, :, None, :].astype(x.dtype)
            sin = jnp.sin(freqs)[None, :, None, :].astype(x.dtype)
            xr = x.reshape(*x.shape[:-1], d // 2, 2)
            x1, x2 = (xr[..., 0], xr[..., 1])
            rot = jnp.stack([-x2, x1], axis=-1).reshape(x.shape)
            return x * cos + rot * sin

        def sdpa(q, k, v):
            d = q.shape[-1]
            scores = jnp.einsum('bshd,bthd->bhst', q, k) * d ** (-0.25)
            w = jax.nn.softmax(scores, axis=-1)
            return jnp.einsum('bhst,bthd->bshd', w, v)
        key = jax.random.key(seed)
        ks = jax.random.split(key, 10)
        scale = 1.0 / math.sqrt(EMBED_DIM)
        return {'x': jax.random.normal(ks[0], (B, S, EMBED_DIM), jnp.float32), 'Wq': jax.random.normal(ks[1], (EMBED_DIM, EMBED_DIM), jnp.float32) * scale, 'Wk': jax.random.normal(ks[2], (EMBED_DIM, EMBED_DIM), jnp.float32) * scale, 'Wv': jax.random.normal(ks[3], (EMBED_DIM, EMBED_DIM), jnp.float32) * scale, 'Wo': jax.random.normal(ks[4], (EMBED_DIM, EMBED_DIM), jnp.float32) * scale, 'lambda_q1': jax.random.normal(ks[5], (HEAD_DIM,), jnp.float32) * 0.1, 'lambda_k1': jax.random.normal(ks[6], (HEAD_DIM,), jnp.float32) * 0.1, 'lambda_q2': jax.random.normal(ks[7], (HEAD_DIM,), jnp.float32) * 0.1, 'lambda_k2': jax.random.normal(ks[8], (HEAD_DIM,), jnp.float32) * 0.1, 'ln_w': jnp.ones((2 * HEAD_DIM,), jnp.float32), 'ln_b': jnp.zeros((2 * HEAD_DIM,), jnp.float32)}
    _L1_attn_all = _L1_attn_setup()
    _L1_attn_in = {k: v for k, v in _L1_attn_all.items() if k in ('Wq', 'Wk', 'Wv', 'Wo', 'lambda_q1', 'lambda_k1', 'lambda_q2', 'lambda_k2', 'ln_w', 'ln_b')}
    del _L1_attn_all

    def _L1_ffn_setup():
        import jax, jax.numpy as jnp
        import numpy as np
        B, S, DIM = (4, 1024, 256)
        BASE_COUPLING = 0.1
        NUM_CYCLES = 3

        def _gelu(x):
            return jax.nn.gelu(x, approximate=False)

        def _coupling_net(h, w1, b1, w2, b2, w3, b3, w4, b4):
            h = _gelu(h @ w1 + b1)
            h = _gelu(h @ w2 + b2)
            h = _gelu(h @ w3 + b3)
            return jax.nn.sigmoid(h @ w4 + b4)

        def _global_net(h, w1, b1, w2, b2, w3, b3):
            h = _gelu(h @ w1 + b1)
            h = _gelu(h @ w2 + b2)
            return jax.nn.sigmoid(h @ w3 + b3)

        def _twist(x):
            o_r, o_i, p_r, p_i = jnp.split(x, 4, axis=-1)
            return jnp.concatenate([p_r, -p_i, -o_r, o_i], axis=-1)
        key = jax.random.key(seed)
        ks = jax.random.split(key, 9)
        d = DIM

        def w(k, fan_in, fan_out):
            return jax.random.normal(k, (fan_in, fan_out), dtype=jnp.float32) / np.sqrt(fan_in).astype(np.float32)
        inp = {'x': jax.random.normal(ks[0], (B, S, d), dtype=jnp.float32)}
        cn_dims = [(d, d), (d, d // 2), (d // 2, d // 4), (d // 4, 1)]
        for i, (a, b) in enumerate(cn_dims):
            inp[f'cn_w{i + 1}'] = w(ks[1 + i], a, b)
            inp[f'cn_b{i + 1}'] = jnp.zeros((b,), dtype=jnp.float32)
        gc_dims = [(d, d // 2), (d // 2, d // 4), (d // 4, 1)]
        for i, (a, b) in enumerate(gc_dims):
            inp[f'gc_w{i + 1}'] = w(ks[5 + i], a, b)
            inp[f'gc_b{i + 1}'] = jnp.zeros((b,), dtype=jnp.float32)
        inp['adaptive_range'] = jnp.full((1,), 0.2, dtype=jnp.float32)
        return inp
    _L1_ffn_all = _L1_ffn_setup()
    _L1_ffn_in = {k: v for k, v in _L1_ffn_all.items() if k in ('cn_w1', 'cn_b1', 'cn_w2', 'cn_b2', 'cn_w3', 'cn_b3', 'cn_w4', 'cn_b4', 'gc_w1', 'gc_b1', 'gc_w2', 'gc_b2', 'gc_w3', 'gc_b3', 'adaptive_range')}
    del _L1_ffn_all

    def _L2_attn_setup():
        import jax, jax.numpy as jnp
        import numpy as np
        B, N, C, H = (8, 1024, 256, 16)
        D = C // H
        EPS = 1e-12

        def _l2norm(x):
            n = jnp.sqrt(jnp.sum(x * x, axis=-1, keepdims=True))
            return x / jnp.maximum(n, EPS)
        key = jax.random.key(seed)
        ks = jax.random.split(key, 5)
        return {'x': jax.random.normal(ks[0], (B, N, C), dtype=jnp.float32), 'qkv_w': jax.random.normal(ks[1], (C, 3 * C), dtype=jnp.float32) * 0.02, 'qkv_b': jax.random.normal(ks[2], (3 * C,), dtype=jnp.float32) * 0.02, 'proj_w': jax.random.normal(ks[3], (C, C), dtype=jnp.float32) * 0.02, 'proj_b': jax.random.normal(ks[4], (C,), dtype=jnp.float32) * 0.02}
    _L2_attn_all = _L2_attn_setup()
    _L2_attn_in = {k: v for k, v in _L2_attn_all.items() if k in ('qkv_w', 'qkv_b', 'proj_w', 'proj_b')}
    del _L2_attn_all

    def _L2_ffn_setup():
        import jax, jax.numpy as jnp
        import numpy as np
        TOP_K = 2
        key = jax.random.key(seed)
        k_x, k_g, k_w1, k_w2, k_w3 = jax.random.split(key, 5)
        B, S, D, H, E = (2, 128, 256, 128, 8)
        x = jax.random.normal(k_x, (B, S, D), dtype=jnp.float32)
        gate_w = jax.random.normal(k_g, (D, E), dtype=jnp.float32) * D ** (-0.5)
        w1 = jax.random.normal(k_w1, (E, D, H), dtype=jnp.float32) * 0.02
        w2 = jax.random.normal(k_w2, (E, H, D), dtype=jnp.float32) * 0.02
        w3 = jax.random.normal(k_w3, (E, D, H), dtype=jnp.float32) * 0.02
        return {'x': x, 'gate_w': gate_w, 'w1': w1, 'w2': w2, 'w3': w3}
    _L2_ffn_all = _L2_ffn_setup()
    _L2_ffn_in = {k: v for k, v in _L2_ffn_all.items() if k in ('gate_w', 'w1', 'w2', 'w3')}
    del _L2_ffn_all

    def _L3_attn_setup():
        import jax, jax.numpy as jnp
        import numpy as np
        B, T, D = (4, 512, 256)
        HID = 2 * D
        EPS = 1e-06

        def _rmsnorm(x, w):
            return x * jax.lax.rsqrt(jnp.mean(x * x, axis=-1, keepdims=True) + EPS) * w

        def _ema_scan(v, alpha):

            def step(prev, v_t):
                cur = alpha * v_t + (1.0 - alpha) * prev
                return (cur, cur)
            v_tm = jnp.swapaxes(v, 0, 1)
            _, out = jax.lax.scan(step, jnp.zeros(v.shape[::2], v.dtype), v_tm)
            return jnp.swapaxes(out, 0, 1)

        def _delta_scan(q, k, v, beta):

            def step(S, inp):
                q_t, k_t, v_t, b_t = inp
                Sk = jnp.einsum('bij,bj->bi', S, k_t)
                S = S + b_t[:, None, None] * (v_t - Sk)[:, :, None] * k_t[:, None, :]
                o_t = jnp.einsum('bij,bj->bi', S, q_t)
                return (S, o_t)
            tm = lambda a: jnp.swapaxes(a, 0, 1)
            S0 = jnp.zeros((q.shape[0], q.shape[2], q.shape[2]), q.dtype)
            _, out = jax.lax.scan(step, S0, (tm(q), tm(k), tm(v), tm(beta)))
            return jnp.swapaxes(out, 0, 1)
        key = jax.random.key(seed)
        ks = jax.random.split(key, 12)
        s = 0.02
        return {'x': jax.random.normal(ks[0], (B, T, D), jnp.float32), 'norm1_w': jnp.ones((D,), jnp.float32), 'Wq': jax.random.normal(ks[1], (D, D), jnp.float32) * s, 'Wk': jax.random.normal(ks[2], (D, D), jnp.float32) * s, 'Wv': jax.random.normal(ks[3], (D, D), jnp.float32) * s, 'beta_w': jax.random.normal(ks[4], (D, 1), jnp.float32) * s, 'beta_b': jnp.zeros((1,), jnp.float32), 'Wo': jax.random.normal(ks[5], (D, D), jnp.float32) * s, 'alpha_logit': jnp.full((D,), float(np.log(0.1 / 0.9)), jnp.float32), 'norm2_w': jnp.ones((D,), jnp.float32), 'w_gate': jax.random.normal(ks[6], (D, HID), jnp.float32) * s, 'w_up': jax.random.normal(ks[7], (D, HID), jnp.float32) * s, 'w_down': jax.random.normal(ks[8], (HID, D), jnp.float32) * s}
    _L3_attn_all = _L3_attn_setup()
    _L3_attn_in = {k: v for k, v in _L3_attn_all.items() if k in ('norm1_w', 'Wq', 'Wk', 'Wv', 'beta_w', 'beta_b', 'Wo', 'alpha_logit', 'norm2_w', 'w_gate', 'w_up', 'w_down')}
    del _L3_attn_all

    def _L3_ffn_setup():
        import jax, jax.numpy as jnp
        import numpy as np
        B, S, D = (1, 512, 256)
        E, K, F = (64, 8, 192)
        SF = 192
        C = 128
        ROUTED_SCALE = 1.0

        def _moe_forward(x, router_w, w_gate, w_up, w_down, ws_gate_up, ws_down):
            T = x.shape[0]
            logits = x.astype(jnp.float32) @ router_w.T
            probs = jax.nn.softmax(logits, axis=-1)
            topk_w, topk_ids = jax.lax.top_k(probs, K)
            topk_w = topk_w / jnp.sum(topk_w, axis=-1, keepdims=True)
            topk_w = topk_w.astype(x.dtype)
            N = T * K
            flat_e = topk_ids.reshape(-1)
            flat_w = topk_w.reshape(-1)
            tok = jnp.arange(N) // K
            onehot = flat_e[:, None] == jnp.arange(E)[None, :]
            pos = jnp.cumsum(onehot, axis=0)[jnp.arange(N), flat_e] - 1
            valid = pos < C
            idx = jnp.where(valid, flat_e * C + pos, E * C)
            x_buf = jnp.zeros((E * C + 1, x.shape[1]), x.dtype).at[idx].set(x[tok])
            xb = x_buf[:E * C].reshape(E, C, -1)
            g = jnp.einsum('ecd,edf->ecf', xb, w_gate)
            u = jnp.einsum('ecd,edf->ecf', xb, w_up)
            h = jax.nn.silu(g) * u
            y = jnp.einsum('ecf,efd->ecd', h, w_down).reshape(E * C, -1)
            safe = jnp.where(valid, idx, 0)
            contrib = y[safe] * (flat_w * valid.astype(flat_w.dtype))[:, None]
            routed = jax.ops.segment_sum(contrib, tok, num_segments=T)
            routed = routed * ROUTED_SCALE
            gu = x @ ws_gate_up
            sg, su = (gu[:, :SF], gu[:, SF:])
            shared = jax.nn.silu(sg) * su @ ws_down
            return routed + shared
        key = jax.random.key(seed)
        ks = jax.random.split(key, 7)
        w = 0.02
        return {'hidden_states': jax.random.normal(ks[0], (B, S, D), jnp.float32), 'router_w': jax.random.normal(ks[1], (E, D), jnp.float32) * w, 'w_gate': jax.random.normal(ks[2], (E, D, F), jnp.float32) * w, 'w_up': jax.random.normal(ks[3], (E, D, F), jnp.float32) * w, 'w_down': jax.random.normal(ks[4], (E, F, D), jnp.float32) * w, 'ws_gate_up': jax.random.normal(ks[5], (D, 2 * SF), jnp.float32) * w, 'ws_down': jax.random.normal(ks[6], (SF, D), jnp.float32) * w}
    _L3_ffn_all = _L3_ffn_setup()
    _L3_ffn_in = {k: v for k, v in _L3_ffn_all.items() if k in ('router_w', 'w_gate', 'w_up', 'w_down', 'ws_gate_up', 'ws_down')}
    del _L3_ffn_all
    return {'x': x, 'cls_tok': cls_tok, 'L0_tok_ln1_w': _L0_tok_in['ln1_w'], 'L0_tok_W': _L0_tok_in['W'], 'L0_tok_ln2_w': _L0_tok_in['ln2_w'], 'L0_attn_w_in': _L0_attn_in['w_in'], 'L0_attn_b_in': _L0_attn_in['b_in'], 'L0_attn_w_out': _L0_attn_in['w_out'], 'L0_attn_b_out': _L0_attn_in['b_out'], 'L0_ffn_gate_w': _L0_ffn_in['gate_w'], 'L0_ffn_w1': _L0_ffn_in['w1'], 'L0_ffn_b1': _L0_ffn_in['b1'], 'L0_ffn_w2': _L0_ffn_in['w2'], 'L0_ffn_b2': _L0_ffn_in['b2'], 'L1_attn_Wq': _L1_attn_in['Wq'], 'L1_attn_Wk': _L1_attn_in['Wk'], 'L1_attn_Wv': _L1_attn_in['Wv'], 'L1_attn_Wo': _L1_attn_in['Wo'], 'L1_attn_lambda_q1': _L1_attn_in['lambda_q1'], 'L1_attn_lambda_k1': _L1_attn_in['lambda_k1'], 'L1_attn_lambda_q2': _L1_attn_in['lambda_q2'], 'L1_attn_lambda_k2': _L1_attn_in['lambda_k2'], 'L1_attn_ln_w': _L1_attn_in['ln_w'], 'L1_attn_ln_b': _L1_attn_in['ln_b'], 'L1_ffn_cn_w1': _L1_ffn_in['cn_w1'], 'L1_ffn_cn_b1': _L1_ffn_in['cn_b1'], 'L1_ffn_cn_w2': _L1_ffn_in['cn_w2'], 'L1_ffn_cn_b2': _L1_ffn_in['cn_b2'], 'L1_ffn_cn_w3': _L1_ffn_in['cn_w3'], 'L1_ffn_cn_b3': _L1_ffn_in['cn_b3'], 'L1_ffn_cn_w4': _L1_ffn_in['cn_w4'], 'L1_ffn_cn_b4': _L1_ffn_in['cn_b4'], 'L1_ffn_gc_w1': _L1_ffn_in['gc_w1'], 'L1_ffn_gc_b1': _L1_ffn_in['gc_b1'], 'L1_ffn_gc_w2': _L1_ffn_in['gc_w2'], 'L1_ffn_gc_b2': _L1_ffn_in['gc_b2'], 'L1_ffn_gc_w3': _L1_ffn_in['gc_w3'], 'L1_ffn_gc_b3': _L1_ffn_in['gc_b3'], 'L1_ffn_adaptive_range': _L1_ffn_in['adaptive_range'], 'L2_attn_qkv_w': _L2_attn_in['qkv_w'], 'L2_attn_qkv_b': _L2_attn_in['qkv_b'], 'L2_attn_proj_w': _L2_attn_in['proj_w'], 'L2_attn_proj_b': _L2_attn_in['proj_b'], 'L2_ffn_gate_w': _L2_ffn_in['gate_w'], 'L2_ffn_w1': _L2_ffn_in['w1'], 'L2_ffn_w2': _L2_ffn_in['w2'], 'L2_ffn_w3': _L2_ffn_in['w3'], 'L3_attn_norm1_w': _L3_attn_in['norm1_w'], 'L3_attn_Wq': _L3_attn_in['Wq'], 'L3_attn_Wk': _L3_attn_in['Wk'], 'L3_attn_Wv': _L3_attn_in['Wv'], 'L3_attn_beta_w': _L3_attn_in['beta_w'], 'L3_attn_beta_b': _L3_attn_in['beta_b'], 'L3_attn_Wo': _L3_attn_in['Wo'], 'L3_attn_alpha_logit': _L3_attn_in['alpha_logit'], 'L3_attn_norm2_w': _L3_attn_in['norm2_w'], 'L3_attn_w_gate': _L3_attn_in['w_gate'], 'L3_attn_w_up': _L3_attn_in['w_up'], 'L3_attn_w_down': _L3_attn_in['w_down'], 'L3_ffn_router_w': _L3_ffn_in['router_w'], 'L3_ffn_w_gate': _L3_ffn_in['w_gate'], 'L3_ffn_w_up': _L3_ffn_in['w_up'], 'L3_ffn_w_down': _L3_ffn_in['w_down'], 'L3_ffn_ws_gate_up': _L3_ffn_in['ws_gate_up'], 'L3_ffn_ws_down': _L3_ffn_in['ws_down']}

def reference(x, cls_tok, L0_tok_ln1_w, L0_tok_W, L0_tok_ln2_w, L0_attn_w_in, L0_attn_b_in, L0_attn_w_out, L0_attn_b_out, L0_ffn_gate_w, L0_ffn_w1, L0_ffn_b1, L0_ffn_w2, L0_ffn_b2, L1_attn_Wq, L1_attn_Wk, L1_attn_Wv, L1_attn_Wo, L1_attn_lambda_q1, L1_attn_lambda_k1, L1_attn_lambda_q2, L1_attn_lambda_k2, L1_attn_ln_w, L1_attn_ln_b, L1_ffn_cn_w1, L1_ffn_cn_b1, L1_ffn_cn_w2, L1_ffn_cn_b2, L1_ffn_cn_w3, L1_ffn_cn_b3, L1_ffn_cn_w4, L1_ffn_cn_b4, L1_ffn_gc_w1, L1_ffn_gc_b1, L1_ffn_gc_w2, L1_ffn_gc_b2, L1_ffn_gc_w3, L1_ffn_gc_b3, L1_ffn_adaptive_range, L2_attn_qkv_w, L2_attn_qkv_b, L2_attn_proj_w, L2_attn_proj_b, L2_ffn_gate_w, L2_ffn_w1, L2_ffn_w2, L2_ffn_w3, L3_attn_norm1_w, L3_attn_Wq, L3_attn_Wk, L3_attn_Wv, L3_attn_beta_w, L3_attn_beta_b, L3_attn_Wo, L3_attn_alpha_logit, L3_attn_norm2_w, L3_attn_w_gate, L3_attn_w_up, L3_attn_w_down, L3_ffn_router_w, L3_ffn_w_gate, L3_ffn_w_up, L3_ffn_w_down, L3_ffn_ws_gate_up, L3_ffn_ws_down):
    import jax
    import jax.numpy as jnp

    def _L0_tok_ref(img, ln1_w, W, ln2_w):
        import jax, jax.numpy as jnp
        import numpy as np
        PATCH = 16
        EPS = 1e-05

        def _patchify(img, p):
            B, C, H, W = img.shape
            h, w = (H // p, W // p)
            x = img.reshape(B, C, h, p, w, p)
            x = x.transpose(0, 2, 4, 1, 3, 5)
            return x.reshape(B, h, w, C * p * p)

        def _layernorm(x, gamma):
            mu = x.mean(axis=-1, keepdims=True)
            var = ((x - mu) ** 2).mean(axis=-1, keepdims=True)
            return (x - mu) * jax.lax.rsqrt(var + EPS) * gamma

        def _posemb_sincos_2d(h, w, dim, temperature=10000.0, dtype=jnp.float32):
            y, x = jnp.meshgrid(jnp.arange(h, dtype=dtype), jnp.arange(w, dtype=dtype), indexing='ij')
            omega = jnp.arange(dim // 4, dtype=dtype) / (dim // 4 - 1)
            omega = 1.0 / temperature ** omega
            y = y.reshape(-1)[:, None] * omega[None, :]
            x = x.reshape(-1)[:, None] * omega[None, :]
            return jnp.concatenate([jnp.sin(x), jnp.cos(x), jnp.sin(y), jnp.cos(y)], axis=1)
        patches = _patchify(img, PATCH)
        B, h, w, d = patches.shape
        x = patches.reshape(B, h * w, d)
        x = _layernorm(x, ln1_w)
        x = jnp.einsum('bnd,ed->bne', x, W)
        x = _layernorm(x, ln2_w)
        pe = _posemb_sincos_2d(h, w, x.shape[-1], dtype=x.dtype)
        return x + pe[None, :, :]

    def _L0_attn_ref(x, w_in, b_in, w_out, b_out):
        import math
        import jax, jax.numpy as jnp
        import numpy as np
        H = 16

        def get_alibi_slopes(n):

            def pow2_slopes(n):
                start = 2 ** (-2 ** (-(math.log2(n) - 3)))
                return [start * start ** i for i in range(n)]
            if math.log2(n).is_integer():
                return pow2_slopes(n)
            c = 2 ** math.floor(math.log2(n))
            return pow2_slopes(c) + get_alibi_slopes(2 * c)[0::2][:n - c]

        def alibi_bias(num_heads, L, dtype=jnp.float32):
            slopes = jnp.asarray(get_alibi_slopes(num_heads), dtype=dtype)
            pos = jnp.arange(L)
            rel = (pos[None, :] - pos[:, None]).astype(dtype)
            bias = slopes[:, None, None] * rel[None, :, :]
            causal = pos[None, :] <= pos[:, None]
            return jnp.where(causal[None, :, :], bias, -jnp.inf)
        B, L, D = x.shape
        dh = D // H
        qkv = x @ w_in + b_in
        q, k, v = jnp.split(qkv, 3, axis=-1)

        def heads(t):
            return t.reshape(B, L, H, dh).transpose(0, 2, 1, 3)
        q, k, v = (heads(q), heads(k), heads(v))
        scores = jnp.einsum('bhqd,bhkd->bhqk', q, k) / math.sqrt(dh)
        scores = scores + alibi_bias(H, L, scores.dtype)[None]
        attn = jax.nn.softmax(scores, axis=-1)
        out = jnp.einsum('bhqk,bhkd->bhqd', attn, v)
        out = out.transpose(0, 2, 1, 3).reshape(B, L, D)
        return out @ w_out + b_out

    def _L0_ffn_ref(x, gate_w, w1, b1, w2, b2):
        import jax, jax.numpy as jnp
        import numpy as np
        B, S, D, E, F, TOP_K = (4, 512, 256, 8, 1024, 2)
        b, s, d = x.shape
        e = gate_w.shape[1]
        xf = x.reshape(-1, d)
        t = xf.shape[0]
        logits = xf @ gate_w
        top_w, top_idx = jax.lax.top_k(logits, TOP_K)
        top_w = jax.nn.softmax(top_w.astype(jnp.float32), axis=-1).astype(x.dtype)
        combine = jnp.zeros((t, e), x.dtype).at[jnp.arange(t)[:, None], top_idx].add(top_w)
        h = jax.nn.gelu(jnp.einsum('td,edf->tef', xf, w1) + b1, approximate=False)
        y = jnp.einsum('tef,efd->ted', h, w2) + b2
        out = jnp.einsum('ted,te->td', y, combine)
        return out.reshape(b, s, d)

    def _L1_attn_ref(x, Wq, Wk, Wv, Wo, lambda_q1, lambda_k1, lambda_q2, lambda_k2, ln_w, ln_b):
        import math
        import jax, jax.numpy as jnp
        import numpy as np
        EMBED_DIM = 256
        NUM_HEADS = 8
        HEAD_DIM = EMBED_DIM // NUM_HEADS // 2
        DEPTH = 12
        LAMBDA_INIT = 0.8 - 0.6 * math.exp(-0.3 * DEPTH)
        B, S = (2, 512)
        ROPE_THETA = 10000.0
        EPS = 1e-08

        def rope_rotate(x):
            d = x.shape[-1]
            inv_freq = 1.0 / ROPE_THETA ** (jnp.arange(0, d, 2, dtype=jnp.float32) / d)
            t = jnp.arange(x.shape[1], dtype=jnp.float32)
            freqs = t[:, None] * inv_freq[None, :]
            freqs = jnp.repeat(freqs, 2, axis=-1)
            cos = jnp.cos(freqs)[None, :, None, :].astype(x.dtype)
            sin = jnp.sin(freqs)[None, :, None, :].astype(x.dtype)
            xr = x.reshape(*x.shape[:-1], d // 2, 2)
            x1, x2 = (xr[..., 0], xr[..., 1])
            rot = jnp.stack([-x2, x1], axis=-1).reshape(x.shape)
            return x * cos + rot * sin

        def sdpa(q, k, v):
            d = q.shape[-1]
            scores = jnp.einsum('bshd,bthd->bhst', q, k) * d ** (-0.25)
            w = jax.nn.softmax(scores, axis=-1)
            return jnp.einsum('bhst,bthd->bshd', w, v)
        b, s, e = x.shape
        H, D = (NUM_HEADS, HEAD_DIM)
        q = (x @ Wq.T).reshape(b, s, 2 * H, D)
        k = (x @ Wk.T).reshape(b, s, 2 * H, D)
        v = (x @ Wv.T).reshape(b, s, H, 2, D)
        q = rope_rotate(q).reshape(b, s, H, 2, D)
        k = rope_rotate(k).reshape(b, s, H, 2, D)
        q1, q2 = (q[..., 0, :], q[..., 1, :])
        k1, k2 = (k[..., 0, :], k[..., 1, :])
        v1, v2 = (v[..., 0, :], v[..., 1, :])
        attn1 = sdpa(q1, k1, v1)
        attn2 = sdpa(q2, k2, v2)
        lam = jnp.exp(jnp.sum(lambda_q1 * lambda_k1)) - jnp.exp(jnp.sum(lambda_q2 * lambda_k2)) + LAMBDA_INIT
        diff = jnp.concatenate([attn1, attn2], axis=0)
        a = attn1 - lam * attn2
        a2 = jnp.concatenate([attn1[..., None, :], attn2[..., None, :]], axis=-2)
        a2 = a2[..., 0, :] - lam * a2[..., 1, :]
        attn1f = sdpa(q1, k1, jnp.concatenate([v1, v2], axis=-1) * 0 + jnp.concatenate([v1, v2], axis=-1))
        vfull = jnp.concatenate([v1, v2], axis=-1)
        o1 = sdpa(q1, k1, vfull)
        o2 = sdpa(q2, k2, vfull)
        o = o1 - lam * o2
        ms = jnp.mean(jnp.square(o), axis=-1, keepdims=True)
        o = o * jax.lax.rsqrt(ms + EPS) * ln_w + ln_b
        o = o * (1.0 - LAMBDA_INIT)
        o = o.reshape(b, s, e)
        return o @ Wo.T

    def _L1_ffn_ref(x, cn_w1, cn_b1, cn_w2, cn_b2, cn_w3, cn_b3, cn_w4, cn_b4, gc_w1, gc_b1, gc_w2, gc_b2, gc_w3, gc_b3, adaptive_range):
        import jax, jax.numpy as jnp
        import numpy as np
        B, S, DIM = (4, 1024, 256)
        BASE_COUPLING = 0.1
        NUM_CYCLES = 3

        def _gelu(x):
            return jax.nn.gelu(x, approximate=False)

        def _coupling_net(h, w1, b1, w2, b2, w3, b3, w4, b4):
            h = _gelu(h @ w1 + b1)
            h = _gelu(h @ w2 + b2)
            h = _gelu(h @ w3 + b3)
            return jax.nn.sigmoid(h @ w4 + b4)

        def _global_net(h, w1, b1, w2, b2, w3, b3):
            h = _gelu(h @ w1 + b1)
            h = _gelu(h @ w2 + b2)
            return jax.nn.sigmoid(h @ w3 + b3)

        def _twist(x):
            o_r, o_i, p_r, p_i = jnp.split(x, 4, axis=-1)
            return jnp.concatenate([p_r, -p_i, -o_r, o_i], axis=-1)
        global_context = x.mean(axis=1, keepdims=True)
        gf = _global_net(global_context, gc_w1, gc_b1, gc_w2, gc_b2, gc_w3, gc_b3)
        out = x
        for _ in range(NUM_CYCLES):
            tf = _coupling_net(out, cn_w1, cn_b1, cn_w2, cn_b2, cn_w3, cn_b3, cn_w4, cn_b4)
            combined = 0.7 * gf + 0.3 * tf
            coupling = BASE_COUPLING + adaptive_range * (combined - 0.5) * 2.0
            out = out + coupling * _twist(out)
        return out

    def _L2_attn_ref(x, qkv_w, qkv_b, proj_w, proj_b):
        import jax, jax.numpy as jnp
        import numpy as np
        B, N, C, H = (8, 1024, 256, 16)
        D = C // H
        EPS = 1e-12

        def _l2norm(x):
            n = jnp.sqrt(jnp.sum(x * x, axis=-1, keepdims=True))
            return x / jnp.maximum(n, EPS)
        b, n, c = x.shape
        qkv = (x @ qkv_w + qkv_b).reshape(b, n, 3, H, D)
        qkv = jnp.transpose(qkv, (2, 0, 3, 1, 4))
        q, k, v = (qkv[0], qkv[1], qkv[2])
        q = _l2norm(q)
        k = _l2norm(k)
        kv = jnp.einsum('bhnd,bhne->bhde', k, v)
        out = jnp.einsum('bhnd,bhde->bhne', q, kv)
        out = jnp.transpose(out, (0, 2, 1, 3)).reshape(b, n, c)
        return out @ proj_w + proj_b

    def _L2_ffn_ref(x, gate_w, w1, w2, w3):
        import jax, jax.numpy as jnp
        import numpy as np
        TOP_K = 2
        B, S, D = x.shape
        E = gate_w.shape[1]
        xf = x.reshape(B * S, D)
        T = B * S
        logits = xf @ gate_w
        scores = jax.nn.softmax(logits, axis=-1)
        top_scores, top_idx = jax.lax.top_k(scores, TOP_K)
        scale = jnp.zeros((T, E), dtype=x.dtype).at[jnp.arange(T)[:, None], top_idx].set(top_scores)
        xs = scale.T[:, :, None] * xf[None, :, :]
        h = jax.nn.silu(jnp.einsum('etd,edh->eth', xs, w1)) * jnp.einsum('etd,edh->eth', xs, w3)
        y = jnp.einsum('eth,ehd->etd', h, w2)
        out = y.sum(axis=0)
        return out.reshape(B, S, D)

    def _L3_attn_ref(x, norm1_w, Wq, Wk, Wv, beta_w, beta_b, Wo, alpha_logit, norm2_w, w_gate, w_up, w_down):
        import jax, jax.numpy as jnp
        import numpy as np
        B, T, D = (4, 512, 256)
        HID = 2 * D
        EPS = 1e-06

        def _rmsnorm(x, w):
            return x * jax.lax.rsqrt(jnp.mean(x * x, axis=-1, keepdims=True) + EPS) * w

        def _ema_scan(v, alpha):

            def step(prev, v_t):
                cur = alpha * v_t + (1.0 - alpha) * prev
                return (cur, cur)
            v_tm = jnp.swapaxes(v, 0, 1)
            _, out = jax.lax.scan(step, jnp.zeros(v.shape[::2], v.dtype), v_tm)
            return jnp.swapaxes(out, 0, 1)

        def _delta_scan(q, k, v, beta):

            def step(S, inp):
                q_t, k_t, v_t, b_t = inp
                Sk = jnp.einsum('bij,bj->bi', S, k_t)
                S = S + b_t[:, None, None] * (v_t - Sk)[:, :, None] * k_t[:, None, :]
                o_t = jnp.einsum('bij,bj->bi', S, q_t)
                return (S, o_t)
            tm = lambda a: jnp.swapaxes(a, 0, 1)
            S0 = jnp.zeros((q.shape[0], q.shape[2], q.shape[2]), q.dtype)
            _, out = jax.lax.scan(step, S0, (tm(q), tm(k), tm(v), tm(beta)))
            return jnp.swapaxes(out, 0, 1)
        h = _rmsnorm(x, norm1_w)
        q = h @ Wq
        k = h @ Wk
        k = k / jnp.maximum(jnp.linalg.norm(k, axis=-1, keepdims=True), 1e-12)
        v = h @ Wv
        v = _ema_scan(v, jax.nn.sigmoid(alpha_logit))
        beta = jax.nn.sigmoid(h @ beta_w + beta_b)[..., 0]
        attn_out = _delta_scan(q, k, v, beta)
        x = x + attn_out @ Wo
        h2 = _rmsnorm(x, norm2_w)
        mlp = jax.nn.silu(h2 @ w_gate) * (h2 @ w_up) @ w_down
        return x + mlp

    def _L3_ffn_ref(hidden_states, router_w, w_gate, w_up, w_down, ws_gate_up, ws_down):
        import jax, jax.numpy as jnp
        import numpy as np
        B, S, D = (1, 512, 256)
        E, K, F = (64, 8, 192)
        SF = 192
        C = 128
        ROUTED_SCALE = 1.0

        def _moe_forward(x, router_w, w_gate, w_up, w_down, ws_gate_up, ws_down):
            T = x.shape[0]
            logits = x.astype(jnp.float32) @ router_w.T
            probs = jax.nn.softmax(logits, axis=-1)
            topk_w, topk_ids = jax.lax.top_k(probs, K)
            topk_w = topk_w / jnp.sum(topk_w, axis=-1, keepdims=True)
            topk_w = topk_w.astype(x.dtype)
            N = T * K
            flat_e = topk_ids.reshape(-1)
            flat_w = topk_w.reshape(-1)
            tok = jnp.arange(N) // K
            onehot = flat_e[:, None] == jnp.arange(E)[None, :]
            pos = jnp.cumsum(onehot, axis=0)[jnp.arange(N), flat_e] - 1
            valid = pos < C
            idx = jnp.where(valid, flat_e * C + pos, E * C)
            x_buf = jnp.zeros((E * C + 1, x.shape[1]), x.dtype).at[idx].set(x[tok])
            xb = x_buf[:E * C].reshape(E, C, -1)
            g = jnp.einsum('ecd,edf->ecf', xb, w_gate)
            u = jnp.einsum('ecd,edf->ecf', xb, w_up)
            h = jax.nn.silu(g) * u
            y = jnp.einsum('ecf,efd->ecd', h, w_down).reshape(E * C, -1)
            safe = jnp.where(valid, idx, 0)
            contrib = y[safe] * (flat_w * valid.astype(flat_w.dtype))[:, None]
            routed = jax.ops.segment_sum(contrib, tok, num_segments=T)
            routed = routed * ROUTED_SCALE
            gu = x @ ws_gate_up
            sg, su = (gu[:, :SF], gu[:, SF:])
            shared = jax.nn.silu(sg) * su @ ws_down
            return routed + shared
        b, s, d = hidden_states.shape
        x = hidden_states.reshape(-1, d)
        out = _moe_forward(x, router_w, w_gate, w_up, w_down, ws_gate_up, ws_down)
        return out.reshape(b, s, d)
    h = _L0_tok_ref(x, L0_tok_ln1_w, L0_tok_W, L0_tok_ln2_w)
    h = jnp.concatenate([jnp.broadcast_to(cls_tok, (h.shape[0], 1, h.shape[2])), h], axis=1)
    h = h + _L0_attn_ref(_layernorm(h, axis=-1), L0_attn_w_in, L0_attn_b_in, L0_attn_w_out, L0_attn_b_out)
    h = h + _L0_ffn_ref(_layernorm(h, axis=-1), L0_ffn_gate_w, L0_ffn_w1, L0_ffn_b1, L0_ffn_w2, L0_ffn_b2)
    h = h + _L1_attn_ref(_layernorm(h, axis=-1), L1_attn_Wq, L1_attn_Wk, L1_attn_Wv, L1_attn_Wo, L1_attn_lambda_q1, L1_attn_lambda_k1, L1_attn_lambda_q2, L1_attn_lambda_k2, L1_attn_ln_w, L1_attn_ln_b)
    h = h + _L1_ffn_ref(_layernorm(h, axis=-1), L1_ffn_cn_w1, L1_ffn_cn_b1, L1_ffn_cn_w2, L1_ffn_cn_b2, L1_ffn_cn_w3, L1_ffn_cn_b3, L1_ffn_cn_w4, L1_ffn_cn_b4, L1_ffn_gc_w1, L1_ffn_gc_b1, L1_ffn_gc_w2, L1_ffn_gc_b2, L1_ffn_gc_w3, L1_ffn_gc_b3, L1_ffn_adaptive_range)
    h = h + _L2_attn_ref(_layernorm(h, axis=-1), L2_attn_qkv_w, L2_attn_qkv_b, L2_attn_proj_w, L2_attn_proj_b)
    h = h + _L2_ffn_ref(_layernorm(h, axis=-1), L2_ffn_gate_w, L2_ffn_w1, L2_ffn_w2, L2_ffn_w3)
    h = h + _L3_attn_ref(_layernorm(h, axis=-1), L3_attn_norm1_w, L3_attn_Wq, L3_attn_Wk, L3_attn_Wv, L3_attn_beta_w, L3_attn_beta_b, L3_attn_Wo, L3_attn_alpha_logit, L3_attn_norm2_w, L3_attn_w_gate, L3_attn_w_up, L3_attn_w_down)
    h = h + _L3_ffn_ref(_layernorm(h, axis=-1), L3_ffn_router_w, L3_ffn_w_gate, L3_ffn_w_up, L3_ffn_w_down, L3_ffn_ws_gate_up, L3_ffn_ws_down)
    return h

_drawn_inputs = setup_inputs


def setup_inputs(seed=0):
    import zlib

    import numpy as np

    out = dict(_drawn_inputs(seed))
    spreads = {'L0_attn_b_in': (0.0, 0.1),
     'L0_attn_b_out': (0.0, 0.1),
     'L0_ffn_b1': (0.0, 0.1),
     'L0_ffn_b2': (0.0, 0.1),
     'L1_attn_ln_w': (1.0, 0.585),
     'L1_attn_ln_b': (0.0, 0.605),
     'L1_ffn_cn_b1': (0.0, 0.8),
     'L1_ffn_cn_b2': (0.0, 0.8),
     'L1_ffn_cn_b3': (0.0, 0.8),
     'L1_ffn_gc_b1': (0.0, 0.8),
     'L1_ffn_gc_b2': (0.0, 0.8),
     'L3_attn_norm1_w': (1.0, 0.6),
     'L3_attn_alpha_logit': (-2.1972246170043945, 0.6),
     'L3_attn_norm2_w': (1.0, 0.6)}
    factors = {'L1_attn_lambda_q1': 8.0,
     'L1_attn_lambda_k1': 2.827,
     'L1_attn_lambda_q2': 8.0,
     'L1_attn_lambda_k2': 8.0,
     'L1_ffn_cn_w1': 7.767,
     'L1_ffn_cn_w2': 8.0,
     'L1_ffn_cn_w3': 8.0,
     'L1_ffn_cn_w4': 8.0,
     'L1_ffn_gc_w1': 3.731,
     'L1_ffn_gc_w2': 6.456,
     'L1_ffn_gc_w3': 2.999,
     'L2_attn_qkv_b': 2.759,
     'L2_attn_proj_b': 6.974,
     'L2_ffn_gate_w': 8.0,
     'L2_ffn_w1': 8.0,
     'L2_ffn_w2': 8.0,
     'L2_ffn_w3': 8.0,
     'L3_attn_Wq': 6.902,
     'L3_attn_Wk': 7.256,
     'L3_attn_Wv': 6.974,
     'L3_attn_beta_w': 8.0,
     'L3_attn_Wo': 6.499,
     'L3_attn_w_gate': 7.215,
     'L3_attn_w_up': 7.095,
     'L3_attn_w_down': 7.06,
     'L3_ffn_router_w': 8.0,
     'L3_ffn_w_gate': 8.0,
     'L3_ffn_w_up': 8.0,
     'L3_ffn_w_down': 8.0,
     'L3_ffn_ws_gate_up': 8.0,
     'L3_ffn_ws_down': 8.0}
    for name, (base, spread) in spreads.items():
        noise = np.random.default_rng([zlib.crc32(name.encode()), seed]).standard_normal(out[name].shape)
        drawn = base * np.exp(spread * noise) if base else spread * noise
        out[name] = jnp.asarray(drawn.astype(out[name].dtype))
    for name, factor in factors.items():
        out[name] = (out[name] * factor).astype(out[name].dtype)
    return out
```

```python
import math
from contextlib import ExitStack

import numpy as np
import concourse.bass as bass
from concourse import mybir

F32 = mybir.dt.float32
I32 = mybir.dt.int32
ALU = mybir.AluOpType
ACT = mybir.ActivationFunctionType
AX = mybir.AxisListType
ET = mybir.EngineType
ADD, SUB, MUL, MAX, MIN = ALU.add, ALU.subtract, ALU.mult, ALU.max, ALU.min

BATCH, SIDE, PATCH, CHANNELS, D = 32, 96, 16, 3, 256
GRID = SIDE // PATCH
L = GRID * GRID + 1
SEQS = 3
P = SEQS * L
T = -(-BATCH // SEQS)
NTOK = T * P
PD = CHANNELS * PATCH * PATCH
PC = PD // 128
H16, DH = 16, 16
G = 3
GC = NTOK // G
GS = GC // L
E0, F0 = 8, 1024
E2, F2 = 8, 128
E3, K3, F3, CAP = 64, 8, 192, 128
FH = F3 // 2
SLOTS = E3 * CAP
SLOT_ROWS = SLOTS + 7 * 128
CW = P + L
LAMBDA_INIT = 0.8 - 0.6 * math.exp(-0.3 * 12)
LEVELS = 6
NEG = -1e30
OVERFLOW = 20000.0


def tile(t, i):
    return t[:, bass.ds(i, 1), :].rearrange("p a n -> p (a n)")


def cols(t, i):
    return t[:, :, bass.ds(i * P, P)]


def spread(ap, axis, n):
    ap = ap.unsqueeze(axis)
    shape = list(ap.shape)
    shape[axis] = n
    return ap.to_broadcast(shape)


SMALL = [
    ("ident", 128), ("mask8", 8), ("vm16", 16), ("vm8", 8), ("alibi", H16 * L), ("mb", SEQS),
    ("cos", DH), ("sin", DH), ("blk", 128), ("tri", P), ("strict", P), ("lvl", LEVELS * P),
    ("lvlT", LEVELS * P), ("mtm", P), ("below8", 64), ("ebase", E3), ("trash", K3), ("run", P), ("sgn", 1),
    ("base", D), ("ln2_w", D), ("b_out0", D), ("b_v0", D), ("ln_w", 32), ("ln_b", 32), ("lam", 64),
    ("qkv_b", 3 * D), ("proj_b", D), ("beta_w", D), ("norm1_row", D), ("beta_b", 1), ("range", 1),
    ("cn_b4", 1), ("gc_b3", 1), ("ln1_w", PC), ("b_q0", 2), ("b_k0", 2), ("b2", 2 * E0), ("cn_b1", 2),
    ("cn_b2", 1), ("cn_b3", 1), ("gc_b1", 1), ("gc_b2", 1), ("alpha", 2), ("norm1", 2), ("norm2", 2),
]
WEIGHTS = [
    ("tok", [("w_tok", PC * D)]),
    ("l0a", [("w_in", 2 * 3 * D), ("w_out", 2 * D), ("gate0", 2 * E0)]),
    ("l1a", [("qk1", 2 * 2 * D), ("v1", 2 * D), ("o1", 2 * D)]),
    ("l1f", [("cn1", 2 * D), ("cn2", 2 * 128), ("cn3", 64), ("cn4", 128), ("gc1", 2 * 128), ("gc2", 64),
             ("gc3", 128)]),
    ("l2a", [("qkv2", 2 * 3 * D), ("proj2", 2 * D), ("gate2", 2 * E2)]),
    ("l2f", [("w1_2", E2 * 2 * F2), ("w3_2", E2 * 2 * F2), ("w2_2", E2 * D)]),
    ("l3a", [("qk3", 2 * 2 * D), ("v3", 2 * D), ("o3", 2 * D), ("gate3", 2 * 512), ("up3", 2 * 512),
             ("down3", 4 * D)]),
    ("l3f", [("router", 2 * E3), ("ws_gu", 2 * 2 * F3), ("ws_down", 2 * D)]),
]


class Mem:
    pass


def setup_memory(nc, ctx, dram):
    M = Mem()
    M.dram = dram

    def sb(name, shape, dt=F32):
        return ctx.enter_context(nc.sbuf_tensor(name, shape, dt))

    M.h = sb("h", [P, T, D])
    M.x = sb("x", [P, T, D])
    M.xT = sb("xT", [128, 2, NTOK])
    M.yT = sb("yT", [128, 2, NTOK])
    M.stats = sb("stats", [P, T, 6])
    M.mean = sb("mean", [P, T])
    M.std = sb("std", [P, T])
    M.rstd = sb("rstd", [P, T])
    M.tmp = sb("ln_tmp", [P, 4, T])
    M.small = sb("small", [128, sum(n for _, n in SMALL)])
    M.at, o = {}, 0
    for name, n in SMALL:
        M.at[name] = (o, n)
        o += n
    M.w, M.loaded = {}, {}
    for array, parts in WEIGHTS:
        buf = sb("w_" + array, [128, sum(n for _, n in parts)])
        M.loaded[array] = ctx.enter_context(nc.semaphore("loaded_" + array))
        M.w[array] = buf
        o = 0
        for name, n in parts:
            M.w[name] = buf[:, o:o + n]
            o += n
    M.w8 = sb("w8", [P, T, K3])
    M.idx8 = sb("idx8", [P, T, K3], I32)
    sems = {}

    def shared_sem(name):
        if name not in sems:
            sems[name] = ctx.enter_context(nc.semaphore(name))
        return sems[name]

    M.sem = shared_sem
    M.bank = [ctx.enter_context(nc.psum_tensor(f"bank{b}", [128, 512], F32)) for b in range(8)]
    M.small_loaded = ctx.enter_context(nc.semaphore("small_loaded"))
    M.slots_cleared = ctx.enter_context(nc.semaphore("slots_cleared"))
    return M


def small(M, name, parts=P):
    o, n = M.at[name]
    return M.small[0:parts, o:o + n]


def dve_ln_stats(nc, v, M, var_ready, std_ready, eps=1e-5):
    with nc.Fori(0, T, engines=(ET.DVE,)) as i:
        nc.vector.bn_stats(tile(M.stats, i), tile(M.h, i))
    v.drain()
    me, ve, mo, vo = (M.stats[:, :, c] for c in (1, 2, 4, 5))
    t0, t1 = M.tmp[:, 0, :], M.tmp[:, 1, :]
    t2, t3 = M.tmp[:, 2, :], M.tmp[:, 3, :]
    nc.vector.tensor_tensor(t0, me, mo, ADD)
    nc.vector.tensor_tensor(t1, me, mo, SUB)
    nc.vector.tensor_tensor(t2, ve, vo, ADD)
    v.drain()
    nc.vector.tensor_scalar(M.mean[:, :], t0, 0.5, None, MUL)
    nc.vector.tensor_tensor(t3, t1, t1, MUL)
    v.drain()
    nc.vector.tensor_scalar(t0, t2, 1.0 / D, eps, MUL, ADD)
    nc.vector.tensor_scalar(t1, t3, 0.25, None, MUL)
    v.drain()
    nc.vector.tensor_tensor(t2, t0, t1, ADD).then_inc(var_ready, 1)
    v.wait_ge(std_ready, 1)
    v.sem_inc(std_ready, -1)
    nc.vector.reciprocal(M.rstd[:, :], M.std[:, :])
    v.drain()


def act_ln_std(nc, a, M, var_ready, std_ready):
    a.wait_ge(var_ready, 1)
    a.sem_inc(var_ready, -1)
    nc.scalar.activation(M.std[:, :], M.tmp[:, 2, :], ACT.Sqrt).then_inc(std_ready, 1)


def ln_apply(nc, M, i, out):
    return nc.vector.tensor_scalar(out, tile(M.h, i), M.mean[:, bass.ds(i, 1)], M.rstd[:, bass.ds(i, 1)],
                                   SUB, MUL)


def pe_turn(nc, M, bank, src, n=2):
    for c in range(n):
        last = nc.tensor.transpose(M.bank[bank][:, c * P:(c + 1) * P], src[:, c * 128:(c + 1) * 128],
                                   small(M, "ident")[:, 0:P])
    return last


def turned(M, bank, n=2):
    return M.bank[bank][:, 0:n * P].rearrange("p (c t) -> p c t", c=n)


def load_everything(nc, M):
    with ExitStack() as ctx:
        zero = ctx.enter_context(nc.sbuf_tensor("zero", [128, D], F32))
        zero_set = ctx.enter_context(nc.semaphore("zero_set"))
        with nc.Block(name="load") as block:
            @block.sync
            def _(sp):
                sp.dma_start(M.small[:, :], M.dram["small"]).then_inc(M.small_loaded, 16)
                for array, _ in WEIGHTS:
                    sp.dma_start(M.w[array][:, :], M.dram[array]).then_inc(M.loaded[array], 16)

            @block.gpsimd
            def _(pool):
                nc.gpsimd.memset(zero[:, :], 0.0).then_inc(zero_set, 1)

            @block.scalar
            def _(act):
                act.wait_ge(zero_set, 1)
                rows = M.dram["slots_x"].rearrange("(p r) d -> p r d", p=128)
                act.dma_start(rows, spread(zero[:, :], 1, rows.shape[1])).then_inc(M.slots_cleared, 16)
                act.wait_ge(M.slots_cleared, 16)


def patch_embedding(nc, M):
    with ExitStack() as ctx:
        sb = lambda n, s: ctx.enter_context(nc.sbuf_tensor(n, s, F32))
        sem = M.sem
        patches = sb("patches", [P, T, PD])
        xn = sb("tok_xn", [P, PD])
        xT = sb("tok_xT", [128, PC, P])
        st = sb("tok_st", [P, 12])
        mv = sb("tok_mv", [P, 2])
        var = sb("tok_var", [P, 1])
        std = sb("tok_std", [P, 1])
        rs = sb("tok_rs", [P, 1])
        y = sb("tok_y", [P, D])
        patches_in, var_ready, std_ready = sem("patches_in"), sem("tok_var_ready"), sem("tok_std_ready")
        xn_ready, turned_ready, xT_ready = sem("tok_xn_ready"), sem("tok_turned"), sem("tok_xT_ready")
        emb_ready, emb_read, w_scaled = sem("tok_emb_ready"), sem("tok_emb_read"), sem("tok_w_scaled")
        w = M.w["w_tok"].rearrange("p (c n) -> p c n", c=PC)
        with nc.Block(name="patch_embedding") as block:
            @block.sync
            def _(sp):
                sp.dma_start(patches[:, :, :], M.dram["patches"].rearrange("t p n -> p t n")).then_inc(patches_in, 16)

            @block.vector
            def _(v):
                v.wait_ge(M.small_loaded, 16)
                v.wait_ge(M.loaded["tok"], 16)
                for c in range(PC):
                    last = nc.vector.tensor_scalar(w[:, c, :], w[:, c, :], small(M, "ln1_w", 128)[:, c:c + 1],
                                                   None, MUL)
                last.then_inc(w_scaled, 1)

                v.wait_ge(patches_in, 16)
                v.sem_inc(patches_in, -16)

                def norm(src, halves, n, out, done):
                    for k in range(halves):
                        nc.vector.bn_stats(st[:, 6 * k:6 * k + 6], src[:, n * k:n * k + n])
                    v.drain()
                    nc.vector.bn_aggr(mv[:, :], st[:, 0:6 * halves])
                    v.drain()
                    nc.vector.tensor_scalar(var[:, :], mv[:, 1:2], 1e-5, None, ADD).then_inc(var_ready, 1)
                    v.wait_ge(std_ready, 1)
                    v.sem_inc(std_ready, -1)
                    nc.vector.reciprocal(rs[:, :], std[:, :])
                    v.drain()
                    nc.vector.tensor_scalar(out, src, mv[:, 0:1], rs[:, 0:1], SUB, MUL).then_inc(done, 1)

                with nc.Fori(0, T, engines=(ET.DVE,)) as i:
                    norm(tile(patches, i), 2, PD // 2, xn[:, :], xn_ready)
                    v.wait_ge(emb_ready, 1)
                    v.sem_inc(emb_ready, -1)
                    norm(M.bank[2][0:P, 0:D], 1, D, y[:, :], emb_read)
                    v.drain()
                    nc.vector.tensor_tensor(y[:, :], y[:, :], small(M, "ln2_w"), MUL)
                    v.drain()
                    nc.vector.tensor_tensor(tile(M.h, i), y[:, :], small(M, "base"), ADD)
                    v.drain()

            @block.scalar
            def _(a):
                a.preload_act_table(ACT.Sqrt)
                with nc.Fori(0, T, engines=(ET.Activation,)) as i:
                    a.wait_ge(var_ready, 1)
                    a.sem_inc(var_ready, -1)
                    nc.scalar.activation(std[:, :], var[:, :], ACT.Sqrt).then_inc(std_ready, 1)
                    a.wait_ge(turned_ready, 1)
                    a.sem_inc(turned_ready, -1)
                    nc.scalar.copy(xT[:, 0:4, :], turned(M, 0, 4))
                    nc.scalar.copy(xT[:, 4:PC, :], turned(M, 1, PC - 4)).then_inc(xT_ready, 1)
                    a.wait_ge(var_ready, 1)
                    a.sem_inc(var_ready, -1)
                    nc.scalar.activation(std[:, :], var[:, :], ACT.Sqrt).then_inc(std_ready, 1)

            @block.tensor
            def _(pe):
                pe.wait_ge(M.small_loaded, 16)
                pe.wait_ge(w_scaled, 1)
                pe.sem_inc(w_scaled, -1)
                with nc.Fori(0, T, engines=(ET.PE,)) as i:
                    pe.wait_ge(xn_ready, 1)
                    pe.sem_inc(xn_ready, -1)
                    pe_turn(nc, M, 0, xn[:, 0:512], 4)
                    pe_turn(nc, M, 1, xn[:, 512:PD], PC - 4).then_inc(turned_ready, 1)
                    pe.wait_ge(xT_ready, 1)
                    pe.sem_inc(xT_ready, -1)
                    for c in range(PC):
                        last = nc.tensor.matmul(M.bank[2][0:P, 0:D], xT[:, c, :], w[:, c, :],
                                                start=(c == 0), stop=(c == PC - 1))
                    last.then_inc(emb_ready, 1)
                    pe.wait_ge(emb_read, 1)
                    pe.sem_inc(emb_read, -1)


def pe_turn_tiles(nc, pe, M, xn, xn_ready, turned_ready, turned_read):
    with nc.Fori(0, T, engines=(ET.PE,)) as i:
        pe.wait_ge(xn_ready, 1)
        pe.sem_inc(xn_ready, -1)
        pe_turn(nc, M, 0, xn).then_inc(turned_ready, 1)
        pe.wait_ge(turned_read, 1)
        pe.sem_inc(turned_read, -1)


def add_back(nc, M, name):
    with ExitStack() as ctx:
        sem = M.sem
        y = ctx.enter_context(nc.sbuf_tensor("back_y" + name, [128, 2, P], F32))
        y_ready, back_ready, y_free, back_read = sem("y_ready"), sem("back_ready"), sem("y_free"), sem("back_read")
        with nc.Block(name="add_back" + name) as block:
            @block.scalar
            def _(a):
                with nc.Fori(0, T, engines=(ET.Activation,)) as i:
                    nc.scalar.copy(y[:, :, :], cols(M.yT, i)).then_inc(y_ready, 1)
                    a.wait_ge(y_free, 1)
                    a.sem_inc(y_free, -1)

            @block.tensor
            def _(pe):
                with nc.Fori(0, T, engines=(ET.PE,)) as i:
                    pe.wait_ge(y_ready, 1)
                    pe.sem_inc(y_ready, -1)
                    for c in range(2):
                        last = nc.tensor.transpose(M.bank[0][0:P, c * 128:(c + 1) * 128], y[:, c, :],
                                                   small(M, "ident", 128))
                    last.then_inc(back_ready, 1)
                    pe.wait_ge(back_read, 1)
                    pe.sem_inc(back_read, -1)

            @block.vector
            def _(v):
                with nc.Fori(0, T, engines=(ET.DVE,)) as i:
                    v.wait_ge(back_ready, 1)
                    v.sem_inc(back_ready, -1)
                    v.sem_inc(y_free, 1)
                    nc.vector.tensor_tensor(tile(M.h, i), tile(M.h, i), M.bank[0][0:P, 0:D], ADD
                                            ).then_inc(back_read, 1)
                v.drain()


def evacuate_q(nc, M, bank, qm, bias=None):
    for c in range(2):
        out = qm[:, c, :].rearrange("p (s w) -> p s w", w=CW)[:, :, 0:L]
        src = M.bank[bank][:, c * P:(c + 1) * P].rearrange("p (s j) -> p s j", s=SEQS)
        last = nc.vector.tensor_scalar(out, src, bias[:, c:c + 1] if bias is not None else 0.0, None, ADD)
    return last


def mask_k_heads(nc, M, kT, km):
    for c in range(2):
        last = nc.vector.tensor_tensor(km[:, c, :, :], spread(kT[:, c, :], 1, 8),
                                       spread(small(M, "mask8", 128), 2, P), MUL)
    return last


def pe_scores(nc, M, bank0, qm, km):
    for c in range(2):
        for s in range(SEQS):
            last = nc.tensor.matmul(M.bank[bank0 + c][0:P, 0:8 * L], qm[:, c, s * P:(s + 1) * P],
                                    km[:, c, :, s * L:(s + 1) * L], start=(s == 0), stop=(s == SEQS - 1))
    return last


def pe_turn_probs(nc, M, bank0, probs, maps):
    groups = -(-maps // 3)
    for g in range(groups):
        n = min(3, maps - 3 * g) * L
        out = M.bank[bank0 + g // 4][0:n, (g % 4) * P:(g % 4 + 1) * P]
        last = nc.tensor.transpose(out, probs[:, 3 * g * L:3 * g * L + n], small(M, "ident")[:, 0:P])
    return last


def evacuate_probs(nc, M, bank0, pm, maps):
    groups = -(-maps // 3)
    full = maps // 3
    pieces = [(g, min(g + 4, full), P) for g in range(0, full, 4)]
    if groups > full:
        pieces.append((full, groups, (maps - 3 * full) * L))
    for g0, g1, n in pieces:
        b = M.bank[bank0 + g0 // 4]
        o = g0 % 4
        for g in range(g0, g1):
            src = b[0:n, (o + g - g0) * P:(o + g - g0 + 1) * P].rearrange("p (s j) -> p s j", s=SEQS)
            out = pm[0:n, g, :].rearrange("p (s w) -> p s w", w=CW)[:, :, 0:L]
            last = nc.scalar.copy(out, src)
    return last


def pe_values(nc, M, bank, pm, vm, maps, dv):
    for g in range(-(-maps // 3)):
        k = min(3, maps - 3 * g)
        for s in range(SEQS):
            last = nc.tensor.matmul(M.bank[bank][0:P, 3 * g * dv:(3 * g + k) * dv],
                                    pm[0:k * L, g, s * P:(s + 1) * P],
                                    vm[0:k * L, s, 3 * g * dv:(3 * g + k) * dv],
                                    start=(s == 0), stop=(s == SEQS - 1))
    return last


def pe_project(nc, M, bank, lhs, w, n0, n1, rows=P, first=0, col=0):
    for k in range(2):
        last = nc.tensor.matmul(M.bank[bank][0:rows, col:col + n1 - n0], lhs[:, k, :], w[:, k, n0:n1],
                                start=(k == 0), stop=(k == 1))
    return last


def repeat_x(nc, M, xr):
    for k in range(2):
        src = M.bank[0][:, k * P:(k + 1) * P].rearrange("p (s j) -> p s j", s=SEQS)
        last = nc.scalar.copy(xr[:, k, :, :].rearrange("p s (r j) -> p s r j", r=3), spread(src, 2, 3))
    return last


def pe_values_in(nc, M, xr, w, n0):
    for s in range(SEQS):
        for k in range(2):
            last = nc.tensor.matmul(M.bank[2 + s // 2][0:P, (s % 2) * D:(s % 2 + 1) * D],
                                    xr[:, k, s, :],
                                    w[:, k, n0:n0 + D], start=(k == 0), stop=(k == 1))
    return last


def mask_v(nc, M, vm, mask, maps):
    dv = D // maps
    m = spread(mask, 2, dv)
    for s in range(SEQS):
        src = M.bank[2 + s // 2][0:P, (s % 2) * D:(s % 2 + 1) * D].rearrange("p (m d) -> p m d", m=maps)
        last = nc.vector.tensor_tensor(vm[:, s, :].rearrange("p (m d) -> p m d", m=maps), src, m, MUL)
    return last


def alibi_attention(nc, M):
    with ExitStack() as ctx:
        sb = lambda n, s: ctx.enter_context(nc.sbuf_tensor("a0_" + n, s, F32))
        sem = M.sem
        xn, xT, kT = sb("xn", [P, D]), sb("xT", [128, 2, P]), sb("kT", [128, 2, P])
        xr, xr_ready = sb("xr", [128, 2, SEQS, P]), sem("xr_ready")
        qm, km = sb("qm", [128, 2, SEQS * CW]), sb("km", [128, 2, 8, P])
        vm, S, Pr = sb("vm", [P, SEQS, D]), sb("S", [P, H16, L]), sb("Pr", [P, H16, L])
        mx, rsum = sb("mx", [P, H16]), sb("rsum", [P, H16])
        pm, o, oT, y = sb("pm", [P, 6, SEQS * CW]), sb("o", [P, D]), sb("oT", [128, 2, P]), sb("y", [P, D])
        var_ready, std_ready = sem("var_ready"), sem("std_ready")
        blank, xn_ready, turned_ready, xT_ready = sem("blank"), sem("xn_ready"), sem("turned"), sem("xT_ready")
        q_ready, k_ready, v_ready = sem("q_ready"), sem("k_ready"), sem("v_ready")
        kT_ready, km_ready, vm_ready = sem("kT_ready"), sem("km_ready"), sem("vm_ready")
        s_ready, shifted, probs_dve, probs_pe = sem("s_ready"), sem("shifted"), sem("probs_dve"), sem("probs_pe")
        pT_ready, pm_ready, o_ready, on_ready = sem("pT_ready"), sem("pm_ready"), sem("o_ready"), sem("on_ready")
        oT_turned, oT_ready, y_ready = sem("oT_turned"), sem("oT_ready"), sem("y_ready")
        pblank = sem("pblank")
        w = M.w["w_in"].rearrange("p (k n) -> p k n", k=2)
        wo = M.w["w_out"].rearrange("p (k n) -> p k n", k=2)
        with nc.Block(name="alibi_attention") as block:
            @block.gpsimd
            def _(pool):
                nc.gpsimd.memset(qm[:, :, :], 0.0).then_inc(blank, 1)
                nc.gpsimd.memset(pm[:, :, :], 0.0).then_inc(pblank, 1)

            @block.vector
            def _(v):
                dve_ln_stats(nc, v, M, var_ready, std_ready)
                v.wait_ge(blank, 1)
                v.sem_inc(blank, -1)
                with nc.Fori(0, T, engines=(ET.DVE,)) as i:
                    ln_apply(nc, M, i, xn[:, :]).then_inc(xn_ready, 1)
                    v.wait_ge(q_ready, 1)
                    v.sem_inc(q_ready, -1)
                    evacuate_q(nc, M, 1, qm, small(M, "b_q0", 128))
                    v.wait_ge(kT_ready, 1)
                    v.sem_inc(kT_ready, -1)
                    mask_k_heads(nc, M, kT, km).then_inc(km_ready, 1)
                    v.wait_ge(v_ready, 1)
                    v.sem_inc(v_ready, -1)
                    mask_v(nc, M, vm, small(M, "vm16"), H16).then_inc(vm_ready, 1)
                    v.wait_ge(s_ready, 1)
                    v.sem_inc(s_ready, -1)
                    for c in range(2):
                        m = slice(8 * c, 8 * c + 8)
                        nc.vector.scalar_tensor_tensor(
                            S[:, m, :], M.bank[4 + c][0:P, 0:8 * L].rearrange("p (m j) -> p m j", m=8),
                            DH ** -0.5, small(M, "alibi").rearrange("p (m j) -> p m j", m=H16)[:, m, :], MUL, ADD)
                    v.drain()
                    nc.vector.tensor_reduce(mx[:, :], S[:, :, :], AX.X, MAX)
                    v.drain()
                    nc.vector.tensor_tensor(S[:, :, :], S[:, :, :], spread(mx[:, :], 2, L), SUB).then_inc(shifted, 1)
                    v.wait_ge(probs_dve, 1)
                    v.sem_inc(probs_dve, -1)
                    nc.vector.tensor_reduce(mx[:, :], Pr[:, :, :], AX.X, ADD)
                    v.drain()
                    nc.vector.reciprocal(rsum[:, :], mx[:, :])
                    v.drain()
                    v.wait_ge(o_ready, 1)
                    v.sem_inc(o_ready, -1)
                    nc.vector.tensor_tensor(o[:, :].rearrange("p (m d) -> p m d", m=H16),
                                            M.bank[5][0:P, 0:D].rearrange("p (m d) -> p m d", m=H16),
                                            spread(rsum[:, :], 2, DH), MUL)
                    v.drain()
                    nc.vector.tensor_tensor(o[:, :], o[:, :], small(M, "b_v0"), ADD).then_inc(on_ready, 1)
                    v.wait_ge(y_ready, 1)
                    v.sem_inc(y_ready, -1)
                    nc.vector.tensor_tensor(y[:, :], M.bank[1][0:P, 0:D], small(M, "b_out0"), ADD)
                    v.drain()
                    nc.vector.tensor_tensor(tile(M.h, i), tile(M.h, i), y[:, :], ADD)
                    v.drain()

            @block.scalar
            def _(a):
                act_ln_std(nc, a, M, var_ready, std_ready)
                a.preload_act_table(ACT.Exp)
                a.wait_ge(pblank, 1)
                a.sem_inc(pblank, -1)
                with nc.Fori(0, T, engines=(ET.Activation,)) as i:
                    a.wait_ge(turned_ready, 1)
                    a.sem_inc(turned_ready, -1)
                    nc.scalar.copy(xT[:, :, :], turned(M, 0)).then_inc(xT_ready, 1)
                    repeat_x(nc, M, xr).then_inc(xr_ready, 1)
                    a.wait_ge(k_ready, 1)
                    a.sem_inc(k_ready, -1)
                    for c in range(2):
                        last = nc.scalar.activation(kT[:, c, :], M.bank[7][:, c * P:(c + 1) * P], ACT.Identity,
                                                    bias=small(M, "b_k0", 128)[:, c:c + 1])
                    last.then_inc(kT_ready, 1)
                    a.wait_ge(shifted, 1)
                    a.sem_inc(shifted, -1)
                    nc.scalar.activation(Pr[:, :, :], S[:, :, :], ACT.Exp).then_inc(probs_dve, 1)
                    a.drain().then_inc(probs_pe, 1)
                    a.wait_ge(pT_ready, 1)
                    a.sem_inc(pT_ready, -1)
                    evacuate_probs(nc, M, 6, pm, H16).then_inc(pm_ready, 1)
                    a.wait_ge(oT_turned, 1)
                    a.sem_inc(oT_turned, -1)
                    nc.scalar.copy(oT[:, :, :], turned(M, 0)).then_inc(oT_ready, 1)
                    a.drain()

            @block.tensor
            def _(pe):
                pe.wait_ge(M.loaded["l0a"], 16)
                with nc.Fori(0, T, engines=(ET.PE,)) as i:
                    pe.wait_ge(xn_ready, 1)
                    pe.sem_inc(xn_ready, -1)
                    pe_turn(nc, M, 0, xn).then_inc(turned_ready, 1)
                    pe.wait_ge(xT_ready, 1)
                    pe.sem_inc(xT_ready, -1)
                    for c in range(4):
                        last = pe_project(nc, M, 1 if c < 2 else 7, w[:, :, c * 128:(c + 1) * 128], xT, 0, P, 128,
                                          col=c % 2 * P)
                        if c == 1:
                            last.then_inc(q_ready, 1)
                    last.then_inc(k_ready, 1)
                    pe.wait_ge(xr_ready, 1)
                    pe.sem_inc(xr_ready, -1)
                    pe_values_in(nc, M, xr, w, 2 * D).then_inc(v_ready, 1)
                    pe.wait_ge(km_ready, 1)
                    pe.sem_inc(km_ready, -1)
                    pe_scores(nc, M, 4, qm, km).then_inc(s_ready, 1)
                    pe.wait_ge(probs_pe, 1)
                    pe.sem_inc(probs_pe, -1)
                    pe_turn_probs(nc, M, 6, Pr[:, :, :].rearrange("p m j -> p (m j)"), H16).then_inc(pT_ready, 1)
                    pe.wait_ge(vm_ready, 1)
                    pe.sem_inc(vm_ready, -1)
                    pe.wait_ge(pm_ready, 1)
                    pe.sem_inc(pm_ready, -1)
                    pe_values(nc, M, 5, pm, vm, H16, DH).then_inc(o_ready, 1)
                    pe.wait_ge(on_ready, 1)
                    pe.sem_inc(on_ready, -1)
                    pe_turn(nc, M, 0, o).then_inc(oT_turned, 1)
                    pe.wait_ge(oT_ready, 1)
                    pe.sem_inc(oT_ready, -1)
                    pe_project(nc, M, 1, oT, wo, 0, D).then_inc(y_ready, 1)


def gate_top2(nc, M, name, gate, dram_cw, full_softmax):
    E = 8
    with ExitStack() as ctx:
        sb = lambda n, s: ctx.enter_context(nc.sbuf_tensor(name + n, s, F32))
        sem = M.sem
        xn, xT = sb("xn", [P, D]), sb("xT", [128, 2, P])
        lg, neg, ex, gt, eq = sb("lg", [P, E]), sb("neg", [P, 1]), sb("ex", [P, E]), sb("gt", [P, E, E]), sb("eq", [P, E, E])
        rank, mask, se, re, cw = sb("rank", [P, E]), sb("mask", [P, E]), sb("se", [P, 1]), sb("re", [P, 1]), sb("cw", [P, E])
        cwT = sb("cwT", [E, P])
        var_ready, std_ready, xn_ready = sem("var_ready"), sem("std_ready"), sem("xn_ready")
        turned_ready, xT_ready, lg_ready = sem("turned"), sem("xT_ready"), sem("lg_ready")
        shifted, ex_ready, cw_ready, cwT_turned = sem("shifted"), sem("ex_ready"), sem("cw_ready"), sem("cwT_turned")
        cwT_ready, cw_stored = sem("cwT_ready"), sem("cw_stored")
        w = gate.rearrange("p (k n) -> p k n", k=2)
        with nc.Block(name=name) as block:
            @block.vector
            def _(v):
                dve_ln_stats(nc, v, M, var_ready, std_ready)
                with nc.Fori(0, T, engines=(ET.DVE,)) as i:
                    ln_apply(nc, M, i, xn[:, :]).then_inc(xn_ready, 1)
                    v.wait_ge(lg_ready, 1)
                    v.sem_inc(lg_ready, -1)
                    nc.vector.tensor_copy(lg[:, :], M.bank[1][0:P, 0:E])
                    v.drain()
                    nc.vector.tensor_reduce(neg[:, :], lg[:, :], AX.X, MAX)
                    other, own = spread(lg[:, :], 1, E), spread(lg[:, :], 2, E)
                    nc.vector.tensor_tensor(gt[:, :, :], other, own, ALU.is_gt)
                    nc.vector.tensor_tensor(eq[:, :, :], other, own, ALU.is_equal)
                    v.drain()
                    nc.vector.tensor_scalar(ex[:, :], lg[:, :], neg[:, 0:1], None, SUB).then_inc(shifted, 1)
                    nc.vector.tensor_tensor(eq[:, :, :], eq[:, :, :],
                                            small(M, "below8").rearrange("p (a b) -> p a b", a=E), MUL)
                    v.drain()
                    nc.vector.tensor_tensor(gt[:, :, :], gt[:, :, :], eq[:, :, :], ADD)
                    v.drain()
                    nc.vector.tensor_reduce(rank[:, :], gt[:, :, :], AX.X, ADD)
                    v.drain()
                    nc.vector.tensor_scalar(mask[:, :], rank[:, :], 2.0, None, ALU.is_lt)
                    v.wait_ge(ex_ready, 1)
                    v.sem_inc(ex_ready, -1)
                    v.drain()
                    nc.vector.tensor_tensor(cw[:, :], ex[:, :], mask[:, :], MUL)
                    v.drain()
                    nc.vector.tensor_reduce(se[:, :], ex[:, :] if full_softmax else cw[:, :], AX.X, ADD)
                    v.drain()
                    nc.vector.reciprocal(re[:, :], se[:, :])
                    v.drain()
                    nc.vector.tensor_scalar(cw[:, :], cw[:, :], re[:, 0:1], None, MUL).then_inc(cw_ready, 1)
                    v.drain()

            @block.scalar
            def _(a):
                act_ln_std(nc, a, M, var_ready, std_ready)
                a.preload_act_table(ACT.Exp)
                with nc.Fori(0, T, engines=(ET.Activation,)) as i:
                    a.wait_ge(turned_ready, 1)
                    a.sem_inc(turned_ready, -1)
                    nc.scalar.copy(xT[:, :, :], turned(M, 0)).then_inc(xT_ready, 1)
                    nc.scalar.copy(cols(M.xT, i), turned(M, 0))
                    a.wait_ge(shifted, 1)
                    a.sem_inc(shifted, -1)
                    nc.scalar.activation(ex[:, :], ex[:, :], ACT.Exp).then_inc(ex_ready, 1)
                    a.wait_ge(cwT_turned, 1)
                    a.sem_inc(cwT_turned, -1)
                    nc.scalar.copy(cwT[:, :], M.bank[2][0:E, 0:P])
                    a.drain()
                    a.dma_start(dram_cw[:, bass.ds(i * P, P)], cwT[:, :]).then_inc(cw_stored, 16)
                    a.wait_ge(cw_stored, 16)
                    a.sem_inc(cw_stored, -16)

            @block.tensor
            def _(pe):
                with nc.Fori(0, T, engines=(ET.PE,)) as i:
                    pe.wait_ge(xn_ready, 1)
                    pe.sem_inc(xn_ready, -1)
                    pe_turn(nc, M, 0, xn).then_inc(turned_ready, 1)
                    pe.wait_ge(xT_ready, 1)
                    pe.sem_inc(xT_ready, -1)
                    pe_project(nc, M, 1, xT, w, 0, E).then_inc(lg_ready, 1)
                    pe.wait_ge(cw_ready, 1)
                    pe.sem_inc(cw_ready, -1)
                    nc.tensor.transpose(M.bank[2][0:E, 0:P], cw[:, :], small(M, "ident")[:, 0:P]).then_inc(cwT_turned, 1)


def experts0(nc, M):
    FC = F0 // 128
    with ExitStack() as ctx:
        sb = lambda n, s: ctx.enter_context(nc.sbuf_tensor("e0_" + n, s, F32))
        sem = M.sem
        w1 = [sb(f"w1_{b}", [128, 2, F0]) for b in range(2)]
        w2 = [sb(f"w2_{b}", [128, FC, D]) for b in range(2)]
        b1 = [sb(f"b1_{b}", [128, FC]) for b in range(2)]
        cw = [sb(f"cw_{b}", [128, NTOK]) for b in range(2)]
        b2 = [sb(f"b2_{b}", [128, 2]) for b in range(2)]
        hid = [sb(f"hid_{b}", [128, GC]) for b in range(2)]
        yw = sb("yw", [128, 2, GC])
        loaded = [sem(f"loaded_{b}") for b in range(2)]
        loaded_act = [sem(f"loaded_act_{b}") for b in range(2)]
        cw_loaded = [sem(f"cw_loaded_{b}") for b in range(2)]
        used, cw_used = [sem(f"e0_used_{b}") for b in range(2)], [sem(f"e0_cw_used_{b}") for b in range(2)]
        h1_ready, hid_ready, y_ready, y_read = sem("h1_ready"), sem("hid_ready"), sem("y_ready"), sem("e0_y_read")
        xg = M.xT[:, :, :].rearrange("p k (g n) -> p k g n", g=G)
        yg = M.yT[:, :, :].rearrange("p k (g n) -> p k g n", g=G)
        with nc.Block(name="experts0") as block:
            @block.sync
            def _(sp):
                with nc.Fori(0, E0 // 2, engines=(ET.SP,)) as p:
                    for b in range(2):
                        e = p * 2 + b
                        sp.wait_ge(used[b], 1)
                        sp.sem_inc(used[b], -1)
                        sp.dma_start(w1[b][:, :, :].rearrange("p k n -> p (k n)"),
                                     M.dram["w1_0"][bass.ds(e, 1)].rearrange("a p n -> (a p) n")).then_inc(loaded[b], 16)
                        sp.dma_start(w2[b][:, :, :].rearrange("p k n -> p (k n)"),
                                     M.dram["w2_0"][bass.ds(e, 1)].rearrange("a p n -> (a p) n")).then_inc(loaded[b], 16)
                        sp.dma_start(b1[b][:, :],
                                     M.dram["b1_0"][bass.ds(e, 1)].rearrange("a p n -> (a p) n")).then_inc(loaded_act[b], 16)
                        sp.wait_ge(cw_used[b], 1)
                        sp.sem_inc(cw_used[b], -1)
                        sp.dma_start(b2[b][:, :],
                                     M.dram["b2_0"][bass.ds(e, 1)].rearrange("a p n -> (a p) n")).then_inc(cw_loaded[b], 16)
                        sp.dma_start(cw[b][:, :],
                                     M.dram["cw0"][bass.ds(e, 1), :].rearrange("a n -> (a n)").partition_broadcast(128)
                                     ).then_inc(cw_loaded[b], 16)

            @block.tensor
            def _(pe):
                for b in range(2):
                    pe.sem_inc(used[b], 1)
                with nc.Fori(0, E0 // 2, engines=(ET.PE,)) as p:
                    for b in range(2):
                        pe.wait_ge(loaded[b], 32)
                        pe.sem_inc(loaded[b], -32)
                        with nc.Fori(0, G, engines=(ET.PE,)) as g:
                            x = xg[:, :, bass.ds(g, 1), :].rearrange("p k a n -> p k (a n)")

                            def up(f):
                                for k in range(2):
                                    last = nc.tensor.matmul(M.bank[f % 2][:, 0:GC], w1[b][:, k, f * 128:(f + 1) * 128],
                                                            x[:, k, :], start=(k == 0), stop=(k == 1))
                                last.then_inc(h1_ready, 1)

                            up(0)
                            for f in range(FC):
                                if f + 1 < FC:
                                    up(f + 1)
                                if f == 0:
                                    pe.wait_ge(y_read, 1)
                                    pe.sem_inc(y_read, -1)
                                pe.wait_ge(hid_ready, 1)
                                pe.sem_inc(hid_ready, -1)
                                for c in range(2):
                                    last = nc.tensor.matmul(M.bank[2 + c][:, 0:GC], w2[b][:, f, c * 128:(c + 1) * 128],
                                                            hid[f % 2][:, :], start=(f == 0), stop=(f == FC - 1))
                            last.then_inc(y_ready, 1)
                        pe.drain().then_inc(used[b], 1)

            @block.scalar
            def _(a):
                a.preload_act_table(ACT.Gelu)
                with nc.Fori(0, E0 // 2, engines=(ET.Activation,)) as p:
                    for b in range(2):
                        a.wait_ge(loaded_act[b], 16)
                        a.sem_inc(loaded_act[b], -16)
                        with nc.Fori(0, G, engines=(ET.Activation,)) as g:
                            for f in range(FC):
                                a.wait_ge(h1_ready, 1)
                                a.sem_inc(h1_ready, -1)
                                nc.scalar.activation(hid[f % 2][:, :], M.bank[f % 2][:, 0:GC], ACT.Gelu,
                                                     bias=b1[b][:, f:f + 1]).then_inc(hid_ready, 1)
                        a.drain()

            @block.vector
            def _(v):
                v.sem_inc(y_read, 1)
                for b in range(2):
                    v.sem_inc(cw_used[b], 1)
                nc.vector.memset(M.yT[:, :, :], 0.0)
                v.drain()
                with nc.Fori(0, E0 // 2, engines=(ET.DVE,)) as p:
                    for b in range(2):
                        v.wait_ge(cw_loaded[b], 32)
                        v.sem_inc(cw_loaded[b], -32)
                        with nc.Fori(0, G, engines=(ET.DVE,)) as g:
                            v.wait_ge(y_ready, 1)
                            v.sem_inc(y_ready, -1)
                            for c in range(2):
                                last = nc.vector.scalar_tensor_tensor(
                                    yw[:, c, :], M.bank[2 + c][:, 0:GC], b2[b][:, c:c + 1],
                                    cw[b][:, bass.ds(g * GC, GC)], ADD, MUL)
                            last.then_inc(y_read, 1)
                            v.drain()
                            y = yg[:, :, bass.ds(g, 1), :].rearrange("p k a n -> p k (a n)")
                            nc.vector.tensor_tensor(y, y, yw[:, :, :], ADD)
                            v.drain()
                        v.drain().then_inc(cw_used[b], 1)


def rotary_attention(nc, M):
    NH, DV = 8, 32
    with ExitStack() as ctx:
        sb = lambda n, s: ctx.enter_context(nc.sbuf_tensor("a1_" + n, s, F32))
        sem = M.sem
        xn, xT, kT = sb("xn", [P, D]), sb("xT", [128, 2, P]), sb("kT", [128, 2, P])
        xr, xr_ready = sb("xr", [128, 2, SEQS, P]), sem("xr_ready")
        qk, rot = sb("qk", [P, 2 * D]), sb("rot", [P, 2 * D])
        qm, km = sb("qm", [128, 2, SEQS * CW]), sb("km", [128, 2, 8, P])
        vm, S, Pr = sb("vm", [P, SEQS, D]), sb("S", [P, H16, L]), sb("Pr", [P, H16, L])
        A = sb("A", [P, NH, L])
        mx, rsum = sb("mx", [P, H16]), sb("rsum", [P, H16])
        pm, o, oT = sb("pm", [P, 3, SEQS * CW]), sb("o", [P, D]), sb("oT", [128, 2, P])
        ms, lamv, lam2, lam = sb("ms", [P, T, NH]), sb("lamv", [P, 32]), sb("lam2", [P, 2]), sb("lam", [P, 1])
        root, var_ready, std_ready = sb("root", [P, T, NH]), sem("var_ready"), sem("std_ready")
        blank, pblank, xn_ready, turned_ready = sem("blank"), sem("pblank"), sem("xn_ready"), sem("turned")
        xT_ready, qk_ready, v_ready, qk_rotated = sem("xT_ready"), sem("qk_ready"), sem("v_ready"), sem("qk_rotated")
        q_turned, k_turned, kT_ready, km_ready = sem("q_turned"), sem("k_turned"), sem("kT_ready"), sem("km_ready")
        vm_ready, s_ready, shifted, probs_ready = sem("vm_ready"), sem("s_ready"), sem("shifted"), sem("probs")
        A_ready, pT_ready, pm_ready, o_ready = sem("A_ready"), sem("pT_ready"), sem("pm_ready"), sem("o_ready")
        lam_dot, lam_exp, ms_ready, root_ready = sem("lam_dot"), sem("lam_exp"), sem("ms_ready"), sem("root_ready")
        on_ready, oT_turned, oT_ready, y_ready = sem("on_ready"), sem("oT_turned"), sem("oT_ready"), sem("y_ready")
        wqk = M.w["qk1"].rearrange("p (k n) -> p k n", k=2)
        wv = M.w["v1"].rearrange("p (k n) -> p k n", k=2)
        wo = M.w["o1"].rearrange("p (k n) -> p k n", k=2)
        with nc.Block(name="rotary_attention") as block:
            @block.gpsimd
            def _(pool):
                nc.gpsimd.memset(qm[:, :, :], 0.0).then_inc(blank, 1)
                nc.gpsimd.memset(pm[:, :, :], 0.0).then_inc(pblank, 1)

            @block.vector
            def _(v):
                dve_ln_stats(nc, v, M, var_ready, std_ready)
                lv = small(M, "lam").rearrange("p (i qk d) -> p i qk d", i=2, qk=2)
                nc.vector.tensor_tensor(lamv[:, :].rearrange("p (i d) -> p i d", i=2), lv[:, :, 0, :], lv[:, :, 1, :], MUL)
                nc.vector.tensor_scalar(small(M, "ln_w"), small(M, "ln_w"), 1.0 - LAMBDA_INIT, None, MUL)
                nc.vector.tensor_scalar(small(M, "ln_b"), small(M, "ln_b"), 1.0 - LAMBDA_INIT, None, MUL)
                v.drain()
                nc.vector.tensor_reduce(lam2[:, :], lamv[:, :].rearrange("p (i d) -> p i d", i=2), AX.X, ADD
                                        ).then_inc(lam_dot, 1)
                v.wait_ge(lam_exp, 1)
                v.sem_inc(lam_exp, -1)
                nc.vector.tensor_tensor(lam[:, :], lam2[:, 1:2], lam2[:, 0:1], SUB)
                v.drain()
                nc.vector.tensor_scalar(lam[:, :], lam[:, :], -LAMBDA_INIT, None, ADD)
                v.drain()
                v.wait_ge(blank, 1)
                v.sem_inc(blank, -1)
                cosv = spread(small(M, "cos"), 1, 2 * H16)
                sinv = small(M, "sin").rearrange("p (d e) -> p d e", e=2)
                with nc.Fori(0, T, engines=(ET.DVE,)) as i:
                    ln_apply(nc, M, i, xn[:, :]).then_inc(xn_ready, 1)
                    v.wait_ge(qk_ready, 1)
                    v.sem_inc(qk_ready, -1)
                    q3 = M.bank[1][0:P, :].rearrange("p (m d) -> p m d", d=DH)
                    nc.vector.tensor_tensor(qk[:, :].rearrange("p (m d) -> p m d", d=DH), q3, cosv, MUL)
                    q4 = M.bank[1][0:P, :].rearrange("p (m d e) -> p m d e", d=DH // 2, e=2)
                    r4 = rot[:, :].rearrange("p (m d e) -> p m d e", d=DH // 2, e=2)
                    for e in range(2):
                        nc.vector.tensor_tensor(r4[:, :, :, e], q4[:, :, :, 1 - e], spread(sinv[:, :, e], 1, 2 * H16), MUL)
                    v.drain()
                    nc.vector.tensor_tensor(qk[:, :], qk[:, :], rot[:, :], ADD).then_inc(qk_rotated, 1)
                    v.wait_ge(v_ready, 1)
                    v.sem_inc(v_ready, -1)
                    mask_v(nc, M, vm, small(M, "vm8"), NH).then_inc(vm_ready, 1)
                    v.wait_ge(q_turned, 1)
                    v.sem_inc(q_turned, -1)
                    evacuate_q(nc, M, 0, qm)
                    v.wait_ge(kT_ready, 1)
                    v.sem_inc(kT_ready, -1)
                    mask_k_heads(nc, M, kT, km).then_inc(km_ready, 1)
                    v.wait_ge(s_ready, 1)
                    v.sem_inc(s_ready, -1)
                    for c in range(2):
                        nc.vector.tensor_scalar(S[:, 8 * c:8 * c + 8, :],
                                                M.bank[4 + c][0:P, 0:8 * L].rearrange("p (m j) -> p m j", m=8),
                                                DH ** -0.25, None, MUL)
                    v.drain()
                    nc.vector.tensor_reduce(mx[:, :], S[:, :, :], AX.X, MAX)
                    v.drain()
                    nc.vector.tensor_tensor(S[:, :, :], S[:, :, :], spread(mx[:, :], 2, L), SUB).then_inc(shifted, 1)
                    v.wait_ge(probs_ready, 1)
                    v.sem_inc(probs_ready, -1)
                    nc.vector.tensor_reduce(mx[:, :], Pr[:, :, :], AX.X, ADD)
                    v.drain()
                    nc.vector.reciprocal(rsum[:, :], mx[:, :])
                    v.drain()
                    pair = rsum[:, :].rearrange("p (h i) -> p h i", i=2)
                    nc.vector.tensor_scalar(pair[:, :, 1], pair[:, :, 1], lam[:, 0:1], None, MUL)
                    v.drain()
                    nc.vector.tensor_tensor(S[:, :, :], Pr[:, :, :], spread(rsum[:, :], 2, L), MUL)
                    v.drain()
                    p2 = S[:, :, :].rearrange("p (h i) j -> p h i j", i=2)
                    nc.vector.tensor_tensor(A[:, :, :], p2[:, :, 0, :], p2[:, :, 1, :], ADD).then_inc(A_ready, 1)
                    v.wait_ge(o_ready, 1)
                    v.sem_inc(o_ready, -1)
                    nc.vector.tensor_copy(tile(M.x, i), M.bank[5][0:P, 0:D])
                    v.drain()
                    nc.vector.tensor_tensor(o[:, :], tile(M.x, i), tile(M.x, i), MUL)
                    v.drain()
                    nc.vector.tensor_reduce(tile(ms, i), o[:, :].rearrange("p (h d) -> p h d", h=NH), AX.X, ADD)
                    v.drain()
                nc.vector.tensor_scalar(ms[:, :, :], ms[:, :, :], 1.0 / DV, 1e-8, MUL, ADD).then_inc(ms_ready, 1)
                v.wait_ge(root_ready, 1)
                v.sem_inc(root_ready, -1)
                nc.vector.reciprocal(ms[:, :, :], root[:, :, :])
                v.drain()
                with nc.Fori(0, T, engines=(ET.DVE,)) as i:
                    o3 = o[:, :].rearrange("p (h d) -> p h d", h=NH)
                    nc.vector.tensor_tensor(o3, tile(M.x, i).rearrange("p (h d) -> p h d", h=NH),
                                            spread(tile(ms, i), 2, DV), MUL)
                    v.drain()
                    nc.vector.tensor_tensor(o3, o3, spread(small(M, "ln_w"), 1, NH), MUL)
                    v.drain()
                    nc.vector.tensor_tensor(o3, o3, spread(small(M, "ln_b"), 1, NH), ADD).then_inc(on_ready, 1)
                    v.wait_ge(y_ready, 1)
                    v.sem_inc(y_ready, -1)
                    nc.vector.tensor_tensor(tile(M.h, i), tile(M.h, i), M.bank[1][0:P, 0:D], ADD)
                    v.drain()

            @block.scalar
            def _(a):
                act_ln_std(nc, a, M, var_ready, std_ready)
                a.preload_act_table(ACT.Exp)
                a.wait_ge(lam_dot, 1)
                a.sem_inc(lam_dot, -1)
                nc.scalar.activation(lam2[:, :], lam2[:, :], ACT.Exp).then_inc(lam_exp, 1)
                a.wait_ge(pblank, 1)
                a.sem_inc(pblank, -1)
                with nc.Fori(0, T, engines=(ET.Activation,)) as i:
                    a.wait_ge(turned_ready, 1)
                    a.sem_inc(turned_ready, -1)
                    nc.scalar.copy(xT[:, :, :], turned(M, 0)).then_inc(xT_ready, 1)
                    repeat_x(nc, M, xr).then_inc(xr_ready, 1)
                    a.wait_ge(k_turned, 1)
                    a.sem_inc(k_turned, -1)
                    nc.scalar.copy(kT[:, :, :], turned(M, 7)).then_inc(kT_ready, 1)
                    a.wait_ge(shifted, 1)
                    a.sem_inc(shifted, -1)
                    nc.scalar.activation(Pr[:, :, :], S[:, :, :], ACT.Exp).then_inc(probs_ready, 1)
                    a.wait_ge(pT_ready, 1)
                    a.sem_inc(pT_ready, -1)
                    evacuate_probs(nc, M, 6, pm, NH).then_inc(pm_ready, 1)
                    a.drain()
                a.wait_ge(ms_ready, 1)
                a.sem_inc(ms_ready, -1)
                nc.scalar.activation(root[:, :, :], ms[:, :, :], ACT.Sqrt).then_inc(root_ready, 1)
                with nc.Fori(0, T, engines=(ET.Activation,)) as i:
                    a.wait_ge(oT_turned, 1)
                    a.sem_inc(oT_turned, -1)
                    nc.scalar.copy(oT[:, :, :], turned(M, 0)).then_inc(oT_ready, 1)
                    a.drain()

            @block.tensor
            def _(pe):
                pe.wait_ge(M.loaded["l1a"], 16)
                with nc.Fori(0, T, engines=(ET.PE,)) as i:
                    pe.wait_ge(xn_ready, 1)
                    pe.sem_inc(xn_ready, -1)
                    pe_turn(nc, M, 0, xn).then_inc(turned_ready, 1)
                    pe.wait_ge(xT_ready, 1)
                    pe.sem_inc(xT_ready, -1)
                    pe_project(nc, M, 1, xT, wqk, 0, 2 * D).then_inc(qk_ready, 1)
                    pe.wait_ge(xr_ready, 1)
                    pe.sem_inc(xr_ready, -1)
                    pe_values_in(nc, M, xr, wv, 0).then_inc(v_ready, 1)
                    pe.wait_ge(qk_rotated, 1)
                    pe.sem_inc(qk_rotated, -1)
                    pe_turn(nc, M, 0, qk).then_inc(q_turned, 1)
                    pe_turn(nc, M, 7, qk[:, D:2 * D]).then_inc(k_turned, 1)
                    pe.wait_ge(km_ready, 1)
                    pe.sem_inc(km_ready, -1)
                    pe_scores(nc, M, 4, qm, km).then_inc(s_ready, 1)
                    pe.wait_ge(A_ready, 1)
                    pe.sem_inc(A_ready, -1)
                    pe_turn_probs(nc, M, 6, A[:, :, :].rearrange("p h j -> p (h j)"), NH).then_inc(pT_ready, 1)
                    pe.wait_ge(vm_ready, 1)
                    pe.sem_inc(vm_ready, -1)
                    pe.wait_ge(pm_ready, 1)
                    pe.sem_inc(pm_ready, -1)
                    pe_values(nc, M, 5, pm, vm, NH, DV).then_inc(o_ready, 1)
                with nc.Fori(0, T, engines=(ET.PE,)) as i:
                    pe.wait_ge(on_ready, 1)
                    pe.sem_inc(on_ready, -1)
                    pe_turn(nc, M, 0, o).then_inc(oT_turned, 1)
                    pe.wait_ge(oT_ready, 1)
                    pe.sem_inc(oT_ready, -1)
                    pe_project(nc, M, 1, oT, wo, 0, D).then_inc(y_ready, 1)


def coupling(nc, M):
    CYCLES = 3
    NS = T * SEQS
    with ExitStack() as ctx:
        sb = lambda n, s: ctx.enter_context(nc.sbuf_tensor("cp_" + n, s, F32))
        sem = M.sem
        xn = sb("xn", [P, D])
        var_ready, std_ready, xn_ready = sem("var_ready"), sem("std_ready"), sem("xn_ready")
        turned_ready, turned_read = sem("turned"), sem("turned_read")
        mean, g1, g2, gf = sb("mean", [128, 2, NS]), sb("g1", [128, NS]), sb("g2", [64, NS]), sb("gf", [128, NS])
        h1, h2, h3 = sb("h1", [128, 2, G, GC]), sb("h2", [128, G, GC]), sb("h3", [64, G, GC])
        tf, m0 = sb("tf", [128, G, GC]), sb("m0", [128, 2, GC])
        r2, r2s, base = sb("r2", [128, 1]), sb("r2s", [128, 1]), sb("base", [128, 1])
        mean_ready, ps_ready, act_done = sem("mean_ready"), sem("ps_ready"), sem("act_done")
        gf_ready, tf_ready, x_moved = sem("gf_ready"), sem("tf_ready"), sem("x_moved")
        cn1, cn2 = (M.w[n].rearrange("p (k n) -> p k n", k=2) for n in ("cn1", "cn2"))
        gc1 = M.w["gc1"].rearrange("p (k n) -> p k n", k=2)
        cn3, cn4, gc2, gc3 = M.w["cn3"], M.w["cn4"][0:64, :], M.w["gc2"], M.w["gc3"][0:64, :]
        with nc.Block(name="coupling_norm") as block:
            @block.vector
            def _(v):
                dve_ln_stats(nc, v, M, var_ready, std_ready)
                with nc.Fori(0, T, engines=(ET.DVE,)) as i:
                    ln_apply(nc, M, i, xn[:, :]).then_inc(xn_ready, 1)
                    v.wait_ge(turned_ready, 1)
                    v.sem_inc(turned_ready, -1)
                    nc.vector.tensor_copy(cols(M.xT, i), turned(M, 0)).then_inc(turned_read, 1)
                    v.drain()

            @block.scalar
            def _(a):
                act_ln_std(nc, a, M, var_ready, std_ready)

            @block.tensor
            def _(pe):
                pe_turn_tiles(nc, pe, M, xn, xn_ready, turned_ready, turned_read)

        with nc.Block(name="coupling_cycles") as block:
            @block.vector
            def _(v):
                nc.vector.tensor_reduce(mean[:, :, :], M.xT[:, :, :].rearrange("p k (s j) -> p k s j", j=L), AX.X, ADD)
                v.drain()
                nc.vector.tensor_scalar(mean[:, :, :], mean[:, :, :], 1.0 / L, None, MUL).then_inc(mean_ready, 1)
                nc.vector.tensor_scalar(r2[:, :], small(M, "range", 128), 2.0, None, MUL)
                nc.vector.tensor_scalar(base[:, :], small(M, "sgn", 128), 0.1, None, MUL)
                v.drain()
                nc.vector.tensor_tensor(r2s[:, :], r2[:, :], small(M, "sgn", 128), MUL)
                v.wait_ge(gf_ready, 1)
                v.sem_inc(gf_ready, -1)
                nc.vector.tensor_scalar(gf[:, :], gf[:, :], 0.7, -0.5, MUL, ADD)
                v.drain()
                with nc.Fori(0, CYCLES, engines=(ET.DVE,)) as cycle:
                    for g in range(G):
                        v.wait_ge(tf_ready, 1)
                        v.sem_inc(tf_ready, -1)
                        t = tf[:, g, :]
                        nc.vector.scalar_tensor_tensor(t.rearrange("p (s j) -> p s j", j=L),
                                                       t.rearrange("p (s j) -> p s j", j=L), 0.3,
                                                       spread(gf[:, g * GS:(g + 1) * GS], 2, L), MUL, ADD)
                        v.drain()
                        nc.vector.tensor_scalar(t, t, r2s[:, 0:1], base[:, 0:1], MUL, ADD)
                        v.drain()
                        x = M.xT[:, :, g * GC:(g + 1) * GC]
                        for c in range(2):
                            nc.vector.tensor_tensor(m0[:, c, :], x[:, 1 - c, :], t, MUL)
                        v.drain()
                        nc.vector.tensor_tensor(x[:, 0, :], x[:, 0, :], m0[:, 0, :], ADD)
                        nc.vector.tensor_tensor(x[:, 1, :], x[:, 1, :], m0[:, 1, :], SUB).then_inc(x_moved, 1)
                        v.drain()
                nc.vector.tensor_copy(M.yT[:, :, :], M.xT[:, :, :])
                v.drain()

            @block.scalar
            def _(a):
                a.preload_act_table(ACT.Gelu)

                def net(out, bank, parts, n, bias, func, done):
                    a.wait_ge(ps_ready, 1)
                    a.sem_inc(ps_ready, -1)
                    nc.scalar.activation(out, M.bank[bank][0:parts, 0:n], func, bias=bias).then_inc(done, 1)

                net(g1[:, :], 0, 128, NS, small(M, "gc_b1", 128), ACT.Gelu, act_done)
                net(g2[:, :], 1, 64, NS, small(M, "gc_b2", 64), ACT.Gelu, act_done)
                net(gf[:, :], 6, 128, NS, small(M, "gc_b3", 128), ACT.Sigmoid, gf_ready)
                a.drain()
                with nc.Fori(0, CYCLES, engines=(ET.Activation,)) as cycle:
                    for g in range(G):
                        for m in range(2):
                            net(h1[:, m, g, :], 2 * g + m, 128, GC, small(M, "cn_b1", 128)[:, m:m + 1], ACT.Gelu, act_done)
                    for g in range(G):
                        net(h2[:, g, :], g, 128, GC, small(M, "cn_b2", 128), ACT.Gelu, act_done)
                    for g in range(G):
                        net(h3[:, g, :], 3 + g, 64, GC, small(M, "cn_b3", 64), ACT.Gelu, act_done)
                    for g in range(G):
                        net(tf[:, g, :], g, 128, GC, small(M, "cn_b4", 128), ACT.Sigmoid, tf_ready)
                    a.drain()

            @block.tensor
            def _(pe):
                pe.wait_ge(M.loaded["l1f"], 16)
                pe.wait_ge(mean_ready, 1)
                pe.sem_inc(mean_ready, -1)
                for k in range(2):
                    last = nc.tensor.matmul(M.bank[0][:, 0:NS], gc1[:, k, :], mean[:, k, :], start=(k == 0), stop=(k == 1))
                last.then_inc(ps_ready, 1)
                pe.wait_ge(act_done, 1)
                pe.sem_inc(act_done, -1)
                nc.tensor.matmul(M.bank[1][0:64, 0:NS], gc2, g1[:, :], start=True, stop=True).then_inc(ps_ready, 1)
                pe.wait_ge(act_done, 1)
                pe.sem_inc(act_done, -1)
                nc.tensor.matmul(M.bank[6][:, 0:NS], gc3, g2[:, :], start=True, stop=True).then_inc(ps_ready, 1)
                with nc.Fori(0, CYCLES, engines=(ET.PE,)) as cycle:
                    for g in range(G):
                        for m in range(2):
                            for k in range(2):
                                last = nc.tensor.matmul(M.bank[2 * g + m][:, 0:GC], cn1[:, k, m * 128:(m + 1) * 128],
                                                        M.xT[:, k, g * GC:(g + 1) * GC], start=(k == 0), stop=(k == 1))
                            last.then_inc(ps_ready, 1)
                    for g in range(G):
                        pe.wait_ge(act_done, 2)
                        pe.sem_inc(act_done, -2)
                    for g in range(G):
                        for k in range(2):
                            last = nc.tensor.matmul(M.bank[g][:, 0:GC], cn2[:, k, :], h1[:, k, g, :], start=(k == 0), stop=(k == 1))
                        last.then_inc(ps_ready, 1)
                    for g in range(G):
                        pe.wait_ge(act_done, 1)
                        pe.sem_inc(act_done, -1)
                        nc.tensor.matmul(M.bank[3 + g][0:64, 0:GC], cn3, h2[:, g, :], start=True, stop=True).then_inc(ps_ready, 1)
                    for g in range(G):
                        pe.wait_ge(act_done, 1)
                        pe.sem_inc(act_done, -1)
                        nc.tensor.matmul(M.bank[g][:, 0:GC], cn4, h3[:, g, :], start=True, stop=True).then_inc(ps_ready, 1)
                    pe.wait_ge(x_moved, G)
                    pe.sem_inc(x_moved, -G)
    add_back(nc, M, "_l1")


def linear_attention(nc, M):
    with ExitStack() as ctx:
        sb = lambda n, s: ctx.enter_context(nc.sbuf_tensor("a2_" + n, s, F32))
        sem = M.sem
        xn, xT, qT = sb("xn", [P, D]), sb("xT", [128, 2, P]), sb("qT", [128, 2, P])
        qkv, sq, ss = sb("qkv", [P, 3 * D]), sb("sq", [P, 2 * D]), sb("ss", [P, 2 * H16])
        root, vb, kv = sb("root", [P, 2 * H16]), sb("vb", [P, SEQS, D]), sb("kv", [128, 2, SEQS, 128])
        oT, y = sb("oT", [128, 2, P]), sb("y", [P, D])
        var_ready, std_ready, xn_ready = sem("var_ready"), sem("std_ready"), sem("xn_ready")
        turned_ready, xT_ready, qkv_ready = sem("turned"), sem("xT_ready"), sem("qkv_ready")
        ss_ready, root_ready, qkn_ready, qT_turned = sem("ss_ready"), sem("root_ready"), sem("qkn_ready"), sem("qT_turned")
        qT_ready, kv_ready, kvm_ready, oT_ready = sem("qT_ready"), sem("kv_ready"), sem("kvm_ready"), sem("oT_ready")
        oT_copied, y_ready = sem("oT_copied"), sem("y_ready")
        w = M.w["qkv2"].rearrange("p (k n) -> p k n", k=2)
        wo = M.w["proj2"].rearrange("p (k n) -> p k n", k=2)
        with nc.Block(name="linear_attention") as block:
            @block.vector
            def _(v):
                dve_ln_stats(nc, v, M, var_ready, std_ready)
                with nc.Fori(0, T, engines=(ET.DVE,)) as i:
                    ln_apply(nc, M, i, xn[:, :]).then_inc(xn_ready, 1)
                    v.wait_ge(qkv_ready, 1)
                    v.sem_inc(qkv_ready, -1)
                    nc.vector.tensor_tensor(qkv[:, 0:2 * D], M.bank[1][0:P, :], small(M, "qkv_b")[:, 0:2 * D], ADD)
                    nc.vector.tensor_tensor(qkv[:, 2 * D:3 * D], M.bank[2][0:P, 0:D], small(M, "qkv_b")[:, 2 * D:3 * D], ADD)
                    v.drain()
                    nc.vector.tensor_tensor(sq[:, :], qkv[:, 0:2 * D], qkv[:, 0:2 * D], MUL)
                    v.drain()
                    nc.vector.tensor_reduce(ss[:, :], sq[:, :].rearrange("p (m d) -> p m d", d=DH), AX.X, ADD)
                    v.drain()
                    nc.vector.tensor_scalar(ss[:, :], ss[:, :], 1e-24, None, MAX).then_inc(ss_ready, 1)
                    nc.vector.tensor_tensor(vb[:, :, :], spread(qkv[:, 2 * D:3 * D], 1, SEQS), spread(small(M, "mb"), 2, D), MUL)
                    v.wait_ge(root_ready, 1)
                    v.sem_inc(root_ready, -1)
                    nc.vector.reciprocal(ss[:, :], root[:, :])
                    v.drain()
                    qk3 = qkv[:, 0:2 * D].rearrange("p (m d) -> p m d", d=DH)
                    nc.vector.tensor_tensor(qk3, qk3, spread(ss[:, :], 2, DH), MUL).then_inc(qkn_ready, 1)
                    v.wait_ge(kv_ready, 1)
                    v.sem_inc(kv_ready, -1)
                    for c in range(2):
                        last = nc.vector.tensor_tensor(kv[:, c, :, :], M.bank[4 + c][:, 0:SEQS * 128].rearrange("p (s n) -> p s n", s=SEQS),
                                                       spread(small(M, "blk", 128), 1, SEQS), MUL)
                    last.then_inc(kvm_ready, 1)
                    v.wait_ge(y_ready, 1)
                    v.sem_inc(y_ready, -1)
                    nc.vector.tensor_tensor(y[:, :], M.bank[7][0:P, 0:D], small(M, "proj_b"), ADD)
                    v.drain()
                    nc.vector.tensor_tensor(tile(M.h, i), tile(M.h, i), y[:, :], ADD)
                    v.drain()

            @block.scalar
            def _(a):
                a.preload_act_table(ACT.Sqrt)
                act_ln_std(nc, a, M, var_ready, std_ready)
                with nc.Fori(0, T, engines=(ET.Activation,)) as i:
                    a.wait_ge(turned_ready, 1)
                    a.sem_inc(turned_ready, -1)
                    nc.scalar.copy(xT[:, :, :], turned(M, 0)).then_inc(xT_ready, 1)
                    a.wait_ge(ss_ready, 1)
                    a.sem_inc(ss_ready, -1)
                    nc.scalar.activation(root[:, :], ss[:, :], ACT.Sqrt).then_inc(root_ready, 1)
                    a.wait_ge(qT_turned, 1)
                    a.sem_inc(qT_turned, -1)
                    nc.scalar.copy(qT[:, :, :], turned(M, 3)).then_inc(qT_ready, 1)
                    a.wait_ge(oT_ready, 1)
                    a.sem_inc(oT_ready, -1)
                    nc.scalar.copy(oT[:, :, :], turned(M, 6)).then_inc(oT_copied, 1)
                    a.drain()

            @block.tensor
            def _(pe):
                pe.wait_ge(M.loaded["l2a"], 16)
                with nc.Fori(0, T, engines=(ET.PE,)) as i:
                    pe.wait_ge(xn_ready, 1)
                    pe.sem_inc(xn_ready, -1)
                    pe_turn(nc, M, 0, xn).then_inc(turned_ready, 1)
                    pe.wait_ge(xT_ready, 1)
                    pe.sem_inc(xT_ready, -1)
                    pe_project(nc, M, 1, xT, w, 0, 2 * D)
                    pe_project(nc, M, 2, xT, w, 2 * D, 3 * D).then_inc(qkv_ready, 1)
                    pe.wait_ge(qkn_ready, 1)
                    pe.sem_inc(qkn_ready, -1)
                    pe_turn(nc, M, 3, qkv[:, 0:D]).then_inc(qT_turned, 1)
                    for c in range(2):
                        last = nc.tensor.matmul(M.bank[4 + c][:, 0:SEQS * 128], qkv[:, D + c * 128:D + (c + 1) * 128],
                                                vb[:, :, c * 128:(c + 1) * 128], start=True, stop=True)
                    last.then_inc(kv_ready, 1)
                    pe.wait_ge(kvm_ready, 1)
                    pe.sem_inc(kvm_ready, -1)
                    pe.wait_ge(qT_ready, 1)
                    pe.sem_inc(qT_ready, -1)
                    for c in range(2):
                        for s in range(SEQS):
                            last = nc.tensor.matmul(M.bank[6][:, c * P + s * L:c * P + (s + 1) * L], kv[:, c, s, :],
                                                    qT[:, c, s * L:(s + 1) * L], start=True, stop=True)
                    last.then_inc(oT_ready, 1)
                    pe.wait_ge(oT_copied, 1)
                    pe.sem_inc(oT_copied, -1)
                    pe_project(nc, M, 7, oT, wo, 0, D).then_inc(y_ready, 1)


def experts2(nc, M):
    with ExitStack() as ctx:
        sb = lambda n, s: ctx.enter_context(nc.sbuf_tensor("e2_" + n, s, F32))
        sem = M.sem
        cw = sb("cw", [128, E2, NTOK])
        ga = [sb(f"ga_{b}", [128, GC]) for b in range(2)]
        gb = [sb(f"gb_{b}", [128, GC]) for b in range(2)]
        sg = [sb(f"sg_{b}", [128, GC]) for b in range(2)]
        hid = [sb(f"hid_{b}", [128, GC]) for b in range(2)]
        cw_loaded, ab_ready, a_scaled, sg_ready = sem("cw_loaded"), sem("ab_ready"), sem("a_scaled"), sem("sg_ready")
        ab_read, hid_ready, y_ready, y_read = sem("ab_read"), sem("hid_ready"), sem("y_ready"), sem("y_read")
        w1 = M.w["w1_2"].rearrange("p (e k n) -> p e k n", e=E2, k=2)
        w3 = M.w["w3_2"].rearrange("p (e k n) -> p e k n", e=E2, k=2)
        w2 = M.w["w2_2"].rearrange("p (e n) -> p e n", e=E2)
        xg = M.xT[:, :, :].rearrange("p k (g n) -> p k g n", g=G)
        yg = M.yT[:, :, :].rearrange("p k (g n) -> p k g n", g=G)
        with nc.Block(name="experts2") as block:
            @block.sync
            def _(sp):
                for e in range(E2):
                    sp.dma_start(cw[:, e, :], M.dram["cw2"][e, :].partition_broadcast(128)).then_inc(cw_loaded, 16)

            @block.tensor
            def _(pe):
                pe.wait_ge(M.loaded["l2f"], 16)
                with nc.Fori(0, G, engines=(ET.PE,)) as g:
                    x = xg[:, :, bass.ds(g, 1), :].rearrange("p k a n -> p k (a n)")

                    def up(e):
                        if e >= 2:
                            pe.wait_ge(ab_read, 1)
                            pe.sem_inc(ab_read, -1)
                        for j, w in enumerate((w1, w3)):
                            for k in range(2):
                                last = nc.tensor.matmul(M.bank[2 * (e % 2) + j][:, 0:GC], w[:, e, k, :], x[:, k, :],
                                                        start=(k == 0), stop=(k == 1))
                        last.then_inc(ab_ready, 1)

                    up(0)
                    for e in range(E2):
                        if e + 1 < E2:
                            up(e + 1)
                        pe.wait_ge(hid_ready, 1)
                        pe.sem_inc(hid_ready, -1)
                        for c in range(2):
                            last = nc.tensor.matmul(M.bank[4 + c][:, 0:GC], w2[:, e, c * 128:(c + 1) * 128], hid[e % 2][:, :],
                                                    start=(e == 0), stop=(e == E2 - 1))
                    last.then_inc(y_ready, 1)
                    pe.wait_ge(ab_read, 2)
                    pe.sem_inc(ab_read, -2)
                    pe.wait_ge(y_read, 1)
                    pe.sem_inc(y_read, -1)

            @block.scalar
            def _(a):
                a.preload_act_table(ACT.Sigmoid)
                with nc.Fori(0, G, engines=(ET.Activation,)) as g:
                    for e in range(E2):
                        a.wait_ge(a_scaled, 1)
                        a.sem_inc(a_scaled, -1)
                        nc.scalar.activation(sg[e % 2][:, :], ga[e % 2][:, :], ACT.Sigmoid).then_inc(sg_ready, 1)
                    a.drain()

            @block.vector
            def _(v):
                v.wait_ge(cw_loaded, 16 * E2)
                v.sem_inc(cw_loaded, -(16 * E2))
                with nc.Fori(0, G, engines=(ET.DVE,)) as g:
                    def scale(e):
                        b = e % 2
                        s = cw[:, e, bass.ds(g * GC, GC)]
                        v.wait_ge(ab_ready, 1)
                        v.sem_inc(ab_ready, -1)
                        nc.vector.tensor_tensor(ga[b][:, :], M.bank[2 * b][:, 0:GC], s, MUL).then_inc(a_scaled, 1)
                        nc.vector.tensor_tensor(gb[b][:, :], M.bank[2 * b + 1][:, 0:GC], s, MUL).then_inc(ab_read, 1)

                    scale(0)
                    for e in range(E2):
                        b = e % 2
                        v.drain()
                        if e + 1 < E2:
                            scale(e + 1)
                        nc.vector.tensor_tensor(gb[b][:, :], ga[b][:, :], gb[b][:, :], MUL)
                        v.wait_ge(sg_ready, 1)
                        v.sem_inc(sg_ready, -1)
                        v.drain()
                        nc.vector.tensor_tensor(hid[b][:, :], gb[b][:, :], sg[b][:, :], MUL).then_inc(hid_ready, 1)
                        if e + 1 < E2:
                            v.drain()
                    v.drain()
                    v.wait_ge(y_ready, 1)
                    v.sem_inc(y_ready, -1)
                    for c in range(2):
                        last = nc.vector.tensor_copy(yg[:, c, bass.ds(g, 1), :].rearrange("p a n -> p (a n)"), M.bank[4 + c][:, 0:GC])
                    last.then_inc(y_read, 1)
                    v.drain()
    add_back(nc, M, "_l2")


def delta_attention(nc, M):
    with ExitStack() as ctx:
        sb = lambda n, s: ctx.enter_context(nc.sbuf_tensor("a3_" + n, s, F32))
        sem = M.sem
        xn, xT, qkT = sb("xn", [P, D]), sb("xT", [128, 2, P]), sb("qkT", [128, 4, P])
        qk, sq = sb("qk", [P, 2 * D]), sb("sq", [P, D])
        ss, z, zw, beta = sb("ss", [P, T]), sb("z", [P, T]), sb("zw", [P, D]), sb("beta", [P, T])
        rr, root, k1, kroot = sb("rr", [P, T]), sb("root", [P, T]), sb("k1", [P, 1]), sb("kroot", [P, 1])
        alpha, keep, decay = sb("alpha", [128, 2]), sb("keep", [128, 2]), sb("decay", [128, 2, P])
        av, ema, bv = sb("av", [128, 2, P]), sb("ema", [128, 2, P]), sb("bv", [P, D])
        C, Cl, ClT = sb("C", [P, P]), sb("Cl", [P, LEVELS, P]), sb("ClT", [P, LEVELS, P])
        XY, CX, mt = sb("XY", [P, 2, P]), sb("CX", [P, 2, P]), sb("mt", [P, P])
        U, oT = sb("U", [P, D]), sb("oT", [128, 2, P])
        hid, sg = sb("hid", [128, 4, P]), sb("sg", [128, 4, P])
        names = ("var_ready std_ready w_folded ss_ready root_ready alpha_ready z_ready beta_ready xn_ready turned "
                 "xT_ready q_ready qk_ready v_ready k_ready kroot_ready kn_ready qk_turned qkT_ready ema_ready "
                 "bv_turned bv_ready G_ready mt_ready C_ready CT_ready levels_ready CX_ready CX_copied XCX_ready "
                 "X_ready U_ready U_copied oT_ready oT_copied y_ready ss2_ready root2_ready gu_ready "
                 "sg_ready hid_ready mlp_ready").split()
        s = {n: sem(n) for n in names}
        wqk = M.w["qk3"].rearrange("p (k n) -> p k n", k=2)
        wv = M.w["v3"].rearrange("p (k n) -> p k n", k=2)
        wo = M.w["o3"].rearrange("p (k n) -> p k n", k=2)
        wg = M.w["gate3"].rearrange("p (k n) -> p k n", k=2)
        wu = M.w["up3"].rearrange("p (k n) -> p k n", k=2)
        wd = M.w["down3"].rearrange("p (f n) -> p f n", f=4)
        ident = small(M, "ident")[:, 0:P]
        with nc.Block(name="delta_attention") as block:
            @block.vector
            def _(v):
                v.wait_ge(M.loaded["l3a"], 16)
                for name, ws in (("norm1", (wqk, wv)), ("norm2", (wg, wu))):
                    for w in ws:
                        for k in range(2):
                            nc.vector.tensor_scalar(w[:, k, :], w[:, k, :], small(M, name, 128)[:, k:k + 1], None, MUL)
                nc.vector.tensor_tensor(zw[:, :], small(M, "beta_w"), small(M, "norm1_row"), MUL)
                v.drain().then_inc(s["w_folded"], 1)
                dve_ln_stats(nc, v, M, s["var_ready"], s["std_ready"])
                with nc.Fori(0, T, engines=(ET.DVE,)) as i:
                    ln_apply(nc, M, i, tile(M.x, i))
                    v.drain()
                    nc.vector.tensor_tensor(sq[:, :], tile(M.x, i), tile(M.x, i), MUL)
                    nc.vector.tensor_tensor(xn[:, :], tile(M.x, i), zw[:, :], MUL)
                    v.drain()
                    nc.vector.tensor_reduce(ss[:, bass.ds(i, 1)], sq[:, :], AX.X, ADD)
                    nc.vector.tensor_reduce(z[:, bass.ds(i, 1)], xn[:, :], AX.X, ADD)
                    v.drain()
                nc.vector.tensor_scalar(ss[:, :], ss[:, :], 1.0 / D, 1e-6, MUL, ADD).then_inc(s["ss_ready"], 1)
                v.wait_ge(s["root_ready"], 1)
                v.sem_inc(s["root_ready"], -1)
                nc.vector.reciprocal(rr[:, :], root[:, :])
                v.drain()
                nc.vector.tensor_tensor(z[:, :], z[:, :], rr[:, :], MUL).then_inc(s["z_ready"], 1)
                v.wait_ge(s["beta_ready"], 1)
                v.sem_inc(s["beta_ready"], -1)
                nc.vector.tensor_scalar(keep[:, :], alpha[:, :], -1.0, 1.0, MUL, ADD)
                v.drain()
                for c in range(2):
                    nc.vector.tensor_scalar(decay[:, c, :], small(M, "run", 128), keep[:, c:c + 1], None, MUL)
                with nc.Fori(0, T, engines=(ET.DVE,)) as i:
                    b = beta[:, bass.ds(i, 1)]
                    nc.vector.tensor_scalar(xn[:, :], tile(M.x, i), rr[:, bass.ds(i, 1)], None, MUL).then_inc(s["xn_ready"], 1)
                    v.wait_ge(s["qk_ready"], 1)
                    v.sem_inc(s["qk_ready"], -1)
                    nc.vector.tensor_copy(qk[:, :], M.bank[1][0:P, :])
                    v.drain()
                    nc.vector.tensor_tensor(sq[:, :], qk[:, D:2 * D], qk[:, D:2 * D], MUL)
                    v.drain()
                    nc.vector.tensor_reduce(k1[:, :], sq[:, :], AX.X, ADD)
                    v.drain()
                    nc.vector.tensor_scalar(k1[:, :], k1[:, :], 1e-24, None, MAX).then_inc(s["k_ready"], 1)
                    v.wait_ge(s["v_ready"], 1)
                    v.sem_inc(s["v_ready"], -1)
                    for c in range(2):
                        nc.vector.tensor_scalar(av[:, c, :], M.bank[2][:, c * P:(c + 1) * P], alpha[:, c:c + 1], None, MUL)
                    v.drain()
                    for c in range(2):
                        last = nc.vector.tensor_tensor_scan(ema[:, c, :], decay[:, c, :], av[:, c, :], 0.0, MUL, ADD)
                    last.then_inc(s["ema_ready"], 1)
                    v.wait_ge(s["kroot_ready"], 1)
                    v.sem_inc(s["kroot_ready"], -1)
                    nc.vector.reciprocal(k1[:, :], kroot[:, :])
                    v.drain()
                    nc.vector.tensor_scalar(qk[:, D:2 * D], qk[:, D:2 * D], k1[:, 0:1], None, MUL).then_inc(s["kn_ready"], 1)
                    v.wait_ge(s["bv_turned"], 1)
                    v.sem_inc(s["bv_turned"], -1)
                    nc.vector.tensor_scalar(bv[:, :], M.bank[5][0:P, 0:D], b, None, MUL)
                    v.wait_ge(s["G_ready"], 1)
                    v.sem_inc(s["G_ready"], -1)
                    nc.vector.scalar_tensor_tensor(C[:, :], M.bank[6][0:P, 0:P], b, small(M, "strict"), MUL, MUL
                                                   ).then_inc(s["C_ready"], 1)
                    nc.vector.tensor_tensor(mt[:, :], M.bank[6][0:P, 128:128 + P], small(M, "mtm"), MUL)
                    v.drain()
                    nc.vector.tensor_tensor(Cl[:, :, :], spread(C[:, :], 1, LEVELS),
                                            small(M, "lvl").rearrange("p (l n) -> p l n", l=LEVELS), MUL)
                    v.wait_ge(s["CT_ready"], 1)
                    v.sem_inc(s["CT_ready"], -1)
                    nc.vector.tensor_tensor(ClT[:, :, :], spread(M.bank[7][0:P, 0:P], 1, LEVELS),
                                            small(M, "lvlT").rearrange("p (l n) -> p l n", l=LEVELS), MUL)
                    v.drain()
                    nc.vector.tensor_tensor(XY[:, 0, :], ident, Cl[:, 0, :], SUB)
                    nc.vector.tensor_tensor(XY[:, 1, :], ident, ClT[:, 0, :], SUB).then_inc(s["X_ready"], 1)
                    for l in range(1, LEVELS):
                        v.wait_ge(s["XCX_ready"], 1)
                        v.sem_inc(s["XCX_ready"], -1)
                        nc.vector.tensor_tensor(XY[:, :, :], XY[:, :, :],
                                                M.bank[2][0:P, 0:2 * P].rearrange("p (a n) -> p a n", a=2), SUB
                                                ).then_inc(s["X_ready"], 1)
                    v.wait_ge(s["y_ready"], 1)
                    v.sem_inc(s["y_ready"], -1)
                    nc.vector.tensor_tensor(tile(M.x, i), tile(M.x, i), M.bank[1][0:P, 0:D], ADD)
                    v.drain()
                    nc.vector.tensor_tensor(sq[:, :], tile(M.x, i), tile(M.x, i), MUL)
                    v.drain()
                    nc.vector.tensor_reduce(ss[:, bass.ds(i, 1)], sq[:, :], AX.X, ADD)
                    v.drain()
                nc.vector.tensor_scalar(ss[:, :], ss[:, :], 1.0 / D, 1e-6, MUL, ADD).then_inc(s["ss2_ready"], 1)
                v.wait_ge(s["root2_ready"], 1)
                v.sem_inc(s["root2_ready"], -1)
                nc.vector.reciprocal(rr[:, :], root[:, :])
                v.drain()
                with nc.Fori(0, T, engines=(ET.DVE,)) as i:
                    nc.vector.tensor_scalar(xn[:, :], tile(M.x, i), rr[:, bass.ds(i, 1)], None, MUL).then_inc(s["xn_ready"], 1)
                    v.wait_ge(s["sg_ready"], 1)
                    v.sem_inc(s["sg_ready"], -1)
                    nc.vector.tensor_tensor(hid[:, :, :], sg[:, :, :], turned(M, 1, 4), MUL)
                    v.drain()
                    nc.vector.tensor_tensor(hid[:, :, :], hid[:, :, :], turned(M, 2, 4), MUL).then_inc(s["hid_ready"], 1)
                    nc.vector.tensor_tensor(tile(M.h, i), tile(M.h, i), tile(M.x, i), ADD)
                    v.drain()
                    v.wait_ge(s["mlp_ready"], 1)
                    v.sem_inc(s["mlp_ready"], -1)
                    nc.vector.tensor_tensor(tile(M.h, i), tile(M.h, i), M.bank[3][0:P, 0:D], ADD)
                    v.drain()

            @block.scalar
            def _(a):
                act_ln_std(nc, a, M, s["var_ready"], s["std_ready"])
                a.wait_ge(s["ss_ready"], 1)
                a.sem_inc(s["ss_ready"], -1)
                nc.scalar.activation(root[:, :], ss[:, :], ACT.Sqrt).then_inc(s["root_ready"], 1)
                nc.scalar.activation(alpha[:, :], small(M, "alpha", 128), ACT.Sigmoid)
                a.wait_ge(s["z_ready"], 1)
                a.sem_inc(s["z_ready"], -1)
                nc.scalar.activation(beta[:, :], z[:, :], ACT.Sigmoid, bias=small(M, "beta_b")).then_inc(s["beta_ready"], 1)
                a.preload_act_table(ACT.Sqrt)
                with nc.Fori(0, T, engines=(ET.Activation,)) as i:
                    a.wait_ge(s["turned"], 1)
                    a.sem_inc(s["turned"], -1)
                    nc.scalar.copy(xT[:, :, :], turned(M, 0)).then_inc(s["xT_ready"], 1)
                    a.wait_ge(s["k_ready"], 1)
                    a.sem_inc(s["k_ready"], -1)
                    nc.scalar.activation(kroot[:, :], k1[:, :], ACT.Sqrt).then_inc(s["kroot_ready"], 1)
                    a.wait_ge(s["qk_turned"], 1)
                    a.sem_inc(s["qk_turned"], -1)
                    nc.scalar.copy(qkT[:, :, :], turned(M, 4, 4)).then_inc(s["qkT_ready"], 1)
                    for l in range(1, LEVELS):
                        a.wait_ge(s["CX_ready"], 1)
                        a.sem_inc(s["CX_ready"], -1)
                        nc.scalar.copy(CX[:, :, :], M.bank[3][0:P, 0:2 * P].rearrange("p (a n) -> p a n", a=2)
                                       ).then_inc(s["CX_copied"], 1)
                    a.wait_ge(s["U_ready"], 1)
                    a.sem_inc(s["U_ready"], -1)
                    nc.scalar.copy(U[:, :], M.bank[5][0:P, 0:D]).then_inc(s["U_copied"], 1)
                    a.wait_ge(s["oT_ready"], 1)
                    a.sem_inc(s["oT_ready"], -1)
                    nc.scalar.copy(oT[:, :, :], turned(M, 0)).then_inc(s["oT_copied"], 1)
                    a.drain()
                a.wait_ge(s["ss2_ready"], 1)
                a.sem_inc(s["ss2_ready"], -1)
                nc.scalar.activation(root[:, :], ss[:, :], ACT.Sqrt).then_inc(s["root2_ready"], 1)
                a.preload_act_table(ACT.Sigmoid)
                with nc.Fori(0, T, engines=(ET.Activation,)) as i:
                    a.wait_ge(s["turned"], 1)
                    a.sem_inc(s["turned"], -1)
                    nc.scalar.copy(xT[:, :, :], turned(M, 0)).then_inc(s["xT_ready"], 1)
                    a.wait_ge(s["gu_ready"], 1)
                    a.sem_inc(s["gu_ready"], -1)
                    nc.scalar.activation(sg[:, :, :], turned(M, 1, 4), ACT.Sigmoid).then_inc(s["sg_ready"], 1)
                    a.drain()

            @block.tensor
            def _(pe):
                pe.wait_ge(s["w_folded"], 1)
                pe.sem_inc(s["w_folded"], -1)
                with nc.Fori(0, T, engines=(ET.PE,)) as i:
                    pe.wait_ge(s["xn_ready"], 1)
                    pe.sem_inc(s["xn_ready"], -1)
                    pe_turn(nc, M, 0, xn).then_inc(s["turned"], 1)
                    pe.wait_ge(s["xT_ready"], 1)
                    pe.sem_inc(s["xT_ready"], -1)
                    pe_project(nc, M, 1, xT, wqk, 0, 2 * D).then_inc(s["qk_ready"], 1)
                    for c in range(2):
                        last = pe_project(nc, M, 2, wv[:, :, c * 128:(c + 1) * 128], xT, 0, P, 128, col=c * P)
                    last.then_inc(s["v_ready"], 1)
                    pe.wait_ge(s["ema_ready"], 1)
                    pe.sem_inc(s["ema_ready"], -1)
                    for c in range(2):
                        last = nc.tensor.transpose(M.bank[5][0:P, c * 128:(c + 1) * 128], ema[:, c, :], small(M, "ident", 128))
                    last.then_inc(s["bv_turned"], 1)
                    pe.wait_ge(s["kn_ready"], 1)
                    pe.sem_inc(s["kn_ready"], -1)
                    pe_turn(nc, M, 4, qk, 4).then_inc(s["qk_turned"], 1)
                    pe.wait_ge(s["qkT_ready"], 1)
                    pe.sem_inc(s["qkT_ready"], -1)
                    for o, rhs in ((0, 2), (128, 0)):
                        for k in range(2):
                            last = nc.tensor.matmul(M.bank[6][0:P, o:o + P], qkT[:, 2 + k, :], qkT[:, rhs + k, :],
                                                    start=(k == 0), stop=(k == 1))
                    last.then_inc(s["G_ready"], 1)
                    pe.wait_ge(s["C_ready"], 1)
                    pe.sem_inc(s["C_ready"], -1)
                    nc.tensor.transpose(M.bank[7][0:P, 0:P], C[:, :], ident).then_inc(s["CT_ready"], 1)
                    for l in range(1, LEVELS):
                        pe.wait_ge(s["X_ready"], 1)
                        pe.sem_inc(s["X_ready"], -1)
                        nc.tensor.matmul(M.bank[3][0:P, 0:P], ClT[:, l, :], XY[:, 0, :], start=True, stop=True)
                        nc.tensor.matmul(M.bank[3][0:P, P:2 * P], Cl[:, l, :], XY[:, 1, :], start=True, stop=True
                                         ).then_inc(s["CX_ready"], 1)
                        pe.wait_ge(s["CX_copied"], 1)
                        pe.sem_inc(s["CX_copied"], -1)
                        nc.tensor.matmul(M.bank[2][0:P, 0:P], XY[:, 1, :], CX[:, 0, :], start=True, stop=True)
                        nc.tensor.matmul(M.bank[2][0:P, P:2 * P], XY[:, 0, :], CX[:, 1, :], start=True, stop=True
                                         ).then_inc(s["XCX_ready"], 1)
                    pe.wait_ge(s["X_ready"], 1)
                    pe.sem_inc(s["X_ready"], -1)
                    nc.tensor.matmul(M.bank[5][0:P, 0:D], XY[:, 1, :], bv[:, :], start=True, stop=True
                                     ).then_inc(s["U_ready"], 1)
                    pe.wait_ge(s["U_copied"], 1)
                    pe.sem_inc(s["U_copied"], -1)
                    for c in range(2):
                        last = nc.tensor.matmul(M.bank[0][:, c * P:(c + 1) * P], U[:, c * 128:(c + 1) * 128], mt[:, :],
                                                start=True, stop=True)
                    last.then_inc(s["oT_ready"], 1)
                    pe.wait_ge(s["oT_copied"], 1)
                    pe.sem_inc(s["oT_copied"], -1)
                    pe_project(nc, M, 1, oT, wo, 0, D).then_inc(s["y_ready"], 1)
                with nc.Fori(0, T, engines=(ET.PE,)) as i:
                    pe.wait_ge(s["xn_ready"], 1)
                    pe.sem_inc(s["xn_ready"], -1)
                    pe_turn(nc, M, 0, xn).then_inc(s["turned"], 1)
                    pe.wait_ge(s["xT_ready"], 1)
                    pe.sem_inc(s["xT_ready"], -1)
                    for b, w in ((1, wg), (2, wu)):
                        for f in range(4):
                            last = pe_project(nc, M, b, w[:, :, f * 128:(f + 1) * 128], xT, 0, P, 128, col=f * P)
                    last.then_inc(s["gu_ready"], 1)
                    pe.wait_ge(s["hid_ready"], 1)
                    pe.sem_inc(s["hid_ready"], -1)
                    for f in range(4):
                        last = nc.tensor.matmul(M.bank[3][0:P, 0:D], hid[:, f, :], wd[:, f, :], start=(f == 0), stop=(f == 3))
                    last.then_inc(s["mlp_ready"], 1)


def route3(nc, M):
    with ExitStack() as ctx:
        sb = lambda n, s, dt=F32: ctx.enter_context(nc.sbuf_tensor("r3_" + n, s, dt))
        sem = M.sem
        xn, xT = sb("xn", [P, D]), sb("xT", [128, 2, P])
        lg, ex, rep, mask, w = (sb(n, [P, E3]) for n in ("lg", "ex", "rep", "mask", "w"))
        seen, key, over = sb("seen", [P, E3]), sb("key", [P, E3]), sb("over", [P, E3])
        ones = sb("ones", [P, P])
        m8, k8, i8 = sb("m8", [P, 8]), sb("k8", [P, 8]), sb("i8", [P, 8])
        idx = sb("idx", [P, 8], I32)
        eq = sb("eq", [P, 8, E3])
        s1, r1 = sb("s1", [P, 1]), sb("r1", [P, 1])
        hid, sg = sb("hid", [FH, 2, P]), sb("sg", [FH, 2, P])
        var_ready, std_ready, xn_ready = sem("var_ready"), sem("std_ready"), sem("xn_ready")
        turned_ready, xT_ready, lg_ready = sem("turned"), sem("xT_ready"), sem("lg_ready")
        shifted, ex_ready, mask_ready, pos_ready = sem("shifted"), sem("ex_ready"), sem("mask_ready"), sem("pos_ready")
        idx_ready, scattered, rows_sent = sem("idx_ready"), sem("scattered"), sem("rows_sent")
        gu_ready, sg_ready, hid_ready, y_ready = sem("gu_ready"), sem("sg_ready"), sem("hid_ready"), sem("y_ready")
        xT_copied = sem("xT_copied")
        router = M.w["router"].rearrange("p (k n) -> p k n", k=2)
        wgu = M.w["ws_gu"].rearrange("p (k n) -> p k n", k=2)
        wd = M.w["ws_down"][0:FH, :].rearrange("p (f n) -> p f n", f=2)
        with nc.Block(name="route3") as block:
            @block.vector
            def _(v):
                nc.vector.memset(seen[:, :], 0.0)
                nc.vector.memset(ones[:, :], 1.0)
                v.wait_ge(M.slots_cleared, 16)
                dve_ln_stats(nc, v, M, var_ready, std_ready)
                with nc.Fori(0, T, engines=(ET.DVE,)) as i:
                    ln_apply(nc, M, i, xn[:, :]).then_inc(xn_ready, 1)
                    v.wait_ge(lg_ready, 1)
                    v.sem_inc(lg_ready, -1)
                    nc.vector.tensor_copy(lg[:, :], M.bank[1][0:P, 0:E3])
                    v.drain()
                    nc.vector.tensor_reduce(s1[:, :], lg[:, :], AX.X, MAX)
                    v.drain()
                    nc.vector.tensor_scalar(lg[:, :], lg[:, :], s1[:, 0:1], None, SUB).then_inc(shifted, 1)
                    v.wait_ge(ex_ready, 1)
                    v.sem_inc(ex_ready, -1)
                    nc.vector.tensor_reduce(s1[:, :], ex[:, :], AX.X, ADD)
                    v.drain()
                    nc.vector.reciprocal(r1[:, :], s1[:, :])
                    v.drain()
                    nc.vector.tensor_scalar(ex[:, :], ex[:, :], r1[:, 0:1], None, MUL)
                    v.drain()
                    nc.vector.max(m8[:, :], ex[:, :])
                    v.drain()
                    nc.vector.match_replace(rep[:, :], m8[:, :], ex[:, :], -1.0)
                    v.drain()
                    nc.vector.tensor_scalar(mask[:, :], rep[:, :], 0.0, None, ALU.is_lt).then_inc(mask_ready, 1)
                    v.drain()
                    nc.vector.tensor_tensor(w[:, :], ex[:, :], mask[:, :], MUL)
                    v.drain()
                    nc.vector.tensor_reduce(s1[:, :], w[:, :], AX.X, ADD)
                    v.drain()
                    nc.vector.reciprocal(r1[:, :], s1[:, :])
                    v.drain()
                    nc.vector.tensor_scalar(w[:, :], w[:, :], r1[:, 0:1], None, MUL)
                    v.wait_ge(pos_ready, 1)
                    v.sem_inc(pos_ready, -1)
                    nc.vector.tensor_scalar(over[:, :], M.bank[2][0:P, 0:E3], float(CAP), OVERFLOW, ALU.is_gt, MUL)
                    nc.vector.tensor_tensor(key[:, :], M.bank[2][0:P, 0:E3], small(M, "ebase"), ADD)
                    v.drain()
                    nc.vector.tensor_tensor(key[:, :], key[:, :], over[:, :], ADD)
                    nc.vector.tensor_tensor(seen[:, :], seen[:, :], mask[:, :], ADD)
                    v.drain()
                    nc.vector.tensor_tensor(key[:, :], key[:, :], mask[:, :], MUL)
                    v.drain()
                    nc.vector.max(k8[:, :], key[:, :])
                    v.drain()
                    nc.vector.tensor_tensor(eq[:, :, :], spread(key[:, :], 1, 8), spread(k8[:, :], 2, E3), ALU.is_equal)
                    v.drain()
                    nc.vector.tensor_tensor(eq[:, :, :], eq[:, :, :], spread(w[:, :], 1, 8), MUL)
                    nc.vector.tensor_scalar(m8[:, :], k8[:, :], float(SLOTS), None, ALU.is_le)
                    nc.vector.scalar_tensor_tensor(i8[:, :], k8[:, :], 1.0, small(M, "trash"), SUB, MIN)
                    v.drain()
                    nc.vector.tensor_copy(idx[:, :], i8[:, :]).then_inc(idx_ready, 1)
                    nc.vector.tensor_reduce(k8[:, :], eq[:, :, :], AX.X, ADD)
                    v.drain()
                    nc.vector.tensor_tensor(tile(M.w8, i), k8[:, :], m8[:, :], MUL)
                    nc.vector.tensor_scalar(i8[:, :], i8[:, :], float(SLOTS - 1), None, MIN)
                    v.drain()
                    nc.vector.tensor_copy(tile(M.idx8, i), i8[:, :])
                    v.wait_ge(rows_sent, 1)
                    v.sem_inc(rows_sent, -1)
                    v.drain()
                with nc.Fori(0, T, engines=(ET.DVE,)) as i:
                    v.wait_ge(sg_ready, 1)
                    v.sem_inc(sg_ready, -1)
                    guT = M.bank[3][0:FH, 0:4 * P].rearrange("p (f t) -> p f t", f=4)
                    nc.vector.tensor_tensor(hid[:, :, :], sg[:, :, :], guT[:, 0:2, :], MUL)
                    v.drain()
                    nc.vector.tensor_tensor(hid[:, :, :], hid[:, :, :], guT[:, 2:4, :], MUL).then_inc(hid_ready, 1)
                    v.wait_ge(y_ready, 1)
                    v.sem_inc(y_ready, -1)
                    nc.vector.tensor_tensor(tile(M.h, i), tile(M.h, i), M.bank[4][0:P, 0:D], ADD)
                    v.drain()

            @block.gpsimd
            def _(pool):
                with nc.Fori(0, T, engines=(ET.Pool,)) as i:
                    pool.wait_ge(idx_ready, 1)
                    pool.sem_inc(idx_ready, -1)
                    for k in range(K3):
                        nc.gpsimd.indirect_dma_start(
                            out=M.dram["slots_x"], out_offset=bass.IndirectOffsetOnAxis(ap=idx[:, k:k + 1], axis=0),
                            in_=xn[:, :], in_offset=None).then_inc(scattered, 16)
                    pool.wait_ge(scattered, i * (16 * K3) + 16 * K3)
                    pool.sem_inc(rows_sent, 1)

            @block.scalar
            def _(a):
                act_ln_std(nc, a, M, var_ready, std_ready)
                a.preload_act_table(ACT.Exp)
                with nc.Fori(0, T, engines=(ET.Activation,)) as i:
                    a.wait_ge(turned_ready, 1)
                    a.sem_inc(turned_ready, -1)
                    nc.scalar.copy(xT[:, :, :], turned(M, 0)).then_inc(xT_ready, 1)
                    nc.scalar.copy(cols(M.xT, i), turned(M, 0))
                    a.wait_ge(shifted, 1)
                    a.sem_inc(shifted, -1)
                    nc.scalar.activation(ex[:, :], lg[:, :], ACT.Exp).then_inc(ex_ready, 1)
                    a.drain()
                a.drain().then_inc(xT_copied, 1)
                a.preload_act_table(ACT.Sigmoid)
                with nc.Fori(0, T, engines=(ET.Activation,)) as i:
                    a.wait_ge(gu_ready, 1)
                    a.sem_inc(gu_ready, -1)
                    nc.scalar.activation(sg[:, :, :], M.bank[3][0:FH, 0:2 * P].rearrange("p (f t) -> p f t", f=2),
                                         ACT.Sigmoid).then_inc(sg_ready, 1)
                    a.drain()

            @block.tensor
            def _(pe):
                pe.wait_ge(M.loaded["l3f"], 16)
                with nc.Fori(0, T, engines=(ET.PE,)) as i:
                    pe.wait_ge(xn_ready, 1)
                    pe.sem_inc(xn_ready, -1)
                    pe_turn(nc, M, 0, xn).then_inc(turned_ready, 1)
                    pe.wait_ge(xT_ready, 1)
                    pe.sem_inc(xT_ready, -1)
                    pe_project(nc, M, 1, xT, router, 0, E3).then_inc(lg_ready, 1)
                    pe.wait_ge(mask_ready, 1)
                    pe.sem_inc(mask_ready, -1)
                    nc.tensor.matmul(M.bank[2][0:P, 0:E3], ones[:, :], seen[:, :], start=True, stop=False)
                    nc.tensor.matmul(M.bank[2][0:P, 0:E3], small(M, "tri"), mask[:, :], start=False, stop=True
                                     ).then_inc(pos_ready, 1)
                pe.wait_ge(xT_copied, 1)
                pe.sem_inc(xT_copied, -1)
                with nc.Fori(0, T, engines=(ET.PE,)) as i:
                    x = cols(M.xT, i)
                    for f in range(4):
                        for k in range(2):
                            last = nc.tensor.matmul(M.bank[3][0:FH, f * P:(f + 1) * P], wgu[:, k, f * FH:(f + 1) * FH],
                                                    x[:, k, :], start=(k == 0), stop=(k == 1))
                    last.then_inc(gu_ready, 1)
                    pe.wait_ge(hid_ready, 1)
                    pe.sem_inc(hid_ready, -1)
                    for f in range(2):
                        last = nc.tensor.matmul(M.bank[4][0:P, 0:D], hid[:, f, :], wd[:, f, :], start=(f == 0), stop=(f == 1))
                    last.then_inc(y_ready, 1)


def experts3(nc, M):
    with ExitStack() as ctx:
        sb = lambda n, s: ctx.enter_context(nc.sbuf_tensor("e3_" + n, s, F32))
        sem = M.sem
        NB = 4
        wgu = [sb(f"wgu{b}", [128, 2, 2 * F3]) for b in range(NB)]
        wd = [sb(f"wd{b}", [FH, 2, D]) for b in range(NB)]
        xe = [sb(f"xe{b}", [CAP, D]) for b in range(NB)]
        xT = [sb(f"xT{b}", [128, 2, CAP]) for b in range(2)]
        sg = [sb(f"sg{b}", [FH, 2, CAP]) for b in range(2)]
        hid = [sb(f"hid{b}", [FH, 2, CAP]) for b in range(2)]
        ye = [sb(f"ye{b}", [CAP, D]) for b in range(NB)]
        loaded, stored = [sem(f"loaded{b}") for b in range(NB)], [sem(f"stored{b}") for b in range(NB)]
        used = sem("e3_used")
        turned_ready, xT_ready, gu_ready, sg_ready = sem("turned"), sem("xT_ready"), sem("gu_ready"), sem("sg_ready")
        hid_ready, y_ready, y_copied = sem("hid_ready"), sem("y_ready"), sem("y_copied")
        with nc.Block(name="experts3") as block:
            @block.sync
            def _(sp):
                with nc.Fori(0, E3 // NB, engines=(ET.SP,)) as p:
                    for b in range(NB):
                        e = p * NB + b
                        sp.wait_ge(used, 1)
                        sp.sem_inc(used, -1)
                        sp.dma_start(xe[b][:, :], M.dram["slots_x"][bass.ds(e * CAP, CAP), :]).then_inc(loaded[b], 16)
                        sp.dma_start(wgu[b][:, :, :].rearrange("p k n -> p (k n)"),
                                     M.dram["gu_3"][bass.ds(e, 1)].rearrange("a p n -> (a p) n")).then_inc(loaded[b], 16)
                        sp.dma_start(wd[b][:, :, :].rearrange("p k n -> p (k n)"),
                                     M.dram["down_3"][bass.ds(e, 1)].rearrange("a p n -> (a p) n")).then_inc(loaded[b], 16)

            @block.tensor
            def _(pe):
                pe.sem_inc(used, NB)

                def turn(b):
                    pe.wait_ge(loaded[b], 48)
                    pe.sem_inc(loaded[b], -48)
                    for k in range(2):
                        last = nc.tensor.transpose(M.bank[b % 2][:, k * CAP:(k + 1) * CAP], xe[b][:, k * 128:(k + 1) * 128],
                                                   small(M, "ident", 128))
                    last.then_inc(turned_ready, 1)

                def up(b):
                    pe.wait_ge(xT_ready, 1)
                    pe.sem_inc(xT_ready, -1)
                    for f in range(4):
                        for k in range(2):
                            last = nc.tensor.matmul(M.bank[2 + b % 2][0:FH, f * CAP:(f + 1) * CAP],
                                                    wgu[b][:, k, f * FH:(f + 1) * FH], xT[b % 2][:, k, :],
                                                    start=(k == 0), stop=(k == 1))
                    last.then_inc(gu_ready, 1)

                def down(b):
                    pe.wait_ge(hid_ready, 1)
                    pe.sem_inc(hid_ready, -1)
                    for f in range(2):
                        last = nc.tensor.matmul(M.bank[4 + b % 2][:, 0:D], hid[b % 2][:, f, :], wd[b][:, f, :],
                                                start=(f == 0), stop=(f == 1))
                    last.then_inc(y_ready, 1)

                with nc.Fori(0, E3 // NB, engines=(ET.PE,)) as p:
                    turn(0)
                    up(0)
                    for b in range(NB):
                        if b + 1 < NB:
                            turn(b + 1)
                            up(b + 1)
                        down(b)
                        pe.drain().then_inc(used, 1)

            @block.scalar
            def _(a):
                a.preload_act_table(ACT.Sigmoid)

                def sig(b):
                    a.wait_ge(turned_ready, 1)
                    a.sem_inc(turned_ready, -1)
                    nc.scalar.copy(xT[b % 2][:, :, :], M.bank[b % 2][:, 0:2 * CAP].rearrange("p (k n) -> p k n", k=2)
                                   ).then_inc(xT_ready, 1)
                    a.wait_ge(gu_ready, 1)
                    a.sem_inc(gu_ready, -1)
                    nc.scalar.activation(sg[b % 2][:, :, :], M.bank[2 + b % 2][0:FH, 0:2 * CAP].rearrange("p (f n) -> p f n", f=2),
                                         ACT.Sigmoid).then_inc(sg_ready, 1)

                for b in range(NB):
                    a.sem_inc(stored[b], 16)
                with nc.Fori(0, E3 // NB, engines=(ET.Activation,)) as p:
                    sig(0)
                    for b in range(NB):
                        if b + 1 < NB:
                            sig(b + 1)
                        a.wait_ge(y_ready, 1)
                        a.sem_inc(y_ready, -1)
                        a.wait_ge(stored[b], 16)
                        a.sem_inc(stored[b], -16)
                        nc.scalar.copy(ye[b][:, :], M.bank[4 + b % 2][:, 0:D])
                        a.drain()
                        a.dma_start(M.dram["slots_y"][bass.ds((p * NB + b) * CAP, CAP), :], ye[b][:, :]).then_inc(stored[b], 16)
                for b in range(NB):
                    a.wait_ge(stored[b], 16)
                    a.sem_inc(stored[b], -16)

            @block.vector
            def _(v):
                with nc.Fori(0, E3 // NB, engines=(ET.DVE,)) as p:
                    for b in range(NB):
                        v.wait_ge(sg_ready, 1)
                        v.sem_inc(sg_ready, -1)
                        gu = M.bank[2 + b % 2][0:FH, :].rearrange("p (f n) -> p f n", f=4)
                        nc.vector.tensor_tensor(hid[b % 2][:, :, :], sg[b % 2][:, :, :], gu[:, 0:2, :], MUL)
                        v.drain()
                        nc.vector.tensor_tensor(hid[b % 2][:, :, :], hid[b % 2][:, :, :], gu[:, 2:4, :], MUL).then_inc(hid_ready, 1)
                        v.drain()


def combine3(nc, M):
    with ExitStack() as ctx:
        sb = lambda n, s, dt=F32: ctx.enter_context(nc.sbuf_tensor("c3_" + n, s, dt))
        sem = M.sem
        rows = sb("rows", [P, K3, D])
        idx = sb("idx", [P, 8], I32)
        idx_ready, gathered, stored, rows_here = sem("idx_ready"), sem("gathered"), sem("c3_stored"), sem("rows_here")
        h_ready = sem("h_ready")
        with nc.Block(name="combine3") as block:
            @block.vector
            def _(v):
                with nc.Fori(0, T, engines=(ET.DVE,)) as i:
                    nc.vector.tensor_copy(idx[:, :], tile(M.idx8, i)).then_inc(idx_ready, 1)
                    v.wait_ge(rows_here, 1)
                    v.sem_inc(rows_here, -1)
                    h = tile(M.h, i)
                    for k in range(K3):
                        last = nc.vector.scalar_tensor_tensor(h, rows[:, k, :], M.w8[:, bass.ds(i, 1), k:k + 1].rearrange("p a n -> p (a n)"),
                                                              h, MUL, ADD)
                        v.drain()
                    v.drain().then_inc(h_ready, 1)

            @block.gpsimd
            def _(pool):
                with nc.Fori(0, T, engines=(ET.Pool,)) as i:
                    pool.wait_ge(idx_ready, 1)
                    pool.sem_inc(idx_ready, -1)
                    for k in range(K3):
                        nc.gpsimd.indirect_dma_start(
                            out=rows[:, k, :], out_offset=None, in_=M.dram["slots_y"],
                            in_offset=bass.IndirectOffsetOnAxis(ap=idx[:, k:k + 1], axis=0)).then_inc(gathered, 16)
                    pool.wait_ge(gathered, i * (16 * K3) + 16 * K3)
                    pool.sem_inc(rows_here, 1)

            @block.sync
            def _(sp):
                with nc.Fori(0, T, engines=(ET.SP,)) as i:
                    sp.wait_ge(h_ready, 1)
                    sp.sem_inc(h_ready, -1)
                    sp.dma_start(M.dram["out"][bass.ds(i, 1)].rearrange("a p d -> (a p) d"), tile(M.h, i)).then_inc(stored, 16)
                sp.wait_ge(stored, 16 * T)


def vit_tower(nc, dram):
    with ExitStack() as ctx:
        M = setup_memory(nc, ctx, dram)
        load_everything(nc, M)
        patch_embedding(nc, M)
        alibi_attention(nc, M)
        gate_top2(nc, M, "g0_", M.w["gate0"], dram["cw0"], False)
        experts0(nc, M)
        add_back(nc, M, "_l0")
        rotary_attention(nc, M)
        coupling(nc, M)
        linear_attention(nc, M)
        gate_top2(nc, M, "g2_", M.w["gate2"], dram["cw2"], True)
        experts2(nc, M)
        delta_attention(nc, M)
        route3(nc, M)
        experts3(nc, M)
        combine3(nc, M)


def chunks(w, parts=128):
    w = np.ascontiguousarray(w)
    return w.reshape((-1, parts) + w.shape[1:]).swapaxes(0, 1)


def flat(w, parts=128):
    w = w.reshape(w.shape[0], -1)
    out = np.zeros((128, w.shape[1]), np.float32)
    out[:w.shape[0]] = w
    return out


def constants():
    f = np.float32
    c = {}
    p = np.arange(128)
    c["ident"] = np.eye(128, dtype=f)
    c["mask8"] = (p[:, None] // DH == np.arange(8)).astype(f)
    r = np.arange(P)
    seq, pos = r // L, r % L
    c["vm16"] = (seq[:, None] == np.arange(16) % 3).astype(f)
    c["vm8"] = (seq[:, None] == np.arange(8) % 3).astype(f)
    start = 2 ** (-2 ** (-(math.log2(H16) - 3)))
    slopes = np.array([start * start ** m for m in range(H16)], f)
    rel = (np.arange(L)[None, :] - pos[:, None]).astype(f)
    bias = slopes[None, :, None] * rel[:, None, :]
    c["alibi"] = np.where(rel[:, None, :] <= 0, bias, f(NEG))
    c["mb"] = (seq[:, None] == np.arange(SEQS)).astype(f)
    inv = (f(1.0) / f(10000.0) ** (np.arange(0, DH, 2, dtype=f) / f(DH))).astype(f)
    ang = np.repeat(pos.astype(f)[:, None] * inv[None, :], 2, axis=-1).astype(f)
    c["cos"] = np.cos(ang).astype(f)
    c["sin"] = (np.sin(ang) * np.where(np.arange(DH) % 2 == 0, -1.0, 1.0)).astype(f)
    c["blk"] = (p[:, None] // DH == p[None, :] // DH).astype(f)
    c["tri"] = (r[:, None] <= r[None, :]).astype(f)
    same = seq[:, None] == seq[None, :]
    c["strict"] = (same & (r[None, :] < r[:, None])).astype(f)
    lvl = np.stack([same & (pos[:, None] >> (l + 1) == pos[None, :] >> (l + 1)) & ((pos[:, None] >> l) % 2 == 1)
                    & ((pos[None, :] >> l) % 2 == 0) for l in range(LEVELS)], 1).astype(f)
    c["lvl"] = lvl
    c["lvlT"] = lvl.transpose(2, 1, 0)
    c["mtm"] = (same & (r[None, :] >= r[:, None])).astype(f)
    c["below8"] = np.broadcast_to((np.arange(8)[None, :] < np.arange(8)[:, None]).astype(f).reshape(1, 64), (P, 64))
    c["ebase"] = np.broadcast_to(CAP * np.arange(E3, dtype=f), (P, E3))
    c["trash"] = (SLOTS + r[:, None] + P * np.arange(K3)).astype(f)
    c["run"] = np.broadcast_to((pos != 0).astype(f), (128, P))
    c["sgn"] = np.where(p < 64, 1.0, -1.0).astype(f)[:, None]
    y, x = (a.reshape(-1).astype(f) for a in np.meshgrid(np.arange(GRID), np.arange(GRID), indexing="ij"))
    om = (np.arange(D // 4, dtype=f) / f(D // 4 - 1)).astype(f)
    om = (f(1.0) / f(10000.0) ** om).astype(f)
    xa, ya = x[:, None] * om[None, :], y[:, None] * om[None, :]
    c["pe"] = np.concatenate([np.sin(xa), np.cos(xa), np.sin(ya), np.cos(ya)], 1).astype(f)
    return c


def lay_out(I):
    c = constants()
    row = lambda v: np.broadcast_to(np.asarray(v).reshape(1, -1), (128, np.asarray(v).size))
    col = lambda v: np.asarray(v).reshape(-1, 128).T if np.asarray(v).size >= 128 else flat(np.asarray(v).reshape(-1, 1))
    s = dict(c)
    s["base"] = np.tile(np.concatenate([I["cls_tok"].reshape(1, D), c["pe"]], 0), (SEQS, 1))
    s["ln2_w"], s["b_out0"] = row(I["L0_tok_ln2_w"]), row(I["L0_attn_b_out"])
    b_in = I["L0_attn_b_in"]
    s["b_q0"], s["b_k0"], s["b_v0"] = col(b_in[:D]), col(b_in[D:2 * D]), row(b_in[2 * D:])
    s["ln_w"], s["ln_b"] = row(I["L1_attn_ln_w"]), row(I["L1_attn_ln_b"])
    s["lam"] = row(np.concatenate([I["L1_attn_lambda_" + n] for n in ("q1", "k1", "q2", "k2")]))
    s["qkv_b"], s["proj_b"] = row(I["L2_attn_qkv_b"]), row(I["L2_attn_proj_b"])
    s["beta_w"], s["norm1_row"], s["beta_b"] = row(I["L3_attn_beta_w"]), row(I["L3_attn_norm1_w"]), row(I["L3_attn_beta_b"])
    s["range"], s["cn_b4"], s["gc_b3"] = row(I["L1_ffn_adaptive_range"]), row(I["L1_ffn_cn_b4"]), row(I["L1_ffn_gc_b3"])
    s["ln1_w"] = col(I["L0_tok_ln1_w"])
    s["b2"] = flat(chunks(I["L0_ffn_b2"].T))
    s["cn_b1"], s["cn_b2"], s["cn_b3"] = col(I["L1_ffn_cn_b1"]), col(I["L1_ffn_cn_b2"]), col(I["L1_ffn_cn_b3"])
    s["gc_b1"], s["gc_b2"] = col(I["L1_ffn_gc_b1"]), col(I["L1_ffn_gc_b2"])
    s["alpha"], s["norm1"], s["norm2"] = col(I["L3_attn_alpha_logit"]), col(I["L3_attn_norm1_w"]), col(I["L3_attn_norm2_w"])
    a = {"small": np.concatenate([flat(s[n]) for n, _ in SMALL], 1)}

    w = {}
    w["w_tok"] = chunks(I["L0_tok_W"].T)
    w["w_in"], w["w_out"], w["gate0"] = chunks(I["L0_attn_w_in"]), chunks(I["L0_attn_w_out"]), chunks(I["L0_ffn_gate_w"])
    w["qk1"] = chunks(np.concatenate([I["L1_attn_Wq"].T, I["L1_attn_Wk"].T], 1))
    w["v1"], w["o1"] = chunks(I["L1_attn_Wv"].T), chunks(I["L1_attn_Wo"].T)
    w["cn1"], w["cn2"], w["cn3"] = chunks(I["L1_ffn_cn_w1"]), chunks(I["L1_ffn_cn_w2"]), chunks(I["L1_ffn_cn_w3"])
    w["cn4"] = np.broadcast_to(I["L1_ffn_cn_w4"], (64, 128))
    w["gc1"], w["gc2"] = chunks(I["L1_ffn_gc_w1"]), chunks(I["L1_ffn_gc_w2"])
    w["gc3"] = np.broadcast_to(I["L1_ffn_gc_w3"], (64, 128))
    w["qkv2"], w["proj2"], w["gate2"] = chunks(I["L2_attn_qkv_w"]), chunks(I["L2_attn_proj_w"]), chunks(I["L2_ffn_gate_w"])
    for n in ("w1", "w3"):
        w[n + "_2"] = I["L2_ffn_" + n].reshape(E2, 2, 128, F2).transpose(2, 0, 1, 3)
    w["w2_2"] = I["L2_ffn_w2"].transpose(1, 0, 2)
    w["qk3"] = chunks(np.concatenate([I["L3_attn_Wq"], I["L3_attn_Wk"]], 1))
    w["v3"], w["o3"] = chunks(I["L3_attn_Wv"]), chunks(I["L3_attn_Wo"])
    w["gate3"], w["up3"], w["down3"] = (chunks(I["L3_attn_w_" + n]) for n in ("gate", "up", "down"))
    w["router"], w["ws_gu"], w["ws_down"] = chunks(I["L3_ffn_router_w"].T), chunks(I["L3_ffn_ws_gate_up"]), chunks(I["L3_ffn_ws_down"], FH)
    for array, parts in WEIGHTS:
        a[array] = np.concatenate([flat(w[n]) for n, _ in parts], 1)

    x = I["x"].reshape(BATCH, CHANNELS, GRID, PATCH, GRID, PATCH).transpose(0, 2, 4, 1, 3, 5).reshape(BATCH, L - 1, PD)
    patches = np.zeros((T * SEQS, L, PD), np.float32)
    patches[:BATCH, 1:] = x
    a["patches"] = patches.reshape(T, P, PD)
    a["w1_0"] = I["L0_ffn_w1"].reshape(E0, 2, 128, F0).transpose(0, 2, 1, 3).reshape(E0, 128, 2 * F0)
    a["w2_0"] = I["L0_ffn_w2"].reshape(E0, F0 // 128, 128, D).transpose(0, 2, 1, 3).reshape(E0, 128, F0 // 128 * D)
    a["b1_0"] = I["L0_ffn_b1"].reshape(E0, F0 // 128, 128).transpose(0, 2, 1)
    a["b2_0"] = I["L0_ffn_b2"].reshape(E0, 2, 128).transpose(0, 2, 1)
    gu = np.concatenate([I["L3_ffn_w_gate"], I["L3_ffn_w_up"]], 2)
    a["gu_3"] = gu.reshape(E3, 2, 128, 2 * F3).transpose(0, 2, 1, 3).reshape(E3, 128, 4 * F3)
    a["down_3"] = I["L3_ffn_w_down"].reshape(E3, 2, FH, D).transpose(0, 2, 1, 3).reshape(E3, FH, 2 * D)
    return {n: np.ascontiguousarray(v) for n, v in a.items()}


def kernel(**inputs):
    import concourse.bacc as bacc
    from concourse.bass_utils import run_bass_kernel_spmd

    arrays = lay_out({n: np.asarray(v) for n, v in inputs.items()})
    nc = bacc.Bacc("TRN2", target_bir_lowering=False, num_devices=1)
    dram = {n: nc.dram_tensor("in_" + n, a.shape, F32, kind="ExternalInput").ap() for n, a in arrays.items()}
    dram["out"] = nc.dram_tensor("out", (T, P, D), F32, kind="ExternalOutput").ap()
    for n, shape in (("cw0", (E0, NTOK)), ("cw2", (E2, NTOK)), ("slots_x", (SLOT_ROWS, D)), ("slots_y", (SLOTS, D))):
        dram[n] = nc.dram_tensor(n, shape, F32).ap()
    vit_tower(nc, dram)
    r = run_bass_kernel_spmd(nc, [{"in_" + n: a for n, a in arrays.items()}], core_ids=[0])
    return r.results[0]["out"].reshape(T * SEQS, L, D)[:BATCH]
```

```python
import math
from contextlib import ExitStack

import numpy as np
import concourse.bass as bass
from concourse import mybir

F32 = mybir.dt.float32
I32 = mybir.dt.int32
ALU = mybir.AluOpType
ACT = mybir.ActivationFunctionType
AX = mybir.AxisListType
ET = mybir.EngineType
ADD, SUB, MUL, MAX, MIN = ALU.add, ALU.subtract, ALU.mult, ALU.max, ALU.min

BATCH, SIDE, PATCH, CHANNELS, D = 32, 96, 16, 3, 256
GRID = SIDE // PATCH
L = GRID * GRID + 1
SEQS = 3
P = SEQS * L
T = -(-BATCH // SEQS)
NTOK = T * P
PD = CHANNELS * PATCH * PATCH
PC = PD // 128
H16, DH = 16, 16
G = 3
GC = NTOK // G
GS = GC // L
E0, F0 = 8, 1024
E2, F2 = 8, 128
E3, K3, F3, CAP = 64, 8, 192, 128
FH = F3 // 2
SLOTS = E3 * CAP
SLOT_ROWS = SLOTS + 7 * 128
CW = P + L
LAMBDA_INIT = 0.8 - 0.6 * math.exp(-0.3 * 12)
LEVELS = 6
NEG = -1e30
OVERFLOW = 20000.0


def tile(t, i):
    return t[:, bass.ds(i, 1), :].rearrange("p a n -> p (a n)")


def cols(t, i):
    return t[:, :, bass.ds(i * P, P)]


def spread(ap, axis, n):
    ap = ap.unsqueeze(axis)
    shape = list(ap.shape)
    shape[axis] = n
    return ap.to_broadcast(shape)


SMALL = [
    ("ident", 128), ("mask8", 8), ("vm16", 16), ("vm8", 8), ("alibi", H16 * L), ("mb", SEQS),
    ("cos", DH), ("sin", DH), ("blk", 128), ("tri", P), ("strict", P), ("lvl", LEVELS * P),
    ("lvlT", LEVELS * P), ("mtm", P), ("below8", 64), ("ebase", E3), ("trash", K3), ("run", P), ("sgn", 1),
    ("base", D), ("ln2_w", D), ("b_out0", D), ("b_v0", D), ("ln_w", 32), ("ln_b", 32), ("lam", 64),
    ("qkv_b", 3 * D), ("proj_b", D), ("beta_w", D), ("norm1_row", D), ("beta_b", 1), ("range", 1),
    ("cn_b4", 1), ("gc_b3", 1), ("ln1_w", PC), ("b_q0", 2), ("b_k0", 2), ("b2", 2 * E0), ("cn_b1", 2),
    ("cn_b2", 1), ("cn_b3", 1), ("gc_b1", 1), ("gc_b2", 1), ("alpha", 2), ("norm1", 2), ("norm2", 2),
]
WEIGHTS = [
    ("tok", [("w_tok", PC * D)]),
    ("l0a", [("w_in", 2 * 3 * D), ("w_out", 2 * D), ("gate0", 2 * E0)]),
    ("l1a", [("qk1", 2 * 2 * D), ("v1", 2 * D), ("o1", 2 * D)]),
    ("l1f", [("cn1", 2 * D), ("cn2", 2 * 128), ("cn3", 64), ("cn4", 128), ("gc1", 2 * 128), ("gc2", 64),
             ("gc3", 128)]),
    ("l2a", [("qkv2", 2 * 3 * D), ("proj2", 2 * D), ("gate2", 2 * E2)]),
    ("l2f", [("w1_2", E2 * 2 * F2), ("w3_2", E2 * 2 * F2), ("w2_2", E2 * D)]),
    ("l3a", [("qk3", 2 * 2 * D), ("v3", 2 * D), ("o3", 2 * D), ("gate3", 2 * 512), ("up3", 2 * 512),
             ("down3", 4 * D)]),
    ("l3f", [("router", 2 * E3), ("ws_gu", 2 * 2 * F3), ("ws_down", 2 * D)]),
]


EARLY = ("tok", "l0a", "l1a", "l1f", "l2a")
LATE = ("l2f", "l3a", "l3f")


class Mem:
    pass


def place_weights(nc, ctx, M, arrays):
    for array, parts in WEIGHTS:
        if array in arrays:
            buf = ctx.enter_context(nc.sbuf_tensor("w_" + array, [128, sum(n for _, n in parts)], F32))
            M.w[array] = buf
            o = 0
            for name, n in parts:
                M.w[name] = buf[:, o:o + n]
                o += n


def load_late(nc, M):
    with nc.Block(name="load_late") as block:
        @block.sync
        def _(sp):
            for array in LATE:
                sp.dma_start(M.w[array][:, :], M.dram[array]).then_inc(M.loaded[array], 16)


def setup_memory(nc, ctx, dram):
    M = Mem()
    M.dram = dram

    def sb(name, shape, dt=F32):
        return ctx.enter_context(nc.sbuf_tensor(name, shape, dt))

    M.h = sb("h", [P, T, D])
    M.x = sb("x", [P, T, D])
    M.xT = sb("xT", [128, 2, NTOK])
    M.yT = sb("yT", [128, 2, NTOK])
    M.stats = sb("stats", [P, T, 6])
    M.mean = sb("mean", [P, T])
    M.std = sb("std", [P, T])
    M.rstd = sb("rstd", [P, T])
    M.tmp = sb("ln_tmp", [P, 4, T])
    M.small = sb("small", [128, sum(n for _, n in SMALL)])
    M.at, o = {}, 0
    for name, n in SMALL:
        M.at[name] = (o, n)
        o += n
    M.w, M.loaded = {}, {}
    for array, _ in WEIGHTS:
        M.loaded[array] = ctx.enter_context(nc.semaphore("loaded_" + array))
    place_weights(nc, ctx, M, EARLY)
    M.w8 = sb("w8", [P, T, K3])
    M.idx8 = sb("idx8", [P, T, K3], I32)
    sems = {}

    def shared_sem(name):
        if name not in sems:
            sems[name] = ctx.enter_context(nc.semaphore(name))
        return sems[name]

    M.sem = shared_sem
    M.bank = [ctx.enter_context(nc.psum_tensor(f"bank{b}", [128, 512], F32)) for b in range(8)]
    M.small_loaded = ctx.enter_context(nc.semaphore("small_loaded"))
    M.slots_cleared = ctx.enter_context(nc.semaphore("slots_cleared"))
    return M


def small(M, name, parts=P):
    o, n = M.at[name]
    return M.small[0:parts, o:o + n]


def dve_ln_stats(nc, v, M, var_ready, std_ready, eps=1e-5):
    with nc.Fori(0, T, engines=(ET.DVE,)) as i:
        nc.vector.bn_stats(tile(M.stats, i), tile(M.h, i))
    v.drain()
    me, ve, mo, vo = (M.stats[:, :, c] for c in (1, 2, 4, 5))
    t0, t1 = M.tmp[:, 0, :], M.tmp[:, 1, :]
    t2, t3 = M.tmp[:, 2, :], M.tmp[:, 3, :]
    nc.vector.tensor_tensor(t0, me, mo, ADD)
    nc.vector.tensor_tensor(t1, me, mo, SUB)
    nc.vector.tensor_tensor(t2, ve, vo, ADD)
    v.drain()
    nc.vector.tensor_scalar(M.mean[:, :], t0, 0.5, None, MUL)
    nc.vector.tensor_tensor(t3, t1, t1, MUL)
    v.drain()
    nc.vector.tensor_scalar(t0, t2, 1.0 / D, eps, MUL, ADD)
    nc.vector.tensor_scalar(t1, t3, 0.25, None, MUL)
    v.drain()
    nc.vector.tensor_tensor(t2, t0, t1, ADD).then_inc(var_ready, 1)
    v.wait_ge(std_ready, 1)
    v.sem_inc(std_ready, -1)
    nc.vector.reciprocal(M.rstd[:, :], M.std[:, :])
    v.drain()


def act_ln_std(nc, a, M, var_ready, std_ready):
    a.wait_ge(var_ready, 1)
    a.sem_inc(var_ready, -1)
    nc.scalar.activation(M.std[:, :], M.tmp[:, 2, :], ACT.Sqrt).then_inc(std_ready, 1)


def ln_apply(nc, M, i, out):
    return nc.vector.tensor_scalar(out, tile(M.h, i), M.mean[:, bass.ds(i, 1)], M.rstd[:, bass.ds(i, 1)],
                                   SUB, MUL)


def pe_turn(nc, M, bank, src, n=2):
    for c in range(n):
        last = nc.tensor.transpose(M.bank[bank][:, c * P:(c + 1) * P], src[:, c * 128:(c + 1) * 128],
                                   small(M, "ident")[:, 0:P])
    return last


def turned(M, bank, n=2):
    return M.bank[bank][:, 0:n * P].rearrange("p (c t) -> p c t", c=n)


def load_everything(nc, M):
    with ExitStack() as ctx:
        zero = ctx.enter_context(nc.sbuf_tensor("zero", [128, D], F32))
        zero_set = ctx.enter_context(nc.semaphore("zero_set"))
        with nc.Block(name="load") as block:
            @block.sync
            def _(sp):
                sp.dma_start(M.small[:, :], M.dram["small"]).then_inc(M.small_loaded, 16)
                for array in EARLY:
                    sp.dma_start(M.w[array][:, :], M.dram[array]).then_inc(M.loaded[array], 16)

            @block.gpsimd
            def _(pool):
                nc.gpsimd.memset(zero[:, :], 0.0).then_inc(zero_set, 1)

            @block.scalar
            def _(act):
                act.wait_ge(zero_set, 1)
                rows = M.dram["slots_x"].rearrange("(p r) d -> p r d", p=128)
                act.dma_start(rows, spread(zero[:, :], 1, rows.shape[1])).then_inc(M.slots_cleared, 16)
                act.wait_ge(M.slots_cleared, 16)


def patch_embedding(nc, M):
    with ExitStack() as ctx:
        sb = lambda n, s: ctx.enter_context(nc.sbuf_tensor(n, s, F32))
        sem = lambda n: M.sem(n + "0")
        patches = sb("patches", [P, T, PD])
        xn = sb("tok_xn", [P, PD])
        xT = sb("tok_xT", [128, PC, P])
        st = sb("tok_st", [P, 12])
        mv = sb("tok_mv", [P, 2])
        var = sb("tok_var", [P, 1])
        std = sb("tok_std", [P, 1])
        rs = sb("tok_rs", [P, 1])
        y = sb("tok_y", [P, D])
        patches_in, var_ready, std_ready = sem("patches_in"), sem("var_ready"), sem("std_ready")
        xn_ready, turned_ready, xT_ready = sem("xn_ready"), sem("turned"), sem("xT_ready")
        emb_ready, emb_read, w_scaled = sem("emb_ready"), sem("emb_read"), sem("w_scaled")
        w = M.w["w_tok"].rearrange("p (c n) -> p c n", c=PC)
        with nc.Block(name="patch_embedding") as block:
            @block.sync
            def _(sp):
                sp.dma_start(patches[:, :, :], M.dram["patches"].rearrange("t p n -> p t n")).then_inc(patches_in, 16)

            @block.vector
            def _(v):
                v.wait_ge(M.small_loaded, 16)
                v.wait_ge(M.loaded["tok"], 16)
                for c in range(PC):
                    last = nc.vector.tensor_scalar(w[:, c, :], w[:, c, :], small(M, "ln1_w", 128)[:, c:c + 1],
                                                   None, MUL)
                last.then_inc(w_scaled, 1)

                v.wait_ge(patches_in, 16)
                v.sem_inc(patches_in, -16)

                def norm(src, halves, n, out, done):
                    for k in range(halves):
                        nc.vector.bn_stats(st[:, 6 * k:6 * k + 6], src[:, n * k:n * k + n])
                    v.drain()
                    nc.vector.bn_aggr(mv[:, :], st[:, 0:6 * halves])
                    v.drain()
                    nc.vector.tensor_scalar(var[:, :], mv[:, 1:2], 1e-5, None, ADD).then_inc(var_ready, 1)
                    v.wait_ge(std_ready, 1)
                    v.sem_inc(std_ready, -1)
                    nc.vector.reciprocal(rs[:, :], std[:, :])
                    v.drain()
                    nc.vector.tensor_scalar(out, src, mv[:, 0:1], rs[:, 0:1], SUB, MUL).then_inc(done, 1)

                with nc.Fori(0, T, engines=(ET.DVE,)) as i:
                    norm(tile(patches, i), 2, PD // 2, xn[:, :], xn_ready)
                    v.wait_ge(emb_ready, 1)
                    v.sem_inc(emb_ready, -1)
                    norm(M.bank[2][0:P, 0:D], 1, D, y[:, :], emb_read)
                    v.drain()
                    nc.vector.tensor_tensor(y[:, :], y[:, :], small(M, "ln2_w"), MUL)
                    v.drain()
                    nc.vector.tensor_tensor(tile(M.h, i), y[:, :], small(M, "base"), ADD)
                    v.drain()

            @block.scalar
            def _(a):
                a.preload_act_table(ACT.Sqrt)
                with nc.Fori(0, T, engines=(ET.Activation,)) as i:
                    a.wait_ge(var_ready, 1)
                    a.sem_inc(var_ready, -1)
                    nc.scalar.activation(std[:, :], var[:, :], ACT.Sqrt).then_inc(std_ready, 1)
                    a.wait_ge(turned_ready, 1)
                    a.sem_inc(turned_ready, -1)
                    nc.scalar.copy(xT[:, 0:4, :], turned(M, 0, 4))
                    nc.scalar.copy(xT[:, 4:PC, :], turned(M, 1, PC - 4)).then_inc(xT_ready, 1)
                    a.wait_ge(var_ready, 1)
                    a.sem_inc(var_ready, -1)
                    nc.scalar.activation(std[:, :], var[:, :], ACT.Sqrt).then_inc(std_ready, 1)

            @block.tensor
            def _(pe):
                pe.wait_ge(M.small_loaded, 16)
                pe.wait_ge(w_scaled, 1)
                pe.sem_inc(w_scaled, -1)
                with nc.Fori(0, T, engines=(ET.PE,)) as i:
                    pe.wait_ge(xn_ready, 1)
                    pe.sem_inc(xn_ready, -1)
                    pe_turn(nc, M, 0, xn[:, 0:512], 4)
                    pe_turn(nc, M, 1, xn[:, 512:PD], PC - 4).then_inc(turned_ready, 1)
                    pe.wait_ge(xT_ready, 1)
                    pe.sem_inc(xT_ready, -1)
                    for c in range(PC):
                        last = nc.tensor.matmul(M.bank[2][0:P, 0:D], xT[:, c, :], w[:, c, :],
                                                start=(c == 0), stop=(c == PC - 1))
                    last.then_inc(emb_ready, 1)
                    pe.wait_ge(emb_read, 1)
                    pe.sem_inc(emb_read, -1)


def pe_turn_tiles(nc, pe, M, xn, xn_ready, turned_ready, turned_read):
    with nc.Fori(0, T, engines=(ET.PE,)) as i:
        pe.wait_ge(xn_ready, 1)
        pe.sem_inc(xn_ready, -1)
        pe_turn(nc, M, 0, xn).then_inc(turned_ready, 1)
        pe.wait_ge(turned_read, 1)
        pe.sem_inc(turned_read, -1)


def add_back(nc, M, name):
    with ExitStack() as ctx:
        sem = lambda n: M.sem(n + "0")
        y = ctx.enter_context(nc.sbuf_tensor("back_y" + name, [128, 2, P], F32))
        y_ready, back_ready, y_free, back_read = sem("y_ready"), sem("oT_turned"), sem("y_free"), sem("back_read")
        with nc.Block(name="add_back" + name) as block:
            @block.scalar
            def _(a):
                with nc.Fori(0, T, engines=(ET.Activation,)) as i:
                    nc.scalar.copy(y[:, :, :], cols(M.yT, i)).then_inc(y_ready, 1)
                    a.wait_ge(y_free, 1)
                    a.sem_inc(y_free, -1)

            @block.tensor
            def _(pe):
                with nc.Fori(0, T, engines=(ET.PE,)) as i:
                    pe.wait_ge(y_ready, 1)
                    pe.sem_inc(y_ready, -1)
                    for c in range(2):
                        last = nc.tensor.transpose(M.bank[0][0:P, c * 128:(c + 1) * 128], y[:, c, :],
                                                   small(M, "ident", 128))
                    last.then_inc(back_ready, 1)
                    pe.wait_ge(back_read, 1)
                    pe.sem_inc(back_read, -1)

            @block.vector
            def _(v):
                with nc.Fori(0, T, engines=(ET.DVE,)) as i:
                    v.wait_ge(back_ready, 1)
                    v.sem_inc(back_ready, -1)
                    v.sem_inc(y_free, 1)
                    nc.vector.tensor_tensor(tile(M.h, i), tile(M.h, i), M.bank[0][0:P, 0:D], ADD
                                            ).then_inc(back_read, 1)
                v.drain()


LANES = 2


def tiles_by_lanes(nc, engine, body):
    with nc.Fori(0, T // LANES, engines=(engine,)) as p:
        body([(b, p * LANES + b) for b in range(LANES)])
    for t in range(T - T % LANES, T):
        body([(0, t)])


def evacuate_q(nc, M, bank, qm, bias=None):
    for c in range(2):
        out = qm[:, c, :].rearrange("p (s w) -> p s w", w=CW)[:, :, 0:L]
        src = M.bank[bank][:, c * P:(c + 1) * P].rearrange("p (s j) -> p s j", s=SEQS)
        last = nc.vector.tensor_scalar(out, src, bias[:, c:c + 1] if bias is not None else 0.0, None, ADD)
    return last


def mask_k_heads(nc, M, kT, km):
    for c in range(2):
        last = nc.vector.tensor_tensor(km[:, c, :, :], spread(kT[:, c, :], 1, 8),
                                       spread(small(M, "mask8", 128), 2, P), MUL)
    return last


def pe_scores(nc, M, banks, qm, km):
    for c in range(2):
        for s in range(SEQS):
            last = nc.tensor.matmul(M.bank[banks[c]][0:P, 0:8 * L], qm[:, c, s * P:(s + 1) * P],
                                    km[:, c, :, s * L:(s + 1) * L], start=(s == 0), stop=(s == SEQS - 1))
    return last


def pe_turn_probs(nc, M, banks, probs, maps):
    groups = -(-maps // 3)
    for g in range(groups):
        n = min(3, maps - 3 * g) * L
        out = M.bank[banks[g // 4]][0:n, (g % 4) * P:(g % 4 + 1) * P]
        last = nc.tensor.transpose(out, probs[:, 3 * g * L:3 * g * L + n], small(M, "ident")[:, 0:P])
    return last


def evacuate_probs(nc, M, banks, pm, maps):
    for g in range(-(-maps // 3)):
        n = min(3, maps - 3 * g) * L
        src = M.bank[banks[g // 4]][0:n, (g % 4) * P:(g % 4 + 1) * P].rearrange("p (s j) -> p s j", s=SEQS)
        out = pm[0:n, g, :].rearrange("p (s w) -> p s w", w=CW)[:, :, 0:L]
        last = nc.scalar.copy(out, src)
    return last


def pe_values(nc, M, bank, pm, vm, maps, dv):
    for g in range(-(-maps // 3)):
        k = min(3, maps - 3 * g)
        for s in range(SEQS):
            last = nc.tensor.matmul(M.bank[bank][0:P, 3 * g * dv:(3 * g + k) * dv],
                                    pm[0:k * L, g, s * P:(s + 1) * P],
                                    vm[0:k * L, s, 3 * g * dv:(3 * g + k) * dv],
                                    start=(s == 0), stop=(s == SEQS - 1))
    return last


def pe_project(nc, M, bank, lhs, w, n0, n1, rows=P, col=0):
    for k in range(2):
        last = nc.tensor.matmul(M.bank[bank][0:rows, col:col + n1 - n0], lhs[:, k, :], w[:, k, n0:n1],
                                start=(k == 0), stop=(k == 1))
    return last


def repeat_x(nc, M, bank, xr):
    for k in range(2):
        src = M.bank[bank][:, k * P:(k + 1) * P].rearrange("p (s j) -> p s j", s=SEQS)
        last = nc.scalar.copy(xr[:, k, :, :].rearrange("p s (r j) -> p s r j", r=3), spread(src, 2, 3))
    return last


def pe_values_in(nc, M, banks, xr, w, n0):
    for s in range(SEQS):
        for k in range(2):
            last = nc.tensor.matmul(M.bank[banks[s // 2]][0:P, (s % 2) * D:(s % 2 + 1) * D],
                                    xr[:, k, s, :], w[:, k, n0:n0 + D], start=(k == 0), stop=(k == 1))
    return last


def mask_v(nc, M, banks, vm, mask, maps):
    dv = D // maps
    m = spread(mask, 2, dv)
    for s in range(SEQS):
        src = M.bank[banks[s // 2]][0:P, (s % 2) * D:(s % 2 + 1) * D].rearrange("p (m d) -> p m d", m=maps)
        last = nc.vector.tensor_tensor(vm[:, s, :].rearrange("p (m d) -> p m d", m=maps), src, m, MUL)
    return last


def alibi_attention(nc, M):
    with ExitStack() as ctx:
        sb = lambda n, s: [ctx.enter_context(nc.sbuf_tensor(f"a0_{n}{b}", s, F32)) for b in range(LANES)]
        sem = lambda n: [M.sem(f"{n}{b}") for b in range(LANES)]
        xn, xT, kT, xr = sb("xn", [P, D]), sb("xT", [128, 2, P]), sb("kT", [128, 2, P]), sb("xr", [128, 2, SEQS, P])
        qm, km = sb("qm", [128, 2, SEQS * CW]), sb("km", [128, 2, 8, P])
        vm, S, Pr = sb("vm", [P, SEQS, D]), sb("S", [P, H16, L]), sb("Pr", [P, H16, L])
        mx, rsum = sb("mx", [P, H16]), sb("rsum", [P, H16])
        pm, o, oT, y = sb("pm", [P, 6, SEQS * CW]), sb("o", [P, D]), sb("oT", [128, 2, P]), sb("y", [P, D])
        var_ready, std_ready, blank, pblank = M.sem("var_ready0"), M.sem("std_ready0"), M.sem("blank"), M.sem("pblank")
        xn_ready, turned_ready, xT_ready, xr_ready = sem("xn_ready"), sem("turned"), sem("xT_ready"), sem("xr_ready")
        q_ready, k_ready, v_ready = sem("q_ready"), sem("k_ready"), sem("v_ready")
        kT_ready, km_ready, vm_ready = sem("kT_ready"), sem("km_ready"), sem("vm_ready")
        s_ready, shifted, probs_dve, probs_pe = sem("s_ready"), sem("shifted"), sem("probs_dve"), sem("probs_pe")
        pT_ready, pm_ready, o_ready, on_ready = sem("pT_ready"), sem("pm_ready"), sem("o_ready"), sem("on_ready")
        oT_turned, oT_ready, y_ready = sem("oT_turned"), sem("oT_ready"), sem("y_ready")
        w = M.w["w_in"].rearrange("p (k n) -> p k n", k=2)
        wo = M.w["w_out"].rearrange("p (k n) -> p k n", k=2)
        A, B, C, Dk = ([4 * b + j for b in range(LANES)] for j in range(4))
        with nc.Block(name="alibi_attention") as block:
            @block.gpsimd
            def _(pool):
                for b in range(LANES):
                    nc.gpsimd.memset(qm[b][:, :, :], 0.0).then_inc(blank, 1)
                    nc.gpsimd.memset(pm[b][:, :, :], 0.0).then_inc(pblank, 1)

            @block.vector
            def _(v):
                dve_ln_stats(nc, v, M, var_ready, std_ready)
                v.wait_ge(blank, LANES)
                v.sem_inc(blank, -LANES)

                def body(lanes):
                    for b, i in lanes:
                        ln_apply(nc, M, i, xn[b][:, :]).then_inc(xn_ready[b], 1)
                    for b, i in lanes:
                        v.wait_ge(q_ready[b], 1)
                        v.sem_inc(q_ready[b], -1)
                        evacuate_q(nc, M, B[b], qm[b], small(M, "b_q0", 128))
                        v.wait_ge(kT_ready[b], 1)
                        v.sem_inc(kT_ready[b], -1)
                        mask_k_heads(nc, M, kT[b], km[b]).then_inc(km_ready[b], 1)
                    for b, i in lanes:
                        v.wait_ge(v_ready[b], 1)
                        v.sem_inc(v_ready[b], -1)
                        mask_v(nc, M, (Dk[b], A[b]), vm[b], small(M, "vm16"), H16).then_inc(vm_ready[b], 1)
                    for b, i in lanes:
                        v.wait_ge(s_ready[b], 1)
                        v.sem_inc(s_ready[b], -1)
                        for c, bank in enumerate((B[b], C[b])):
                            m = slice(8 * c, 8 * c + 8)
                            nc.vector.scalar_tensor_tensor(
                                S[b][:, m, :], M.bank[bank][0:P, 0:8 * L].rearrange("p (m j) -> p m j", m=8),
                                DH ** -0.5, small(M, "alibi").rearrange("p (m j) -> p m j", m=H16)[:, m, :], MUL, ADD)
                        v.drain()
                        nc.vector.tensor_reduce(mx[b][:, :], S[b][:, :, :], AX.X, MAX)
                        v.drain()
                        nc.vector.tensor_tensor(S[b][:, :, :], S[b][:, :, :], spread(mx[b][:, :], 2, L), SUB
                                                ).then_inc(shifted[b], 1)
                    for b, i in lanes:
                        v.wait_ge(probs_dve[b], 1)
                        v.sem_inc(probs_dve[b], -1)
                        nc.vector.tensor_reduce(mx[b][:, :], Pr[b][:, :, :], AX.X, ADD)
                        v.drain()
                        nc.vector.reciprocal(rsum[b][:, :], mx[b][:, :])
                    v.drain()
                    for b, i in lanes:
                        v.wait_ge(o_ready[b], 1)
                        v.sem_inc(o_ready[b], -1)
                        nc.vector.tensor_tensor(o[b][:, :].rearrange("p (m d) -> p m d", m=H16),
                                                M.bank[B[b]][0:P, 0:D].rearrange("p (m d) -> p m d", m=H16),
                                                spread(rsum[b][:, :], 2, DH), MUL)
                        v.drain()
                        nc.vector.tensor_tensor(o[b][:, :], o[b][:, :], small(M, "b_v0"), ADD).then_inc(on_ready[b], 1)
                    for b, i in lanes:
                        v.wait_ge(y_ready[b], 1)
                        v.sem_inc(y_ready[b], -1)
                        nc.vector.tensor_tensor(y[b][:, :], M.bank[Dk[b]][0:P, 0:D], small(M, "b_out0"), ADD)
                        v.drain()
                        nc.vector.tensor_tensor(tile(M.h, i), tile(M.h, i), y[b][:, :], ADD)
                    v.drain()

                tiles_by_lanes(nc, ET.DVE, body)

            @block.scalar
            def _(a):
                act_ln_std(nc, a, M, var_ready, std_ready)
                a.preload_act_table(ACT.Exp)
                a.wait_ge(pblank, LANES)
                a.sem_inc(pblank, -LANES)

                def body(lanes):
                    for b, i in lanes:
                        a.wait_ge(turned_ready[b], 1)
                        a.sem_inc(turned_ready[b], -1)
                        nc.scalar.copy(xT[b][:, :, :], turned(M, A[b])).then_inc(xT_ready[b], 1)
                        repeat_x(nc, M, A[b], xr[b]).then_inc(xr_ready[b], 1)
                    for b, i in lanes:
                        a.wait_ge(k_ready[b], 1)
                        a.sem_inc(k_ready[b], -1)
                        for c in range(2):
                            last = nc.scalar.activation(kT[b][:, c, :], M.bank[C[b]][:, c * P:(c + 1) * P], ACT.Identity,
                                                        bias=small(M, "b_k0", 128)[:, c:c + 1])
                        last.then_inc(kT_ready[b], 1)
                    for b, i in lanes:
                        a.wait_ge(shifted[b], 1)
                        a.sem_inc(shifted[b], -1)
                        nc.scalar.activation(Pr[b][:, :, :], S[b][:, :, :], ACT.Exp).then_inc(probs_dve[b], 1)
                        a.drain().then_inc(probs_pe[b], 1)
                    for b, i in lanes:
                        a.wait_ge(pT_ready[b], 1)
                        a.sem_inc(pT_ready[b], -1)
                        evacuate_probs(nc, M, (Dk[b], A[b]), pm[b], H16).then_inc(pm_ready[b], 1)
                    for b, i in lanes:
                        a.wait_ge(oT_turned[b], 1)
                        a.sem_inc(oT_turned[b], -1)
                        nc.scalar.copy(oT[b][:, :, :], turned(M, C[b])).then_inc(oT_ready[b], 1)
                    a.drain()

                tiles_by_lanes(nc, ET.Activation, body)

            @block.tensor
            def _(pe):
                def body(lanes):
                    for b, i in lanes:
                        pe.wait_ge(xn_ready[b], 1)
                        pe.sem_inc(xn_ready[b], -1)
                        pe_turn(nc, M, A[b], xn[b]).then_inc(turned_ready[b], 1)
                    for b, i in lanes:
                        pe.wait_ge(xT_ready[b], 1)
                        pe.sem_inc(xT_ready[b], -1)
                        for c in range(2):
                            last = pe_project(nc, M, B[b], w[:, :, c * 128:(c + 1) * 128], xT[b], 0, P, 128, col=c * P)
                        last.then_inc(q_ready[b], 1)
                        for c in range(2):
                            last = pe_project(nc, M, C[b], w[:, :, D + c * 128:D + (c + 1) * 128], xT[b], 0, P, 128, col=c * P)
                        last.then_inc(k_ready[b], 1)
                    for b, i in lanes:
                        pe.wait_ge(xr_ready[b], 1)
                        pe.sem_inc(xr_ready[b], -1)
                        pe_values_in(nc, M, (Dk[b], A[b]), xr[b], w, 2 * D).then_inc(v_ready[b], 1)
                    for b, i in lanes:
                        pe.wait_ge(km_ready[b], 1)
                        pe.sem_inc(km_ready[b], -1)
                        pe_scores(nc, M, (B[b], C[b]), qm[b], km[b]).then_inc(s_ready[b], 1)
                    for b, i in lanes:
                        pe.wait_ge(probs_pe[b], 1)
                        pe.sem_inc(probs_pe[b], -1)
                        pe.wait_ge(vm_ready[b], 1)
                        pe.sem_inc(vm_ready[b], -1)
                        pe_turn_probs(nc, M, (Dk[b], A[b]), Pr[b][:, :, :].rearrange("p m j -> p (m j)"), H16
                                      ).then_inc(pT_ready[b], 1)
                    for b, i in lanes:
                        pe.wait_ge(pm_ready[b], 1)
                        pe.sem_inc(pm_ready[b], -1)
                        pe_values(nc, M, B[b], pm[b], vm[b], H16, DH).then_inc(o_ready[b], 1)
                    for b, i in lanes:
                        pe.wait_ge(on_ready[b], 1)
                        pe.sem_inc(on_ready[b], -1)
                        pe_turn(nc, M, C[b], o[b]).then_inc(oT_turned[b], 1)
                    for b, i in lanes:
                        pe.wait_ge(oT_ready[b], 1)
                        pe.sem_inc(oT_ready[b], -1)
                        pe_project(nc, M, Dk[b], oT[b], wo, 0, D).then_inc(y_ready[b], 1)

                pe.wait_ge(M.loaded["l0a"], 16)
                tiles_by_lanes(nc, ET.PE, body)


def gate_top2(nc, M, name, gate, dram_cw, full_softmax):
    E = 8
    with ExitStack() as ctx:
        sb = lambda n, s: ctx.enter_context(nc.sbuf_tensor(name + n, s, F32))
        sem = lambda n: M.sem(n + "0")
        xn, xT = sb("xn", [P, D]), sb("xT", [128, 2, P])
        lg, neg, ex, gt, eq = sb("lg", [P, E]), sb("neg", [P, 1]), sb("ex", [P, E]), sb("gt", [P, E, E]), sb("eq", [P, E, E])
        rank, mask, se, re, cw = sb("rank", [P, E]), sb("mask", [P, E]), sb("se", [P, 1]), sb("re", [P, 1]), sb("cw", [P, E])
        cwT = sb("cwT", [E, P])
        var_ready, std_ready, xn_ready = sem("var_ready"), sem("std_ready"), sem("xn_ready")
        turned_ready, xT_ready, lg_ready = sem("turned"), sem("xT_ready"), sem("q_ready")
        shifted, ex_ready, cw_ready, cwT_turned = sem("shifted"), sem("probs_dve"), sem("on_ready"), sem("oT_turned")
        cwT_ready, cw_stored = sem("oT_ready"), sem("cw_stored")
        w = gate.rearrange("p (k n) -> p k n", k=2)
        with nc.Block(name=name) as block:
            @block.vector
            def _(v):
                dve_ln_stats(nc, v, M, var_ready, std_ready)
                with nc.Fori(0, T, engines=(ET.DVE,)) as i:
                    ln_apply(nc, M, i, xn[:, :]).then_inc(xn_ready, 1)
                    v.wait_ge(lg_ready, 1)
                    v.sem_inc(lg_ready, -1)
                    nc.vector.tensor_copy(lg[:, :], M.bank[1][0:P, 0:E])
                    v.drain()
                    nc.vector.tensor_reduce(neg[:, :], lg[:, :], AX.X, MAX)
                    other, own = spread(lg[:, :], 1, E), spread(lg[:, :], 2, E)
                    nc.vector.tensor_tensor(gt[:, :, :], other, own, ALU.is_gt)
                    nc.vector.tensor_tensor(eq[:, :, :], other, own, ALU.is_equal)
                    v.drain()
                    nc.vector.tensor_scalar(ex[:, :], lg[:, :], neg[:, 0:1], None, SUB).then_inc(shifted, 1)
                    nc.vector.tensor_tensor(eq[:, :, :], eq[:, :, :],
                                            small(M, "below8").rearrange("p (a b) -> p a b", a=E), MUL)
                    v.drain()
                    nc.vector.tensor_tensor(gt[:, :, :], gt[:, :, :], eq[:, :, :], ADD)
                    v.drain()
                    nc.vector.tensor_reduce(rank[:, :], gt[:, :, :], AX.X, ADD)
                    v.drain()
                    nc.vector.tensor_scalar(mask[:, :], rank[:, :], 2.0, None, ALU.is_lt)
                    v.wait_ge(ex_ready, 1)
                    v.sem_inc(ex_ready, -1)
                    v.drain()
                    nc.vector.tensor_tensor(cw[:, :], ex[:, :], mask[:, :], MUL)
                    v.drain()
                    nc.vector.tensor_reduce(se[:, :], ex[:, :] if full_softmax else cw[:, :], AX.X, ADD)
                    v.drain()
                    nc.vector.reciprocal(re[:, :], se[:, :])
                    v.drain()
                    nc.vector.tensor_scalar(cw[:, :], cw[:, :], re[:, 0:1], None, MUL).then_inc(cw_ready, 1)
                    v.drain()

            @block.scalar
            def _(a):
                act_ln_std(nc, a, M, var_ready, std_ready)
                a.preload_act_table(ACT.Exp)
                with nc.Fori(0, T, engines=(ET.Activation,)) as i:
                    a.wait_ge(turned_ready, 1)
                    a.sem_inc(turned_ready, -1)
                    nc.scalar.copy(xT[:, :, :], turned(M, 0)).then_inc(xT_ready, 1)
                    nc.scalar.copy(cols(M.xT, i), turned(M, 0))
                    a.wait_ge(shifted, 1)
                    a.sem_inc(shifted, -1)
                    nc.scalar.activation(ex[:, :], ex[:, :], ACT.Exp).then_inc(ex_ready, 1)
                    a.wait_ge(cwT_turned, 1)
                    a.sem_inc(cwT_turned, -1)
                    nc.scalar.copy(cwT[:, :], M.bank[2][0:E, 0:P])
                    a.drain()
                    a.dma_start(dram_cw[:, bass.ds(i * P, P)], cwT[:, :]).then_inc(cw_stored, 16)
                    a.wait_ge(cw_stored, 16)
                    a.sem_inc(cw_stored, -16)

            @block.tensor
            def _(pe):
                with nc.Fori(0, T, engines=(ET.PE,)) as i:
                    pe.wait_ge(xn_ready, 1)
                    pe.sem_inc(xn_ready, -1)
                    pe_turn(nc, M, 0, xn).then_inc(turned_ready, 1)
                    pe.wait_ge(xT_ready, 1)
                    pe.sem_inc(xT_ready, -1)
                    pe_project(nc, M, 1, xT, w, 0, E).then_inc(lg_ready, 1)
                    pe.wait_ge(cw_ready, 1)
                    pe.sem_inc(cw_ready, -1)
                    nc.tensor.transpose(M.bank[2][0:E, 0:P], cw[:, :], small(M, "ident")[:, 0:P]).then_inc(cwT_turned, 1)


def experts0(nc, M):
    FC = F0 // 128
    with ExitStack() as ctx:
        sb = lambda n, s: ctx.enter_context(nc.sbuf_tensor("e0_" + n, s, F32))
        sem = lambda n: M.sem(n + "0")
        w1 = [sb(f"w1_{b}", [128, 2, F0]) for b in range(2)]
        w2 = [sb(f"w2_{b}", [128, FC, D]) for b in range(2)]
        b1 = [sb(f"b1_{b}", [128, FC]) for b in range(2)]
        cw = [sb(f"cw_{b}", [128, NTOK]) for b in range(2)]
        b2 = [sb(f"b2_{b}", [128, 2]) for b in range(2)]
        hid = [sb(f"hid_{b}", [128, GC]) for b in range(2)]
        yw = sb("yw", [128, 2, GC])
        loaded = [sem(f"loaded{b}") for b in range(2)]
        loaded_act = [sem(f"loaded_act_{b}") for b in range(2)]
        cw_loaded = [sem(f"cw_loaded_{b}") for b in range(2)]
        used, cw_used = [sem(f"e0_used_{b}") for b in range(2)], [sem(f"e0_cw_used_{b}") for b in range(2)]
        h1_ready, hid_ready, y_ready, y_read = sem("h1_ready"), sem("hid_ready"), sem("y_ready"), sem("e0_y_read")
        xg = M.xT[:, :, :].rearrange("p k (g n) -> p k g n", g=G)
        yg = M.yT[:, :, :].rearrange("p k (g n) -> p k g n", g=G)
        with nc.Block(name="experts0") as block:
            @block.sync
            def _(sp):
                with nc.Fori(0, E0 // 2, engines=(ET.SP,)) as p:
                    for b in range(2):
                        e = p * 2 + b
                        sp.wait_ge(used[b], 1)
                        sp.sem_inc(used[b], -1)
                        sp.dma_start(w1[b][:, :, :].rearrange("p k n -> p (k n)"),
                                     M.dram["w1_0"][bass.ds(e, 1)].rearrange("a p n -> (a p) n")).then_inc(loaded[b], 16)
                        sp.dma_start(w2[b][:, :, :].rearrange("p k n -> p (k n)"),
                                     M.dram["w2_0"][bass.ds(e, 1)].rearrange("a p n -> (a p) n")).then_inc(loaded[b], 16)
                        sp.dma_start(b1[b][:, :],
                                     M.dram["b1_0"][bass.ds(e, 1)].rearrange("a p n -> (a p) n")).then_inc(loaded_act[b], 16)
                        sp.wait_ge(cw_used[b], 1)
                        sp.sem_inc(cw_used[b], -1)
                        sp.dma_start(b2[b][:, :],
                                     M.dram["b2_0"][bass.ds(e, 1)].rearrange("a p n -> (a p) n")).then_inc(cw_loaded[b], 16)
                        sp.dma_start(cw[b][:, :],
                                     M.dram["cw0"][bass.ds(e, 1), :].rearrange("a n -> (a n)").partition_broadcast(128)
                                     ).then_inc(cw_loaded[b], 16)

            @block.tensor
            def _(pe):
                for b in range(2):
                    pe.sem_inc(used[b], 1)
                with nc.Fori(0, E0 // 2, engines=(ET.PE,)) as p:
                    for b in range(2):
                        pe.wait_ge(loaded[b], 32)
                        pe.sem_inc(loaded[b], -32)
                        with nc.Fori(0, G, engines=(ET.PE,)) as g:
                            x = xg[:, :, bass.ds(g, 1), :].rearrange("p k a n -> p k (a n)")

                            def up(f):
                                for k in range(2):
                                    last = nc.tensor.matmul(M.bank[f % 2][:, 0:GC], w1[b][:, k, f * 128:(f + 1) * 128],
                                                            x[:, k, :], start=(k == 0), stop=(k == 1))
                                last.then_inc(h1_ready, 1)

                            up(0)
                            for f in range(FC):
                                if f + 1 < FC:
                                    up(f + 1)
                                if f == 0:
                                    pe.wait_ge(y_read, 1)
                                    pe.sem_inc(y_read, -1)
                                pe.wait_ge(hid_ready, 1)
                                pe.sem_inc(hid_ready, -1)
                                for c in range(2):
                                    last = nc.tensor.matmul(M.bank[2 + c][:, 0:GC], w2[b][:, f, c * 128:(c + 1) * 128],
                                                            hid[f % 2][:, :], start=(f == 0), stop=(f == FC - 1))
                            last.then_inc(y_ready, 1)
                        pe.drain().then_inc(used[b], 1)

            @block.scalar
            def _(a):
                a.preload_act_table(ACT.Gelu)
                with nc.Fori(0, E0 // 2, engines=(ET.Activation,)) as p:
                    for b in range(2):
                        a.wait_ge(loaded_act[b], 16)
                        a.sem_inc(loaded_act[b], -16)
                        with nc.Fori(0, G, engines=(ET.Activation,)) as g:
                            for f in range(FC):
                                a.wait_ge(h1_ready, 1)
                                a.sem_inc(h1_ready, -1)
                                nc.scalar.activation(hid[f % 2][:, :], M.bank[f % 2][:, 0:GC], ACT.Gelu,
                                                     bias=b1[b][:, f:f + 1]).then_inc(hid_ready, 1)
                        a.drain()

            @block.vector
            def _(v):
                v.sem_inc(y_read, 1)
                for b in range(2):
                    v.sem_inc(cw_used[b], 1)
                nc.vector.memset(M.yT[:, :, :], 0.0)
                v.drain()
                with nc.Fori(0, E0 // 2, engines=(ET.DVE,)) as p:
                    for b in range(2):
                        v.wait_ge(cw_loaded[b], 32)
                        v.sem_inc(cw_loaded[b], -32)
                        with nc.Fori(0, G, engines=(ET.DVE,)) as g:
                            v.wait_ge(y_ready, 1)
                            v.sem_inc(y_ready, -1)
                            for c in range(2):
                                last = nc.vector.scalar_tensor_tensor(
                                    yw[:, c, :], M.bank[2 + c][:, 0:GC], b2[b][:, c:c + 1],
                                    cw[b][:, bass.ds(g * GC, GC)], ADD, MUL)
                            last.then_inc(y_read, 1)
                            v.drain()
                            y = yg[:, :, bass.ds(g, 1), :].rearrange("p k a n -> p k (a n)")
                            nc.vector.tensor_tensor(y, y, yw[:, :, :], ADD)
                            v.drain()
                        v.drain().then_inc(cw_used[b], 1)


def rotary_attention(nc, M):
    NH, DV = 8, 32
    with ExitStack() as ctx:
        one = lambda n, s: ctx.enter_context(nc.sbuf_tensor("a1_" + n, s, F32))
        sb = lambda n, s: [one(f"{n}{b}", s) for b in range(LANES)]
        sem = lambda n: [M.sem(f"{n}{b}") for b in range(LANES)]
        xn, xT, kT, xr = sb("xn", [P, D]), sb("xT", [128, 2, P]), sb("kT", [128, 2, P]), sb("xr", [128, 2, SEQS, P])
        qk, rot = sb("qk", [P, 2 * D]), sb("rot", [P, 2 * D])
        qm, km = sb("qm", [128, 2, SEQS * CW]), sb("km", [128, 2, 8, P])
        vm, S, Pr = sb("vm", [P, SEQS, D]), sb("S", [P, H16, L]), sb("Pr", [P, H16, L])
        probs, mx, rsum = sb("A", [P, NH, L]), sb("mx", [P, H16]), sb("rsum", [P, H16])
        pm, o, oT = sb("pm", [P, 3, SEQS * CW]), sb("o", [P, D]), sb("oT", [128, 2, P])
        ms, lamv, lam2, lam = one("ms", [P, T, NH]), one("lamv", [P, 32]), one("lam2", [P, 2]), one("lam", [P, 1])
        root = one("root", [P, T, NH])
        var_ready, std_ready, blank, pblank = M.sem("var_ready0"), M.sem("std_ready0"), M.sem("blank"), M.sem("pblank")
        lam_dot, lam_exp, ms_ready, root_ready = M.sem("lam_dot"), M.sem("lam_exp"), M.sem("ms_ready"), M.sem("root_ready")
        xn_ready, turned_ready, xT_ready, xr_ready = sem("xn_ready"), sem("turned"), sem("xT_ready"), sem("xr_ready")
        q_ready, k_ready, v_ready, qk_rotated = sem("q_ready"), sem("k_ready"), sem("v_ready"), sem("qk_rotated")
        q_turned, k_turned, kT_ready, km_ready = sem("q_turned"), sem("k_turned"), sem("kT_ready"), sem("km_ready")
        vm_ready, s_ready, shifted, probs_ready = sem("vm_ready"), sem("s_ready"), sem("shifted"), sem("probs_dve")
        mixed, pT_ready, pm_ready, o_ready = sem("mixed"), sem("pT_ready"), sem("pm_ready"), sem("o_ready")
        on_ready, oT_turned, oT_ready, y_ready = sem("on_ready"), sem("oT_turned"), sem("oT_ready"), sem("y_ready")
        wqk = M.w["qk1"].rearrange("p (k n) -> p k n", k=2)
        wv = M.w["v1"].rearrange("p (k n) -> p k n", k=2)
        wo = M.w["o1"].rearrange("p (k n) -> p k n", k=2)
        A, B, C, Dk = ([4 * b + j for b in range(LANES)] for j in range(4))
        with nc.Block(name="rotary_attention") as block:
            @block.gpsimd
            def _(pool):
                for b in range(LANES):
                    nc.gpsimd.memset(qm[b][:, :, :], 0.0).then_inc(blank, 1)
                    nc.gpsimd.memset(pm[b][:, :, :], 0.0).then_inc(pblank, 1)

            @block.vector
            def _(v):
                dve_ln_stats(nc, v, M, var_ready, std_ready)
                lv = small(M, "lam").rearrange("p (i qk d) -> p i qk d", i=2, qk=2)
                nc.vector.tensor_tensor(lamv[:, :].rearrange("p (i d) -> p i d", i=2), lv[:, :, 0, :], lv[:, :, 1, :], MUL)
                nc.vector.tensor_scalar(small(M, "ln_w"), small(M, "ln_w"), 1.0 - LAMBDA_INIT, None, MUL)
                nc.vector.tensor_scalar(small(M, "ln_b"), small(M, "ln_b"), 1.0 - LAMBDA_INIT, None, MUL)
                v.drain()
                nc.vector.tensor_reduce(lam2[:, :], lamv[:, :].rearrange("p (i d) -> p i d", i=2), AX.X, ADD
                                        ).then_inc(lam_dot, 1)
                v.wait_ge(lam_exp, 1)
                v.sem_inc(lam_exp, -1)
                nc.vector.tensor_tensor(lam[:, :], lam2[:, 1:2], lam2[:, 0:1], SUB)
                v.drain()
                nc.vector.tensor_scalar(lam[:, :], lam[:, :], -LAMBDA_INIT, None, ADD)
                v.drain()
                v.wait_ge(blank, LANES)
                v.sem_inc(blank, -LANES)
                cosv = spread(small(M, "cos"), 1, 2 * H16)
                sinv = small(M, "sin").rearrange("p (d e) -> p d e", e=2)

                def scores(lanes):
                    for b, i in lanes:
                        ln_apply(nc, M, i, xn[b][:, :]).then_inc(xn_ready[b], 1)
                    for b, i in lanes:
                        v.wait_ge(q_ready[b], 1)
                        v.sem_inc(q_ready[b], -1)
                        q3 = M.bank[B[b]][0:P, :].rearrange("p (m d) -> p m d", d=DH)
                        nc.vector.tensor_tensor(qk[b][:, :].rearrange("p (m d) -> p m d", d=DH), q3, cosv, MUL)
                        q4 = M.bank[B[b]][0:P, :].rearrange("p (m d e) -> p m d e", d=DH // 2, e=2)
                        r4 = rot[b][:, :].rearrange("p (m d e) -> p m d e", d=DH // 2, e=2)
                        for e in range(2):
                            nc.vector.tensor_tensor(r4[:, :, :, e], q4[:, :, :, 1 - e], spread(sinv[:, :, e], 1, 2 * H16), MUL)
                        v.drain()
                        nc.vector.tensor_tensor(qk[b][:, :], qk[b][:, :], rot[b][:, :], ADD).then_inc(qk_rotated[b], 1)
                    for b, i in lanes:
                        v.wait_ge(v_ready[b], 1)
                        v.sem_inc(v_ready[b], -1)
                        mask_v(nc, M, (Dk[b], A[b]), vm[b], small(M, "vm8"), NH).then_inc(vm_ready[b], 1)
                    for b, i in lanes:
                        v.wait_ge(q_turned[b], 1)
                        v.sem_inc(q_turned[b], -1)
                        evacuate_q(nc, M, B[b], qm[b])
                        v.wait_ge(kT_ready[b], 1)
                        v.sem_inc(kT_ready[b], -1)
                        mask_k_heads(nc, M, kT[b], km[b]).then_inc(km_ready[b], 1)
                    for b, i in lanes:
                        v.wait_ge(s_ready[b], 1)
                        v.sem_inc(s_ready[b], -1)
                        for c, bank in enumerate((B[b], C[b])):
                            nc.vector.tensor_scalar(S[b][:, 8 * c:8 * c + 8, :],
                                                    M.bank[bank][0:P, 0:8 * L].rearrange("p (m j) -> p m j", m=8),
                                                    DH ** -0.25, None, MUL)
                        v.drain()
                        nc.vector.tensor_reduce(mx[b][:, :], S[b][:, :, :], AX.X, MAX)
                        v.drain()
                        nc.vector.tensor_tensor(S[b][:, :, :], S[b][:, :, :], spread(mx[b][:, :], 2, L), SUB
                                                ).then_inc(shifted[b], 1)
                    for b, i in lanes:
                        v.wait_ge(probs_ready[b], 1)
                        v.sem_inc(probs_ready[b], -1)
                        nc.vector.tensor_reduce(mx[b][:, :], Pr[b][:, :, :], AX.X, ADD)
                        v.drain()
                        nc.vector.reciprocal(rsum[b][:, :], mx[b][:, :])
                        v.drain()
                        pair = rsum[b][:, :].rearrange("p (h i) -> p h i", i=2)
                        nc.vector.tensor_scalar(pair[:, :, 1], pair[:, :, 1], lam[:, 0:1], None, MUL)
                        v.drain()
                        nc.vector.tensor_tensor(S[b][:, :, :], Pr[b][:, :, :], spread(rsum[b][:, :], 2, L), MUL)
                        v.drain()
                        p2 = S[b][:, :, :].rearrange("p (h i) j -> p h i j", i=2)
                        nc.vector.tensor_tensor(probs[b][:, :, :], p2[:, :, 0, :], p2[:, :, 1, :], ADD
                                                ).then_inc(mixed[b], 1)
                    for b, i in lanes:
                        v.wait_ge(o_ready[b], 1)
                        v.sem_inc(o_ready[b], -1)
                        nc.vector.tensor_copy(tile(M.x, i), M.bank[B[b]][0:P, 0:D])
                    v.drain()
                    for b, i in lanes:
                        nc.vector.tensor_tensor(o[b][:, :], tile(M.x, i), tile(M.x, i), MUL)
                    v.drain()
                    for b, i in lanes:
                        nc.vector.tensor_reduce(tile(ms, i), o[b][:, :].rearrange("p (h d) -> p h d", h=NH), AX.X, ADD)
                    v.drain()

                def project(lanes):
                    for b, i in lanes:
                        o3 = o[b][:, :].rearrange("p (h d) -> p h d", h=NH)
                        nc.vector.tensor_tensor(o3, tile(M.x, i).rearrange("p (h d) -> p h d", h=NH),
                                                spread(tile(ms, i), 2, DV), MUL)
                        v.drain()
                        nc.vector.tensor_tensor(o3, o3, spread(small(M, "ln_w"), 1, NH), MUL)
                        v.drain()
                        nc.vector.tensor_tensor(o3, o3, spread(small(M, "ln_b"), 1, NH), ADD).then_inc(on_ready[b], 1)
                    for b, i in lanes:
                        v.wait_ge(y_ready[b], 1)
                        v.sem_inc(y_ready[b], -1)
                        nc.vector.tensor_tensor(tile(M.h, i), tile(M.h, i), M.bank[Dk[b]][0:P, 0:D], ADD)
                    v.drain()

                tiles_by_lanes(nc, ET.DVE, scores)
                nc.vector.tensor_scalar(ms[:, :, :], ms[:, :, :], 1.0 / DV, 1e-8, MUL, ADD).then_inc(ms_ready, 1)
                v.wait_ge(root_ready, 1)
                v.sem_inc(root_ready, -1)
                nc.vector.reciprocal(ms[:, :, :], root[:, :, :])
                v.drain()
                tiles_by_lanes(nc, ET.DVE, project)

            @block.scalar
            def _(a):
                act_ln_std(nc, a, M, var_ready, std_ready)
                a.preload_act_table(ACT.Exp)
                a.wait_ge(lam_dot, 1)
                a.sem_inc(lam_dot, -1)
                nc.scalar.activation(lam2[:, :], lam2[:, :], ACT.Exp).then_inc(lam_exp, 1)
                a.wait_ge(pblank, LANES)
                a.sem_inc(pblank, -LANES)

                def scores(lanes):
                    for b, i in lanes:
                        a.wait_ge(turned_ready[b], 1)
                        a.sem_inc(turned_ready[b], -1)
                        nc.scalar.copy(xT[b][:, :, :], turned(M, A[b])).then_inc(xT_ready[b], 1)
                        repeat_x(nc, M, A[b], xr[b]).then_inc(xr_ready[b], 1)
                    for b, i in lanes:
                        a.wait_ge(k_turned[b], 1)
                        a.sem_inc(k_turned[b], -1)
                        nc.scalar.copy(kT[b][:, :, :], turned(M, C[b])).then_inc(kT_ready[b], 1)
                    for b, i in lanes:
                        a.wait_ge(shifted[b], 1)
                        a.sem_inc(shifted[b], -1)
                        nc.scalar.activation(Pr[b][:, :, :], S[b][:, :, :], ACT.Exp).then_inc(probs_ready[b], 1)
                    for b, i in lanes:
                        a.wait_ge(pT_ready[b], 1)
                        a.sem_inc(pT_ready[b], -1)
                        evacuate_probs(nc, M, (Dk[b], A[b]), pm[b], NH).then_inc(pm_ready[b], 1)
                    a.drain()

                def project(lanes):
                    for b, i in lanes:
                        a.wait_ge(oT_turned[b], 1)
                        a.sem_inc(oT_turned[b], -1)
                        nc.scalar.copy(oT[b][:, :, :], turned(M, C[b])).then_inc(oT_ready[b], 1)
                    a.drain()

                tiles_by_lanes(nc, ET.Activation, scores)
                a.wait_ge(ms_ready, 1)
                a.sem_inc(ms_ready, -1)
                nc.scalar.activation(root[:, :, :], ms[:, :, :], ACT.Sqrt).then_inc(root_ready, 1)
                tiles_by_lanes(nc, ET.Activation, project)

            @block.tensor
            def _(pe):
                def scores(lanes):
                    for b, i in lanes:
                        pe.wait_ge(xn_ready[b], 1)
                        pe.sem_inc(xn_ready[b], -1)
                        pe_turn(nc, M, A[b], xn[b]).then_inc(turned_ready[b], 1)
                    for b, i in lanes:
                        pe.wait_ge(xT_ready[b], 1)
                        pe.sem_inc(xT_ready[b], -1)
                        pe_project(nc, M, B[b], xT[b], wqk, 0, 2 * D).then_inc(q_ready[b], 1)
                    for b, i in lanes:
                        pe.wait_ge(xr_ready[b], 1)
                        pe.sem_inc(xr_ready[b], -1)
                        pe_values_in(nc, M, (Dk[b], A[b]), xr[b], wv, 0).then_inc(v_ready[b], 1)
                    for b, i in lanes:
                        pe.wait_ge(qk_rotated[b], 1)
                        pe.sem_inc(qk_rotated[b], -1)
                        pe_turn(nc, M, B[b], qk[b]).then_inc(q_turned[b], 1)
                        pe_turn(nc, M, C[b], qk[b][:, D:2 * D]).then_inc(k_turned[b], 1)
                    for b, i in lanes:
                        pe.wait_ge(km_ready[b], 1)
                        pe.sem_inc(km_ready[b], -1)
                        pe_scores(nc, M, (B[b], C[b]), qm[b], km[b]).then_inc(s_ready[b], 1)
                    for b, i in lanes:
                        pe.wait_ge(mixed[b], 1)
                        pe.sem_inc(mixed[b], -1)
                        pe.wait_ge(vm_ready[b], 1)
                        pe.sem_inc(vm_ready[b], -1)
                        pe_turn_probs(nc, M, (Dk[b], A[b]), probs[b][:, :, :].rearrange("p h j -> p (h j)"), NH
                                      ).then_inc(pT_ready[b], 1)
                    for b, i in lanes:
                        pe.wait_ge(pm_ready[b], 1)
                        pe.sem_inc(pm_ready[b], -1)
                        pe_values(nc, M, B[b], pm[b], vm[b], NH, DV).then_inc(o_ready[b], 1)

                def project(lanes):
                    for b, i in lanes:
                        pe.wait_ge(on_ready[b], 1)
                        pe.sem_inc(on_ready[b], -1)
                        pe_turn(nc, M, C[b], o[b]).then_inc(oT_turned[b], 1)
                    for b, i in lanes:
                        pe.wait_ge(oT_ready[b], 1)
                        pe.sem_inc(oT_ready[b], -1)
                        pe_project(nc, M, Dk[b], oT[b], wo, 0, D).then_inc(y_ready[b], 1)

                pe.wait_ge(M.loaded["l1a"], 16)
                tiles_by_lanes(nc, ET.PE, scores)
                tiles_by_lanes(nc, ET.PE, project)


def coupling(nc, M):
    CYCLES = 3
    NS = T * SEQS
    with ExitStack() as ctx:
        sb = lambda n, s: ctx.enter_context(nc.sbuf_tensor("cp_" + n, s, F32))
        sem = lambda n: M.sem(n + "0")
        xn = sb("xn", [P, D])
        var_ready, std_ready, xn_ready = sem("var_ready"), sem("std_ready"), sem("xn_ready")
        turned_ready, turned_read = sem("turned"), sem("turned_read")
        mean, g1, g2, gf = sb("mean", [128, 2, NS]), sb("g1", [128, NS]), sb("g2", [64, NS]), sb("gf", [128, NS])
        h1, h2, h3 = sb("h1", [128, 2, G, GC]), sb("h2", [128, G, GC]), sb("h3", [64, G, GC])
        tf, m0 = sb("tf", [128, G, GC]), sb("m0", [128, 2, GC])
        r2, r2s, base = sb("r2", [128, 1]), sb("r2s", [128, 1]), sb("base", [128, 1])
        mean_ready, ps_ready, act_done = sem("mean_ready"), sem("ps_ready"), sem("act_done")
        gf_ready, tf_ready, x_moved = sem("gf_ready"), sem("tf_ready"), sem("x_moved")
        cn1, cn2 = (M.w[n].rearrange("p (k n) -> p k n", k=2) for n in ("cn1", "cn2"))
        gc1 = M.w["gc1"].rearrange("p (k n) -> p k n", k=2)
        cn3, cn4, gc2, gc3 = M.w["cn3"], M.w["cn4"][0:64, :], M.w["gc2"], M.w["gc3"][0:64, :]
        with nc.Block(name="coupling_norm") as block:
            @block.vector
            def _(v):
                dve_ln_stats(nc, v, M, var_ready, std_ready)
                with nc.Fori(0, T, engines=(ET.DVE,)) as i:
                    ln_apply(nc, M, i, xn[:, :]).then_inc(xn_ready, 1)
                    v.wait_ge(turned_ready, 1)
                    v.sem_inc(turned_ready, -1)
                    nc.vector.tensor_copy(cols(M.xT, i), turned(M, 0)).then_inc(turned_read, 1)
                    v.drain()

            @block.scalar
            def _(a):
                act_ln_std(nc, a, M, var_ready, std_ready)

            @block.tensor
            def _(pe):
                pe_turn_tiles(nc, pe, M, xn, xn_ready, turned_ready, turned_read)

        with nc.Block(name="coupling_cycles") as block:
            @block.vector
            def _(v):
                nc.vector.tensor_reduce(mean[:, :, :], M.xT[:, :, :].rearrange("p k (s j) -> p k s j", j=L), AX.X, ADD)
                v.drain()
                nc.vector.tensor_scalar(mean[:, :, :], mean[:, :, :], 1.0 / L, None, MUL).then_inc(mean_ready, 1)
                nc.vector.tensor_scalar(r2[:, :], small(M, "range", 128), 2.0, None, MUL)
                nc.vector.tensor_scalar(base[:, :], small(M, "sgn", 128), 0.1, None, MUL)
                v.drain()
                nc.vector.tensor_tensor(r2s[:, :], r2[:, :], small(M, "sgn", 128), MUL)
                v.wait_ge(gf_ready, 1)
                v.sem_inc(gf_ready, -1)
                nc.vector.tensor_scalar(gf[:, :], gf[:, :], 0.7, -0.5, MUL, ADD)
                v.drain()
                with nc.Fori(0, CYCLES, engines=(ET.DVE,)) as cycle:
                    for g in range(G):
                        v.wait_ge(tf_ready, 1)
                        v.sem_inc(tf_ready, -1)
                        t = tf[:, g, :]
                        nc.vector.scalar_tensor_tensor(t.rearrange("p (s j) -> p s j", j=L),
                                                       t.rearrange("p (s j) -> p s j", j=L), 0.3,
                                                       spread(gf[:, g * GS:(g + 1) * GS], 2, L), MUL, ADD)
                        v.drain()
                        nc.vector.tensor_scalar(t, t, r2s[:, 0:1], base[:, 0:1], MUL, ADD)
                        v.drain()
                        x = M.xT[:, :, g * GC:(g + 1) * GC]
                        for c in range(2):
                            nc.vector.tensor_tensor(m0[:, c, :], x[:, 1 - c, :], t, MUL)
                        v.drain()
                        nc.vector.tensor_tensor(x[:, 0, :], x[:, 0, :], m0[:, 0, :], ADD)
                        nc.vector.tensor_tensor(x[:, 1, :], x[:, 1, :], m0[:, 1, :], SUB).then_inc(x_moved, 1)
                        v.drain()
                nc.vector.tensor_copy(M.yT[:, :, :], M.xT[:, :, :])
                v.drain()

            @block.scalar
            def _(a):
                a.preload_act_table(ACT.Gelu)

                def net(out, bank, parts, n, bias, func, done):
                    a.wait_ge(ps_ready, 1)
                    a.sem_inc(ps_ready, -1)
                    nc.scalar.activation(out, M.bank[bank][0:parts, 0:n], func, bias=bias).then_inc(done, 1)

                net(g1[:, :], 0, 128, NS, small(M, "gc_b1", 128), ACT.Gelu, act_done)
                net(g2[:, :], 1, 64, NS, small(M, "gc_b2", 64), ACT.Gelu, act_done)
                net(gf[:, :], 6, 128, NS, small(M, "gc_b3", 128), ACT.Sigmoid, gf_ready)
                a.drain()
                with nc.Fori(0, CYCLES, engines=(ET.Activation,)) as cycle:
                    for g in range(G):
                        for m in range(2):
                            net(h1[:, m, g, :], 2 * g + m, 128, GC, small(M, "cn_b1", 128)[:, m:m + 1], ACT.Gelu, act_done)
                    for g in range(G):
                        net(h2[:, g, :], g, 128, GC, small(M, "cn_b2", 128), ACT.Gelu, act_done)
                    for g in range(G):
                        net(h3[:, g, :], 3 + g, 64, GC, small(M, "cn_b3", 64), ACT.Gelu, act_done)
                    for g in range(G):
                        net(tf[:, g, :], g, 128, GC, small(M, "cn_b4", 128), ACT.Sigmoid, tf_ready)
                    a.drain()

            @block.tensor
            def _(pe):
                pe.wait_ge(M.loaded["l1f"], 16)
                pe.wait_ge(mean_ready, 1)
                pe.sem_inc(mean_ready, -1)
                for k in range(2):
                    last = nc.tensor.matmul(M.bank[0][:, 0:NS], gc1[:, k, :], mean[:, k, :], start=(k == 0), stop=(k == 1))
                last.then_inc(ps_ready, 1)
                pe.wait_ge(act_done, 1)
                pe.sem_inc(act_done, -1)
                nc.tensor.matmul(M.bank[1][0:64, 0:NS], gc2, g1[:, :], start=True, stop=True).then_inc(ps_ready, 1)
                pe.wait_ge(act_done, 1)
                pe.sem_inc(act_done, -1)
                nc.tensor.matmul(M.bank[6][:, 0:NS], gc3, g2[:, :], start=True, stop=True).then_inc(ps_ready, 1)
                with nc.Fori(0, CYCLES, engines=(ET.PE,)) as cycle:
                    for g in range(G):
                        for m in range(2):
                            for k in range(2):
                                last = nc.tensor.matmul(M.bank[2 * g + m][:, 0:GC], cn1[:, k, m * 128:(m + 1) * 128],
                                                        M.xT[:, k, g * GC:(g + 1) * GC], start=(k == 0), stop=(k == 1))
                            last.then_inc(ps_ready, 1)
                    for g in range(G):
                        pe.wait_ge(act_done, 2)
                        pe.sem_inc(act_done, -2)
                    for g in range(G):
                        for k in range(2):
                            last = nc.tensor.matmul(M.bank[g][:, 0:GC], cn2[:, k, :], h1[:, k, g, :], start=(k == 0), stop=(k == 1))
                        last.then_inc(ps_ready, 1)
                    for g in range(G):
                        pe.wait_ge(act_done, 1)
                        pe.sem_inc(act_done, -1)
                        nc.tensor.matmul(M.bank[3 + g][0:64, 0:GC], cn3, h2[:, g, :], start=True, stop=True).then_inc(ps_ready, 1)
                    for g in range(G):
                        pe.wait_ge(act_done, 1)
                        pe.sem_inc(act_done, -1)
                        nc.tensor.matmul(M.bank[g][:, 0:GC], cn4, h3[:, g, :], start=True, stop=True).then_inc(ps_ready, 1)
                    pe.wait_ge(x_moved, G)
                    pe.sem_inc(x_moved, -G)
    add_back(nc, M, "_l1")


def linear_attention(nc, M):
    with ExitStack() as ctx:
        sb = lambda n, s: [ctx.enter_context(nc.sbuf_tensor(f"a2_{n}{b}", s, F32)) for b in range(LANES)]
        sem = lambda n: [M.sem(f"{n}{b}") for b in range(LANES)]
        xn, xT, qT = sb("xn", [P, D]), sb("xT", [128, 2, P]), sb("qT", [128, 2, P])
        qkv, sq, ss = sb("qkv", [P, 3 * D]), sb("sq", [P, 2 * D]), sb("ss", [P, 2 * H16])
        root, vb, kv = sb("root", [P, 2 * H16]), sb("vb", [P, SEQS, D]), sb("kv", [128, 2, SEQS, 128])
        oT, y = sb("oT", [128, 2, P]), sb("y", [P, D])
        var_ready, std_ready = M.sem("var_ready0"), M.sem("std_ready0")
        xn_ready, turned_ready, xT_ready, qkv_ready = sem("xn_ready"), sem("turned"), sem("xT_ready"), sem("q_ready")
        ss_ready, root_ready, qkn_ready, qT_turned = sem("k_ready"), sem("kroot_ready"), sem("kn_ready"), sem("q_turned")
        qT_ready, kv_ready, kvm_ready, oT_made = sem("kT_ready"), sem("kv_ready"), sem("km_ready"), sem("oT_turned")
        oT_copied, y_ready = sem("oT_ready"), sem("y_ready")
        w = M.w["qkv2"].rearrange("p (k n) -> p k n", k=2)
        wo = M.w["proj2"].rearrange("p (k n) -> p k n", k=2)
        A, B, C, Dk = ([4 * b + j for b in range(LANES)] for j in range(4))
        with nc.Block(name="linear_attention") as block:
            @block.vector
            def _(v):
                dve_ln_stats(nc, v, M, var_ready, std_ready)

                def body(lanes):
                    for b, i in lanes:
                        ln_apply(nc, M, i, xn[b][:, :]).then_inc(xn_ready[b], 1)
                    for b, i in lanes:
                        v.wait_ge(qkv_ready[b], 1)
                        v.sem_inc(qkv_ready[b], -1)
                        nc.vector.tensor_tensor(qkv[b][:, 0:2 * D], M.bank[B[b]][0:P, :], small(M, "qkv_b")[:, 0:2 * D], ADD)
                        nc.vector.tensor_tensor(qkv[b][:, 2 * D:3 * D], M.bank[C[b]][0:P, 0:D],
                                                small(M, "qkv_b")[:, 2 * D:3 * D], ADD)
                        v.drain()
                        nc.vector.tensor_tensor(sq[b][:, :], qkv[b][:, 0:2 * D], qkv[b][:, 0:2 * D], MUL)
                        v.drain()
                        nc.vector.tensor_reduce(ss[b][:, :], sq[b][:, :].rearrange("p (m d) -> p m d", d=DH), AX.X, ADD)
                        v.drain()
                        nc.vector.tensor_scalar(ss[b][:, :], ss[b][:, :], 1e-24, None, MAX).then_inc(ss_ready[b], 1)
                        nc.vector.tensor_tensor(vb[b][:, :, :], spread(qkv[b][:, 2 * D:3 * D], 1, SEQS),
                                                spread(small(M, "mb"), 2, D), MUL)
                    for b, i in lanes:
                        v.wait_ge(root_ready[b], 1)
                        v.sem_inc(root_ready[b], -1)
                        nc.vector.reciprocal(ss[b][:, :], root[b][:, :])
                        v.drain()
                        qk3 = qkv[b][:, 0:2 * D].rearrange("p (m d) -> p m d", d=DH)
                        nc.vector.tensor_tensor(qk3, qk3, spread(ss[b][:, :], 2, DH), MUL).then_inc(qkn_ready[b], 1)
                    for b, i in lanes:
                        v.wait_ge(kv_ready[b], 1)
                        v.sem_inc(kv_ready[b], -1)
                        for c, bank in enumerate((Dk[b], A[b])):
                            last = nc.vector.tensor_tensor(kv[b][:, c, :, :],
                                                           M.bank[bank][:, 0:SEQS * 128].rearrange("p (s n) -> p s n", s=SEQS),
                                                           spread(small(M, "blk", 128), 1, SEQS), MUL)
                        last.then_inc(kvm_ready[b], 1)
                    for b, i in lanes:
                        v.wait_ge(y_ready[b], 1)
                        v.sem_inc(y_ready[b], -1)
                        nc.vector.tensor_tensor(y[b][:, :], M.bank[Dk[b]][0:P, 0:D], small(M, "proj_b"), ADD)
                        v.drain()
                        nc.vector.tensor_tensor(tile(M.h, i), tile(M.h, i), y[b][:, :], ADD)
                    v.drain()

                tiles_by_lanes(nc, ET.DVE, body)

            @block.scalar
            def _(a):
                a.preload_act_table(ACT.Sqrt)
                act_ln_std(nc, a, M, var_ready, std_ready)

                def body(lanes):
                    for b, i in lanes:
                        a.wait_ge(turned_ready[b], 1)
                        a.sem_inc(turned_ready[b], -1)
                        nc.scalar.copy(xT[b][:, :, :], turned(M, A[b])).then_inc(xT_ready[b], 1)
                    for b, i in lanes:
                        a.wait_ge(ss_ready[b], 1)
                        a.sem_inc(ss_ready[b], -1)
                        nc.scalar.activation(root[b][:, :], ss[b][:, :], ACT.Sqrt).then_inc(root_ready[b], 1)
                    for b, i in lanes:
                        a.wait_ge(qT_turned[b], 1)
                        a.sem_inc(qT_turned[b], -1)
                        nc.scalar.copy(qT[b][:, :, :], turned(M, B[b])).then_inc(qT_ready[b], 1)
                    for b, i in lanes:
                        a.wait_ge(oT_made[b], 1)
                        a.sem_inc(oT_made[b], -1)
                        nc.scalar.copy(oT[b][:, :, :], turned(M, C[b])).then_inc(oT_copied[b], 1)
                    a.drain()

                tiles_by_lanes(nc, ET.Activation, body)

            @block.tensor
            def _(pe):
                def body(lanes):
                    for b, i in lanes:
                        pe.wait_ge(xn_ready[b], 1)
                        pe.sem_inc(xn_ready[b], -1)
                        pe_turn(nc, M, A[b], xn[b]).then_inc(turned_ready[b], 1)
                    for b, i in lanes:
                        pe.wait_ge(xT_ready[b], 1)
                        pe.sem_inc(xT_ready[b], -1)
                        pe_project(nc, M, B[b], xT[b], w, 0, 2 * D)
                        pe_project(nc, M, C[b], xT[b], w, 2 * D, 3 * D).then_inc(qkv_ready[b], 1)
                    for b, i in lanes:
                        pe.wait_ge(qkn_ready[b], 1)
                        pe.sem_inc(qkn_ready[b], -1)
                        pe_turn(nc, M, B[b], qkv[b][:, 0:D]).then_inc(qT_turned[b], 1)
                        for c, bank in enumerate((Dk[b], A[b])):
                            last = nc.tensor.matmul(M.bank[bank][:, 0:SEQS * 128], qkv[b][:, D + c * 128:D + (c + 1) * 128],
                                                    vb[b][:, :, c * 128:(c + 1) * 128], start=True, stop=True)
                        last.then_inc(kv_ready[b], 1)
                    for b, i in lanes:
                        pe.wait_ge(kvm_ready[b], 1)
                        pe.sem_inc(kvm_ready[b], -1)
                        pe.wait_ge(qT_ready[b], 1)
                        pe.sem_inc(qT_ready[b], -1)
                        for c in range(2):
                            for s in range(SEQS):
                                last = nc.tensor.matmul(M.bank[C[b]][:, c * P + s * L:c * P + (s + 1) * L], kv[b][:, c, s, :],
                                                        qT[b][:, c, s * L:(s + 1) * L], start=True, stop=True)
                        last.then_inc(oT_made[b], 1)
                    for b, i in lanes:
                        pe.wait_ge(oT_copied[b], 1)
                        pe.sem_inc(oT_copied[b], -1)
                        pe_project(nc, M, Dk[b], oT[b], wo, 0, D).then_inc(y_ready[b], 1)

                pe.wait_ge(M.loaded["l2a"], 16)
                tiles_by_lanes(nc, ET.PE, body)


def experts2(nc, M):
    with ExitStack() as ctx:
        sb = lambda n, s: ctx.enter_context(nc.sbuf_tensor("e2_" + n, s, F32))
        sem = lambda n: M.sem(n + "0")
        cw = sb("cw", [128, E2, NTOK])
        ga = [sb(f"ga_{b}", [128, GC]) for b in range(2)]
        gb = [sb(f"gb_{b}", [128, GC]) for b in range(2)]
        sg = [sb(f"sg_{b}", [128, GC]) for b in range(2)]
        hid = [sb(f"hid_{b}", [128, GC]) for b in range(2)]
        cw_loaded, ab_ready, a_scaled, sg_ready = sem("cw_loaded"), sem("ab_ready"), sem("a_scaled"), sem("sg_ready")
        ab_read, hid_ready, y_ready, y_read = sem("ab_read"), sem("hid_ready"), sem("y_ready"), sem("y_read")
        w1 = M.w["w1_2"].rearrange("p (e k n) -> p e k n", e=E2, k=2)
        w3 = M.w["w3_2"].rearrange("p (e k n) -> p e k n", e=E2, k=2)
        w2 = M.w["w2_2"].rearrange("p (e n) -> p e n", e=E2)
        xg = M.xT[:, :, :].rearrange("p k (g n) -> p k g n", g=G)
        yg = M.yT[:, :, :].rearrange("p k (g n) -> p k g n", g=G)
        with nc.Block(name="experts2") as block:
            @block.sync
            def _(sp):
                for e in range(E2):
                    sp.dma_start(cw[:, e, :], M.dram["cw2"][e, :].partition_broadcast(128)).then_inc(cw_loaded, 16)

            @block.tensor
            def _(pe):
                pe.wait_ge(M.loaded["l2f"], 16)
                with nc.Fori(0, G, engines=(ET.PE,)) as g:
                    x = xg[:, :, bass.ds(g, 1), :].rearrange("p k a n -> p k (a n)")

                    def up(e):
                        if e >= 2:
                            pe.wait_ge(ab_read, 1)
                            pe.sem_inc(ab_read, -1)
                        for j, w in enumerate((w1, w3)):
                            for k in range(2):
                                last = nc.tensor.matmul(M.bank[2 * (e % 2) + j][:, 0:GC], w[:, e, k, :], x[:, k, :],
                                                        start=(k == 0), stop=(k == 1))
                        last.then_inc(ab_ready, 1)

                    up(0)
                    for e in range(E2):
                        if e + 1 < E2:
                            up(e + 1)
                        pe.wait_ge(hid_ready, 1)
                        pe.sem_inc(hid_ready, -1)
                        for c in range(2):
                            last = nc.tensor.matmul(M.bank[4 + c][:, 0:GC], w2[:, e, c * 128:(c + 1) * 128], hid[e % 2][:, :],
                                                    start=(e == 0), stop=(e == E2 - 1))
                    last.then_inc(y_ready, 1)
                    pe.wait_ge(ab_read, 2)
                    pe.sem_inc(ab_read, -2)
                    pe.wait_ge(y_read, 1)
                    pe.sem_inc(y_read, -1)

            @block.scalar
            def _(a):
                a.preload_act_table(ACT.Sigmoid)
                with nc.Fori(0, G, engines=(ET.Activation,)) as g:
                    for e in range(E2):
                        a.wait_ge(a_scaled, 1)
                        a.sem_inc(a_scaled, -1)
                        nc.scalar.activation(sg[e % 2][:, :], ga[e % 2][:, :], ACT.Sigmoid).then_inc(sg_ready, 1)
                    a.drain()

            @block.vector
            def _(v):
                v.wait_ge(cw_loaded, 16 * E2)
                v.sem_inc(cw_loaded, -(16 * E2))
                with nc.Fori(0, G, engines=(ET.DVE,)) as g:
                    def scale(e):
                        b = e % 2
                        s = cw[:, e, bass.ds(g * GC, GC)]
                        v.wait_ge(ab_ready, 1)
                        v.sem_inc(ab_ready, -1)
                        nc.vector.tensor_tensor(ga[b][:, :], M.bank[2 * b][:, 0:GC], s, MUL).then_inc(a_scaled, 1)
                        nc.vector.tensor_tensor(gb[b][:, :], M.bank[2 * b + 1][:, 0:GC], s, MUL).then_inc(ab_read, 1)

                    scale(0)
                    for e in range(E2):
                        b = e % 2
                        v.drain()
                        if e + 1 < E2:
                            scale(e + 1)
                        nc.vector.tensor_tensor(gb[b][:, :], ga[b][:, :], gb[b][:, :], MUL)
                        v.wait_ge(sg_ready, 1)
                        v.sem_inc(sg_ready, -1)
                        v.drain()
                        nc.vector.tensor_tensor(hid[b][:, :], gb[b][:, :], sg[b][:, :], MUL).then_inc(hid_ready, 1)
                        if e + 1 < E2:
                            v.drain()
                    v.drain()
                    v.wait_ge(y_ready, 1)
                    v.sem_inc(y_ready, -1)
                    for c in range(2):
                        last = nc.vector.tensor_copy(yg[:, c, bass.ds(g, 1), :].rearrange("p a n -> p (a n)"), M.bank[4 + c][:, 0:GC])
                    last.then_inc(y_read, 1)
                    v.drain()
    add_back(nc, M, "_l2")


def delta_attention(nc, M):
    with ExitStack() as ctx:
        one = lambda n, s: ctx.enter_context(nc.sbuf_tensor("a3_" + n, s, F32))
        sb = lambda n, s: [one(f"{n}{b}", s) for b in range(LANES)]
        sem = lambda n: [M.sem(f"{n}{b}") for b in range(LANES)]
        ss, z, zw, beta = one("ss", [P, T]), one("z", [P, T]), one("zw", [P, D]), one("beta", [P, T])
        rr, root = one("rr", [P, T]), one("root", [P, T])
        alpha, keep, decay = one("alpha", [128, 2]), one("keep", [128, 2]), one("decay", [128, 2, P])
        xn, xT, qkT = sb("xn", [P, D]), sb("xT", [128, 2, P]), sb("qkT", [128, 4, P])
        qk, sq, k1, kroot = sb("qk", [P, 2 * D]), sb("sq", [P, D]), sb("k1", [P, 1]), sb("kroot", [P, 1])
        av, ema, bv = sb("av", [128, 2, P]), sb("ema", [128, 2, P]), sb("bv", [P, D])
        low, Cl, ClT = sb("C", [P, P]), sb("Cl", [P, LEVELS, P]), sb("ClT", [P, LEVELS, P])
        XY, CX, mt = sb("XY", [P, 2, P]), sb("CX", [P, 2, P]), sb("mt", [P, P])
        U, oT = sb("U", [P, D]), sb("oT", [128, 2, P])
        hid, sg = sb("hid", [128, 4, P]), sb("sg", [128, 4, P])
        var_ready, std_ready, w_folded = M.sem("var_ready0"), M.sem("std_ready0"), M.sem("w_folded")
        ss_ready, root_ready, z_ready = M.sem("ms_ready"), M.sem("root_ready"), M.sem("z_ready")
        beta_ready, ss2_ready, root2_ready = M.sem("beta_ready"), M.sem("ss2_ready"), M.sem("root2_ready")
        xn_ready, turned_ready, xT_ready, qk_ready = sem("xn_ready"), sem("turned"), sem("xT_ready"), sem("q_ready")
        v_ready, k_ready, kroot_ready, kn_ready = sem("v_ready"), sem("k_ready"), sem("kroot_ready"), sem("kn_ready")
        qk_turned, qkT_ready, ema_ready, bv_turned = sem("q_turned"), sem("kT_ready"), sem("xr_ready"), sem("k_turned")
        G_ready, C_ready, CT_ready, X_ready = sem("s_ready"), sem("shifted"), sem("pT_ready"), sem("probs_dve")
        CX_ready, CX_copied, XCX_ready = sem("vm_ready"), sem("pm_ready"), sem("probs_pe")
        U_ready, U_copied, oT_made, oT_copied = sem("o_ready"), sem("on_ready"), sem("oT_turned"), sem("oT_ready")
        y_ready, gu_ready, sg_ready, hid_ready = sem("y_ready"), sem("gu_ready"), sem("sg_ready"), sem("hid_ready")
        wqk = M.w["qk3"].rearrange("p (k n) -> p k n", k=2)
        wv = M.w["v3"].rearrange("p (k n) -> p k n", k=2)
        wo = M.w["o3"].rearrange("p (k n) -> p k n", k=2)
        wg = M.w["gate3"].rearrange("p (k n) -> p k n", k=2)
        wu = M.w["up3"].rearrange("p (k n) -> p k n", k=2)
        wd = M.w["down3"].rearrange("p (f n) -> p f n", f=4)
        ident = small(M, "ident")[:, 0:P]
        A, B, C, Dk = ([4 * b + j for b in range(LANES)] for j in range(4))
        both = lambda bank: M.bank[bank][0:P, 0:2 * P].rearrange("p (a n) -> p a n", a=2)
        with nc.Block(name="delta_attention") as block:
            @block.vector
            def _(v):
                v.wait_ge(M.loaded["l3a"], 16)
                for name, ws in (("norm1", (wqk, wv)), ("norm2", (wg, wu))):
                    for w in ws:
                        for k in range(2):
                            nc.vector.tensor_scalar(w[:, k, :], w[:, k, :], small(M, name, 128)[:, k:k + 1], None, MUL)
                nc.vector.tensor_tensor(zw[:, :], small(M, "beta_w"), small(M, "norm1_row"), MUL)
                v.drain().then_inc(w_folded, 1)
                dve_ln_stats(nc, v, M, var_ready, std_ready)

                def norm(lanes):
                    for b, i in lanes:
                        ln_apply(nc, M, i, tile(M.x, i))
                    v.drain()
                    for b, i in lanes:
                        nc.vector.tensor_tensor(sq[b][:, :], tile(M.x, i), tile(M.x, i), MUL)
                        nc.vector.tensor_tensor(xn[b][:, :], tile(M.x, i), zw[:, :], MUL)
                    v.drain()
                    for b, i in lanes:
                        nc.vector.tensor_reduce(ss[:, bass.ds(i, 1)], sq[b][:, :], AX.X, ADD)
                        nc.vector.tensor_reduce(z[:, bass.ds(i, 1)], xn[b][:, :], AX.X, ADD)
                    v.drain()

                def delta(lanes):
                    beta_of = lambda i: beta[:, bass.ds(i, 1)]
                    for b, i in lanes:
                        nc.vector.tensor_scalar(xn[b][:, :], tile(M.x, i), rr[:, bass.ds(i, 1)], None, MUL
                                                ).then_inc(xn_ready[b], 1)
                    for b, i in lanes:
                        v.wait_ge(qk_ready[b], 1)
                        v.sem_inc(qk_ready[b], -1)
                        nc.vector.tensor_copy(qk[b][:, :], M.bank[B[b]][0:P, :])
                        v.drain()
                        nc.vector.tensor_tensor(sq[b][:, :], qk[b][:, D:2 * D], qk[b][:, D:2 * D], MUL)
                        v.drain()
                        nc.vector.tensor_reduce(k1[b][:, :], sq[b][:, :], AX.X, ADD)
                        v.drain()
                        nc.vector.tensor_scalar(k1[b][:, :], k1[b][:, :], 1e-24, None, MAX).then_inc(k_ready[b], 1)
                    for b, i in lanes:
                        v.wait_ge(v_ready[b], 1)
                        v.sem_inc(v_ready[b], -1)
                        for c in range(2):
                            nc.vector.tensor_scalar(av[b][:, c, :], M.bank[C[b]][:, c * P:(c + 1) * P], alpha[:, c:c + 1],
                                                    None, MUL)
                        v.drain()
                        for c in range(2):
                            last = nc.vector.tensor_tensor_scan(ema[b][:, c, :], decay[:, c, :], av[b][:, c, :], 0.0, MUL, ADD)
                        last.then_inc(ema_ready[b], 1)
                        v.wait_ge(kroot_ready[b], 1)
                        v.sem_inc(kroot_ready[b], -1)
                        nc.vector.reciprocal(k1[b][:, :], kroot[b][:, :])
                        v.drain()
                        nc.vector.tensor_scalar(qk[b][:, D:2 * D], qk[b][:, D:2 * D], k1[b][:, 0:1], None, MUL
                                                ).then_inc(kn_ready[b], 1)
                    for b, i in lanes:
                        v.wait_ge(bv_turned[b], 1)
                        v.sem_inc(bv_turned[b], -1)
                        nc.vector.tensor_scalar(bv[b][:, :], M.bank[Dk[b]][0:P, 0:D], beta_of(i), None, MUL)
                        v.wait_ge(G_ready[b], 1)
                        v.sem_inc(G_ready[b], -1)
                        nc.vector.scalar_tensor_tensor(low[b][:, :], M.bank[B[b]][0:P, 0:P], beta_of(i),
                                                       small(M, "strict"), MUL, MUL).then_inc(C_ready[b], 1)
                        nc.vector.tensor_tensor(mt[b][:, :], M.bank[B[b]][0:P, 128:128 + P], small(M, "mtm"), MUL)
                        v.drain()
                        nc.vector.tensor_tensor(Cl[b][:, :, :], spread(low[b][:, :], 1, LEVELS),
                                                small(M, "lvl").rearrange("p (l n) -> p l n", l=LEVELS), MUL)
                    for b, i in lanes:
                        v.wait_ge(CT_ready[b], 1)
                        v.sem_inc(CT_ready[b], -1)
                        nc.vector.tensor_tensor(ClT[b][:, :, :], spread(M.bank[C[b]][0:P, 0:P], 1, LEVELS),
                                                small(M, "lvlT").rearrange("p (l n) -> p l n", l=LEVELS), MUL)
                        v.drain()
                        nc.vector.tensor_tensor(XY[b][:, 0, :], ident, Cl[b][:, 0, :], SUB)
                        nc.vector.tensor_tensor(XY[b][:, 1, :], ident, ClT[b][:, 0, :], SUB).then_inc(X_ready[b], 1)
                    for l in range(1, LEVELS):
                        for b, i in lanes:
                            v.wait_ge(XCX_ready[b], 1)
                            v.sem_inc(XCX_ready[b], -1)
                            nc.vector.tensor_tensor(XY[b][:, :, :], XY[b][:, :, :], both(A[b]), SUB).then_inc(X_ready[b], 1)
                    for b, i in lanes:
                        v.wait_ge(y_ready[b], 1)
                        v.sem_inc(y_ready[b], -1)
                        nc.vector.tensor_tensor(tile(M.x, i), tile(M.x, i), M.bank[Dk[b]][0:P, 0:D], ADD)
                    v.drain()
                    for b, i in lanes:
                        nc.vector.tensor_tensor(sq[b][:, :], tile(M.x, i), tile(M.x, i), MUL)
                    v.drain()
                    for b, i in lanes:
                        nc.vector.tensor_reduce(ss[:, bass.ds(i, 1)], sq[b][:, :], AX.X, ADD)
                    v.drain()

                def mlp(lanes):
                    for b, i in lanes:
                        nc.vector.tensor_scalar(xn[b][:, :], tile(M.x, i), rr[:, bass.ds(i, 1)], None, MUL
                                                ).then_inc(xn_ready[b], 1)
                    for b, i in lanes:
                        nc.vector.tensor_tensor(tile(M.h, i), tile(M.h, i), tile(M.x, i), ADD)
                    for b, i in lanes:
                        v.wait_ge(sg_ready[b], 1)
                        v.sem_inc(sg_ready[b], -1)
                        nc.vector.tensor_tensor(hid[b][:, :, :], sg[b][:, :, :], turned(M, B[b], 4), MUL)
                        v.drain()
                        nc.vector.tensor_tensor(hid[b][:, :, :], hid[b][:, :, :], turned(M, C[b], 4), MUL
                                                ).then_inc(hid_ready[b], 1)
                    for b, i in lanes:
                        v.wait_ge(y_ready[b], 1)
                        v.sem_inc(y_ready[b], -1)
                        nc.vector.tensor_tensor(tile(M.h, i), tile(M.h, i), M.bank[Dk[b]][0:P, 0:D], ADD)
                    v.drain()

                tiles_by_lanes(nc, ET.DVE, norm)
                nc.vector.tensor_scalar(ss[:, :], ss[:, :], 1.0 / D, 1e-6, MUL, ADD).then_inc(ss_ready, 1)
                v.wait_ge(root_ready, 1)
                v.sem_inc(root_ready, -1)
                nc.vector.reciprocal(rr[:, :], root[:, :])
                v.drain()
                nc.vector.tensor_tensor(z[:, :], z[:, :], rr[:, :], MUL).then_inc(z_ready, 1)
                v.wait_ge(beta_ready, 1)
                v.sem_inc(beta_ready, -1)
                nc.vector.tensor_scalar(keep[:, :], alpha[:, :], -1.0, 1.0, MUL, ADD)
                v.drain()
                for c in range(2):
                    nc.vector.tensor_scalar(decay[:, c, :], small(M, "run", 128), keep[:, c:c + 1], None, MUL)
                tiles_by_lanes(nc, ET.DVE, delta)
                nc.vector.tensor_scalar(ss[:, :], ss[:, :], 1.0 / D, 1e-6, MUL, ADD).then_inc(ss2_ready, 1)
                v.wait_ge(root2_ready, 1)
                v.sem_inc(root2_ready, -1)
                nc.vector.reciprocal(rr[:, :], root[:, :])
                v.drain()
                tiles_by_lanes(nc, ET.DVE, mlp)

            @block.scalar
            def _(a):
                act_ln_std(nc, a, M, var_ready, std_ready)
                a.wait_ge(ss_ready, 1)
                a.sem_inc(ss_ready, -1)
                nc.scalar.activation(root[:, :], ss[:, :], ACT.Sqrt).then_inc(root_ready, 1)
                nc.scalar.activation(alpha[:, :], small(M, "alpha", 128), ACT.Sigmoid)
                a.wait_ge(z_ready, 1)
                a.sem_inc(z_ready, -1)
                nc.scalar.activation(beta[:, :], z[:, :], ACT.Sigmoid, bias=small(M, "beta_b")).then_inc(beta_ready, 1)
                a.preload_act_table(ACT.Sqrt)

                def delta(lanes):
                    for b, i in lanes:
                        a.wait_ge(turned_ready[b], 1)
                        a.sem_inc(turned_ready[b], -1)
                        nc.scalar.copy(xT[b][:, :, :], turned(M, A[b])).then_inc(xT_ready[b], 1)
                    for b, i in lanes:
                        a.wait_ge(k_ready[b], 1)
                        a.sem_inc(k_ready[b], -1)
                        nc.scalar.activation(kroot[b][:, :], k1[b][:, :], ACT.Sqrt).then_inc(kroot_ready[b], 1)
                    for b, i in lanes:
                        a.wait_ge(qk_turned[b], 1)
                        a.sem_inc(qk_turned[b], -1)
                        nc.scalar.copy(qkT[b][:, :, :], turned(M, A[b], 4)).then_inc(qkT_ready[b], 1)
                    for l in range(1, LEVELS):
                        for b, i in lanes:
                            a.wait_ge(CX_ready[b], 1)
                            a.sem_inc(CX_ready[b], -1)
                            nc.scalar.copy(CX[b][:, :, :], both(Dk[b])).then_inc(CX_copied[b], 1)
                    for b, i in lanes:
                        a.wait_ge(U_ready[b], 1)
                        a.sem_inc(U_ready[b], -1)
                        nc.scalar.copy(U[b][:, :], M.bank[B[b]][0:P, 0:D]).then_inc(U_copied[b], 1)
                    for b, i in lanes:
                        a.wait_ge(oT_made[b], 1)
                        a.sem_inc(oT_made[b], -1)
                        nc.scalar.copy(oT[b][:, :, :], turned(M, C[b])).then_inc(oT_copied[b], 1)
                    a.drain()

                def mlp(lanes):
                    for b, i in lanes:
                        a.wait_ge(turned_ready[b], 1)
                        a.sem_inc(turned_ready[b], -1)
                        nc.scalar.copy(xT[b][:, :, :], turned(M, A[b])).then_inc(xT_ready[b], 1)
                    for b, i in lanes:
                        a.wait_ge(gu_ready[b], 1)
                        a.sem_inc(gu_ready[b], -1)
                        nc.scalar.activation(sg[b][:, :, :], turned(M, B[b], 4), ACT.Sigmoid).then_inc(sg_ready[b], 1)
                    a.drain()

                tiles_by_lanes(nc, ET.Activation, delta)
                a.wait_ge(ss2_ready, 1)
                a.sem_inc(ss2_ready, -1)
                nc.scalar.activation(root[:, :], ss[:, :], ACT.Sqrt).then_inc(root2_ready, 1)
                a.preload_act_table(ACT.Sigmoid)
                tiles_by_lanes(nc, ET.Activation, mlp)

            @block.tensor
            def _(pe):
                def delta(lanes):
                    for b, i in lanes:
                        pe.wait_ge(xn_ready[b], 1)
                        pe.sem_inc(xn_ready[b], -1)
                        pe_turn(nc, M, A[b], xn[b]).then_inc(turned_ready[b], 1)
                    for b, i in lanes:
                        pe.wait_ge(xT_ready[b], 1)
                        pe.sem_inc(xT_ready[b], -1)
                        pe_project(nc, M, B[b], xT[b], wqk, 0, 2 * D).then_inc(qk_ready[b], 1)
                        for c in range(2):
                            last = pe_project(nc, M, C[b], wv[:, :, c * 128:(c + 1) * 128], xT[b], 0, P, 128, col=c * P)
                        last.then_inc(v_ready[b], 1)
                    for b, i in lanes:
                        pe.wait_ge(ema_ready[b], 1)
                        pe.sem_inc(ema_ready[b], -1)
                        for c in range(2):
                            last = nc.tensor.transpose(M.bank[Dk[b]][0:P, c * 128:(c + 1) * 128], ema[b][:, c, :],
                                                       small(M, "ident", 128))
                        last.then_inc(bv_turned[b], 1)
                        pe.wait_ge(kn_ready[b], 1)
                        pe.sem_inc(kn_ready[b], -1)
                        pe_turn(nc, M, A[b], qk[b], 4).then_inc(qk_turned[b], 1)
                    for b, i in lanes:
                        pe.wait_ge(qkT_ready[b], 1)
                        pe.sem_inc(qkT_ready[b], -1)
                        for o, rhs in ((0, 2), (128, 0)):
                            for k in range(2):
                                last = nc.tensor.matmul(M.bank[B[b]][0:P, o:o + P], qkT[b][:, 2 + k, :],
                                                        qkT[b][:, rhs + k, :], start=(k == 0), stop=(k == 1))
                        last.then_inc(G_ready[b], 1)
                    for b, i in lanes:
                        pe.wait_ge(C_ready[b], 1)
                        pe.sem_inc(C_ready[b], -1)
                        nc.tensor.transpose(M.bank[C[b]][0:P, 0:P], low[b][:, :], ident).then_inc(CT_ready[b], 1)
                    for l in range(1, LEVELS):
                        for b, i in lanes:
                            pe.wait_ge(X_ready[b], 1)
                            pe.sem_inc(X_ready[b], -1)
                            nc.tensor.matmul(M.bank[Dk[b]][0:P, 0:P], ClT[b][:, l, :], XY[b][:, 0, :], start=True, stop=True)
                            nc.tensor.matmul(M.bank[Dk[b]][0:P, P:2 * P], Cl[b][:, l, :], XY[b][:, 1, :], start=True,
                                             stop=True).then_inc(CX_ready[b], 1)
                        for b, i in lanes:
                            pe.wait_ge(CX_copied[b], 1)
                            pe.sem_inc(CX_copied[b], -1)
                            nc.tensor.matmul(M.bank[A[b]][0:P, 0:P], XY[b][:, 1, :], CX[b][:, 0, :], start=True, stop=True)
                            nc.tensor.matmul(M.bank[A[b]][0:P, P:2 * P], XY[b][:, 0, :], CX[b][:, 1, :], start=True,
                                             stop=True).then_inc(XCX_ready[b], 1)
                    for b, i in lanes:
                        pe.wait_ge(X_ready[b], 1)
                        pe.sem_inc(X_ready[b], -1)
                        nc.tensor.matmul(M.bank[B[b]][0:P, 0:D], XY[b][:, 1, :], bv[b][:, :], start=True, stop=True
                                         ).then_inc(U_ready[b], 1)
                    for b, i in lanes:
                        pe.wait_ge(U_copied[b], 1)
                        pe.sem_inc(U_copied[b], -1)
                        for c in range(2):
                            last = nc.tensor.matmul(M.bank[C[b]][:, c * P:(c + 1) * P], U[b][:, c * 128:(c + 1) * 128],
                                                    mt[b][:, :], start=True, stop=True)
                        last.then_inc(oT_made[b], 1)
                    for b, i in lanes:
                        pe.wait_ge(oT_copied[b], 1)
                        pe.sem_inc(oT_copied[b], -1)
                        pe_project(nc, M, Dk[b], oT[b], wo, 0, D).then_inc(y_ready[b], 1)

                def mlp(lanes):
                    for b, i in lanes:
                        pe.wait_ge(xn_ready[b], 1)
                        pe.sem_inc(xn_ready[b], -1)
                        pe_turn(nc, M, A[b], xn[b]).then_inc(turned_ready[b], 1)
                    for b, i in lanes:
                        pe.wait_ge(xT_ready[b], 1)
                        pe.sem_inc(xT_ready[b], -1)
                        for bank, w in ((B[b], wg), (C[b], wu)):
                            for f in range(4):
                                last = pe_project(nc, M, bank, w[:, :, f * 128:(f + 1) * 128], xT[b], 0, P, 128, col=f * P)
                        last.then_inc(gu_ready[b], 1)
                    for b, i in lanes:
                        pe.wait_ge(hid_ready[b], 1)
                        pe.sem_inc(hid_ready[b], -1)
                        for f in range(4):
                            last = nc.tensor.matmul(M.bank[Dk[b]][0:P, 0:D], hid[b][:, f, :], wd[:, f, :], start=(f == 0),
                                                    stop=(f == 3))
                        last.then_inc(y_ready[b], 1)

                pe.wait_ge(w_folded, 1)
                pe.sem_inc(w_folded, -1)
                tiles_by_lanes(nc, ET.PE, delta)
                tiles_by_lanes(nc, ET.PE, mlp)


def route3(nc, M):
    with ExitStack() as ctx:
        sb = lambda n, s, dt=F32: ctx.enter_context(nc.sbuf_tensor("r3_" + n, s, dt))
        sem = lambda n: M.sem(n + "0")
        xn, xT = sb("xn", [P, D]), sb("xT", [128, 2, P])
        lg, ex, rep, mask, w = (sb(n, [P, E3]) for n in ("lg", "ex", "rep", "mask", "w"))
        seen, key, over = sb("seen", [P, E3]), sb("key", [P, E3]), sb("over", [P, E3])
        ones = sb("ones", [P, P])
        m8, k8, i8 = sb("m8", [P, 8]), sb("k8", [P, 8]), sb("i8", [P, 8])
        idx = sb("idx", [P, 8], I32)
        eq = sb("eq", [P, 8, E3])
        s1, r1 = sb("s1", [P, 1]), sb("r1", [P, 1])
        hid, sg = sb("hid", [FH, 2, P]), sb("sg", [FH, 2, P])
        var_ready, std_ready, xn_ready = sem("var_ready"), sem("std_ready"), sem("xn_ready")
        turned_ready, xT_ready, lg_ready = sem("turned"), sem("xT_ready"), sem("q_ready")
        shifted, ex_ready, mask_ready, pos_ready = sem("shifted"), sem("probs_dve"), sem("kn_ready"), sem("s_ready")
        idx_ready, scattered, rows_sent = sem("idx_ready"), sem("scattered"), sem("rows_sent")
        gu_ready, sg_ready, hid_ready, y_ready = sem("gu_ready"), sem("sg_ready"), sem("hid_ready"), sem("y_ready")
        xT_copied = sem("xT_copied")
        router = M.w["router"].rearrange("p (k n) -> p k n", k=2)
        wgu = M.w["ws_gu"].rearrange("p (k n) -> p k n", k=2)
        wd = M.w["ws_down"][0:FH, :].rearrange("p (f n) -> p f n", f=2)
        with nc.Block(name="route3") as block:
            @block.vector
            def _(v):
                nc.vector.memset(seen[:, :], 0.0)
                nc.vector.memset(ones[:, :], 1.0)
                v.wait_ge(M.slots_cleared, 16)
                dve_ln_stats(nc, v, M, var_ready, std_ready)
                with nc.Fori(0, T, engines=(ET.DVE,)) as i:
                    ln_apply(nc, M, i, xn[:, :]).then_inc(xn_ready, 1)
                    v.wait_ge(lg_ready, 1)
                    v.sem_inc(lg_ready, -1)
                    nc.vector.tensor_copy(lg[:, :], M.bank[1][0:P, 0:E3])
                    v.drain()
                    nc.vector.tensor_reduce(s1[:, :], lg[:, :], AX.X, MAX)
                    v.drain()
                    nc.vector.tensor_scalar(lg[:, :], lg[:, :], s1[:, 0:1], None, SUB).then_inc(shifted, 1)
                    v.wait_ge(ex_ready, 1)
                    v.sem_inc(ex_ready, -1)
                    nc.vector.tensor_reduce(s1[:, :], ex[:, :], AX.X, ADD)
                    v.drain()
                    nc.vector.reciprocal(r1[:, :], s1[:, :])
                    v.drain()
                    nc.vector.tensor_scalar(ex[:, :], ex[:, :], r1[:, 0:1], None, MUL)
                    v.drain()
                    nc.vector.max(m8[:, :], ex[:, :])
                    v.drain()
                    nc.vector.match_replace(rep[:, :], m8[:, :], ex[:, :], -1.0)
                    v.drain()
                    nc.vector.tensor_scalar(mask[:, :], rep[:, :], 0.0, None, ALU.is_lt).then_inc(mask_ready, 1)
                    v.drain()
                    nc.vector.tensor_tensor(w[:, :], ex[:, :], mask[:, :], MUL)
                    v.drain()
                    nc.vector.tensor_reduce(s1[:, :], w[:, :], AX.X, ADD)
                    v.drain()
                    nc.vector.reciprocal(r1[:, :], s1[:, :])
                    v.drain()
                    nc.vector.tensor_scalar(w[:, :], w[:, :], r1[:, 0:1], None, MUL)
                    v.wait_ge(pos_ready, 1)
                    v.sem_inc(pos_ready, -1)
                    nc.vector.tensor_scalar(over[:, :], M.bank[2][0:P, 0:E3], float(CAP), OVERFLOW, ALU.is_gt, MUL)
                    nc.vector.tensor_tensor(key[:, :], M.bank[2][0:P, 0:E3], small(M, "ebase"), ADD)
                    v.drain()
                    nc.vector.tensor_tensor(key[:, :], key[:, :], over[:, :], ADD)
                    nc.vector.tensor_tensor(seen[:, :], seen[:, :], mask[:, :], ADD)
                    v.drain()
                    nc.vector.tensor_tensor(key[:, :], key[:, :], mask[:, :], MUL)
                    v.drain()
                    nc.vector.max(k8[:, :], key[:, :])
                    v.drain()
                    nc.vector.tensor_tensor(eq[:, :, :], spread(key[:, :], 1, 8), spread(k8[:, :], 2, E3), ALU.is_equal)
                    v.drain()
                    nc.vector.tensor_tensor(eq[:, :, :], eq[:, :, :], spread(w[:, :], 1, 8), MUL)
                    nc.vector.tensor_scalar(m8[:, :], k8[:, :], float(SLOTS), None, ALU.is_le)
                    nc.vector.scalar_tensor_tensor(i8[:, :], k8[:, :], 1.0, small(M, "trash"), SUB, MIN)
                    v.drain()
                    nc.vector.tensor_copy(idx[:, :], i8[:, :]).then_inc(idx_ready, 1)
                    nc.vector.tensor_reduce(k8[:, :], eq[:, :, :], AX.X, ADD)
                    v.drain()
                    nc.vector.tensor_tensor(tile(M.w8, i), k8[:, :], m8[:, :], MUL)
                    nc.vector.tensor_scalar(i8[:, :], i8[:, :], float(SLOTS - 1), None, MIN)
                    v.drain()
                    nc.vector.tensor_copy(tile(M.idx8, i), i8[:, :])
                    v.wait_ge(rows_sent, 1)
                    v.sem_inc(rows_sent, -1)
                    v.drain()
                with nc.Fori(0, T, engines=(ET.DVE,)) as i:
                    v.wait_ge(sg_ready, 1)
                    v.sem_inc(sg_ready, -1)
                    guT = M.bank[3][0:FH, 0:4 * P].rearrange("p (f t) -> p f t", f=4)
                    nc.vector.tensor_tensor(hid[:, :, :], sg[:, :, :], guT[:, 0:2, :], MUL)
                    v.drain()
                    nc.vector.tensor_tensor(hid[:, :, :], hid[:, :, :], guT[:, 2:4, :], MUL).then_inc(hid_ready, 1)
                    v.wait_ge(y_ready, 1)
                    v.sem_inc(y_ready, -1)
                    nc.vector.tensor_tensor(tile(M.h, i), tile(M.h, i), M.bank[4][0:P, 0:D], ADD)
                    v.drain()

            @block.gpsimd
            def _(pool):
                with nc.Fori(0, T, engines=(ET.Pool,)) as i:
                    pool.wait_ge(idx_ready, 1)
                    pool.sem_inc(idx_ready, -1)
                    for k in range(K3):
                        nc.gpsimd.indirect_dma_start(
                            out=M.dram["slots_x"], out_offset=bass.IndirectOffsetOnAxis(ap=idx[:, k:k + 1], axis=0),
                            in_=xn[:, :], in_offset=None).then_inc(scattered, 16)
                    pool.wait_ge(scattered, i * (16 * K3) + 16 * K3)
                    pool.sem_inc(rows_sent, 1)

            @block.scalar
            def _(a):
                act_ln_std(nc, a, M, var_ready, std_ready)
                a.preload_act_table(ACT.Exp)
                with nc.Fori(0, T, engines=(ET.Activation,)) as i:
                    a.wait_ge(turned_ready, 1)
                    a.sem_inc(turned_ready, -1)
                    nc.scalar.copy(xT[:, :, :], turned(M, 0)).then_inc(xT_ready, 1)
                    nc.scalar.copy(cols(M.xT, i), turned(M, 0))
                    a.wait_ge(shifted, 1)
                    a.sem_inc(shifted, -1)
                    nc.scalar.activation(ex[:, :], lg[:, :], ACT.Exp).then_inc(ex_ready, 1)
                    a.drain()
                a.drain().then_inc(xT_copied, 1)
                a.preload_act_table(ACT.Sigmoid)
                with nc.Fori(0, T, engines=(ET.Activation,)) as i:
                    a.wait_ge(gu_ready, 1)
                    a.sem_inc(gu_ready, -1)
                    nc.scalar.activation(sg[:, :, :], M.bank[3][0:FH, 0:2 * P].rearrange("p (f t) -> p f t", f=2),
                                         ACT.Sigmoid).then_inc(sg_ready, 1)
                    a.drain()

            @block.tensor
            def _(pe):
                pe.wait_ge(M.loaded["l3f"], 16)
                with nc.Fori(0, T, engines=(ET.PE,)) as i:
                    pe.wait_ge(xn_ready, 1)
                    pe.sem_inc(xn_ready, -1)
                    pe_turn(nc, M, 0, xn).then_inc(turned_ready, 1)
                    pe.wait_ge(xT_ready, 1)
                    pe.sem_inc(xT_ready, -1)
                    pe_project(nc, M, 1, xT, router, 0, E3).then_inc(lg_ready, 1)
                    pe.wait_ge(mask_ready, 1)
                    pe.sem_inc(mask_ready, -1)
                    nc.tensor.matmul(M.bank[2][0:P, 0:E3], ones[:, :], seen[:, :], start=True, stop=False)
                    nc.tensor.matmul(M.bank[2][0:P, 0:E3], small(M, "tri"), mask[:, :], start=False, stop=True
                                     ).then_inc(pos_ready, 1)
                pe.wait_ge(xT_copied, 1)
                pe.sem_inc(xT_copied, -1)
                with nc.Fori(0, T, engines=(ET.PE,)) as i:
                    x = cols(M.xT, i)
                    for f in range(4):
                        for k in range(2):
                            last = nc.tensor.matmul(M.bank[3][0:FH, f * P:(f + 1) * P], wgu[:, k, f * FH:(f + 1) * FH],
                                                    x[:, k, :], start=(k == 0), stop=(k == 1))
                    last.then_inc(gu_ready, 1)
                    pe.wait_ge(hid_ready, 1)
                    pe.sem_inc(hid_ready, -1)
                    for f in range(2):
                        last = nc.tensor.matmul(M.bank[4][0:P, 0:D], hid[:, f, :], wd[:, f, :], start=(f == 0), stop=(f == 1))
                    last.then_inc(y_ready, 1)


def experts3(nc, M):
    with ExitStack() as ctx:
        sb = lambda n, s: ctx.enter_context(nc.sbuf_tensor("e3_" + n, s, F32))
        sem = lambda n: M.sem(n + "0")
        NB = 4
        wgu = [sb(f"wgu{b}", [128, 2, 2 * F3]) for b in range(NB)]
        wd = [sb(f"wd{b}", [FH, 2, D]) for b in range(NB)]
        xe = [sb(f"xe{b}", [CAP, D]) for b in range(NB)]
        xT = [sb(f"xT{b}", [128, 2, CAP]) for b in range(2)]
        sg = [sb(f"sg{b}", [FH, 2, CAP]) for b in range(2)]
        hid = [sb(f"hid{b}", [FH, 2, CAP]) for b in range(2)]
        ye = [sb(f"ye{b}", [CAP, D]) for b in range(NB)]
        loaded, stored = [sem(f"loaded{b}") for b in range(NB)], [sem(f"stored{b}") for b in range(NB)]
        used = sem("e3_used")
        turned_ready, xT_ready, gu_ready, sg_ready = sem("turned"), sem("xT_ready"), sem("gu_ready"), sem("sg_ready")
        hid_ready, y_ready = sem("hid_ready"), sem("y_ready")
        with nc.Block(name="experts3") as block:
            @block.sync
            def _(sp):
                with nc.Fori(0, E3 // NB, engines=(ET.SP,)) as p:
                    for b in range(NB):
                        e = p * NB + b
                        sp.wait_ge(used, 1)
                        sp.sem_inc(used, -1)
                        sp.dma_start(xe[b][:, :], M.dram["slots_x"][bass.ds(e * CAP, CAP), :]).then_inc(loaded[b], 16)
                        sp.dma_start(wgu[b][:, :, :].rearrange("p k n -> p (k n)"),
                                     M.dram["gu_3"][bass.ds(e, 1)].rearrange("a p n -> (a p) n")).then_inc(loaded[b], 16)
                        sp.dma_start(wd[b][:, :, :].rearrange("p k n -> p (k n)"),
                                     M.dram["down_3"][bass.ds(e, 1)].rearrange("a p n -> (a p) n")).then_inc(loaded[b], 16)

            @block.tensor
            def _(pe):
                pe.sem_inc(used, NB)

                def turn(b):
                    pe.wait_ge(loaded[b], 48)
                    pe.sem_inc(loaded[b], -48)
                    for k in range(2):
                        last = nc.tensor.transpose(M.bank[b % 2][:, k * CAP:(k + 1) * CAP], xe[b][:, k * 128:(k + 1) * 128],
                                                   small(M, "ident", 128))
                    last.then_inc(turned_ready, 1)

                def up(b):
                    pe.wait_ge(xT_ready, 1)
                    pe.sem_inc(xT_ready, -1)
                    for f in range(4):
                        for k in range(2):
                            last = nc.tensor.matmul(M.bank[2 + b % 2][0:FH, f * CAP:(f + 1) * CAP],
                                                    wgu[b][:, k, f * FH:(f + 1) * FH], xT[b % 2][:, k, :],
                                                    start=(k == 0), stop=(k == 1))
                    last.then_inc(gu_ready, 1)

                def down(b):
                    pe.wait_ge(hid_ready, 1)
                    pe.sem_inc(hid_ready, -1)
                    for f in range(2):
                        last = nc.tensor.matmul(M.bank[4 + b % 2][:, 0:D], hid[b % 2][:, f, :], wd[b][:, f, :],
                                                start=(f == 0), stop=(f == 1))
                    last.then_inc(y_ready, 1)

                with nc.Fori(0, E3 // NB, engines=(ET.PE,)) as p:
                    turn(0)
                    up(0)
                    for b in range(NB):
                        if b + 1 < NB:
                            turn(b + 1)
                            up(b + 1)
                        down(b)
                        pe.drain().then_inc(used, 1)

            @block.scalar
            def _(a):
                a.preload_act_table(ACT.Sigmoid)

                def sig(b):
                    a.wait_ge(turned_ready, 1)
                    a.sem_inc(turned_ready, -1)
                    nc.scalar.copy(xT[b % 2][:, :, :], M.bank[b % 2][:, 0:2 * CAP].rearrange("p (k n) -> p k n", k=2)
                                   ).then_inc(xT_ready, 1)
                    a.wait_ge(gu_ready, 1)
                    a.sem_inc(gu_ready, -1)
                    nc.scalar.activation(sg[b % 2][:, :, :], M.bank[2 + b % 2][0:FH, 0:2 * CAP].rearrange("p (f n) -> p f n", f=2),
                                         ACT.Sigmoid).then_inc(sg_ready, 1)

                for b in range(NB):
                    a.sem_inc(stored[b], 16)
                with nc.Fori(0, E3 // NB, engines=(ET.Activation,)) as p:
                    sig(0)
                    for b in range(NB):
                        if b + 1 < NB:
                            sig(b + 1)
                        a.wait_ge(y_ready, 1)
                        a.sem_inc(y_ready, -1)
                        a.wait_ge(stored[b], 16)
                        a.sem_inc(stored[b], -16)
                        nc.scalar.copy(ye[b][:, :], M.bank[4 + b % 2][:, 0:D])
                        a.drain()
                        a.dma_start(M.dram["slots_y"][bass.ds((p * NB + b) * CAP, CAP), :], ye[b][:, :]).then_inc(stored[b], 16)
                for b in range(NB):
                    a.wait_ge(stored[b], 16)
                    a.sem_inc(stored[b], -16)

            @block.vector
            def _(v):
                with nc.Fori(0, E3 // NB, engines=(ET.DVE,)) as p:
                    for b in range(NB):
                        v.wait_ge(sg_ready, 1)
                        v.sem_inc(sg_ready, -1)
                        gu = M.bank[2 + b % 2][0:FH, :].rearrange("p (f n) -> p f n", f=4)
                        nc.vector.tensor_tensor(hid[b % 2][:, :, :], sg[b % 2][:, :, :], gu[:, 0:2, :], MUL)
                        v.drain()
                        nc.vector.tensor_tensor(hid[b % 2][:, :, :], hid[b % 2][:, :, :], gu[:, 2:4, :], MUL).then_inc(hid_ready, 1)
                        v.drain()


def combine3(nc, M):
    with ExitStack() as ctx:
        sb = lambda n, s, dt=F32: ctx.enter_context(nc.sbuf_tensor("c3_" + n, s, dt))
        sem = lambda n: M.sem(n + "0")
        rows = sb("rows", [P, K3, D])
        idx = sb("idx", [P, 8], I32)
        idx_ready, gathered, stored, rows_here = sem("idx_ready"), sem("gathered"), sem("c3_stored"), sem("rows_here")
        h_ready = sem("h_ready")
        with nc.Block(name="combine3") as block:
            @block.vector
            def _(v):
                with nc.Fori(0, T, engines=(ET.DVE,)) as i:
                    nc.vector.tensor_copy(idx[:, :], tile(M.idx8, i)).then_inc(idx_ready, 1)
                    v.wait_ge(rows_here, 1)
                    v.sem_inc(rows_here, -1)
                    h = tile(M.h, i)
                    for k in range(K3):
                        last = nc.vector.scalar_tensor_tensor(h, rows[:, k, :], M.w8[:, bass.ds(i, 1), k:k + 1].rearrange("p a n -> p (a n)"),
                                                              h, MUL, ADD)
                        v.drain()
                    v.drain().then_inc(h_ready, 1)

            @block.gpsimd
            def _(pool):
                with nc.Fori(0, T, engines=(ET.Pool,)) as i:
                    pool.wait_ge(idx_ready, 1)
                    pool.sem_inc(idx_ready, -1)
                    for k in range(K3):
                        nc.gpsimd.indirect_dma_start(
                            out=rows[:, k, :], out_offset=None, in_=M.dram["slots_y"],
                            in_offset=bass.IndirectOffsetOnAxis(ap=idx[:, k:k + 1], axis=0)).then_inc(gathered, 16)
                    pool.wait_ge(gathered, i * (16 * K3) + 16 * K3)
                    pool.sem_inc(rows_here, 1)

            @block.sync
            def _(sp):
                with nc.Fori(0, T, engines=(ET.SP,)) as i:
                    sp.wait_ge(h_ready, 1)
                    sp.sem_inc(h_ready, -1)
                    sp.dma_start(M.dram["out"][bass.ds(i, 1)].rearrange("a p d -> (a p) d"), tile(M.h, i)).then_inc(stored, 16)
                sp.wait_ge(stored, 16 * T)


def vit_tower(nc, dram):
    with ExitStack() as ctx:
        M = setup_memory(nc, ctx, dram)
        load_everything(nc, M)
        patch_embedding(nc, M)
        alibi_attention(nc, M)
        gate_top2(nc, M, "g0_", M.w["gate0"], dram["cw0"], False)
        experts0(nc, M)
        add_back(nc, M, "_l0")
        rotary_attention(nc, M)
        coupling(nc, M)
        place_weights(nc, ctx, M, LATE)
        load_late(nc, M)
        linear_attention(nc, M)
        gate_top2(nc, M, "g2_", M.w["gate2"], dram["cw2"], True)
        experts2(nc, M)
        delta_attention(nc, M)
        route3(nc, M)
        experts3(nc, M)
        combine3(nc, M)


def chunks(w, parts=128):
    w = np.ascontiguousarray(w)
    return w.reshape((-1, parts) + w.shape[1:]).swapaxes(0, 1)


def flat(w, parts=128):
    w = w.reshape(w.shape[0], -1)
    out = np.zeros((128, w.shape[1]), np.float32)
    out[:w.shape[0]] = w
    return out


def constants():
    f = np.float32
    c = {}
    p = np.arange(128)
    c["ident"] = np.eye(128, dtype=f)
    c["mask8"] = (p[:, None] // DH == np.arange(8)).astype(f)
    r = np.arange(P)
    seq, pos = r // L, r % L
    c["vm16"] = (seq[:, None] == np.arange(16) % 3).astype(f)
    c["vm8"] = (seq[:, None] == np.arange(8) % 3).astype(f)
    start = 2 ** (-2 ** (-(math.log2(H16) - 3)))
    slopes = np.array([start * start ** m for m in range(H16)], f)
    rel = (np.arange(L)[None, :] - pos[:, None]).astype(f)
    bias = slopes[None, :, None] * rel[:, None, :]
    c["alibi"] = np.where(rel[:, None, :] <= 0, bias, f(NEG))
    c["mb"] = (seq[:, None] == np.arange(SEQS)).astype(f)
    inv = (f(1.0) / f(10000.0) ** (np.arange(0, DH, 2, dtype=f) / f(DH))).astype(f)
    ang = np.repeat(pos.astype(f)[:, None] * inv[None, :], 2, axis=-1).astype(f)
    c["cos"] = np.cos(ang).astype(f)
    c["sin"] = (np.sin(ang) * np.where(np.arange(DH) % 2 == 0, -1.0, 1.0)).astype(f)
    c["blk"] = (p[:, None] // DH == p[None, :] // DH).astype(f)
    c["tri"] = (r[:, None] <= r[None, :]).astype(f)
    same = seq[:, None] == seq[None, :]
    c["strict"] = (same & (r[None, :] < r[:, None])).astype(f)
    lvl = np.stack([same & (pos[:, None] >> (l + 1) == pos[None, :] >> (l + 1)) & ((pos[:, None] >> l) % 2 == 1)
                    & ((pos[None, :] >> l) % 2 == 0) for l in range(LEVELS)], 1).astype(f)
    c["lvl"] = lvl
    c["lvlT"] = lvl.transpose(2, 1, 0)
    c["mtm"] = (same & (r[None, :] >= r[:, None])).astype(f)
    c["below8"] = np.broadcast_to((np.arange(8)[None, :] < np.arange(8)[:, None]).astype(f).reshape(1, 64), (P, 64))
    c["ebase"] = np.broadcast_to(CAP * np.arange(E3, dtype=f), (P, E3))
    c["trash"] = (SLOTS + r[:, None] + P * np.arange(K3)).astype(f)
    c["run"] = np.broadcast_to((pos != 0).astype(f), (128, P))
    c["sgn"] = np.where(p < 64, 1.0, -1.0).astype(f)[:, None]
    y, x = (a.reshape(-1).astype(f) for a in np.meshgrid(np.arange(GRID), np.arange(GRID), indexing="ij"))
    om = (np.arange(D // 4, dtype=f) / f(D // 4 - 1)).astype(f)
    om = (f(1.0) / f(10000.0) ** om).astype(f)
    xa, ya = x[:, None] * om[None, :], y[:, None] * om[None, :]
    c["pe"] = np.concatenate([np.sin(xa), np.cos(xa), np.sin(ya), np.cos(ya)], 1).astype(f)
    return c


def lay_out(I):
    c = constants()
    row = lambda v: np.broadcast_to(np.asarray(v).reshape(1, -1), (128, np.asarray(v).size))
    col = lambda v: np.asarray(v).reshape(-1, 128).T if np.asarray(v).size >= 128 else flat(np.asarray(v).reshape(-1, 1))
    s = dict(c)
    s["base"] = np.tile(np.concatenate([I["cls_tok"].reshape(1, D), c["pe"]], 0), (SEQS, 1))
    s["ln2_w"], s["b_out0"] = row(I["L0_tok_ln2_w"]), row(I["L0_attn_b_out"])
    b_in = I["L0_attn_b_in"]
    s["b_q0"], s["b_k0"], s["b_v0"] = col(b_in[:D]), col(b_in[D:2 * D]), row(b_in[2 * D:])
    s["ln_w"], s["ln_b"] = row(I["L1_attn_ln_w"]), row(I["L1_attn_ln_b"])
    s["lam"] = row(np.concatenate([I["L1_attn_lambda_" + n] for n in ("q1", "k1", "q2", "k2")]))
    s["qkv_b"], s["proj_b"] = row(I["L2_attn_qkv_b"]), row(I["L2_attn_proj_b"])
    s["beta_w"], s["norm1_row"], s["beta_b"] = row(I["L3_attn_beta_w"]), row(I["L3_attn_norm1_w"]), row(I["L3_attn_beta_b"])
    s["range"], s["cn_b4"], s["gc_b3"] = row(I["L1_ffn_adaptive_range"]), row(I["L1_ffn_cn_b4"]), row(I["L1_ffn_gc_b3"])
    s["ln1_w"] = col(I["L0_tok_ln1_w"])
    s["b2"] = flat(chunks(I["L0_ffn_b2"].T))
    s["cn_b1"], s["cn_b2"], s["cn_b3"] = col(I["L1_ffn_cn_b1"]), col(I["L1_ffn_cn_b2"]), col(I["L1_ffn_cn_b3"])
    s["gc_b1"], s["gc_b2"] = col(I["L1_ffn_gc_b1"]), col(I["L1_ffn_gc_b2"])
    s["alpha"], s["norm1"], s["norm2"] = col(I["L3_attn_alpha_logit"]), col(I["L3_attn_norm1_w"]), col(I["L3_attn_norm2_w"])
    a = {"small": np.concatenate([flat(s[n]) for n, _ in SMALL], 1)}

    w = {}
    w["w_tok"] = chunks(I["L0_tok_W"].T)
    w["w_in"], w["w_out"], w["gate0"] = chunks(I["L0_attn_w_in"]), chunks(I["L0_attn_w_out"]), chunks(I["L0_ffn_gate_w"])
    w["qk1"] = chunks(np.concatenate([I["L1_attn_Wq"].T, I["L1_attn_Wk"].T], 1))
    w["v1"], w["o1"] = chunks(I["L1_attn_Wv"].T), chunks(I["L1_attn_Wo"].T)
    w["cn1"], w["cn2"], w["cn3"] = chunks(I["L1_ffn_cn_w1"]), chunks(I["L1_ffn_cn_w2"]), chunks(I["L1_ffn_cn_w3"])
    w["cn4"] = np.broadcast_to(I["L1_ffn_cn_w4"], (64, 128))
    w["gc1"], w["gc2"] = chunks(I["L1_ffn_gc_w1"]), chunks(I["L1_ffn_gc_w2"])
    w["gc3"] = np.broadcast_to(I["L1_ffn_gc_w3"], (64, 128))
    w["qkv2"], w["proj2"], w["gate2"] = chunks(I["L2_attn_qkv_w"]), chunks(I["L2_attn_proj_w"]), chunks(I["L2_ffn_gate_w"])
    for n in ("w1", "w3"):
        w[n + "_2"] = I["L2_ffn_" + n].reshape(E2, 2, 128, F2).transpose(2, 0, 1, 3)
    w["w2_2"] = I["L2_ffn_w2"].transpose(1, 0, 2)
    w["qk3"] = chunks(np.concatenate([I["L3_attn_Wq"], I["L3_attn_Wk"]], 1))
    w["v3"], w["o3"] = chunks(I["L3_attn_Wv"]), chunks(I["L3_attn_Wo"])
    w["gate3"], w["up3"], w["down3"] = (chunks(I["L3_attn_w_" + n]) for n in ("gate", "up", "down"))
    w["router"], w["ws_gu"], w["ws_down"] = chunks(I["L3_ffn_router_w"].T), chunks(I["L3_ffn_ws_gate_up"]), chunks(I["L3_ffn_ws_down"], FH)
    for array, parts in WEIGHTS:
        a[array] = np.concatenate([flat(w[n]) for n, _ in parts], 1)

    x = I["x"].reshape(BATCH, CHANNELS, GRID, PATCH, GRID, PATCH).transpose(0, 2, 4, 1, 3, 5).reshape(BATCH, L - 1, PD)
    patches = np.zeros((T * SEQS, L, PD), np.float32)
    patches[:BATCH, 1:] = x
    a["patches"] = patches.reshape(T, P, PD)
    a["w1_0"] = I["L0_ffn_w1"].reshape(E0, 2, 128, F0).transpose(0, 2, 1, 3).reshape(E0, 128, 2 * F0)
    a["w2_0"] = I["L0_ffn_w2"].reshape(E0, F0 // 128, 128, D).transpose(0, 2, 1, 3).reshape(E0, 128, F0 // 128 * D)
    a["b1_0"] = I["L0_ffn_b1"].reshape(E0, F0 // 128, 128).transpose(0, 2, 1)
    a["b2_0"] = I["L0_ffn_b2"].reshape(E0, 2, 128).transpose(0, 2, 1)
    gu = np.concatenate([I["L3_ffn_w_gate"], I["L3_ffn_w_up"]], 2)
    a["gu_3"] = gu.reshape(E3, 2, 128, 2 * F3).transpose(0, 2, 1, 3).reshape(E3, 128, 4 * F3)
    a["down_3"] = I["L3_ffn_w_down"].reshape(E3, 2, FH, D).transpose(0, 2, 1, 3).reshape(E3, FH, 2 * D)
    return {n: np.ascontiguousarray(v) for n, v in a.items()}


def kernel(**inputs):
    import concourse.bacc as bacc
    from concourse.bass_utils import run_bass_kernel_spmd

    arrays = lay_out({n: np.asarray(v) for n, v in inputs.items()})
    nc = bacc.Bacc("TRN2", target_bir_lowering=False, num_devices=1)
    dram = {n: nc.dram_tensor("in_" + n, a.shape, F32, kind="ExternalInput").ap() for n, a in arrays.items()}
    dram["out"] = nc.dram_tensor("out", (T, P, D), F32, kind="ExternalOutput").ap()
    for n, shape in (("cw0", (E0, NTOK)), ("cw2", (E2, NTOK)), ("slots_x", (SLOT_ROWS, D)), ("slots_y", (SLOTS, D))):
        dram[n] = nc.dram_tensor(n, shape, F32).ap()
    vit_tower(nc, dram)
    r = run_bass_kernel_spmd(nc, [{"in_" + n: a for n, a in arrays.items()}], core_ids=[0])
    return r.results[0]["out"].reshape(T * SEQS, L, D)[:BATCH]
```

```python
import math
from contextlib import ExitStack

import numpy as np
import concourse.bass as bass
from concourse import mybir

F32 = mybir.dt.float32
F32R = mybir.dt.float32r
I32 = mybir.dt.int32
ALU = mybir.AluOpType
ACT = mybir.ActivationFunctionType
AX = mybir.AxisListType
ET = mybir.EngineType
ADD, SUB, MUL, MAX, MIN = ALU.add, ALU.subtract, ALU.mult, ALU.max, ALU.min

BATCH, SIDE, PATCH, CHANNELS, D = 32, 96, 16, 3, 256
GRID = SIDE // PATCH
L = GRID * GRID + 1
SEQS = 3
P = SEQS * L
T = -(-BATCH // SEQS)
NTOK = T * P
PD = CHANNELS * PATCH * PATCH
PC = PD // 128
H16, DH = 16, 16
LANES = 2
G = 3
GC = NTOK // G
GS = GC // L
GE = GC + GC % 2
E0, F0 = 8, 1024
E2, F2 = 8, 128
E3, K3, F3, CAP = 64, 8, 192, 128
FH = F3 // 2
SLOTS = E3 * CAP
SLOT_ROWS = SLOTS + 14 * 128
CW = P + L
LAMBDA_INIT = 0.8 - 0.6 * math.exp(-0.3 * 12)
LEVELS = 6
NEG = -1e30
OVERFLOW = 20000.0


def tile(t, i):
    return t[:, bass.ds(i, 1), :].rearrange("p a n -> p (a n)")


def cols(t, i):
    return t[:, :, bass.ds(i * P, P)]


def spread(ap, axis, n):
    ap = ap.unsqueeze(axis)
    shape = list(ap.shape)
    shape[axis] = n
    return ap.to_broadcast(shape)


SMALL = [
    ("ident", 128), ("base", D), ("ln2_w", D), ("ln1_w", PC), ("mask8", 8), ("vm16", 16), ("vm8", 8), ("alibi", H16 * L), ("mb", SEQS),
    ("cos", DH), ("sin", DH), ("blk", 128), ("tri", P), ("strict", P), ("lvl", LEVELS * P),
    ("lvlT", LEVELS * P), ("mtm", P), ("below8", 64), ("ebase", E3), ("trash", LANES * K3), ("run", P), ("sgn", 1),
    ("b_out0", D), ("b_v0", D), ("ln_w", 32), ("ln_b", 32), ("lam", 64),
    ("qkv_b", 3 * D), ("proj_b", D), ("beta_w", D), ("norm1_row", D), ("beta_b", 1), ("range", 1),
    ("cn_b4", 1), ("gc_b3", 1), ("b_q0", 2), ("b_k0", 2), ("b2", 2 * E0), ("cn_b1", 2),
    ("cn_b2", 1), ("cn_b3", 1), ("gc_b1", 1), ("gc_b2", 1), ("alpha", 2), ("norm1", 2), ("norm2", 2),
]
FIRST = 128 + 2 * D + PC
WEIGHTS = [
    ("tok", [("w_tok", PC * D)]),
    ("l0a", [("w_in", 2 * 3 * D), ("w_out", 2 * D), ("gate0", 2 * E0)]),
    ("l1a", [("qk1", 2 * 2 * D), ("v1", 2 * D), ("o1", 2 * D)]),
    ("l1f", [("cn1", 2 * D), ("cn2", 2 * 128), ("cn3", 64), ("cn4", 128), ("gc1", 2 * 128), ("gc2", 64),
             ("gc3", 128)]),
    ("l2a", [("qkv2", 2 * 3 * D), ("proj2", 2 * D), ("gate2", 2 * E2)]),
    ("l2f", [("w1_2", E2 * 2 * F2), ("w3_2", E2 * 2 * F2), ("w2_2", E2 * D)]),
    ("l3a", [("qk3", 2 * 2 * D), ("v3", 2 * D), ("o3", 2 * D), ("gate3", 2 * 512), ("up3", 2 * 512),
             ("down3", 4 * D)]),
    ("l3f", [("router", 2 * E3), ("ws_gu", 2 * 2 * F3), ("ws_down", 2 * D)]),
]


EARLY = ("tok", "l0a", "l1a", "l1f", "l2a")
LATE = ("l2f", "l3a", "l3f")


class Mem:
    pass


def place_weights(nc, ctx, M, arrays):
    for array, parts in WEIGHTS:
        if array in arrays:
            buf = ctx.enter_context(nc.sbuf_tensor("w_" + array, [128, sum(n for _, n in parts)], F32))
            M.w[array] = buf
            o = 0
            for name, n in parts:
                M.w[name] = buf[:, o:o + n]
                o += n


def load_late(nc, M):
    with nc.Block(name="load_late") as block:
        @block.sync
        def _(sp):
            for array in LATE:
                sp.dma_start(M.w[array][:, :], M.dram[array]).then_inc(M.loaded[array], 16)

        @block.scalar
        def _(act):
            rows = M.dram["slots_x"].rearrange("(p r) d -> p r d", p=128)
            act.dma_start(rows, spread(M.zero[:, :], 1, rows.shape[1])).then_inc(M.slots_cleared, 16)


def setup_memory(nc, ctx, dram):
    M = Mem()
    M.dram = dram

    def sb(name, shape, dt=F32):
        return ctx.enter_context(nc.sbuf_tensor(name, shape, dt))

    M.h = sb("h", [P, T, D])
    M.x_all = sb("x", [128, T * D])
    M.x = M.x_all[0:P, :].rearrange("p (t d) -> p t d", t=T)
    M.xT = sb("xT", [128, 2, NTOK])
    M.yT_even = sb("yT", [128, 2, G * GE])
    M.yT = M.yT_even[:, :, 0:NTOK]
    M.stats = sb("stats", [P, T, 6])
    M.mean = sb("mean", [P, T])
    M.std = sb("std", [P, T])
    M.rstd = sb("rstd", [P, T])
    M.tmp = sb("ln_tmp", [P, 4, T])
    M.small = sb("small", [128, sum(n for _, n in SMALL)])
    M.zero = sb("zero", [128, D])
    M.at, o = {}, 0
    for name, n in SMALL:
        M.at[name] = (o, n)
        o += n
    M.w, M.loaded = {}, {}
    for array, _ in WEIGHTS:
        M.loaded[array] = ctx.enter_context(nc.semaphore("loaded_" + array))
    place_weights(nc, ctx, M, EARLY)
    M.w8 = sb("w8", [P, T, K3])
    M.idx8 = sb("idx8", [P, T, K3], I32)
    sems = {}

    def shared_sem(name):
        if name not in sems:
            sems[name] = ctx.enter_context(nc.semaphore(name))
        return sems[name]

    M.sem = shared_sem
    M.bank = [ctx.enter_context(nc.psum_tensor(f"bank{b}", [128, 512], F32)) for b in range(8)]
    M.first_loaded = ctx.enter_context(nc.semaphore("first_loaded"))
    M.small_loaded = ctx.enter_context(nc.semaphore("small_loaded"))
    M.slots_cleared = ctx.enter_context(nc.semaphore("slots_cleared"))
    return M


def small(M, name, parts=P):
    o, n = M.at[name]
    return M.small[0:parts, o:o + n]


def dve_tile_stats(nc, M, lanes):
    for b, i in lanes:
        nc.vector.bn_stats(tile(M.stats, i), tile(M.h, i))


def dve_ln_stats(nc, v, M, var_ready, std_ready, eps=1e-5):
    v.drain()
    me, ve, mo, vo = (M.stats[:, :, c] for c in (1, 2, 4, 5))
    t0, t1 = M.tmp[:, 0, :], M.tmp[:, 1, :]
    t2, t3 = M.tmp[:, 2, :], M.tmp[:, 3, :]
    nc.vector.tensor_tensor(t0, me, mo, ADD)
    nc.vector.tensor_tensor(t1, me, mo, SUB)
    nc.vector.tensor_tensor(t2, ve, vo, ADD)
    v.drain()
    nc.vector.tensor_scalar(M.mean[:, :], t0, 0.5, None, MUL)
    nc.vector.tensor_tensor(t3, t1, t1, MUL)
    v.drain()
    nc.vector.tensor_scalar(t0, t2, 1.0 / D, eps, MUL, ADD)
    nc.vector.tensor_scalar(t1, t3, 0.25, None, MUL)
    v.drain()
    nc.vector.tensor_tensor(t2, t0, t1, ADD).then_inc(var_ready, 1)
    v.wait_ge(std_ready, 1)
    v.sem_inc(std_ready, -1)
    nc.vector.reciprocal(M.rstd[:, :], M.std[:, :])
    v.drain()


def act_ln_std(nc, a, M, var_ready, std_ready):
    a.preload_act_table(ACT.Sqrt)
    a.wait_ge(var_ready, 1)
    a.sem_inc(var_ready, -1)
    nc.scalar.activation(M.std[:, :], M.tmp[:, 2, :], ACT.Sqrt).then_inc(std_ready, 1)


def ln_apply(nc, M, i, out):
    return nc.vector.tensor_scalar(out, tile(M.h, i), M.mean[:, bass.ds(i, 1)], M.rstd[:, bass.ds(i, 1)],
                                   SUB, MUL)


def pe_turn(nc, M, bank, src, n=2):
    for c in range(n):
        last = nc.tensor.transpose(M.bank[bank][:, c * P:(c + 1) * P], src[:, c * 128:(c + 1) * 128],
                                   small(M, "ident")[:, 0:P])
    return last


def turned(M, bank, n=2):
    return M.bank[bank][:, 0:n * P].rearrange("p (c t) -> p c t", c=n)


def patch_embedding(nc, M):
    with ExitStack() as ctx:
        sb = lambda n, s: [ctx.enter_context(nc.sbuf_tensor(f"tok_{n}{b}", s, F32)) for b in range(LANES)]
        sem = lambda n: [M.sem(f"{n}{b}") for b in range(LANES)]
        patches, xn, xT = sb("patches", [P, PD]), sb("xn", [P, PD]), sb("xT", [128, PC, P])
        st, mv, y = sb("st", [P, 12]), sb("mv", [P, 2]), sb("y", [P, D])
        var, std, rs = sb("var", [P, 1]), sb("std", [P, 1]), sb("rs", [P, 1])
        patches_in, patches_read = sem("loaded"), sem("patches_read")
        var_ready, std_ready, w_scaled = M.sem("var_ready0"), M.sem("std_ready0"), M.sem("w_folded")
        xn_ready, turned_ready, xT_ready = sem("xn_ready"), sem("turned"), sem("xT_ready")
        emb_ready = sem("q_ready")
        w = M.w["w_tok"].rearrange("p (c n) -> p c n", c=PC)
        A, B, C = ([4 * b + j for b in range(LANES)] for j in range(3))
        with nc.Block(name="patch_embedding") as block:
            @block.sync
            def _(sp):
                sp.dma_start(M.small[:, 0:FIRST], M.dram["small"][:, 0:FIRST]).then_inc(M.first_loaded, 16)

                def body(lanes):
                    for b, i in lanes:
                        sp.wait_ge(patches_read[b], 1)
                        sp.sem_inc(patches_read[b], -1)
                        sp.dma_start(patches[b][:, :], M.dram["patches"][bass.ds(i, 1)].rearrange("a p n -> (a p) n")
                                     ).then_inc(patches_in[b], 16)

                tiles_by_lanes(nc, ET.SP, body)
                for b in range(LANES):
                    sp.wait_ge(patches_read[b], 1)
                    sp.sem_inc(patches_read[b], -1)

            @block.gpsimd
            def _(pool):
                nc.gpsimd.memset(M.zero[:, :], 0.0)

            @block.vector
            def _(v):
                for b in range(LANES):
                    v.sem_inc(patches_read[b], 1)

                def norm(b, src, halves, n, out):
                    for k in range(halves):
                        nc.vector.bn_stats(st[b][:, 6 * k:6 * k + 6], src[:, n * k:n * k + n])
                    v.drain()
                    nc.vector.bn_aggr(mv[b][:, :], st[b][:, 0:6 * halves])
                    v.drain()
                    nc.vector.tensor_scalar(var[b][:, :], mv[b][:, 1:2], 1e-5, None, ADD).then_inc(var_ready, 1)
                    v.wait_ge(std_ready, 1)
                    v.sem_inc(std_ready, -1)
                    nc.vector.reciprocal(rs[b][:, :], std[b][:, :])
                    v.drain()
                    return nc.vector.tensor_scalar(out[b][:, :], src, mv[b][:, 0:1], rs[b][:, 0:1], SUB, MUL)

                def patch_norm(b):
                    v.wait_ge(patches_in[b], 16)
                    v.sem_inc(patches_in[b], -16)
                    norm(b, patches[b][:, :], 2, PD // 2, xn).then_inc(xn_ready[b], 1)
                    v.drain()
                    v.sem_inc(patches_read[b], 1)

                def embedding_norm(b, i):
                    v.wait_ge(emb_ready[b], 1)
                    v.sem_inc(emb_ready[b], -1)
                    norm(b, M.bank[C[b]][0:P, 0:D], 1, D, y)
                    v.drain()
                    nc.vector.tensor_tensor(y[b][:, :], y[b][:, :], small(M, "ln2_w"), MUL)
                    v.drain()
                    nc.vector.tensor_tensor(tile(M.h, i), y[b][:, :], small(M, "base"), ADD)
                    v.drain()
                    dve_tile_stats(nc, M, [(b, i)])

                v.wait_ge(M.first_loaded, 16)
                v.wait_ge(M.loaded["tok"], 16)
                for c in range(PC):
                    last = nc.vector.tensor_scalar(w[:, c, :], w[:, c, :], small(M, "ln1_w", 128)[:, c:c + 1],
                                                   None, MUL)
                last.then_inc(w_scaled, 1)

                patch_norm(0)
                with nc.Fori(0, T // LANES, engines=(ET.DVE,)) as p:
                    for b in range(LANES):
                        patch_norm(1 - b)
                        embedding_norm(b, p * LANES + b)
                embedding_norm(0, T - 1)

            @block.scalar
            def _(a):
                for array in EARLY:
                    a.dma_start(M.w[array][:, :], M.dram[array]).then_inc(M.loaded[array], 16)
                    if array == "tok":
                        a.dma_start(M.small[:, FIRST:], M.dram["small"][:, FIRST:]).then_inc(M.small_loaded, 16)
                a.preload_act_table(ACT.Sqrt)

                def root(b):
                    a.wait_ge(var_ready, 1)
                    a.sem_inc(var_ready, -1)
                    nc.scalar.activation(std[b][:, :], var[b][:, :], ACT.Sqrt).then_inc(std_ready, 1)

                def copy_xT(b):
                    a.wait_ge(turned_ready[b], 1)
                    a.sem_inc(turned_ready[b], -1)
                    nc.scalar.copy(xT[b][:, 0:4, :], turned(M, A[b], 4))
                    nc.scalar.copy(xT[b][:, 4:PC, :], turned(M, B[b], PC - 4)).then_inc(xT_ready[b], 1)

                root(0)
                with nc.Fori(0, T // LANES, engines=(ET.Activation,)) as p:
                    for b in range(LANES):
                        copy_xT(b)
                        root(1 - b)
                        root(b)
                copy_xT(0)
                root(0)

            @block.tensor
            def _(pe):
                pe.wait_ge(M.first_loaded, 16)
                pe.wait_ge(w_scaled, 1)
                pe.sem_inc(w_scaled, -1)

                def body(lanes):
                    for b, i in lanes:
                        pe.wait_ge(xn_ready[b], 1)
                        pe.sem_inc(xn_ready[b], -1)
                        pe_turn(nc, M, A[b], xn[b][:, 0:512], 4)
                        pe_turn(nc, M, B[b], xn[b][:, 512:PD], PC - 4).then_inc(turned_ready[b], 1)
                        pe.wait_ge(xT_ready[b], 1)
                        pe.sem_inc(xT_ready[b], -1)
                        for c in range(PC):
                            last = nc.tensor.matmul(M.bank[C[b]][0:P, 0:D], xT[b][:, c, :], w[:, c, :],
                                                    start=(c == 0), stop=(c == PC - 1))
                        last.then_inc(emb_ready[b], 1)

                tiles_by_lanes(nc, ET.PE, body)




def tiles_by_lanes(nc, engine, body):
    with nc.Fori(0, T // LANES, engines=(engine,)) as p:
        body([(b, p * LANES + b) for b in range(LANES)])
    for t in range(T - T % LANES, T):
        body([(0, t)])


def tiles_with_next(nc, engine, first, body):
    pair = lambda p: [(b, p * LANES + b) for b in range(LANES)]
    first(pair(0))
    with nc.Fori(0, T // LANES - 1, engines=(engine,)) as p:
        body(pair(p), [(b, p * LANES + (LANES + b)) for b in range(LANES)])
    rest = [(t % LANES, t) for t in range(T - T % LANES, T)]
    body(pair(T // LANES - 1), rest)
    body(rest, [])


def add_back(nc, M, name):
    with ExitStack() as ctx:
        sem = lambda n: [M.sem(f"{n}{b}") for b in range(LANES)]
        y = [ctx.enter_context(nc.sbuf_tensor(f"back_y{name}{b}", [128, 2, P], F32)) for b in range(LANES)]
        y_ready, y_turned, y_free, turned_free = sem("y_ready"), sem("oT_turned"), sem("back_y_free"), sem("back_free")
        with nc.Block(name="add_back" + name) as block:
            @block.scalar
            def _(a):
                def body(lanes):
                    for b, i in lanes:
                        a.wait_ge(y_free[b], 1)
                        a.sem_inc(y_free[b], -1)
                        nc.scalar.copy(y[b][:, :, :], cols(M.yT, i)).then_inc(y_ready[b], 1)

                tiles_by_lanes(nc, ET.Activation, body)
                for b in range(LANES):
                    a.wait_ge(y_free[b], 1)
                    a.sem_inc(y_free[b], -1)

            @block.tensor
            def _(pe):
                for b in range(LANES):
                    pe.sem_inc(y_free[b], 1)

                def body(lanes):
                    for b, i in lanes:
                        pe.wait_ge(turned_free[b], 1)
                        pe.sem_inc(turned_free[b], -1)
                        pe.wait_ge(y_ready[b], 1)
                        pe.sem_inc(y_ready[b], -1)
                        for c in range(2):
                            last = nc.tensor.transpose(M.bank[4 * b][0:P, c * 128:(c + 1) * 128], y[b][:, c, :],
                                                       small(M, "ident", 128))
                        last.then_inc(y_turned[b], 1)

                tiles_by_lanes(nc, ET.PE, body)
                for b in range(LANES):
                    pe.wait_ge(turned_free[b], 1)
                    pe.sem_inc(turned_free[b], -1)

            @block.vector
            def _(v):
                for b in range(LANES):
                    v.sem_inc(turned_free[b], 1)

                def body(lanes):
                    for b, i in lanes:
                        v.wait_ge(y_turned[b], 1)
                        v.sem_inc(y_turned[b], -1)
                        v.sem_inc(y_free[b], 1)
                        nc.vector.tensor_tensor(tile(M.h, i), tile(M.h, i), M.bank[4 * b][0:P, 0:D], ADD
                                                ).then_inc(turned_free[b], 1)
                    v.drain()
                    dve_tile_stats(nc, M, lanes)

                tiles_by_lanes(nc, ET.DVE, body)


def evacuate_q(nc, M, bank, qm, bias=None):
    for c in range(2):
        out = qm[:, c, :].rearrange("p (s w) -> p s w", w=CW)[:, :, 0:L]
        src = M.bank[bank][:, c * P:(c + 1) * P].rearrange("p (s j) -> p s j", s=SEQS)
        if bias is None:
            last = nc.scalar.copy(out, src)
        else:
            last = nc.scalar.activation(out, src, ACT.Identity, bias=bias[:, c:c + 1])
    return last


def mask_k_heads(nc, M, kT, km, c):
    return nc.vector.tensor_tensor(km[:, c, :, :], spread(kT[:, c, :], 1, 8),
                                   spread(small(M, "mask8", 128), 2, P), MUL)


def pe_scores(nc, M, bank, qm, km, c):
    for s in range(SEQS):
        last = nc.tensor.matmul(M.bank[bank][0:P, 0:8 * L], qm[:, c, s * P:(s + 1) * P],
                                km[:, c, :, s * L:(s + 1) * L], start=(s == 0), stop=(s == SEQS - 1))
    return last


def pe_turn_probs(nc, M, banks, probs, maps):
    groups = -(-maps // 3)
    for g in range(groups):
        n = min(3, maps - 3 * g) * L
        out = M.bank[banks[g // 4]][0:n, (g % 4) * P:(g % 4 + 1) * P]
        last = nc.tensor.transpose(out, probs[:, 3 * g * L:3 * g * L + n], small(M, "ident")[:, 0:P])
    return last


def evacuate_probs(nc, M, banks, pm, maps):
    for g in range(-(-maps // 3)):
        n = min(3, maps - 3 * g) * L
        src = M.bank[banks[g // 4]][0:n, (g % 4) * P:(g % 4 + 1) * P].rearrange("p (s j) -> p s j", s=SEQS)
        out = pm[0:n, g, :].rearrange("p (s w) -> p s w", w=CW)[:, :, 0:L]
        last = nc.scalar.copy(out, src)
    return last


def pe_values(nc, M, bank, pm, vm, maps, dv):
    for g in range(-(-maps // 3)):
        k = min(3, maps - 3 * g)
        for s in range(SEQS):
            last = nc.tensor.matmul(M.bank[bank][0:P, 3 * g * dv:(3 * g + k) * dv],
                                    pm[0:k * L, g, s * P:(s + 1) * P],
                                    vm[0:k * L, s, 3 * g * dv:(3 * g + k) * dv],
                                    start=(s == 0), stop=(s == SEQS - 1))
    return last


def pe_project(nc, M, bank, lhs, w, n0, n1, rows=P, col=0):
    for k in range(2):
        last = nc.tensor.matmul(M.bank[bank][0:rows, col:col + n1 - n0], lhs[:, k, :], w[:, k, n0:n1],
                                start=(k == 0), stop=(k == 1))
    return last


def repeat_x(nc, M, bank, xr):
    for k in range(2):
        src = M.bank[bank][:, k * P:(k + 1) * P].rearrange("p (s j) -> p s j", s=SEQS)
        last = nc.scalar.copy(xr[:, k, :, :].rearrange("p s (r j) -> p s r j", r=3), spread(src, 2, 3))
    return last


def pe_values_in(nc, M, banks, xr, w, n0):
    for s in range(SEQS):
        for k in range(2):
            last = nc.tensor.matmul(M.bank[banks[s // 2]][0:P, (s % 2) * D:(s % 2 + 1) * D],
                                    xr[:, k, s, :], w[:, k, n0:n0 + D], start=(k == 0), stop=(k == 1))
    return last


def mask_v(nc, M, banks, vm, mask, maps):
    dv = D // maps
    m = spread(mask, 2, dv)
    for s in range(SEQS):
        src = M.bank[banks[s // 2]][0:P, (s % 2) * D:(s % 2 + 1) * D].rearrange("p (m d) -> p m d", m=maps)
        last = nc.vector.tensor_tensor(vm[:, s, :].rearrange("p (m d) -> p m d", m=maps), src, m, MUL)
    return last


def alibi_attention(nc, M):
    with ExitStack() as ctx:
        sb = lambda n, s: [ctx.enter_context(nc.sbuf_tensor(f"a0_{n}{b}", s, F32)) for b in range(LANES)]
        sem = lambda n: [M.sem(f"{n}{b}") for b in range(LANES)]
        xn, xT, kT, xr = sb("xn", [P, D]), sb("xT", [128, 2, P]), sb("kT", [128, 2, P]), sb("xr", [128, 2, SEQS, P])
        qm, km = sb("qm", [128, 2, SEQS * CW]), sb("km", [128, 2, 8, P])
        vm, S, Pr = sb("vm", [P, SEQS, D]), sb("S", [P, H16, L]), sb("Pr", [P, H16, L])
        mx, rsum = sb("mx", [P, H16]), sb("rsum", [P, H16])
        pm, o, oT, y = sb("pm", [P, 6, SEQS * CW]), sb("o", [P, D]), sb("oT", [128, 2, P]), sb("y", [P, D])
        var_ready, std_ready, blank, pblank = M.sem("var_ready0"), M.sem("std_ready0"), M.sem("blank"), M.sem("pblank")
        xn_ready, turned_ready, xT_ready, xr_ready = sem("xn_ready"), sem("turned"), sem("xT_ready"), sem("xr_ready")
        q_ready, k_ready, v_ready = sem("q_ready"), sem("k_ready"), sem("v_ready")
        kT_ready, km_ready, vm_ready, qm_ready = sem("kT_ready"), sem("km_ready"), sem("vm_ready"), sem("q_turned")
        s_ready, shifted, probs_dve, probs_pe = sem("s_ready"), sem("shifted"), sem("probs_dve"), sem("probs_pe")
        pT_ready, pm_ready, o_ready, on_ready = sem("pT_ready"), sem("pm_ready"), sem("o_ready"), sem("on_ready")
        oT_turned, oT_ready, y_ready, y_read = sem("oT_turned"), sem("oT_ready"), sem("y_ready"), sem("k_turned")
        w = M.w["w_in"].rearrange("p (k n) -> p k n", k=2)
        wo = M.w["w_out"].rearrange("p (k n) -> p k n", k=2)
        A, B, C, Dk = ([4 * b + j for b in range(LANES)] for j in range(4))
        with nc.Block(name="alibi_attention") as block:
            @block.gpsimd
            def _(pool):
                for b in range(LANES):
                    nc.gpsimd.memset(qm[b][:, :, :], 0.0).then_inc(blank, 1)
                    nc.gpsimd.memset(pm[b][:, :, :], 0.0).then_inc(pblank, 1)

            @block.vector
            def _(v):
                for b in range(LANES):
                    v.sem_inc(y_read[b], 1)
                dve_ln_stats(nc, v, M, var_ready, std_ready)
                v.wait_ge(M.small_loaded, 16)

                def normalise(lanes):
                    for b, i in lanes:
                        ln_apply(nc, M, i, xn[b][:, :]).then_inc(xn_ready[b], 1)

                def body(lanes, following):
                    for b, i in lanes:
                        v.wait_ge(kT_ready[b], 1)
                        v.sem_inc(kT_ready[b], -1)
                        for c in range(2):
                            mask_k_heads(nc, M, kT[b], km[b], c).then_inc(km_ready[b], 1)
                    for b, i in lanes:
                        v.wait_ge(v_ready[b], 1)
                        v.sem_inc(v_ready[b], -1)
                        mask_v(nc, M, (Dk[b], A[b]), vm[b], small(M, "vm16"), H16).then_inc(vm_ready[b], 1)
                    for b, i in lanes:
                        for c, bank in enumerate((B[b], C[b])):
                            v.wait_ge(s_ready[b], 1)
                            v.sem_inc(s_ready[b], -1)
                            m = slice(8 * c, 8 * c + 8)
                            nc.vector.scalar_tensor_tensor(
                                S[b][:, m, :], M.bank[bank][0:P, 0:8 * L].rearrange("p (m j) -> p m j", m=8),
                                DH ** -0.5, small(M, "alibi").rearrange("p (m j) -> p m j", m=H16)[:, m, :], MUL, ADD)
                        v.drain()
                        nc.vector.tensor_reduce(mx[b][:, :], S[b][:, :, :], AX.X, MAX)
                        v.drain()
                        nc.vector.tensor_tensor(S[b][:, :, :], S[b][:, :, :], spread(mx[b][:, :], 2, L), SUB
                                                ).then_inc(shifted[b], 1)
                    for b, i in lanes:
                        v.wait_ge(probs_dve[b], 1)
                        v.sem_inc(probs_dve[b], -1)
                        nc.vector.tensor_reduce(mx[b][:, :], Pr[b][:, :, :], AX.X, ADD)
                        v.drain()
                        nc.vector.reciprocal(rsum[b][:, :], mx[b][:, :])
                    v.drain()
                    normalise(following)
                    for b, i in lanes:
                        v.wait_ge(o_ready[b], 1)
                        v.sem_inc(o_ready[b], -1)
                        nc.vector.tensor_tensor(o[b][:, :].rearrange("p (m d) -> p m d", m=H16),
                                                M.bank[B[b]][0:P, 0:D].rearrange("p (m d) -> p m d", m=H16),
                                                spread(rsum[b][:, :], 2, DH), MUL)
                        v.drain()
                        nc.vector.tensor_tensor(o[b][:, :], o[b][:, :], small(M, "b_v0"), ADD).then_inc(on_ready[b], 1)
                    for b, i in lanes:
                        v.wait_ge(y_ready[b], 1)
                        v.sem_inc(y_ready[b], -1)
                        nc.vector.tensor_tensor(y[b][:, :], M.bank[Dk[b]][0:P, 0:D], small(M, "b_out0"), ADD
                                                ).then_inc(y_read[b], 1)
                        v.drain()
                        nc.vector.tensor_tensor(tile(M.h, i), tile(M.h, i), y[b][:, :], ADD)
                    v.drain()
                    dve_tile_stats(nc, M, lanes)

                tiles_with_next(nc, ET.DVE, normalise, body)

            @block.scalar
            def _(a):
                act_ln_std(nc, a, M, var_ready, std_ready)
                a.preload_act_table(ACT.Exp)
                a.wait_ge(M.small_loaded, 16)
                a.wait_ge(pblank, LANES)
                a.sem_inc(pblank, -LANES)
                a.wait_ge(blank, LANES)
                a.sem_inc(blank, -LANES)

                def copy_x(lanes):
                    for b, i in lanes:
                        a.wait_ge(turned_ready[b], 1)
                        a.sem_inc(turned_ready[b], -1)
                        nc.scalar.copy(xT[b][:, :, :], turned(M, A[b])).then_inc(xT_ready[b], 1)
                    for b, i in lanes:
                        repeat_x(nc, M, A[b], xr[b]).then_inc(xr_ready[b], 1)

                def body(lanes, following):
                    for b, i in lanes:
                        a.wait_ge(k_ready[b], 1)
                        a.sem_inc(k_ready[b], -1)
                        for c in range(2):
                            last = nc.scalar.activation(kT[b][:, c, :], M.bank[C[b]][:, c * P:(c + 1) * P], ACT.Identity,
                                                        bias=small(M, "b_k0", 128)[:, c:c + 1])
                        last.then_inc(kT_ready[b], 1)
                        a.wait_ge(q_ready[b], 1)
                        a.sem_inc(q_ready[b], -1)
                        evacuate_q(nc, M, B[b], qm[b], small(M, "b_q0", 128)).then_inc(qm_ready[b], 1)
                    for b, i in lanes:
                        a.wait_ge(shifted[b], 1)
                        a.sem_inc(shifted[b], -1)
                        nc.scalar.activation(Pr[b][:, :, :], S[b][:, :, :], ACT.Exp).then_inc(probs_dve[b], 1)
                        a.drain().then_inc(probs_pe[b], 1)
                    for b, i in lanes:
                        a.wait_ge(pT_ready[b], 1)
                        a.sem_inc(pT_ready[b], -1)
                        evacuate_probs(nc, M, (Dk[b], A[b]), pm[b], H16).then_inc(pm_ready[b], 1)
                    copy_x(following)
                    for b, i in lanes:
                        a.wait_ge(oT_turned[b], 1)
                        a.sem_inc(oT_turned[b], -1)
                        nc.scalar.copy(oT[b][:, :, :], turned(M, C[b])).then_inc(oT_ready[b], 1)
                    a.drain()

                tiles_with_next(nc, ET.Activation, copy_x, body)

            @block.tensor
            def _(pe):
                def turn_x(lanes):
                    for b, i in lanes:
                        pe.wait_ge(xn_ready[b], 1)
                        pe.sem_inc(xn_ready[b], -1)
                        pe_turn(nc, M, A[b], xn[b]).then_inc(turned_ready[b], 1)

                def project_q(lanes):
                    for b, i in lanes:
                        pe.wait_ge(xT_ready[b], 1)
                        pe.sem_inc(xT_ready[b], -1)
                        for c in range(2):
                            last = pe_project(nc, M, B[b], w[:, :, c * 128:(c + 1) * 128], xT[b], 0, P, 128, col=c * P)
                        last.then_inc(q_ready[b], 1)

                def project_k(lanes):
                    for b, i in lanes:
                        for c in range(2):
                            last = pe_project(nc, M, C[b], w[:, :, D + c * 128:D + (c + 1) * 128], xT[b], 0, P, 128, col=c * P)
                        last.then_inc(k_ready[b], 1)

                def first(lanes):
                    turn_x(lanes)
                    project_q(lanes)
                    project_k(lanes)

                def body(lanes, following):
                    for b, i in lanes:
                        pe.wait_ge(y_read[b], 1)
                        pe.sem_inc(y_read[b], -1)
                        pe.wait_ge(xr_ready[b], 1)
                        pe.sem_inc(xr_ready[b], -1)
                        pe_values_in(nc, M, (Dk[b], A[b]), xr[b], w, 2 * D).then_inc(v_ready[b], 1)
                    for b, i in lanes:
                        pe.wait_ge(qm_ready[b], 1)
                        pe.sem_inc(qm_ready[b], -1)
                        for c, bank in enumerate((B[b], C[b])):
                            pe.wait_ge(km_ready[b], 1)
                            pe.sem_inc(km_ready[b], -1)
                            pe_scores(nc, M, bank, qm[b], km[b], c).then_inc(s_ready[b], 1)
                    for b, i in lanes:
                        pe.wait_ge(probs_pe[b], 1)
                        pe.sem_inc(probs_pe[b], -1)
                        pe.wait_ge(vm_ready[b], 1)
                        pe.sem_inc(vm_ready[b], -1)
                        pe_turn_probs(nc, M, (Dk[b], A[b]), Pr[b][:, :, :].rearrange("p m j -> p (m j)"), H16
                                      ).then_inc(pT_ready[b], 1)
                    for b, i in lanes:
                        pe.wait_ge(pm_ready[b], 1)
                        pe.sem_inc(pm_ready[b], -1)
                        pe_values(nc, M, B[b], pm[b], vm[b], H16, DH).then_inc(o_ready[b], 1)
                    turn_x(following)
                    for b, i in lanes:
                        pe.wait_ge(on_ready[b], 1)
                        pe.sem_inc(on_ready[b], -1)
                        pe_turn(nc, M, C[b], o[b]).then_inc(oT_turned[b], 1)
                    project_q(following)
                    for b, i in lanes:
                        pe.wait_ge(oT_ready[b], 1)
                        pe.sem_inc(oT_ready[b], -1)
                        pe_project(nc, M, Dk[b], oT[b], wo, 0, D).then_inc(y_ready[b], 1)
                    project_k(following)

                pe.wait_ge(M.loaded["l0a"], 16)
                pe.wait_ge(M.small_loaded, 16)
                tiles_with_next(nc, ET.PE, first, body)
                for b in range(LANES):
                    pe.wait_ge(y_read[b], 1)
                    pe.sem_inc(y_read[b], -1)


def gate_top2(nc, M, name, gate, dram_cw, full_softmax, beside=None):
    E = 8
    with ExitStack() as ctx:
        sb = lambda n, s: [ctx.enter_context(nc.sbuf_tensor(f"{name}{n}{b}", s, F32)) for b in range(LANES)]
        sem = lambda n: [M.sem(f"{n}{b}") for b in range(LANES)]
        xn, xT = sb("xn", [P, D]), sb("xT", [128, 2, P])
        lg, neg, ex, gt, eq = sb("lg", [P, E]), sb("neg", [P, 1]), sb("ex", [P, E]), sb("gt", [P, E, E]), sb("eq", [P, E, E])
        rank, mask, se, re, cw = sb("rank", [P, E]), sb("mask", [P, E]), sb("se", [P, 1]), sb("re", [P, 1]), sb("cw", [P, E])
        cwT = M.yT[0:E, 0, :]
        var_ready, std_ready, xn_ready = M.sem("var_ready0"), M.sem("std_ready0"), sem("xn_ready")
        turned_ready, xT_ready, lg_ready = sem("turned"), sem("xT_ready"), sem("q_ready")
        shifted, ex_ready, cw_ready, cwT_turned = sem("shifted"), sem("probs_dve"), sem("on_ready"), sem("oT_turned")
        cw_stored = M.sem("cw_stored")
        w = gate.rearrange("p (k n) -> p k n", k=2)
        A, B, C = ([4 * b + j for b in range(LANES)] for j in range(3))
        with nc.Block(name=name) as block:
            if beside:
                beside(block)

            @block.vector
            def _(v):
                dve_ln_stats(nc, v, M, var_ready, std_ready)

                def normalise(lanes):
                    for b, i in lanes:
                        ln_apply(nc, M, i, xn[b][:, :]).then_inc(xn_ready[b], 1)

                def body(lanes, following):
                    for b, i in lanes:
                        v.wait_ge(lg_ready[b], 1)
                        v.sem_inc(lg_ready[b], -1)
                        nc.vector.tensor_copy(lg[b][:, :], M.bank[B[b]][0:P, 0:E])
                    v.drain()
                    for b, i in lanes:
                        nc.vector.tensor_reduce(neg[b][:, :], lg[b][:, :], AX.X, MAX)
                        other, own = spread(lg[b][:, :], 1, E), spread(lg[b][:, :], 2, E)
                        nc.vector.tensor_tensor(gt[b][:, :, :], other, own, ALU.is_gt)
                        nc.vector.tensor_tensor(eq[b][:, :, :], other, own, ALU.is_equal)
                    v.drain()
                    for b, i in lanes:
                        nc.vector.tensor_scalar(ex[b][:, :], lg[b][:, :], neg[b][:, 0:1], None, SUB).then_inc(shifted[b], 1)
                        nc.vector.tensor_tensor(eq[b][:, :, :], eq[b][:, :, :],
                                                small(M, "below8").rearrange("p (a b) -> p a b", a=E), MUL)
                    v.drain()
                    for b, i in lanes:
                        nc.vector.tensor_tensor(gt[b][:, :, :], gt[b][:, :, :], eq[b][:, :, :], ADD)
                    v.drain()
                    for b, i in lanes:
                        nc.vector.tensor_reduce(rank[b][:, :], gt[b][:, :, :], AX.X, ADD)
                    v.drain()
                    for b, i in lanes:
                        nc.vector.tensor_scalar(mask[b][:, :], rank[b][:, :], 2.0, None, ALU.is_lt)
                    v.drain()
                    normalise(following)
                    for b, i in lanes:
                        v.wait_ge(ex_ready[b], 1)
                        v.sem_inc(ex_ready[b], -1)
                        nc.vector.tensor_tensor(cw[b][:, :], ex[b][:, :], mask[b][:, :], MUL)
                    v.drain()
                    for b, i in lanes:
                        nc.vector.tensor_reduce(se[b][:, :], ex[b][:, :] if full_softmax else cw[b][:, :], AX.X, ADD)
                    v.drain()
                    for b, i in lanes:
                        nc.vector.reciprocal(re[b][:, :], se[b][:, :])
                    v.drain()
                    for b, i in lanes:
                        nc.vector.tensor_scalar(cw[b][:, :], cw[b][:, :], re[b][:, 0:1], None, MUL).then_inc(cw_ready[b], 1)
                    v.drain()

                tiles_with_next(nc, ET.DVE, normalise, body)

            @block.scalar
            def _(a):
                act_ln_std(nc, a, M, var_ready, std_ready)
                a.preload_act_table(ACT.Exp)

                def copy_x(lanes):
                    for b, i in lanes:
                        a.wait_ge(turned_ready[b], 1)
                        a.sem_inc(turned_ready[b], -1)
                        nc.scalar.copy(xT[b][:, :, :], turned(M, A[b])).then_inc(xT_ready[b], 1)
                    for b, i in lanes:
                        nc.scalar.copy(cols(M.xT, i), turned(M, A[b]))

                def body(lanes, following):
                    for b, i in lanes:
                        a.wait_ge(shifted[b], 1)
                        a.sem_inc(shifted[b], -1)
                        nc.scalar.activation(ex[b][:, :], ex[b][:, :], ACT.Exp).then_inc(ex_ready[b], 1)
                    for b, i in lanes:
                        a.wait_ge(cwT_turned[b], 1)
                        a.sem_inc(cwT_turned[b], -1)
                        nc.scalar.copy(cwT[:, bass.ds(i * P, P)], M.bank[C[b]][0:E, 0:P])
                    copy_x(following)

                tiles_with_next(nc, ET.Activation, copy_x, body)
                a.drain()
                a.dma_start(dram_cw[:, :], cwT).then_inc(cw_stored, 16)
                a.wait_ge(cw_stored, 16)
                a.sem_inc(cw_stored, -16)

            @block.tensor
            def _(pe):
                def first(lanes):
                    for b, i in lanes:
                        pe.wait_ge(xn_ready[b], 1)
                        pe.sem_inc(xn_ready[b], -1)
                        pe_turn(nc, M, A[b], xn[b]).then_inc(turned_ready[b], 1)
                    for b, i in lanes:
                        pe.wait_ge(xT_ready[b], 1)
                        pe.sem_inc(xT_ready[b], -1)
                        pe_project(nc, M, B[b], xT[b], w, 0, E).then_inc(lg_ready[b], 1)

                def body(lanes, following):
                    for b, i in lanes:
                        pe.wait_ge(cw_ready[b], 1)
                        pe.sem_inc(cw_ready[b], -1)
                        nc.tensor.transpose(M.bank[C[b]][0:E, 0:P], cw[b][:, :], small(M, "ident")[:, 0:P]
                                            ).then_inc(cwT_turned[b], 1)
                    first(following)

                tiles_with_next(nc, ET.PE, first, body)


def split(engine, e, x, high, low):
    engine.tensor_copy(high, x)
    e.drain()
    return engine.tensor_tensor(low, x, high.bitcast(F32), SUB)


def pe_product(nc, out, w, x, start, stop):
    nc.tensor.matmul(out, w[0], x[1], start=start, stop=False)
    nc.tensor.matmul(out, w[1], x[0], start=False, stop=False)
    return nc.tensor.matmul(out, w[0], x[0], start=False, stop=stop)


def feed_forward0(nc, M):
    FC = F0 // 128
    AHEAD = 2
    NH = AHEAD + 1
    with ExitStack() as ctx:
        sb = lambda n, s, dt=F32: ctx.enter_context(nc.sbuf_tensor("e0_" + n, s, dt))
        sem = lambda n: M.sem(n + "0")
        halves = lambda n, s: tuple(sb(n + part, s, F32R) for part in ("_high", "_low"))
        WC = 2 * F0
        w = sb("w", [128, WC])
        ws = [halves(f"w{b}", [128, 2 * WC]) for b in range(2)]
        b1 = [sb(f"b1_{b}", [128, FC]) for b in range(2)]
        b2 = [sb(f"b2_{b}", [128, 2]) for b in range(2)]
        cw = [M.x_all[:, b * G * GE:(b + 1) * G * GE] for b in range(2)]
        hid = [M.w["w_tok"][:, b * GE:(b + 1) * GE] for b in range(NH)]
        yw = M.w["w_in"][:, 0:2 * GE].rearrange("p (c n) -> p c n", c=2)
        loaded, w_read, x_split = sem("loaded"), sem("e0_w_read"), sem("xn_ready")
        loaded_act = [sem(f"loaded_act_{b}") for b in range(2)]
        cw_loaded = [sem(f"cw_loaded_{b}") for b in range(2)]
        w_split = [sem(f"w_split_{b}") for b in range(2)]
        used, cw_used = [sem(f"e0_used_{b}") for b in range(2)], [sem(f"e0_cw_used_{b}") for b in range(2)]
        h1_ready, gelu_ready, hid_ready = sem("h1_ready"), sem("pm_ready"), sem("hid_ready")
        y_ready, y_read = sem("y_ready"), sem("e0_y_read")
        yg = M.yT_even[:, :, :].rearrange("p k (g n) -> p k g n", g=G)

        def load_weights(sp, e):
            for array in ("w1_0", "w2_0"):
                sp.wait_ge(w_read, 1)
                sp.sem_inc(w_read, -1)
                sp.dma_start(w[:, :], M.dram[array][bass.ds(e, 1)].rearrange("a p n -> (a p) n")).then_inc(loaded, 16)

        def split_weights(pool, b):
            for half in range(2):
                pool.wait_ge(loaded, 16)
                pool.sem_inc(loaded, -16)
                high, low = (t[:, half * WC:(half + 1) * WC] for t in ws[b])
                split(nc.gpsimd, pool, w[:, :], high, low).then_inc(w_read, 1)
            pool.drain().then_inc(w_split[b], 1)

        def first_weights(block):
            @block.sync
            def _(sp):
                load_weights(sp, 0)

            @block.gpsimd
            def _(pool):
                pool.sem_inc(w_read, 1)
                split_weights(pool, 0)

        gate_top2(nc, M, "g0_", M.w["gate0"], M.dram["cw0"], False, first_weights)
        xs = halves("x", [128, 2, G * GE])
        hs = [halves(f"hid{b}", [128, GE]) for b in range(NH)]
        with nc.Block(name="experts0") as block:
            @block.sync
            def _(sp):
                def load_rest(b, e):
                    sp.wait_ge(cw_used[b], 1)
                    sp.sem_inc(cw_used[b], -1)
                    sp.dma_start(b1[b][:, :],
                                 M.dram["b1_0"][bass.ds(e, 1)].rearrange("a p n -> (a p) n")).then_inc(loaded_act[b], 16)
                    sp.dma_start(b2[b][:, :],
                                 M.dram["b2_0"][bass.ds(e, 1)].rearrange("a p n -> (a p) n")).then_inc(cw_loaded[b], 16)
                    sp.dma_start(cw[b][:, 0:NTOK],
                                 M.dram["cw0"][bass.ds(e, 1), :].rearrange("a n -> (a n)").partition_broadcast(128)
                                 ).then_inc(cw_loaded[b], 16)

                load_rest(0, 0)
                load_weights(sp, 1)
                load_rest(1, 1)
                with nc.Fori(0, E0 // 2 - 1, engines=(ET.SP,)) as p:
                    for b in range(2):
                        load_weights(sp, p * 2 + (2 + b))
                        load_rest(b, p * 2 + (2 + b))

            @block.gpsimd
            def _(pool):
                pool.wait_ge(used[1], 1)
                pool.sem_inc(used[1], -1)
                split_weights(pool, 1)
                with nc.Fori(0, E0 // 2 - 1, engines=(ET.Pool,)) as p:
                    for b in range(2):
                        pool.wait_ge(used[b], 1)
                        pool.sem_inc(used[b], -1)
                        split_weights(pool, b)

            @block.tensor
            def _(pe):
                pe.sem_inc(used[1], 1)
                pe.wait_ge(x_split, 1)
                pe.sem_inc(x_split, -1)
                with nc.Fori(0, E0 // 2, engines=(ET.PE,)) as p:
                    for b in range(2):
                        pe.wait_ge(w_split[b], 1)
                        pe.sem_inc(w_split[b], -1)
                        w1 = [t[:, 0:WC].rearrange("p (k n) -> p k n", k=2) for t in ws[b]]
                        w2 = [t[:, WC:].rearrange("p (f n) -> p f n", f=FC) for t in ws[b]]
                        with nc.Fori(0, G, engines=(ET.PE,)) as g:
                            x = [t[:, :, bass.ds(g * GE, GE)] for t in xs]

                            def up(f):
                                for k in range(2):
                                    last = pe_product(nc, M.bank[f % NH][:, 0:GE], [t[:, k, f * 128:(f + 1) * 128] for t in w1],
                                                      [t[:, k, :] for t in x], k == 0, k == 1)
                                last.then_inc(h1_ready, 1)

                            for f in range(AHEAD):
                                up(f)
                            for f in range(FC):
                                if f + AHEAD < FC:
                                    up(f + AHEAD)
                                if f == 0:
                                    pe.wait_ge(y_read, 1)
                                    pe.sem_inc(y_read, -1)
                                pe.wait_ge(hid_ready, 1)
                                pe.sem_inc(hid_ready, -1)
                                for c in range(2):
                                    last = pe_product(nc, M.bank[NH + c][:, 0:GE], [t[:, f, c * 128:(c + 1) * 128] for t in w2],
                                                      [t[:, :] for t in hs[f % NH]], f == 0, f == FC - 1)
                            last.then_inc(y_ready, 1)
                        pe.drain().then_inc(used[b], 1)

            @block.scalar
            def _(a):
                a.preload_act_table(ACT.Gelu)
                with nc.Fori(0, E0 // 2, engines=(ET.Activation,)) as p:
                    for b in range(2):
                        a.wait_ge(loaded_act[b], 16)
                        a.sem_inc(loaded_act[b], -16)
                        with nc.Fori(0, G, engines=(ET.Activation,)) as g:
                            for f in range(FC):
                                a.wait_ge(h1_ready, 1)
                                a.sem_inc(h1_ready, -1)
                                nc.scalar.activation(hid[f % NH], M.bank[f % NH][:, 0:GE], ACT.Gelu,
                                                     bias=b1[b][:, f:f + 1]).then_inc(gelu_ready, 1)
                        a.drain()

            @block.vector
            def _(v):
                v.sem_inc(y_read, 1)
                for b in range(2):
                    v.sem_inc(cw_used[b], 1)
                nc.vector.memset(M.yT_even[:, :, NTOK:], 0.0)
                v.drain()
                for part in xs:
                    nc.vector.tensor_copy(part[:, :, NTOK:], M.yT_even[:, :, NTOK:])
                for b in range(2):
                    nc.vector.memset(cw[b][:, NTOK:], 0.0)
                split(nc.vector, v, M.xT[:, :, :], xs[0][:, :, 0:NTOK], xs[1][:, :, 0:NTOK]).then_inc(x_split, 1)
                nc.vector.memset(M.yT[:, :, :], 0.0)
                v.drain()
                with nc.Fori(0, E0 // 2, engines=(ET.DVE,)) as p:
                    for b in range(2):
                        v.wait_ge(cw_loaded[b], 32)
                        v.sem_inc(cw_loaded[b], -32)
                        with nc.Fori(0, G, engines=(ET.DVE,)) as g:
                            for f in range(FC):
                                v.wait_ge(gelu_ready, 1)
                                v.sem_inc(gelu_ready, -1)
                                split(nc.vector, v, hid[f % NH], hs[f % NH][0][:, :], hs[f % NH][1][:, :]
                                      ).then_inc(hid_ready, 1)
                            v.wait_ge(y_ready, 1)
                            v.sem_inc(y_ready, -1)
                            for c in range(2):
                                last = nc.vector.scalar_tensor_tensor(
                                    yw[:, c, :], M.bank[NH + c][:, 0:GE], b2[b][:, c:c + 1],
                                    cw[b][:, bass.ds(g * GE, GE)], ADD, MUL)
                            last.then_inc(y_read, 1)
                            v.drain()
                            y = yg[:, :, bass.ds(g, 1), :].rearrange("p k a n -> p k (a n)")
                            nc.vector.tensor_tensor(y, y, yw[:, :, :], ADD)
                            v.drain()
                        v.drain().then_inc(cw_used[b], 1)


def rotary_attention(nc, M):
    NH, DV = 8, 32
    with ExitStack() as ctx:
        one = lambda n, s: ctx.enter_context(nc.sbuf_tensor("a1_" + n, s, F32))
        sb = lambda n, s: [one(f"{n}{b}", s) for b in range(LANES)]
        sem = lambda n: [M.sem(f"{n}{b}") for b in range(LANES)]
        xn, xT, kT, xr = sb("xn", [P, D]), sb("xT", [128, 2, P]), sb("kT", [128, 2, P]), sb("xr", [128, 2, SEQS, P])
        qk, rot = sb("qk", [P, 2 * D]), sb("rot", [P, 2 * D])
        qm, km = sb("qm", [128, 2, SEQS * CW]), sb("km", [128, 2, 8, P])
        vm, S, Pr = sb("vm", [P, SEQS, D]), sb("S", [P, H16, L]), sb("Pr", [P, H16, L])
        probs, mx, rsum = sb("A", [P, NH, L]), sb("mx", [P, H16]), sb("rsum", [P, H16])
        pm, o, oT = sb("pm", [P, 3, SEQS * CW]), sb("o", [P, D]), sb("oT", [128, 2, P])
        ms, lamv, lam2, lam = one("ms", [P, T, NH]), one("lamv", [P, 32]), one("lam2", [P, 2]), one("lam", [P, 1])
        root = one("root", [P, T, NH])
        var_ready, std_ready, blank, pblank = M.sem("var_ready0"), M.sem("std_ready0"), M.sem("blank"), M.sem("pblank")
        lam_dot, lam_exp, ms_ready, root_ready = M.sem("lam_dot"), M.sem("lam_exp"), M.sem("ms_ready"), M.sem("root_ready")
        xn_ready, turned_ready, xT_ready, xr_ready = sem("xn_ready"), sem("turned"), sem("xT_ready"), sem("xr_ready")
        q_ready, o_read, v_ready, qk_rotated = sem("q_ready"), sem("k_ready"), sem("v_ready"), sem("qk_rotated")
        q_turned, k_turned, kT_ready, km_ready = sem("q_turned"), sem("k_turned"), sem("kT_ready"), sem("km_ready")
        qm_ready = sem("kv_ready")
        vm_ready, s_ready, shifted, probs_ready = sem("vm_ready"), sem("s_ready"), sem("shifted"), sem("probs_dve")
        mixed, pT_ready, pm_ready, o_ready = sem("mixed"), sem("pT_ready"), sem("pm_ready"), sem("o_ready")
        on_ready, oT_turned, oT_ready, y_ready = sem("on_ready"), sem("oT_turned"), sem("oT_ready"), sem("y_ready")
        wqk = M.w["qk1"].rearrange("p (k n) -> p k n", k=2)
        wv = M.w["v1"].rearrange("p (k n) -> p k n", k=2)
        wo = M.w["o1"].rearrange("p (k n) -> p k n", k=2)
        A, B, C, Dk = ([4 * b + j for b in range(LANES)] for j in range(4))
        with nc.Block(name="rotary_attention") as block:
            @block.gpsimd
            def _(pool):
                for b in range(LANES):
                    nc.gpsimd.memset(qm[b][:, :, :], 0.0).then_inc(blank, 1)
                    nc.gpsimd.memset(pm[b][:, :, :], 0.0).then_inc(pblank, 1)

            @block.vector
            def _(v):
                for b in range(LANES):
                    v.sem_inc(o_read[b], 1)
                dve_ln_stats(nc, v, M, var_ready, std_ready)
                lv = small(M, "lam").rearrange("p (i qk d) -> p i qk d", i=2, qk=2)
                nc.vector.tensor_tensor(lamv[:, :].rearrange("p (i d) -> p i d", i=2), lv[:, :, 0, :], lv[:, :, 1, :], MUL)
                nc.vector.tensor_scalar(small(M, "ln_w"), small(M, "ln_w"), 1.0 - LAMBDA_INIT, None, MUL)
                nc.vector.tensor_scalar(small(M, "ln_b"), small(M, "ln_b"), 1.0 - LAMBDA_INIT, None, MUL)
                v.drain()
                nc.vector.tensor_reduce(lam2[:, :], lamv[:, :].rearrange("p (i d) -> p i d", i=2), AX.X, ADD
                                        ).then_inc(lam_dot, 1)
                v.wait_ge(lam_exp, 1)
                v.sem_inc(lam_exp, -1)
                nc.vector.tensor_tensor(lam[:, :], lam2[:, 1:2], lam2[:, 0:1], SUB)
                v.drain()
                nc.vector.tensor_scalar(lam[:, :], lam[:, :], -LAMBDA_INIT, None, ADD)
                v.drain()
                cosv = spread(small(M, "cos"), 1, 2 * H16)
                sinv = small(M, "sin").rearrange("p (d e) -> p d e", e=2)

                def normalise(lanes):
                    for b, i in lanes:
                        ln_apply(nc, M, i, xn[b][:, :]).then_inc(xn_ready[b], 1)

                def scores(lanes, following):
                    for b, i in lanes:
                        v.wait_ge(q_ready[b], 1)
                        v.sem_inc(q_ready[b], -1)
                        q3 = M.bank[B[b]][0:P, :].rearrange("p (m d) -> p m d", d=DH)
                        nc.vector.tensor_tensor(qk[b][:, :].rearrange("p (m d) -> p m d", d=DH), q3, cosv, MUL)
                        q4 = M.bank[B[b]][0:P, :].rearrange("p (m d e) -> p m d e", d=DH // 2, e=2)
                        r4 = rot[b][:, :].rearrange("p (m d e) -> p m d e", d=DH // 2, e=2)
                        for e in range(2):
                            nc.vector.tensor_tensor(r4[:, :, :, e], q4[:, :, :, 1 - e], spread(sinv[:, :, e], 1, 2 * H16), MUL)
                        v.drain()
                        nc.vector.tensor_tensor(qk[b][:, :], qk[b][:, :], rot[b][:, :], ADD).then_inc(qk_rotated[b], 1)
                    for b, i in lanes:
                        v.wait_ge(v_ready[b], 1)
                        v.sem_inc(v_ready[b], -1)
                        mask_v(nc, M, (Dk[b], A[b]), vm[b], small(M, "vm8"), NH).then_inc(vm_ready[b], 1)
                    for b, i in lanes:
                        v.wait_ge(kT_ready[b], 1)
                        v.sem_inc(kT_ready[b], -1)
                        for c in range(2):
                            mask_k_heads(nc, M, kT[b], km[b], c).then_inc(km_ready[b], 1)
                    for b, i in lanes:
                        part = lambda bank: M.bank[bank][0:P, 0:8 * L].rearrange("p (m j) -> p m j", m=8)
                        for c, bank in enumerate((B[b], C[b])):
                            v.wait_ge(s_ready[b], 1)
                            v.sem_inc(s_ready[b], -1)
                            nc.vector.tensor_reduce(mx[b][:, 8 * c:8 * c + 8], part(bank), AX.X, MAX)
                        v.drain()
                        for c, bank in enumerate((B[b], C[b])):
                            last = nc.vector.tensor_tensor(S[b][:, 8 * c:8 * c + 8, :], part(bank),
                                                           spread(mx[b][:, 8 * c:8 * c + 8], 2, L), SUB)
                        last.then_inc(shifted[b], 1)
                    for b, i in lanes:
                        v.wait_ge(probs_ready[b], 1)
                        v.sem_inc(probs_ready[b], -1)
                        nc.vector.tensor_reduce(mx[b][:, :], Pr[b][:, :, :], AX.X, ADD)
                        v.drain()
                        nc.vector.reciprocal(rsum[b][:, :], mx[b][:, :])
                        v.drain()
                        pair = rsum[b][:, :].rearrange("p (h i) -> p h i", i=2)
                        nc.vector.tensor_scalar(pair[:, :, 1], pair[:, :, 1], lam[:, 0:1], None, MUL)
                        v.drain()
                        nc.vector.tensor_tensor(S[b][:, :, :], Pr[b][:, :, :], spread(rsum[b][:, :], 2, L), MUL)
                        v.drain()
                        p2 = S[b][:, :, :].rearrange("p (h i) j -> p h i j", i=2)
                        nc.vector.tensor_tensor(probs[b][:, :, :], p2[:, :, 0, :], p2[:, :, 1, :], ADD
                                                ).then_inc(mixed[b], 1)
                    normalise(following)
                    for b, i in lanes:
                        v.wait_ge(o_ready[b], 1)
                        v.sem_inc(o_ready[b], -1)
                        nc.vector.tensor_copy(tile(M.x, i), M.bank[B[b]][0:P, 0:D]).then_inc(o_read[b], 1)
                    v.drain()
                    for b, i in lanes:
                        nc.vector.tensor_tensor(o[b][:, :], tile(M.x, i), tile(M.x, i), MUL)
                    v.drain()
                    for b, i in lanes:
                        nc.vector.tensor_reduce(tile(ms, i), o[b][:, :].rearrange("p (h d) -> p h d", h=NH), AX.X, ADD)
                    v.drain()

                def project(lanes):
                    for b, i in lanes:
                        o3 = o[b][:, :].rearrange("p (h d) -> p h d", h=NH)
                        nc.vector.tensor_tensor(o3, tile(M.x, i).rearrange("p (h d) -> p h d", h=NH),
                                                spread(tile(ms, i), 2, DV), MUL)
                        v.drain()
                        nc.vector.tensor_tensor(o3, o3, spread(small(M, "ln_w"), 1, NH), MUL)
                        v.drain()
                        nc.vector.tensor_tensor(o3, o3, spread(small(M, "ln_b"), 1, NH), ADD).then_inc(on_ready[b], 1)
                    for b, i in lanes:
                        v.wait_ge(y_ready[b], 1)
                        v.sem_inc(y_ready[b], -1)
                        nc.vector.tensor_tensor(tile(M.h, i), tile(M.h, i), M.bank[Dk[b]][0:P, 0:D], ADD)
                    v.drain()
                    dve_tile_stats(nc, M, lanes)

                tiles_with_next(nc, ET.DVE, normalise, scores)
                nc.vector.tensor_scalar(ms[:, :, :], ms[:, :, :], 1.0 / DV, 1e-8, MUL, ADD).then_inc(ms_ready, 1)
                v.wait_ge(root_ready, 1)
                v.sem_inc(root_ready, -1)
                nc.vector.reciprocal(ms[:, :, :], root[:, :, :])
                v.drain()
                tiles_by_lanes(nc, ET.DVE, project)

            @block.scalar
            def _(a):
                act_ln_std(nc, a, M, var_ready, std_ready)
                a.preload_act_table(ACT.Exp)
                a.wait_ge(lam_dot, 1)
                a.sem_inc(lam_dot, -1)
                nc.scalar.activation(lam2[:, :], lam2[:, :], ACT.Exp).then_inc(lam_exp, 1)
                a.wait_ge(pblank, LANES)
                a.sem_inc(pblank, -LANES)
                a.wait_ge(blank, LANES)
                a.sem_inc(blank, -LANES)

                def copy_x(lanes):
                    for b, i in lanes:
                        a.wait_ge(turned_ready[b], 1)
                        a.sem_inc(turned_ready[b], -1)
                        nc.scalar.copy(xT[b][:, :, :], turned(M, A[b])).then_inc(xT_ready[b], 1)
                    for b, i in lanes:
                        repeat_x(nc, M, A[b], xr[b]).then_inc(xr_ready[b], 1)

                def scores(lanes, following):
                    for b, i in lanes:
                        a.wait_ge(k_turned[b], 1)
                        a.sem_inc(k_turned[b], -1)
                        nc.scalar.copy(kT[b][:, :, :], turned(M, C[b])).then_inc(kT_ready[b], 1)
                        a.wait_ge(q_turned[b], 1)
                        a.sem_inc(q_turned[b], -1)
                        evacuate_q(nc, M, B[b], qm[b]).then_inc(qm_ready[b], 1)
                    for b, i in lanes:
                        a.wait_ge(shifted[b], 1)
                        a.sem_inc(shifted[b], -1)
                        nc.scalar.activation(Pr[b][:, :, :], S[b][:, :, :], ACT.Exp, scale=DH ** -0.25).then_inc(probs_ready[b], 1)
                    for b, i in lanes:
                        a.wait_ge(pT_ready[b], 1)
                        a.sem_inc(pT_ready[b], -1)
                        evacuate_probs(nc, M, (Dk[b], A[b]), pm[b], NH).then_inc(pm_ready[b], 1)
                    copy_x(following)
                    a.drain()

                def project(lanes):
                    for b, i in lanes:
                        a.wait_ge(oT_turned[b], 1)
                        a.sem_inc(oT_turned[b], -1)
                        nc.scalar.copy(oT[b][:, :, :], turned(M, C[b])).then_inc(oT_ready[b], 1)
                    a.drain()

                tiles_with_next(nc, ET.Activation, copy_x, scores)
                a.wait_ge(ms_ready, 1)
                a.sem_inc(ms_ready, -1)
                nc.scalar.activation(root[:, :, :], ms[:, :, :], ACT.Sqrt).then_inc(root_ready, 1)
                tiles_by_lanes(nc, ET.Activation, project)

            @block.tensor
            def _(pe):
                def turn_x(lanes):
                    for b, i in lanes:
                        pe.wait_ge(xn_ready[b], 1)
                        pe.sem_inc(xn_ready[b], -1)
                        pe_turn(nc, M, A[b], xn[b]).then_inc(turned_ready[b], 1)

                def project_qk(lanes):
                    for b, i in lanes:
                        pe.wait_ge(o_read[b], 1)
                        pe.sem_inc(o_read[b], -1)
                        pe.wait_ge(xT_ready[b], 1)
                        pe.sem_inc(xT_ready[b], -1)
                        pe_project(nc, M, B[b], xT[b], wqk, 0, 2 * D).then_inc(q_ready[b], 1)

                def first(lanes):
                    turn_x(lanes)
                    project_qk(lanes)

                def scores(lanes, following):
                    for b, i in lanes:
                        pe.wait_ge(xr_ready[b], 1)
                        pe.sem_inc(xr_ready[b], -1)
                        pe_values_in(nc, M, (Dk[b], A[b]), xr[b], wv, 0).then_inc(v_ready[b], 1)
                    for b, i in lanes:
                        pe.wait_ge(qk_rotated[b], 1)
                        pe.sem_inc(qk_rotated[b], -1)
                        pe_turn(nc, M, B[b], qk[b]).then_inc(q_turned[b], 1)
                        pe_turn(nc, M, C[b], qk[b][:, D:2 * D]).then_inc(k_turned[b], 1)
                    for b, i in lanes:
                        pe.wait_ge(qm_ready[b], 1)
                        pe.sem_inc(qm_ready[b], -1)
                        for c, bank in enumerate((B[b], C[b])):
                            pe.wait_ge(km_ready[b], 1)
                            pe.sem_inc(km_ready[b], -1)
                            pe_scores(nc, M, bank, qm[b], km[b], c).then_inc(s_ready[b], 1)
                    for b, i in lanes:
                        pe.wait_ge(mixed[b], 1)
                        pe.sem_inc(mixed[b], -1)
                        pe.wait_ge(vm_ready[b], 1)
                        pe.sem_inc(vm_ready[b], -1)
                        pe_turn_probs(nc, M, (Dk[b], A[b]), probs[b][:, :, :].rearrange("p h j -> p (h j)"), NH
                                      ).then_inc(pT_ready[b], 1)
                    for b, i in lanes:
                        pe.wait_ge(pm_ready[b], 1)
                        pe.sem_inc(pm_ready[b], -1)
                        pe_values(nc, M, B[b], pm[b], vm[b], NH, DV).then_inc(o_ready[b], 1)
                    turn_x(following)
                    project_qk(following)

                def project(lanes):
                    for b, i in lanes:
                        pe.wait_ge(on_ready[b], 1)
                        pe.sem_inc(on_ready[b], -1)
                        pe_turn(nc, M, C[b], o[b]).then_inc(oT_turned[b], 1)
                    for b, i in lanes:
                        pe.wait_ge(oT_ready[b], 1)
                        pe.sem_inc(oT_ready[b], -1)
                        pe_project(nc, M, Dk[b], oT[b], wo, 0, D).then_inc(y_ready[b], 1)

                pe.wait_ge(M.loaded["l1a"], 16)
                tiles_with_next(nc, ET.PE, first, scores)
                for b in range(LANES):
                    pe.wait_ge(o_read[b], 1)
                    pe.sem_inc(o_read[b], -1)
                tiles_by_lanes(nc, ET.PE, project)


def coupling(nc, M):
    CYCLES = 3
    NS = T * SEQS
    with ExitStack() as ctx:
        sb = lambda n, s: ctx.enter_context(nc.sbuf_tensor("cp_" + n, s, F32))
        sem = lambda n: M.sem(n + "0")
        by_lane = lambda n: [M.sem(f"{n}{b}") for b in range(LANES)]
        xn = [sb(f"xn{b}", [P, D]) for b in range(LANES)]
        var_ready, std_ready, xn_ready = sem("var_ready"), sem("std_ready"), by_lane("xn_ready")
        turned_ready, turned_read = by_lane("turned"), by_lane("xT_ready")
        mean, g1, g2, gf = sb("mean", [128, 2, NS]), sb("g1", [128, NS]), sb("g2", [64, NS]), sb("gf", [128, NS])
        h1, h2, h3 = sb("h1", [128, 2, G, GC]), sb("h2", [128, G, GC]), sb("h3", [64, G, GC])
        tf, m0 = sb("tf", [128, G, GC]), sb("m0", [128, 2, GC])
        r2, r2s, base = sb("r2", [128, 1]), sb("r2s", [128, 1]), sb("base", [128, 1])
        mean_ready, ps_ready, act_done = sem("mean_ready"), sem("ps_ready"), sem("act_done")
        gf_ready, tf_ready, x_moved = sem("gf_ready"), sem("tf_ready"), sem("x_moved")
        cn1, cn2 = (M.w[n].rearrange("p (k n) -> p k n", k=2) for n in ("cn1", "cn2"))
        gc1 = M.w["gc1"].rearrange("p (k n) -> p k n", k=2)
        cn3, cn4, gc2, gc3 = M.w["cn3"], M.w["cn4"][0:64, :], M.w["gc2"], M.w["gc3"][0:64, :]
        with nc.Block(name="coupling_norm") as block:
            @block.vector
            def _(v):
                dve_ln_stats(nc, v, M, var_ready, std_ready)

                def body(lanes):
                    for b, i in lanes:
                        ln_apply(nc, M, i, xn[b][:, :]).then_inc(xn_ready[b], 1)
                    for b, i in lanes:
                        v.wait_ge(turned_read[b], 1)
                        v.sem_inc(turned_read[b], -1)

                tiles_by_lanes(nc, ET.DVE, body)

            @block.scalar
            def _(a):
                act_ln_std(nc, a, M, var_ready, std_ready)

                def body(lanes):
                    for b, i in lanes:
                        a.wait_ge(turned_ready[b], 1)
                        a.sem_inc(turned_ready[b], -1)
                        nc.scalar.copy(cols(M.xT, i), turned(M, 4 * b)).then_inc(turned_read[b], 1)

                tiles_by_lanes(nc, ET.Activation, body)

            @block.tensor
            def _(pe):
                def body(lanes):
                    for b, i in lanes:
                        pe.wait_ge(xn_ready[b], 1)
                        pe.sem_inc(xn_ready[b], -1)
                        pe_turn(nc, M, 4 * b, xn[b]).then_inc(turned_ready[b], 1)

                tiles_by_lanes(nc, ET.PE, body)

        with nc.Block(name="coupling_cycles") as block:
            @block.vector
            def _(v):
                nc.vector.tensor_reduce(mean[:, :, :], M.xT[:, :, :].rearrange("p k (s j) -> p k s j", j=L), AX.X, ADD)
                v.drain()
                nc.vector.tensor_scalar(mean[:, :, :], mean[:, :, :], 1.0 / L, None, MUL).then_inc(mean_ready, 1)
                nc.vector.tensor_scalar(r2[:, :], small(M, "range", 128), 2.0, None, MUL)
                nc.vector.tensor_scalar(base[:, :], small(M, "sgn", 128), 0.1, None, MUL)
                v.drain()
                nc.vector.tensor_tensor(r2s[:, :], r2[:, :], small(M, "sgn", 128), MUL)
                v.wait_ge(gf_ready, 1)
                v.sem_inc(gf_ready, -1)
                nc.vector.tensor_scalar(gf[:, :], gf[:, :], 0.7, -0.5, MUL, ADD)
                v.drain()
                v.sem_inc(x_moved, G)
                with nc.Fori(0, CYCLES, engines=(ET.DVE,)) as cycle:
                    for g in range(G):
                        v.wait_ge(tf_ready, 1)
                        v.sem_inc(tf_ready, -1)
                        t = tf[:, g, :]
                        nc.vector.scalar_tensor_tensor(t.rearrange("p (s j) -> p s j", j=L),
                                                       t.rearrange("p (s j) -> p s j", j=L), 0.3,
                                                       spread(gf[:, g * GS:(g + 1) * GS], 2, L), MUL, ADD)
                        v.drain()
                        nc.vector.tensor_scalar(t, t, r2s[:, 0:1], base[:, 0:1], MUL, ADD)
                        v.drain()
                        x = M.xT[:, :, g * GC:(g + 1) * GC]
                        for c in range(2):
                            nc.vector.tensor_tensor(m0[:, c, :], x[:, 1 - c, :], t, MUL)
                        v.drain()
                        nc.vector.tensor_tensor(x[:, 0, :], x[:, 0, :], m0[:, 0, :], ADD)
                        nc.vector.tensor_tensor(x[:, 1, :], x[:, 1, :], m0[:, 1, :], SUB).then_inc(x_moved, 1)
                        v.drain()
                nc.vector.tensor_copy(M.yT[:, :, :], M.xT[:, :, :])
                v.drain()

            @block.scalar
            def _(a):
                a.preload_act_table(ACT.Gelu)

                def net(out, bank, parts, n, bias, func, done):
                    a.wait_ge(ps_ready, 1)
                    a.sem_inc(ps_ready, -1)
                    nc.scalar.activation(out, M.bank[bank][0:parts, 0:n], func, bias=bias).then_inc(done, 1)

                net(g1[:, :], 0, 128, NS, small(M, "gc_b1", 128), ACT.Gelu, act_done)
                net(g2[:, :], 1, 64, NS, small(M, "gc_b2", 64), ACT.Gelu, act_done)
                net(gf[:, :], 6, 128, NS, small(M, "gc_b3", 128), ACT.Sigmoid, gf_ready)
                a.drain()
                with nc.Fori(0, CYCLES, engines=(ET.Activation,)) as cycle:
                    for g in range(G):
                        for m in range(2):
                            net(h1[:, m, g, :], 2 * g + m, 128, GC, small(M, "cn_b1", 128)[:, m:m + 1], ACT.Gelu, act_done)
                    for g in range(G):
                        net(h2[:, g, :], g, 128, GC, small(M, "cn_b2", 128), ACT.Gelu, act_done)
                    for g in range(G):
                        net(h3[:, g, :], 3 + g, 64, GC, small(M, "cn_b3", 64), ACT.Gelu, act_done)
                    for g in range(G):
                        net(tf[:, g, :], 3 + g, 128, GC, small(M, "cn_b4", 128), ACT.Sigmoid, tf_ready)
                    a.drain()

            @block.tensor
            def _(pe):
                pe.wait_ge(M.loaded["l1f"], 16)
                pe.wait_ge(mean_ready, 1)
                pe.sem_inc(mean_ready, -1)
                for k in range(2):
                    last = nc.tensor.matmul(M.bank[0][:, 0:NS], gc1[:, k, :], mean[:, k, :], start=(k == 0), stop=(k == 1))
                last.then_inc(ps_ready, 1)
                pe.wait_ge(act_done, 1)
                pe.sem_inc(act_done, -1)
                nc.tensor.matmul(M.bank[1][0:64, 0:NS], gc2, g1[:, :], start=True, stop=True).then_inc(ps_ready, 1)
                pe.wait_ge(act_done, 1)
                pe.sem_inc(act_done, -1)
                nc.tensor.matmul(M.bank[6][:, 0:NS], gc3, g2[:, :], start=True, stop=True).then_inc(ps_ready, 1)
                with nc.Fori(0, CYCLES, engines=(ET.PE,)) as cycle:
                    for g in range(G):
                        pe.wait_ge(x_moved, 1)
                        pe.sem_inc(x_moved, -1)
                        for m in range(2):
                            for k in range(2):
                                last = nc.tensor.matmul(M.bank[2 * g + m][:, 0:GC], cn1[:, k, m * 128:(m + 1) * 128],
                                                        M.xT[:, k, g * GC:(g + 1) * GC], start=(k == 0), stop=(k == 1))
                            last.then_inc(ps_ready, 1)
                    for g in range(G):
                        pe.wait_ge(act_done, 2)
                        pe.sem_inc(act_done, -2)
                    for g in range(G):
                        for k in range(2):
                            last = nc.tensor.matmul(M.bank[g][:, 0:GC], cn2[:, k, :], h1[:, k, g, :], start=(k == 0), stop=(k == 1))
                        last.then_inc(ps_ready, 1)
                    for g in range(G):
                        pe.wait_ge(act_done, 1)
                        pe.sem_inc(act_done, -1)
                        nc.tensor.matmul(M.bank[3 + g][0:64, 0:GC], cn3, h2[:, g, :], start=True, stop=True).then_inc(ps_ready, 1)
                    for g in range(G):
                        pe.wait_ge(act_done, 1)
                        pe.sem_inc(act_done, -1)
                        nc.tensor.matmul(M.bank[3 + g][:, 0:GC], cn4, h3[:, g, :], start=True, stop=True).then_inc(ps_ready, 1)
                pe.wait_ge(x_moved, G)
                pe.sem_inc(x_moved, -G)
    add_back(nc, M, "_l1")


def linear_attention(nc, M):
    with ExitStack() as ctx:
        sb = lambda n, s: [ctx.enter_context(nc.sbuf_tensor(f"a2_{n}{b}", s, F32)) for b in range(LANES)]
        sem = lambda n: [M.sem(f"{n}{b}") for b in range(LANES)]
        xn, xT, qT = sb("xn", [P, D]), sb("xT", [128, 2, P]), sb("qT", [128, 2, P])
        qkv, sq, ss = sb("qkv", [P, 3 * D]), sb("sq", [P, 2 * D]), sb("ss", [P, 2 * H16])
        root, vb, kv = sb("root", [P, 2 * H16]), sb("vb", [P, SEQS, D]), sb("kv", [128, 2, SEQS, 128])
        oT, y = sb("oT", [128, 2, P]), sb("y", [P, D])
        var_ready, std_ready = M.sem("var_ready0"), M.sem("std_ready0")
        xn_ready, turned_ready, xT_ready, qkv_ready = sem("xn_ready"), sem("turned"), sem("xT_ready"), sem("q_ready")
        ss_ready, root_ready, qkn_ready, qT_turned = sem("k_ready"), sem("kroot_ready"), sem("kn_ready"), sem("q_turned")
        qT_ready, kv_ready, kvm_ready, oT_made = sem("kT_ready"), sem("kv_ready"), sem("km_ready"), sem("oT_turned")
        oT_copied, y_ready = sem("oT_ready"), sem("y_ready")
        w = M.w["qkv2"].rearrange("p (k n) -> p k n", k=2)
        wo = M.w["proj2"].rearrange("p (k n) -> p k n", k=2)
        A, B, C, Dk = ([4 * b + j for b in range(LANES)] for j in range(4))
        with nc.Block(name="linear_attention") as block:
            @block.vector
            def _(v):
                dve_ln_stats(nc, v, M, var_ready, std_ready)

                def normalise(lanes):
                    for b, i in lanes:
                        ln_apply(nc, M, i, xn[b][:, :]).then_inc(xn_ready[b], 1)

                def body(lanes, following):
                    for b, i in lanes:
                        v.wait_ge(qkv_ready[b], 1)
                        v.sem_inc(qkv_ready[b], -1)
                        nc.vector.tensor_tensor(qkv[b][:, 0:2 * D], M.bank[B[b]][0:P, :], small(M, "qkv_b")[:, 0:2 * D], ADD)
                        nc.vector.tensor_tensor(qkv[b][:, 2 * D:3 * D], M.bank[C[b]][0:P, 0:D],
                                                small(M, "qkv_b")[:, 2 * D:3 * D], ADD)
                        v.drain()
                        nc.vector.tensor_tensor(sq[b][:, :], qkv[b][:, 0:2 * D], qkv[b][:, 0:2 * D], MUL)
                        v.drain()
                        nc.vector.tensor_reduce(ss[b][:, :], sq[b][:, :].rearrange("p (m d) -> p m d", d=DH), AX.X, ADD)
                        v.drain()
                        nc.vector.tensor_scalar(ss[b][:, :], ss[b][:, :], 1e-24, None, MAX).then_inc(ss_ready[b], 1)
                        nc.vector.tensor_tensor(vb[b][:, :, :], spread(qkv[b][:, 2 * D:3 * D], 1, SEQS),
                                                spread(small(M, "mb"), 2, D), MUL)
                    for b, i in lanes:
                        v.wait_ge(root_ready[b], 1)
                        v.sem_inc(root_ready[b], -1)
                        nc.vector.reciprocal(ss[b][:, :], root[b][:, :])
                        v.drain()
                        qk3 = qkv[b][:, 0:2 * D].rearrange("p (m d) -> p m d", d=DH)
                        nc.vector.tensor_tensor(qk3, qk3, spread(ss[b][:, :], 2, DH), MUL).then_inc(qkn_ready[b], 1)
                    normalise(following)
                    for b, i in lanes:
                        v.wait_ge(kv_ready[b], 1)
                        v.sem_inc(kv_ready[b], -1)
                        for c, bank in enumerate((Dk[b], A[b])):
                            last = nc.vector.tensor_tensor(kv[b][:, c, :, :],
                                                           M.bank[bank][:, 0:SEQS * 128].rearrange("p (s n) -> p s n", s=SEQS),
                                                           spread(small(M, "blk", 128), 1, SEQS), MUL)
                        last.then_inc(kvm_ready[b], 1)
                    for b, i in lanes:
                        v.wait_ge(y_ready[b], 1)
                        v.sem_inc(y_ready[b], -1)
                        nc.vector.tensor_tensor(y[b][:, :], M.bank[Dk[b]][0:P, 0:D], small(M, "proj_b"), ADD)
                        v.drain()
                        nc.vector.tensor_tensor(tile(M.h, i), tile(M.h, i), y[b][:, :], ADD)
                    v.drain()
                    dve_tile_stats(nc, M, lanes)

                tiles_with_next(nc, ET.DVE, normalise, body)

            @block.scalar
            def _(a):
                act_ln_std(nc, a, M, var_ready, std_ready)

                def copy_x(lanes):
                    for b, i in lanes:
                        a.wait_ge(turned_ready[b], 1)
                        a.sem_inc(turned_ready[b], -1)
                        nc.scalar.copy(xT[b][:, :, :], turned(M, A[b])).then_inc(xT_ready[b], 1)

                def body(lanes, following):
                    for b, i in lanes:
                        a.wait_ge(ss_ready[b], 1)
                        a.sem_inc(ss_ready[b], -1)
                        nc.scalar.activation(root[b][:, :], ss[b][:, :], ACT.Sqrt).then_inc(root_ready[b], 1)
                    for b, i in lanes:
                        a.wait_ge(qT_turned[b], 1)
                        a.sem_inc(qT_turned[b], -1)
                        nc.scalar.copy(qT[b][:, :, :], turned(M, B[b])).then_inc(qT_ready[b], 1)
                    for b, i in lanes:
                        a.wait_ge(oT_made[b], 1)
                        a.sem_inc(oT_made[b], -1)
                        nc.scalar.copy(oT[b][:, :, :], turned(M, C[b])).then_inc(oT_copied[b], 1)
                    copy_x(following)

                tiles_with_next(nc, ET.Activation, copy_x, body)

            @block.tensor
            def _(pe):
                def turn_x(lanes):
                    for b, i in lanes:
                        pe.wait_ge(xn_ready[b], 1)
                        pe.sem_inc(xn_ready[b], -1)
                        pe_turn(nc, M, A[b], xn[b]).then_inc(turned_ready[b], 1)

                def project_qkv(lanes):
                    for b, i in lanes:
                        pe.wait_ge(xT_ready[b], 1)
                        pe.sem_inc(xT_ready[b], -1)
                        pe_project(nc, M, B[b], xT[b], w, 0, 2 * D)
                        pe_project(nc, M, C[b], xT[b], w, 2 * D, 3 * D).then_inc(qkv_ready[b], 1)

                def first(lanes):
                    turn_x(lanes)
                    project_qkv(lanes)

                def body(lanes, following):
                    for b, i in lanes:
                        pe.wait_ge(qkn_ready[b], 1)
                        pe.sem_inc(qkn_ready[b], -1)
                        pe_turn(nc, M, B[b], qkv[b][:, 0:D]).then_inc(qT_turned[b], 1)
                        for c, bank in enumerate((Dk[b], A[b])):
                            last = nc.tensor.matmul(M.bank[bank][:, 0:SEQS * 128], qkv[b][:, D + c * 128:D + (c + 1) * 128],
                                                    vb[b][:, :, c * 128:(c + 1) * 128], start=True, stop=True)
                        last.then_inc(kv_ready[b], 1)
                    for b, i in lanes:
                        pe.wait_ge(kvm_ready[b], 1)
                        pe.sem_inc(kvm_ready[b], -1)
                        pe.wait_ge(qT_ready[b], 1)
                        pe.sem_inc(qT_ready[b], -1)
                        for c in range(2):
                            for s in range(SEQS):
                                last = nc.tensor.matmul(M.bank[C[b]][:, c * P + s * L:c * P + (s + 1) * L], kv[b][:, c, s, :],
                                                        qT[b][:, c, s * L:(s + 1) * L], start=True, stop=True)
                        last.then_inc(oT_made[b], 1)
                    turn_x(following)
                    for b, i in lanes:
                        pe.wait_ge(oT_copied[b], 1)
                        pe.sem_inc(oT_copied[b], -1)
                        pe_project(nc, M, Dk[b], oT[b], wo, 0, D).then_inc(y_ready[b], 1)
                    project_qkv(following)

                pe.wait_ge(M.loaded["l2a"], 16)
                tiles_with_next(nc, ET.PE, first, body)


def experts2(nc, M):
    with ExitStack() as ctx:
        sb = lambda n, s: ctx.enter_context(nc.sbuf_tensor("e2_" + n, s, F32))
        sem = lambda n: M.sem(n + "0")
        cw = sb("cw", [128, E2, NTOK])
        ga = [sb(f"ga_{b}", [128, GC]) for b in range(2)]
        gb = [sb(f"gb_{b}", [128, GC]) for b in range(2)]
        sg = [sb(f"sg_{b}", [128, GC]) for b in range(2)]
        hid = [sb(f"hid_{b}", [128, GC]) for b in range(2)]
        cw_loaded, ab_ready, a_scaled, sg_ready = sem("cw_loaded"), sem("ab_ready"), sem("a_scaled"), sem("sg_ready")
        cw_here = sem("cw_here")
        ab_read, hid_ready, y_ready, y_read = sem("ab_read"), sem("hid_ready"), sem("y_ready"), sem("y_read")
        w1 = M.w["w1_2"].rearrange("p (e k n) -> p e k n", e=E2, k=2)
        w3 = M.w["w3_2"].rearrange("p (e k n) -> p e k n", e=E2, k=2)
        w2 = M.w["w2_2"].rearrange("p (e n) -> p e n", e=E2)
        xg = M.xT[:, :, :].rearrange("p k (g n) -> p k g n", g=G)
        yg = M.yT[:, :, :].rearrange("p k (g n) -> p k g n", g=G)
        with nc.Block(name="experts2") as block:
            @block.sync
            def _(sp):
                with nc.Fori(0, G, engines=(ET.SP,)) as g:
                    for e in range(E2):
                        sp.dma_start(cw[:, e, bass.ds(g * GC, GC)],
                                     M.dram["cw2"][e, bass.ds(g * GC, GC)].partition_broadcast(128)).then_inc(cw_loaded, 16)
                    sp.wait_ge(cw_loaded, 16 * E2)
                    sp.sem_inc(cw_loaded, -(16 * E2))
                    sp.sem_inc(cw_here, 1)

            @block.tensor
            def _(pe):
                pe.wait_ge(M.loaded["l2f"], 16)
                with nc.Fori(0, G, engines=(ET.PE,)) as g:
                    x = xg[:, :, bass.ds(g, 1), :].rearrange("p k a n -> p k (a n)")

                    def up(e):
                        if e >= 2:
                            pe.wait_ge(ab_read, 1)
                            pe.sem_inc(ab_read, -1)
                        for j, w in enumerate((w1, w3)):
                            for k in range(2):
                                last = nc.tensor.matmul(M.bank[2 * (e % 2) + j][:, 0:GC], w[:, e, k, :], x[:, k, :],
                                                        start=(k == 0), stop=(k == 1))
                        last.then_inc(ab_ready, 1)

                    up(0)
                    for e in range(E2):
                        if e + 1 < E2:
                            up(e + 1)
                        pe.wait_ge(hid_ready, 1)
                        pe.sem_inc(hid_ready, -1)
                        for c in range(2):
                            last = nc.tensor.matmul(M.bank[4 + c][:, 0:GC], w2[:, e, c * 128:(c + 1) * 128], hid[e % 2][:, :],
                                                    start=(e == 0), stop=(e == E2 - 1))
                    last.then_inc(y_ready, 1)
                    pe.wait_ge(ab_read, 2)
                    pe.sem_inc(ab_read, -2)
                    pe.wait_ge(y_read, 1)
                    pe.sem_inc(y_read, -1)

            @block.scalar
            def _(a):
                a.preload_act_table(ACT.Sigmoid)
                with nc.Fori(0, G, engines=(ET.Activation,)) as g:
                    for e in range(E2):
                        a.wait_ge(a_scaled, 1)
                        a.sem_inc(a_scaled, -1)
                        nc.scalar.activation(sg[e % 2][:, :], ga[e % 2][:, :], ACT.Sigmoid).then_inc(sg_ready, 1)
                    a.drain()

            @block.vector
            def _(v):
                with nc.Fori(0, G, engines=(ET.DVE,)) as g:
                    v.wait_ge(cw_here, 1)
                    v.sem_inc(cw_here, -1)

                    def scale(e):
                        b = e % 2
                        s = cw[:, e, bass.ds(g * GC, GC)]
                        v.wait_ge(ab_ready, 1)
                        v.sem_inc(ab_ready, -1)
                        nc.vector.tensor_tensor(ga[b][:, :], M.bank[2 * b][:, 0:GC], s, MUL).then_inc(a_scaled, 1)
                        nc.vector.tensor_tensor(gb[b][:, :], M.bank[2 * b + 1][:, 0:GC], s, MUL).then_inc(ab_read, 1)

                    for e in range(E2):
                        b = e % 2
                        scale(e)
                        v.drain()
                        nc.vector.tensor_tensor(gb[b][:, :], ga[b][:, :], gb[b][:, :], MUL)
                        v.wait_ge(sg_ready, 1)
                        v.sem_inc(sg_ready, -1)
                        v.drain()
                        nc.vector.tensor_tensor(hid[b][:, :], gb[b][:, :], sg[b][:, :], MUL).then_inc(hid_ready, 1)
                    v.drain()
                    v.wait_ge(y_ready, 1)
                    v.sem_inc(y_ready, -1)
                    for c in range(2):
                        last = nc.vector.tensor_copy(yg[:, c, bass.ds(g, 1), :].rearrange("p a n -> p (a n)"), M.bank[4 + c][:, 0:GC])
                    last.then_inc(y_read, 1)
                    v.drain()
    add_back(nc, M, "_l2")


def delta_attention(nc, M):
    with ExitStack() as ctx:
        one = lambda n, s: ctx.enter_context(nc.sbuf_tensor("a3_" + n, s, F32))
        sb = lambda n, s: [one(f"{n}{b}", s) for b in range(LANES)]
        sem = lambda n: [M.sem(f"{n}{b}") for b in range(LANES)]
        ss, z, zw, beta = one("ss", [P, T]), one("z", [P, T]), one("zw", [P, D]), one("beta", [P, T])
        rr, root = one("rr", [P, T]), one("root", [P, T])
        alpha, keep, decay = one("alpha", [128, 2]), one("keep", [128, 2]), one("decay", [128, 2, P])
        xn, xT, qkT = sb("xn", [P, D]), sb("xT", [128, 2, P]), sb("qkT", [128, 4, P])
        qk, sq, k1, kroot = sb("qk", [P, 2 * D]), sb("sq", [P, D]), sb("k1", [P, 1]), sb("kroot", [P, 1])
        av, ema, bv = sb("av", [128, 2, P]), sb("ema", [128, 2, P]), sb("bv", [P, D])
        low, Cl, ClT = sb("C", [P, P]), sb("Cl", [P, LEVELS, P]), sb("ClT", [P, LEVELS, P])
        XY, CX, mt = sb("XY", [P, 2, P]), sb("CX", [P, 2, P]), sb("mt", [P, P])
        U, oT = sb("U", [P, D]), sb("oT", [128, 2, P])
        hid, sg = sb("hid", [128, 4, P]), sb("sg", [128, 4, P])
        var_ready, std_ready, w_folded = M.sem("var_ready0"), M.sem("std_ready0"), M.sem("w_folded")
        ss_ready, root_ready, z_ready = M.sem("ms_ready"), M.sem("root_ready"), M.sem("z_ready")
        beta_ready, ss2_ready, root2_ready = M.sem("beta_ready"), M.sem("ss2_ready"), M.sem("root2_ready")
        xn_ready, turned_ready, xT_ready, qk_ready = sem("xn_ready"), sem("turned"), sem("xT_ready"), sem("q_ready")
        v_ready, k_ready, kroot_ready, kn_ready = sem("v_ready"), sem("k_ready"), sem("kroot_ready"), sem("kn_ready")
        qk_turned, qkT_ready, ema_ready, bv_turned = sem("q_turned"), sem("kT_ready"), sem("xr_ready"), sem("k_turned")
        G_ready, C_ready, CT_ready, X_ready = sem("s_ready"), sem("shifted"), sem("pT_ready"), sem("probs_dve")
        CX_ready, CX_copied, XCX_ready = sem("vm_ready"), sem("pm_ready"), sem("probs_pe")
        U_ready, U_copied, oT_made, oT_copied = sem("o_ready"), sem("on_ready"), sem("oT_turned"), sem("oT_ready")
        y_ready, gu_ready, sg_ready, hid_ready = sem("y_ready"), sem("gu_ready"), sem("sg_ready"), sem("hid_ready")
        qk_copied, av_ready = sem("kv_ready"), sem("km_ready")
        wqk = M.w["qk3"].rearrange("p (k n) -> p k n", k=2)
        wv = M.w["v3"].rearrange("p (k n) -> p k n", k=2)
        wo = M.w["o3"].rearrange("p (k n) -> p k n", k=2)
        wg = M.w["gate3"].rearrange("p (k n) -> p k n", k=2)
        wu = M.w["up3"].rearrange("p (k n) -> p k n", k=2)
        wd = M.w["down3"].rearrange("p (f n) -> p f n", f=4)
        ident = small(M, "ident")[:, 0:P]
        A, B, C, Dk = ([4 * b + j for b in range(LANES)] for j in range(4))
        both = lambda bank: M.bank[bank][0:P, 0:2 * P].rearrange("p (a n) -> p a n", a=2)
        with nc.Block(name="delta_attention") as block:
            @block.vector
            def _(v):
                v.wait_ge(M.loaded["l3a"], 16)
                for name, ws in (("norm1", (wqk, wv)), ("norm2", (wg, wu))):
                    for w in ws:
                        for k in range(2):
                            nc.vector.tensor_scalar(w[:, k, :], w[:, k, :], small(M, name, 128)[:, k:k + 1], None, MUL)
                nc.vector.tensor_tensor(zw[:, :], small(M, "beta_w"), small(M, "norm1_row"), MUL)
                v.drain().then_inc(w_folded, 1)
                dve_ln_stats(nc, v, M, var_ready, std_ready)

                def norm(lanes):
                    for b, i in lanes:
                        ln_apply(nc, M, i, tile(M.x, i))
                    v.drain()
                    for b, i in lanes:
                        nc.vector.tensor_tensor(sq[b][:, :], tile(M.x, i), tile(M.x, i), MUL)
                        nc.vector.tensor_tensor(xn[b][:, :], tile(M.x, i), zw[:, :], MUL)
                    v.drain()
                    for b, i in lanes:
                        nc.vector.tensor_reduce(ss[:, bass.ds(i, 1)], sq[b][:, :], AX.X, ADD)
                        nc.vector.tensor_reduce(z[:, bass.ds(i, 1)], xn[b][:, :], AX.X, ADD)
                    v.drain()

                def rms_norm(lanes):
                    for b, i in lanes:
                        nc.vector.tensor_scalar(xn[b][:, :], tile(M.x, i), rr[:, bass.ds(i, 1)], None, MUL
                                                ).then_inc(xn_ready[b], 1)

                def delta(lanes, following):
                    beta_of = lambda i: beta[:, bass.ds(i, 1)]
                    for b, i in lanes:
                        v.wait_ge(qk_copied[b], 1)
                        v.sem_inc(qk_copied[b], -1)
                        nc.vector.tensor_tensor(sq[b][:, :], qk[b][:, D:2 * D], qk[b][:, D:2 * D], MUL)
                        v.drain()
                        nc.vector.tensor_reduce(k1[b][:, :], sq[b][:, :], AX.X, ADD)
                        v.drain()
                        nc.vector.tensor_scalar(k1[b][:, :], k1[b][:, :], 1e-24, None, MAX).then_inc(k_ready[b], 1)
                    for b, i in lanes:
                        v.wait_ge(av_ready[b], 1)
                        v.sem_inc(av_ready[b], -1)
                        for c in range(2):
                            last = nc.vector.tensor_tensor_scan(ema[b][:, c, :], decay[:, c, :], av[b][:, c, :], 0.0, MUL, ADD)
                        last.then_inc(ema_ready[b], 1)
                        v.wait_ge(kroot_ready[b], 1)
                        v.sem_inc(kroot_ready[b], -1)
                        nc.vector.reciprocal(k1[b][:, :], kroot[b][:, :])
                        v.drain()
                        nc.vector.tensor_scalar(qk[b][:, D:2 * D], qk[b][:, D:2 * D], k1[b][:, 0:1], None, MUL
                                                ).then_inc(kn_ready[b], 1)
                    for b, i in lanes:
                        v.wait_ge(bv_turned[b], 1)
                        v.sem_inc(bv_turned[b], -1)
                        nc.vector.tensor_scalar(bv[b][:, :], M.bank[Dk[b]][0:P, 0:D], beta_of(i), None, MUL)
                        v.wait_ge(G_ready[b], 1)
                        v.sem_inc(G_ready[b], -1)
                        nc.vector.scalar_tensor_tensor(low[b][:, :], M.bank[B[b]][0:P, 0:P], beta_of(i),
                                                       small(M, "strict"), MUL, MUL).then_inc(C_ready[b], 1)
                        nc.vector.tensor_tensor(mt[b][:, :], M.bank[B[b]][0:P, 128:128 + P], small(M, "mtm"), MUL)
                        v.drain()
                        nc.vector.tensor_tensor(Cl[b][:, :, :], spread(low[b][:, :], 1, LEVELS),
                                                small(M, "lvl").rearrange("p (l n) -> p l n", l=LEVELS), MUL)
                    for b, i in lanes:
                        v.wait_ge(CT_ready[b], 1)
                        v.sem_inc(CT_ready[b], -1)
                        nc.vector.tensor_tensor(ClT[b][:, :, :], spread(M.bank[C[b]][0:P, 0:P], 1, LEVELS),
                                                small(M, "lvlT").rearrange("p (l n) -> p l n", l=LEVELS), MUL)
                        v.drain()
                        nc.vector.tensor_tensor(XY[b][:, 0, :], ident, Cl[b][:, 0, :], SUB)
                        nc.vector.tensor_tensor(XY[b][:, 1, :], ident, ClT[b][:, 0, :], SUB).then_inc(X_ready[b], 1)
                    rms_norm(following)
                    for l in range(1, LEVELS):
                        for b, i in lanes:
                            v.wait_ge(XCX_ready[b], 1)
                            v.sem_inc(XCX_ready[b], -1)
                            nc.vector.tensor_tensor(XY[b][:, :, :], XY[b][:, :, :], both(A[b]), SUB).then_inc(X_ready[b], 1)
                    for b, i in lanes:
                        v.wait_ge(y_ready[b], 1)
                        v.sem_inc(y_ready[b], -1)
                        nc.vector.tensor_tensor(tile(M.x, i), tile(M.x, i), M.bank[A[b]][0:P, 0:D], ADD)
                    v.drain()
                    for b, i in lanes:
                        nc.vector.tensor_tensor(sq[b][:, :], tile(M.x, i), tile(M.x, i), MUL)
                    v.drain()
                    for b, i in lanes:
                        nc.vector.tensor_reduce(ss[:, bass.ds(i, 1)], sq[b][:, :], AX.X, ADD)
                    v.drain()

                def mlp(lanes, following):
                    for b, i in lanes:
                        nc.vector.tensor_tensor(tile(M.h, i), tile(M.h, i), tile(M.x, i), ADD)
                    for b, i in lanes:
                        v.wait_ge(sg_ready[b], 1)
                        v.sem_inc(sg_ready[b], -1)
                        nc.vector.tensor_tensor(hid[b][:, :, :], sg[b][:, :, :], turned(M, B[b], 4), MUL)
                        v.drain()
                        nc.vector.tensor_tensor(hid[b][:, :, :], hid[b][:, :, :], turned(M, C[b], 4), MUL
                                                ).then_inc(hid_ready[b], 1)
                    rms_norm(following)
                    for b, i in lanes:
                        v.wait_ge(y_ready[b], 1)
                        v.sem_inc(y_ready[b], -1)
                        nc.vector.tensor_tensor(tile(M.h, i), tile(M.h, i), M.bank[Dk[b]][0:P, 0:D], ADD)
                    v.drain()
                    dve_tile_stats(nc, M, lanes)

                tiles_by_lanes(nc, ET.DVE, norm)
                nc.vector.tensor_scalar(ss[:, :], ss[:, :], 1.0 / D, 1e-6, MUL, ADD).then_inc(ss_ready, 1)
                v.wait_ge(root_ready, 1)
                v.sem_inc(root_ready, -1)
                nc.vector.reciprocal(rr[:, :], root[:, :])
                v.drain()
                nc.vector.tensor_tensor(z[:, :], z[:, :], rr[:, :], MUL).then_inc(z_ready, 1)
                v.wait_ge(beta_ready, 1)
                v.sem_inc(beta_ready, -1)
                nc.vector.tensor_scalar(keep[:, :], alpha[:, :], -1.0, 1.0, MUL, ADD)
                v.drain()
                for c in range(2):
                    nc.vector.tensor_scalar(decay[:, c, :], small(M, "run", 128), keep[:, c:c + 1], None, MUL)
                tiles_with_next(nc, ET.DVE, rms_norm, delta)
                nc.vector.tensor_scalar(ss[:, :], ss[:, :], 1.0 / D, 1e-6, MUL, ADD).then_inc(ss2_ready, 1)
                v.wait_ge(root2_ready, 1)
                v.sem_inc(root2_ready, -1)
                nc.vector.reciprocal(rr[:, :], root[:, :])
                v.drain()
                tiles_with_next(nc, ET.DVE, rms_norm, mlp)

            @block.scalar
            def _(a):
                act_ln_std(nc, a, M, var_ready, std_ready)
                a.wait_ge(ss_ready, 1)
                a.sem_inc(ss_ready, -1)
                nc.scalar.activation(root[:, :], ss[:, :], ACT.Sqrt).then_inc(root_ready, 1)
                nc.scalar.activation(alpha[:, :], small(M, "alpha", 128), ACT.Sigmoid)
                a.wait_ge(z_ready, 1)
                a.sem_inc(z_ready, -1)
                nc.scalar.activation(beta[:, :], z[:, :], ACT.Sigmoid, bias=small(M, "beta_b")).then_inc(beta_ready, 1)
                a.preload_act_table(ACT.Sqrt)

                def copy_x(lanes):
                    for b, i in lanes:
                        a.wait_ge(turned_ready[b], 1)
                        a.sem_inc(turned_ready[b], -1)
                        nc.scalar.copy(xT[b][:, :, :], turned(M, C[b])).then_inc(xT_ready[b], 1)

                def copy_qkv(lanes):
                    for b, i in lanes:
                        a.wait_ge(qk_ready[b], 1)
                        a.sem_inc(qk_ready[b], -1)
                        nc.scalar.copy(qk[b][:, :], M.bank[B[b]][0:P, :]).then_inc(qk_copied[b], 1)
                        a.wait_ge(v_ready[b], 1)
                        a.sem_inc(v_ready[b], -1)
                        for c in range(2):
                            last = nc.scalar.activation(av[b][:, c, :], M.bank[C[b]][:, c * P:(c + 1) * P], ACT.Copy,
                                                        scale=alpha[:, c:c + 1])
                        last.then_inc(av_ready[b], 1)

                def first(lanes):
                    copy_x(lanes)
                    copy_qkv(lanes)

                def delta(lanes, following):
                    for b, i in lanes:
                        a.wait_ge(k_ready[b], 1)
                        a.sem_inc(k_ready[b], -1)
                        nc.scalar.activation(kroot[b][:, :], k1[b][:, :], ACT.Sqrt).then_inc(kroot_ready[b], 1)
                    for b, i in lanes:
                        a.wait_ge(qk_turned[b], 1)
                        a.sem_inc(qk_turned[b], -1)
                        nc.scalar.copy(qkT[b][:, :, :], turned(M, A[b], 4)).then_inc(qkT_ready[b], 1)
                    for l in range(1, LEVELS):
                        for b, i in lanes:
                            a.wait_ge(CX_ready[b], 1)
                            a.sem_inc(CX_ready[b], -1)
                            nc.scalar.copy(CX[b][:, :, :], both(Dk[b])).then_inc(CX_copied[b], 1)
                        if l == 1:
                            copy_x(following)
                        elif l == 4:
                            copy_qkv(following)
                    for b, i in lanes:
                        a.wait_ge(U_ready[b], 1)
                        a.sem_inc(U_ready[b], -1)
                        nc.scalar.copy(U[b][:, :], M.bank[A[b]][0:P, 0:D]).then_inc(U_copied[b], 1)
                    for b, i in lanes:
                        a.wait_ge(oT_made[b], 1)
                        a.sem_inc(oT_made[b], -1)
                        nc.scalar.copy(oT[b][:, :, :], turned(M, Dk[b])).then_inc(oT_copied[b], 1)
                    a.drain()

                def copy_mlp_x(lanes):
                    for b, i in lanes:
                        a.wait_ge(turned_ready[b], 1)
                        a.sem_inc(turned_ready[b], -1)
                        nc.scalar.copy(xT[b][:, :, :], turned(M, A[b])).then_inc(xT_ready[b], 1)

                def mlp(lanes, following):
                    for b, i in lanes:
                        a.wait_ge(gu_ready[b], 1)
                        a.sem_inc(gu_ready[b], -1)
                        nc.scalar.activation(sg[b][:, :, :], turned(M, B[b], 4), ACT.Sigmoid).then_inc(sg_ready[b], 1)
                    copy_mlp_x(following)

                tiles_with_next(nc, ET.Activation, first, delta)
                a.wait_ge(ss2_ready, 1)
                a.sem_inc(ss2_ready, -1)
                nc.scalar.activation(root[:, :], ss[:, :], ACT.Sqrt).then_inc(root2_ready, 1)
                a.preload_act_table(ACT.Sigmoid)
                tiles_with_next(nc, ET.Activation, copy_mlp_x, mlp)

            @block.tensor
            def _(pe):
                def turn_x(lanes):
                    for b, i in lanes:
                        pe.wait_ge(xn_ready[b], 1)
                        pe.sem_inc(xn_ready[b], -1)
                        pe_turn(nc, M, C[b], xn[b]).then_inc(turned_ready[b], 1)

                def project_qkv(lanes):
                    for b, i in lanes:
                        pe.wait_ge(xT_ready[b], 1)
                        pe.sem_inc(xT_ready[b], -1)
                        pe_project(nc, M, B[b], xT[b], wqk, 0, 2 * D).then_inc(qk_ready[b], 1)
                        for c in range(2):
                            last = pe_project(nc, M, C[b], wv[:, :, c * 128:(c + 1) * 128], xT[b], 0, P, 128, col=c * P)
                        last.then_inc(v_ready[b], 1)

                def first(lanes):
                    turn_x(lanes)
                    project_qkv(lanes)

                def delta(lanes, following):
                    for b, i in lanes:
                        pe.wait_ge(ema_ready[b], 1)
                        pe.sem_inc(ema_ready[b], -1)
                        for c in range(2):
                            last = nc.tensor.transpose(M.bank[Dk[b]][0:P, c * 128:(c + 1) * 128], ema[b][:, c, :],
                                                       small(M, "ident", 128))
                        last.then_inc(bv_turned[b], 1)
                        pe.wait_ge(kn_ready[b], 1)
                        pe.sem_inc(kn_ready[b], -1)
                        pe_turn(nc, M, A[b], qk[b], 4).then_inc(qk_turned[b], 1)
                    for b, i in lanes:
                        pe.wait_ge(qkT_ready[b], 1)
                        pe.sem_inc(qkT_ready[b], -1)
                        for o, rhs in ((0, 2), (128, 0)):
                            for k in range(2):
                                last = nc.tensor.matmul(M.bank[B[b]][0:P, o:o + P], qkT[b][:, 2 + k, :],
                                                        qkT[b][:, rhs + k, :], start=(k == 0), stop=(k == 1))
                        last.then_inc(G_ready[b], 1)
                    for b, i in lanes:
                        pe.wait_ge(C_ready[b], 1)
                        pe.sem_inc(C_ready[b], -1)
                        nc.tensor.transpose(M.bank[C[b]][0:P, 0:P], low[b][:, :], ident).then_inc(CT_ready[b], 1)
                    for l in range(1, LEVELS):
                        for b, i in lanes:
                            pe.wait_ge(X_ready[b], 1)
                            pe.sem_inc(X_ready[b], -1)
                            nc.tensor.matmul(M.bank[Dk[b]][0:P, 0:P], ClT[b][:, l, :], XY[b][:, 0, :], start=True, stop=True)
                            nc.tensor.matmul(M.bank[Dk[b]][0:P, P:2 * P], Cl[b][:, l, :], XY[b][:, 1, :], start=True,
                                             stop=True).then_inc(CX_ready[b], 1)
                        for b, i in lanes:
                            pe.wait_ge(CX_copied[b], 1)
                            pe.sem_inc(CX_copied[b], -1)
                            nc.tensor.matmul(M.bank[A[b]][0:P, 0:P], XY[b][:, 1, :], CX[b][:, 0, :], start=True, stop=True)
                            nc.tensor.matmul(M.bank[A[b]][0:P, P:2 * P], XY[b][:, 0, :], CX[b][:, 1, :], start=True,
                                             stop=True).then_inc(XCX_ready[b], 1)
                        if l == 1:
                            turn_x(following)
                        elif l < 4:
                            project_qkv(following[l - 2:l - 1])
                    for b, i in lanes:
                        pe.wait_ge(X_ready[b], 1)
                        pe.sem_inc(X_ready[b], -1)
                        nc.tensor.matmul(M.bank[A[b]][0:P, 0:D], XY[b][:, 1, :], bv[b][:, :], start=True, stop=True
                                         ).then_inc(U_ready[b], 1)
                    for b, i in lanes:
                        pe.wait_ge(U_copied[b], 1)
                        pe.sem_inc(U_copied[b], -1)
                        for c in range(2):
                            last = nc.tensor.matmul(M.bank[Dk[b]][:, c * P:(c + 1) * P], U[b][:, c * 128:(c + 1) * 128],
                                                    mt[b][:, :], start=True, stop=True)
                        last.then_inc(oT_made[b], 1)
                    for b, i in lanes:
                        pe.wait_ge(oT_copied[b], 1)
                        pe.sem_inc(oT_copied[b], -1)
                        pe_project(nc, M, A[b], oT[b], wo, 0, D).then_inc(y_ready[b], 1)

                def turn_mlp_x(lanes):
                    for b, i in lanes:
                        pe.wait_ge(xn_ready[b], 1)
                        pe.sem_inc(xn_ready[b], -1)
                        pe_turn(nc, M, A[b], xn[b]).then_inc(turned_ready[b], 1)

                def mlp(lanes, following):
                    for b, i in lanes:
                        pe.wait_ge(xT_ready[b], 1)
                        pe.sem_inc(xT_ready[b], -1)
                        for bank, w in ((B[b], wg), (C[b], wu)):
                            for f in range(4):
                                last = pe_project(nc, M, bank, w[:, :, f * 128:(f + 1) * 128], xT[b], 0, P, 128, col=f * P)
                        last.then_inc(gu_ready[b], 1)
                    for b, i in lanes:
                        pe.wait_ge(hid_ready[b], 1)
                        pe.sem_inc(hid_ready[b], -1)
                        for f in range(4):
                            last = nc.tensor.matmul(M.bank[Dk[b]][0:P, 0:D], hid[b][:, f, :], wd[:, f, :], start=(f == 0),
                                                    stop=(f == 3))
                        last.then_inc(y_ready[b], 1)
                    turn_mlp_x(following)

                pe.wait_ge(w_folded, 1)
                pe.sem_inc(w_folded, -1)
                tiles_with_next(nc, ET.PE, first, delta)
                tiles_with_next(nc, ET.PE, turn_mlp_x, mlp)


def route3(nc, M, beside):
    with ExitStack() as ctx:
        one = lambda n, s: ctx.enter_context(nc.sbuf_tensor("r3_" + n, s, F32))
        sb = lambda n, s, dt=F32: [ctx.enter_context(nc.sbuf_tensor(f"r3_{n}{b}", s, dt)) for b in range(LANES)]
        sem = lambda n: [M.sem(f"{n}{b}") for b in range(LANES)]
        seen, ones = one("seen", [P, E3]), one("ones", [P, P])
        slot8 = ctx.enter_context(nc.sbuf_tensor("r3_slot8", [P, T, K3], I32))
        xn, xT = sb("xn", [P, D]), sb("xT", [128, 2, P])
        lg, ex, rep, mask, w = (sb(n, [P, E3]) for n in ("lg", "ex", "rep", "mask", "w"))
        key, over, eq = sb("key", [P, E3]), sb("over", [P, E3]), sb("eq", [P, 8, E3])
        m8, k8, i8 = sb("m8", [P, 8]), sb("k8", [P, 8]), sb("i8", [P, 8])
        rows, idx = sb("rows", [P, D]), sb("idx", [P, K3], I32)
        s1, r1 = sb("s1", [P, 1]), sb("r1", [P, 1])
        var_ready, std_ready = M.sem("var_ready0"), M.sem("std_ready0")
        xn_ready, turned_ready, xT_ready, lg_ready = sem("xn_ready"), sem("turned"), sem("xT_ready"), sem("q_ready")
        shifted, ex_ready, mask_ready, pos_ready = sem("shifted"), sem("probs_dve"), sem("kn_ready"), sem("s_ready")
        idx_ready, scattered = sem("idx_ready"), sem("scattered")
        router = M.w["router"].rearrange("p (k n) -> p k n", k=2)
        A, B, C = ([4 * b + j for b in range(LANES)] for j in range(3))
        with nc.Block(name="route3") as block:
            beside(block)

            @block.vector
            def _(v):
                nc.vector.memset(seen[:, :], 0.0)
                nc.vector.memset(ones[:, :], 1.0)
                v.wait_ge(M.slots_cleared, 16)
                dve_ln_stats(nc, v, M, var_ready, std_ready)

                def route(lanes):
                    for b, i in lanes:
                        ln_apply(nc, M, i, xn[b][:, :]).then_inc(xn_ready[b], 1)
                    for b, i in lanes:
                        ln_apply(nc, M, i, tile(M.x, i))
                    for b, i in lanes:
                        v.wait_ge(lg_ready[b], 1)
                        v.sem_inc(lg_ready[b], -1)
                        nc.vector.tensor_copy(lg[b][:, :], M.bank[B[b]][0:P, 0:E3])
                    v.drain()
                    for b, i in lanes:
                        nc.vector.tensor_reduce(s1[b][:, :], lg[b][:, :], AX.X, MAX)
                    v.drain()
                    for b, i in lanes:
                        nc.vector.tensor_scalar(lg[b][:, :], lg[b][:, :], s1[b][:, 0:1], None, SUB).then_inc(shifted[b], 1)
                    for b, i in lanes:
                        v.wait_ge(ex_ready[b], 1)
                        v.sem_inc(ex_ready[b], -1)
                        nc.vector.tensor_reduce(s1[b][:, :], ex[b][:, :], AX.X, ADD)
                    v.drain()
                    for b, i in lanes:
                        nc.vector.reciprocal(r1[b][:, :], s1[b][:, :])
                    v.drain()
                    for b, i in lanes:
                        nc.vector.tensor_scalar(ex[b][:, :], ex[b][:, :], r1[b][:, 0:1], None, MUL)
                    v.drain()
                    for b, i in lanes:
                        nc.vector.max(m8[b][:, :], ex[b][:, :])
                    v.drain()
                    for b, i in lanes:
                        nc.vector.match_replace(rep[b][:, :], m8[b][:, :], ex[b][:, :], -1.0)
                    v.drain()
                    for b, i in lanes:
                        nc.vector.tensor_scalar(mask[b][:, :], rep[b][:, :], 0.0, None, ALU.is_lt).then_inc(mask_ready[b], 1)
                    v.drain()
                    for b, i in lanes:
                        nc.vector.tensor_tensor(w[b][:, :], ex[b][:, :], mask[b][:, :], MUL)
                    v.drain()
                    for b, i in lanes:
                        nc.vector.tensor_reduce(s1[b][:, :], w[b][:, :], AX.X, ADD)
                    v.drain()
                    for b, i in lanes:
                        nc.vector.reciprocal(r1[b][:, :], s1[b][:, :])
                    v.drain()
                    for b, i in lanes:
                        nc.vector.tensor_scalar(w[b][:, :], w[b][:, :], r1[b][:, 0:1], None, MUL)
                    for b, i in lanes:
                        v.wait_ge(pos_ready[b], 1)
                        v.sem_inc(pos_ready[b], -1)
                        nc.vector.tensor_scalar(over[b][:, :], M.bank[C[b]][0:P, 0:E3], float(CAP), OVERFLOW, ALU.is_gt, MUL)
                        nc.vector.tensor_tensor(key[b][:, :], M.bank[C[b]][0:P, 0:E3], small(M, "ebase"), ADD)
                    v.drain()
                    for b, i in lanes:
                        nc.vector.tensor_tensor(key[b][:, :], key[b][:, :], over[b][:, :], ADD)
                        nc.vector.tensor_tensor(seen[:, :], seen[:, :], mask[b][:, :], ADD)
                        v.drain()
                    for b, i in lanes:
                        nc.vector.tensor_tensor(key[b][:, :], key[b][:, :], mask[b][:, :], MUL)
                    v.drain()
                    for b, i in lanes:
                        nc.vector.max(k8[b][:, :], key[b][:, :])
                    v.drain()
                    for b, i in lanes:
                        nc.vector.scalar_tensor_tensor(i8[b][:, :], k8[b][:, :], 1.0, small(M, "trash")[:, b * K3:(b + 1) * K3],
                                                       SUB, MIN)
                    v.drain()
                    for b, i in lanes:
                        nc.vector.tensor_copy(tile(slot8, i), i8[b][:, :]).then_inc(idx_ready[b], 1)
                    for b, i in lanes:
                        nc.vector.tensor_tensor(eq[b][:, :, :], spread(key[b][:, :], 1, 8), spread(k8[b][:, :], 2, E3),
                                                ALU.is_equal)
                        nc.vector.tensor_scalar(m8[b][:, :], k8[b][:, :], float(SLOTS), None, ALU.is_le)
                    v.drain()
                    for b, i in lanes:
                        nc.vector.tensor_tensor(eq[b][:, :, :], eq[b][:, :, :], spread(w[b][:, :], 1, 8), MUL)
                        nc.vector.tensor_scalar(i8[b][:, :], i8[b][:, :], float(SLOTS - 1), None, MIN)
                    v.drain()
                    for b, i in lanes:
                        nc.vector.tensor_reduce(k8[b][:, :], eq[b][:, :, :], AX.X, ADD)
                        nc.vector.tensor_copy(tile(M.idx8, i), i8[b][:, :])
                    v.drain()
                    for b, i in lanes:
                        nc.vector.tensor_tensor(tile(M.w8, i), k8[b][:, :], m8[b][:, :], MUL)
                    v.drain()

                tiles_by_lanes(nc, ET.DVE, route)

            @block.gpsimd
            def _(pool):
                def scatter(b, i):
                    pool.wait_ge(idx_ready[b], 1)
                    pool.sem_inc(idx_ready[b], -1)
                    nc.gpsimd.tensor_copy(rows[b][:, :], tile(M.x, i))
                    nc.gpsimd.tensor_copy(idx[b][:, :], tile(slot8, i))
                    pool.drain()
                    for k in range(K3):
                        nc.gpsimd.indirect_dma_start(
                            out=M.dram["slots_x"], out_offset=bass.IndirectOffsetOnAxis(ap=idx[b][:, k:k + 1], axis=0),
                            in_=rows[b][:, :], in_offset=None).then_inc(scattered[b], 16)

                def scattered_by(b, count):
                    pool.wait_ge(scattered[b], count)

                scatter(0, 0)
                with nc.Fori(0, (T - 1) // LANES, engines=(ET.Pool,)) as p:
                    scatter(1, p * LANES + 1)
                    scattered_by(0, p * (16 * K3) + 16 * K3)
                    scatter(0, p * LANES + 2)
                    scattered_by(1, p * (16 * K3) + 16 * K3)
                scattered_by(0, (T // LANES + 1) * 16 * K3)

            @block.scalar
            def _(a):
                act_ln_std(nc, a, M, var_ready, std_ready)
                a.preload_act_table(ACT.Exp)

                def route(lanes):
                    for b, i in lanes:
                        a.wait_ge(turned_ready[b], 1)
                        a.sem_inc(turned_ready[b], -1)
                        nc.scalar.copy(xT[b][:, :, :], turned(M, A[b])).then_inc(xT_ready[b], 1)
                    for b, i in lanes:
                        nc.scalar.copy(cols(M.xT, i), turned(M, A[b]))
                    for b, i in lanes:
                        a.wait_ge(shifted[b], 1)
                        a.sem_inc(shifted[b], -1)
                        nc.scalar.activation(ex[b][:, :], lg[b][:, :], ACT.Exp).then_inc(ex_ready[b], 1)
                    a.drain()

                tiles_by_lanes(nc, ET.Activation, route)

            @block.tensor
            def _(pe):
                def route(lanes):
                    for b, i in lanes:
                        pe.wait_ge(xn_ready[b], 1)
                        pe.sem_inc(xn_ready[b], -1)
                        pe_turn(nc, M, A[b], xn[b]).then_inc(turned_ready[b], 1)
                    for b, i in lanes:
                        pe.wait_ge(xT_ready[b], 1)
                        pe.sem_inc(xT_ready[b], -1)
                        pe_project(nc, M, B[b], xT[b], router, 0, E3).then_inc(lg_ready[b], 1)
                    for b, i in lanes:
                        pe.wait_ge(mask_ready[b], 1)
                        pe.sem_inc(mask_ready[b], -1)
                        pos = M.bank[C[b]][0:P, 0:E3]
                        nc.tensor.matmul(pos, ones[:, :], seen[:, :], start=True, stop=False)
                        for earlier in range(b):
                            nc.tensor.matmul(pos, ones[:, :], mask[earlier][:, :], start=False, stop=False)
                        nc.tensor.matmul(pos, small(M, "tri"), mask[b][:, :], start=False, stop=True
                                         ).then_inc(pos_ready[b], 1)

                pe.wait_ge(M.loaded["l3f"], 16)
                tiles_by_lanes(nc, ET.PE, route)


def route_and_experts3(nc, M):
    with ExitStack() as ctx:
        sb = lambda n, s: ctx.enter_context(nc.sbuf_tensor("e3_" + n, s, F32))
        sem = lambda n: M.sem(n + "0")
        NB, NY = 8, 4
        wgu = [sb(f"wgu{b}", [128, 2, 2 * F3]) for b in range(NB)]
        wd = [sb(f"wd{b}", [FH, 2, D]) for b in range(NB)]
        ye = [M.yT[:, 0, b * D:(b + 1) * D] for b in range(NY)]
        loaded, stored = [sem(f"loaded{b}") for b in range(NB)], [sem(f"stored{b}") for b in range(NY)]
        used = sem("e3_used")
        turned_ready, xT_ready, gu_ready, sg_ready = sem("turned"), sem("xT_ready"), sem("gu_ready"), sem("sg_ready")
        hid_ready, y_ready = sem("hid_ready"), sem("y_ready")

        def load_weights(sp, b, e):
            sp.dma_start(wgu[b][:, :, :].rearrange("p k n -> p (k n)"),
                         M.dram["gu_3"][bass.ds(e, 1)].rearrange("a p n -> (a p) n")).then_inc(loaded[b], 16)
            sp.dma_start(wd[b][:, :, :].rearrange("p k n -> p (k n)"),
                         M.dram["down_3"][bass.ds(e, 1)].rearrange("a p n -> (a p) n")).then_inc(loaded[b], 16)

        def first_weights(block):
            @block.sync
            def _(sp):
                for b in range(NB):
                    load_weights(sp, b, b)

        route3(nc, M, first_weights)
        xe = [sb(f"xe{b}", [CAP, D]) for b in range(NB)]
        xT = [sb(f"xT{b}", [128, 2, CAP]) for b in range(2)]
        sg = [sb(f"sg{b}", [FH, 2, CAP]) for b in range(2)]
        hid = [sb(f"hid{b}", [FH, 2, CAP]) for b in range(2)]
        with nc.Block(name="experts3") as block:
            @block.sync
            def _(sp):
                def load_rows(b, e):
                    sp.dma_start(xe[b][:, :], M.dram["slots_x"][bass.ds(e * CAP, CAP), :]).then_inc(loaded[b], 16)

                for b in range(NB):
                    load_rows(b, b)
                with nc.Fori(0, E3 // NB - 1, engines=(ET.SP,)) as p:
                    for b in range(NB):
                        sp.wait_ge(used, 1)
                        sp.sem_inc(used, -1)
                        load_rows(b, p * NB + (NB + b))
                        load_weights(sp, b, p * NB + (NB + b))
                sp.wait_ge(used, NB)
                sp.sem_inc(used, -NB)

            @block.tensor
            def _(pe):
                def turn(b):
                    pe.wait_ge(loaded[b], 48)
                    pe.sem_inc(loaded[b], -48)
                    for k in range(2):
                        last = nc.tensor.transpose(M.bank[b % 2][:, k * CAP:(k + 1) * CAP], xe[b][:, k * 128:(k + 1) * 128],
                                                   small(M, "ident", 128))
                    last.then_inc(turned_ready, 1)

                def up(b):
                    pe.wait_ge(xT_ready, 1)
                    pe.sem_inc(xT_ready, -1)
                    for f in range(4):
                        for k in range(2):
                            last = nc.tensor.matmul(M.bank[2 + b % 2][0:FH, f * CAP:(f + 1) * CAP],
                                                    wgu[b][:, k, f * FH:(f + 1) * FH], xT[b % 2][:, k, :],
                                                    start=(k == 0), stop=(k == 1))
                    last.then_inc(gu_ready, 1)

                def down(b):
                    pe.wait_ge(hid_ready, 1)
                    pe.sem_inc(hid_ready, -1)
                    for f in range(2):
                        last = nc.tensor.matmul(M.bank[4 + b % 2][:, 0:D], hid[b % 2][:, f, :], wd[b][:, f, :],
                                                start=(f == 0), stop=(f == 1))
                    last.then_inc(y_ready, 1)
                    pe.drain().then_inc(used, 1)

                turn(0)
                up(0)
                turn(1)
                with nc.Fori(0, E3 // NB - 1, engines=(ET.PE,)) as p:
                    for b in range(NB):
                        turn((b + 2) % NB)
                        up((b + 1) % NB)
                        down(b)
                for b in range(NB):
                    if b + 2 < NB:
                        turn(b + 2)
                    if b + 1 < NB:
                        up(b + 1)
                    down(b)

            @block.scalar
            def _(a):
                a.preload_act_table(ACT.Sigmoid)

                def copy_xT(b):
                    a.wait_ge(turned_ready, 1)
                    a.sem_inc(turned_ready, -1)
                    nc.scalar.copy(xT[b % 2][:, :, :], M.bank[b % 2][:, 0:2 * CAP].rearrange("p (k n) -> p k n", k=2)
                                   ).then_inc(xT_ready, 1)

                def sigmoid(b):
                    a.wait_ge(gu_ready, 1)
                    a.sem_inc(gu_ready, -1)
                    nc.scalar.activation(sg[b % 2][:, :, :], M.bank[2 + b % 2][0:FH, 0:2 * CAP].rearrange("p (f n) -> p f n", f=2),
                                         ACT.Sigmoid).then_inc(sg_ready, 1)

                def store_y(b, e):
                    y = b % NY
                    a.wait_ge(y_ready, 1)
                    a.sem_inc(y_ready, -1)
                    a.wait_ge(stored[y], 16)
                    a.sem_inc(stored[y], -16)
                    nc.scalar.copy(ye[y], M.bank[4 + b % 2][:, 0:D])
                    a.drain()
                    a.dma_start(M.dram["slots_y"][bass.ds(e * CAP, CAP), :], ye[y]).then_inc(stored[y], 16)

                for b in range(NY):
                    a.sem_inc(stored[b], 16)
                copy_xT(0)
                sigmoid(0)
                copy_xT(1)
                with nc.Fori(0, E3 // NB - 1, engines=(ET.Activation,)) as p:
                    for b in range(NB):
                        copy_xT((b + 2) % NB)
                        sigmoid((b + 1) % NB)
                        store_y(b, p * NB + b)
                for b in range(NB):
                    if b + 2 < NB:
                        copy_xT(b + 2)
                    if b + 1 < NB:
                        sigmoid(b + 1)
                    store_y(b, E3 - NB + b)
                for b in range(NY):
                    a.wait_ge(stored[b], 16)
                    a.sem_inc(stored[b], -16)

            @block.vector
            def _(v):
                with nc.Fori(0, E3 // NB, engines=(ET.DVE,)) as p:
                    for b in range(NB):
                        v.wait_ge(sg_ready, 1)
                        v.sem_inc(sg_ready, -1)
                        gu = M.bank[2 + b % 2][0:FH, :].rearrange("p (f n) -> p f n", f=4)
                        nc.vector.tensor_tensor(hid[b % 2][:, :, :], sg[b % 2][:, :, :], gu[:, 0:2, :], MUL)
                        v.drain()
                        nc.vector.tensor_tensor(hid[b % 2][:, :, :], hid[b % 2][:, :, :], gu[:, 2:4, :], MUL).then_inc(hid_ready, 1)
                        v.drain()


def combine3(nc, M):
    with ExitStack() as ctx:
        sb = lambda n, s, dt=F32: [ctx.enter_context(nc.sbuf_tensor(f"c3_{n}{b}", s, dt)) for b in range(LANES)]
        sem = lambda n: [M.sem(f"{n}{b}") for b in range(LANES)]
        rows, idx = sb("rows", [P, K3, D]), sb("idx", [P, 8], I32)
        idx_ready, gathered, rows_here = sem("idx_ready"), sem("c3_gathered"), sem("rows_sent")
        hid, sg = sb("hid", [FH, 2, P]), sb("sg", [FH, 2, P])
        gu_ready, sg_ready, hid_ready, y_ready = sem("gu_ready"), sem("sg_ready"), sem("hid_ready"), sem("y_ready")
        h_ready, stored = M.sem("h_ready"), M.sem("c3_stored")
        wgu = M.w["ws_gu"].rearrange("p (k n) -> p k n", k=2)
        wd = M.w["ws_down"][0:FH, :].rearrange("p (f n) -> p f n", f=2)
        A, B = ([4 * b + j for b in range(LANES)] for j in range(2))
        with nc.Block(name="combine3") as block:
            @block.vector
            def _(v):
                def copy_indices(b, i):
                    nc.vector.tensor_copy(idx[b][:, :], tile(M.idx8, i)).then_inc(idx_ready[b], 1)

                def combine(b, i):
                    v.wait_ge(rows_here[b], 1)
                    v.sem_inc(rows_here[b], -1)
                    h = tile(M.h, i)
                    for k in range(K3):
                        nc.vector.scalar_tensor_tensor(
                            h, rows[b][:, k, :], M.w8[:, bass.ds(i, 1), k:k + 1].rearrange("p a n -> p (a n)"), h, MUL, ADD)
                        v.drain()
                    v.drain().then_inc(h_ready, 1)

                def shared(lanes):
                    guT = lambda b: M.bank[A[b]][0:FH, 0:4 * P].rearrange("p (f t) -> p f t", f=4)
                    for b, i in lanes:
                        v.wait_ge(sg_ready[b], 1)
                        v.sem_inc(sg_ready[b], -1)
                        nc.vector.tensor_tensor(hid[b][:, :, :], sg[b][:, :, :], guT(b)[:, 0:2, :], MUL)
                    v.drain()
                    for b, i in lanes:
                        nc.vector.tensor_tensor(hid[b][:, :, :], hid[b][:, :, :], guT(b)[:, 2:4, :], MUL
                                                ).then_inc(hid_ready[b], 1)
                    for b, i in lanes:
                        v.wait_ge(y_ready[b], 1)
                        v.sem_inc(y_ready[b], -1)
                        nc.vector.tensor_tensor(tile(M.h, i), tile(M.h, i), M.bank[B[b]][0:P, 0:D], ADD)
                    v.drain()

                for b in range(LANES):
                    copy_indices(b, b)
                tiles_by_lanes(nc, ET.DVE, shared)
                with nc.Fori(0, T // LANES - 1, engines=(ET.DVE,)) as p:
                    for b in range(LANES):
                        combine(b, p * LANES + b)
                        copy_indices(b, p * LANES + (LANES + b))
                for t in range((T // LANES - 1) * LANES, T):
                    combine(t % LANES, t)
                    if t + LANES < T:
                        copy_indices(t % LANES, t + LANES)

            @block.gpsimd
            def _(pool):
                def gather(b):
                    pool.wait_ge(idx_ready[b], 1)
                    pool.sem_inc(idx_ready[b], -1)
                    for k in range(K3):
                        nc.gpsimd.indirect_dma_start(
                            out=rows[b][:, k, :], out_offset=None, in_=M.dram["slots_y"],
                            in_offset=bass.IndirectOffsetOnAxis(ap=idx[b][:, k:k + 1], axis=0)).then_inc(gathered[b], 16)

                def pass_on(b, count):
                    pool.wait_ge(gathered[b], count)
                    pool.sem_inc(rows_here[b], 1)

                gather(0)
                with nc.Fori(0, (T - 1) // LANES, engines=(ET.Pool,)) as p:
                    gather(1)
                    pass_on(0, p * (16 * K3) + 16 * K3)
                    gather(0)
                    pass_on(1, p * (16 * K3) + 16 * K3)
                pass_on(0, (T // LANES + 1) * 16 * K3)

            @block.scalar
            def _(a):
                def shared(lanes):
                    for b, i in lanes:
                        a.wait_ge(gu_ready[b], 1)
                        a.sem_inc(gu_ready[b], -1)
                        nc.scalar.activation(sg[b][:, :, :], M.bank[A[b]][0:FH, 0:2 * P].rearrange("p (f t) -> p f t", f=2),
                                             ACT.Sigmoid).then_inc(sg_ready[b], 1)
                    a.drain()

                a.preload_act_table(ACT.Sigmoid)
                tiles_by_lanes(nc, ET.Activation, shared)

            @block.tensor
            def _(pe):
                def shared(lanes):
                    for b, i in lanes:
                        x = cols(M.xT, i)
                        for f in range(4):
                            for k in range(2):
                                last = nc.tensor.matmul(M.bank[A[b]][0:FH, f * P:(f + 1) * P],
                                                        wgu[:, k, f * FH:(f + 1) * FH], x[:, k, :],
                                                        start=(k == 0), stop=(k == 1))
                        last.then_inc(gu_ready[b], 1)
                    for b, i in lanes:
                        pe.wait_ge(hid_ready[b], 1)
                        pe.sem_inc(hid_ready[b], -1)
                        for f in range(2):
                            last = nc.tensor.matmul(M.bank[B[b]][0:P, 0:D], hid[b][:, f, :], wd[:, f, :],
                                                    start=(f == 0), stop=(f == 1))
                        last.then_inc(y_ready[b], 1)

                tiles_by_lanes(nc, ET.PE, shared)

            @block.sync
            def _(sp):
                with nc.Fori(0, T, engines=(ET.SP,)) as i:
                    sp.wait_ge(h_ready, 1)
                    sp.sem_inc(h_ready, -1)
                    sp.dma_start(M.dram["out"][bass.ds(i, 1)].rearrange("a p d -> (a p) d"), tile(M.h, i)).then_inc(stored, 16)
                sp.wait_ge(stored, 16 * T)


def vit_tower(nc, dram):
    with ExitStack() as ctx:
        M = setup_memory(nc, ctx, dram)
        patch_embedding(nc, M)
        alibi_attention(nc, M)
        feed_forward0(nc, M)
        add_back(nc, M, "_l0")
        rotary_attention(nc, M)
        coupling(nc, M)
        place_weights(nc, ctx, M, LATE)
        load_late(nc, M)
        linear_attention(nc, M)
        gate_top2(nc, M, "g2_", M.w["gate2"], dram["cw2"], True)
        experts2(nc, M)
        delta_attention(nc, M)
        route_and_experts3(nc, M)
        combine3(nc, M)


def chunks(w, parts=128):
    w = np.ascontiguousarray(w)
    return w.reshape((-1, parts) + w.shape[1:]).swapaxes(0, 1)


def flat(w, parts=128):
    w = w.reshape(w.shape[0], -1)
    out = np.zeros((128, w.shape[1]), np.float32)
    out[:w.shape[0]] = w
    return out


def constants():
    f = np.float32
    c = {}
    p = np.arange(128)
    c["ident"] = np.eye(128, dtype=f)
    c["mask8"] = (p[:, None] // DH == np.arange(8)).astype(f)
    r = np.arange(P)
    seq, pos = r // L, r % L
    c["vm16"] = (seq[:, None] == np.arange(16) % 3).astype(f)
    c["vm8"] = (seq[:, None] == np.arange(8) % 3).astype(f)
    start = 2 ** (-2 ** (-(math.log2(H16) - 3)))
    slopes = np.array([start * start ** m for m in range(H16)], f)
    rel = (np.arange(L)[None, :] - pos[:, None]).astype(f)
    bias = slopes[None, :, None] * rel[:, None, :]
    c["alibi"] = np.where(rel[:, None, :] <= 0, bias, f(NEG))
    c["mb"] = (seq[:, None] == np.arange(SEQS)).astype(f)
    inv = (f(1.0) / f(10000.0) ** (np.arange(0, DH, 2, dtype=f) / f(DH))).astype(f)
    ang = np.repeat(pos.astype(f)[:, None] * inv[None, :], 2, axis=-1).astype(f)
    c["cos"] = np.cos(ang).astype(f)
    c["sin"] = (np.sin(ang) * np.where(np.arange(DH) % 2 == 0, -1.0, 1.0)).astype(f)
    c["blk"] = (p[:, None] // DH == p[None, :] // DH).astype(f)
    c["tri"] = (r[:, None] <= r[None, :]).astype(f)
    same = seq[:, None] == seq[None, :]
    c["strict"] = (same & (r[None, :] < r[:, None])).astype(f)
    lvl = np.stack([same & (pos[:, None] >> (l + 1) == pos[None, :] >> (l + 1)) & ((pos[:, None] >> l) % 2 == 1)
                    & ((pos[None, :] >> l) % 2 == 0) for l in range(LEVELS)], 1).astype(f)
    c["lvl"] = lvl
    c["lvlT"] = lvl.transpose(2, 1, 0)
    c["mtm"] = (same & (r[None, :] >= r[:, None])).astype(f)
    c["below8"] = np.broadcast_to((np.arange(8)[None, :] < np.arange(8)[:, None]).astype(f).reshape(1, 64), (P, 64))
    c["ebase"] = np.broadcast_to(CAP * np.arange(E3, dtype=f), (P, E3))
    c["trash"] = (SLOTS + r[:, None] + P * np.arange(LANES * K3)).astype(f)
    c["run"] = np.broadcast_to((pos != 0).astype(f), (128, P))
    c["sgn"] = np.where(p < 64, 1.0, -1.0).astype(f)[:, None]
    y, x = (a.reshape(-1).astype(f) for a in np.meshgrid(np.arange(GRID), np.arange(GRID), indexing="ij"))
    om = (np.arange(D // 4, dtype=f) / f(D // 4 - 1)).astype(f)
    om = (f(1.0) / f(10000.0) ** om).astype(f)
    xa, ya = x[:, None] * om[None, :], y[:, None] * om[None, :]
    c["pe"] = np.concatenate([np.sin(xa), np.cos(xa), np.sin(ya), np.cos(ya)], 1).astype(f)
    return c


def lay_out(I):
    c = constants()
    row = lambda v: np.broadcast_to(np.asarray(v).reshape(1, -1), (128, np.asarray(v).size))
    col = lambda v: np.asarray(v).reshape(-1, 128).T if np.asarray(v).size >= 128 else flat(np.asarray(v).reshape(-1, 1))
    s = dict(c)
    s["base"] = np.tile(np.concatenate([I["cls_tok"].reshape(1, D), c["pe"]], 0), (SEQS, 1))
    s["ln2_w"], s["b_out0"] = row(I["L0_tok_ln2_w"]), row(I["L0_attn_b_out"])
    b_in = I["L0_attn_b_in"]
    s["b_q0"], s["b_k0"], s["b_v0"] = col(b_in[:D]), col(b_in[D:2 * D]), row(b_in[2 * D:])
    s["ln_w"], s["ln_b"] = row(I["L1_attn_ln_w"]), row(I["L1_attn_ln_b"])
    s["lam"] = row(np.concatenate([I["L1_attn_lambda_" + n] for n in ("q1", "k1", "q2", "k2")]))
    s["qkv_b"], s["proj_b"] = row(I["L2_attn_qkv_b"]), row(I["L2_attn_proj_b"])
    s["beta_w"], s["norm1_row"], s["beta_b"] = row(I["L3_attn_beta_w"]), row(I["L3_attn_norm1_w"]), row(I["L3_attn_beta_b"])
    s["range"], s["cn_b4"], s["gc_b3"] = row(I["L1_ffn_adaptive_range"]), row(I["L1_ffn_cn_b4"]), row(I["L1_ffn_gc_b3"])
    s["ln1_w"] = col(I["L0_tok_ln1_w"])
    s["b2"] = flat(chunks(I["L0_ffn_b2"].T))
    s["cn_b1"], s["cn_b2"], s["cn_b3"] = col(I["L1_ffn_cn_b1"]), col(I["L1_ffn_cn_b2"]), col(I["L1_ffn_cn_b3"])
    s["gc_b1"], s["gc_b2"] = col(I["L1_ffn_gc_b1"]), col(I["L1_ffn_gc_b2"])
    s["alpha"], s["norm1"], s["norm2"] = col(I["L3_attn_alpha_logit"]), col(I["L3_attn_norm1_w"]), col(I["L3_attn_norm2_w"])
    a = {"small": np.concatenate([flat(s[n]) for n, _ in SMALL], 1)}

    w = {}
    w["w_tok"] = chunks(I["L0_tok_W"].T)
    w["w_in"], w["w_out"], w["gate0"] = chunks(I["L0_attn_w_in"]), chunks(I["L0_attn_w_out"]), chunks(I["L0_ffn_gate_w"])
    w["qk1"] = chunks(np.concatenate([I["L1_attn_Wq"].T, I["L1_attn_Wk"].T], 1))
    w["v1"], w["o1"] = chunks(I["L1_attn_Wv"].T), chunks(I["L1_attn_Wo"].T)
    w["cn1"], w["cn2"], w["cn3"] = chunks(I["L1_ffn_cn_w1"]), chunks(I["L1_ffn_cn_w2"]), chunks(I["L1_ffn_cn_w3"])
    w["cn4"] = np.broadcast_to(I["L1_ffn_cn_w4"], (64, 128))
    w["gc1"], w["gc2"] = chunks(I["L1_ffn_gc_w1"]), chunks(I["L1_ffn_gc_w2"])
    w["gc3"] = np.broadcast_to(I["L1_ffn_gc_w3"], (64, 128))
    w["qkv2"], w["proj2"], w["gate2"] = chunks(I["L2_attn_qkv_w"]), chunks(I["L2_attn_proj_w"]), chunks(I["L2_ffn_gate_w"])
    for n in ("w1", "w3"):
        w[n + "_2"] = I["L2_ffn_" + n].reshape(E2, 2, 128, F2).transpose(2, 0, 1, 3)
    w["w2_2"] = I["L2_ffn_w2"].transpose(1, 0, 2)
    w["qk3"] = chunks(np.concatenate([I["L3_attn_Wq"], I["L3_attn_Wk"]], 1))
    w["v3"], w["o3"] = chunks(I["L3_attn_Wv"]), chunks(I["L3_attn_Wo"])
    w["gate3"], w["up3"], w["down3"] = (chunks(I["L3_attn_w_" + n]) for n in ("gate", "up", "down"))
    w["router"], w["ws_gu"], w["ws_down"] = chunks(I["L3_ffn_router_w"].T), chunks(I["L3_ffn_ws_gate_up"]), chunks(I["L3_ffn_ws_down"], FH)
    for array, parts in WEIGHTS:
        a[array] = np.concatenate([flat(w[n]) for n, _ in parts], 1)

    x = I["x"].reshape(BATCH, CHANNELS, GRID, PATCH, GRID, PATCH).transpose(0, 2, 4, 1, 3, 5).reshape(BATCH, L - 1, PD)
    patches = np.zeros((T * SEQS, L, PD), np.float32)
    patches[:BATCH, 1:] = x
    a["patches"] = patches.reshape(T, P, PD)
    a["w1_0"] = I["L0_ffn_w1"].reshape(E0, 2, 128, F0).transpose(0, 2, 1, 3).reshape(E0, 128, 2 * F0)
    a["w2_0"] = I["L0_ffn_w2"].reshape(E0, F0 // 128, 128, D).transpose(0, 2, 1, 3).reshape(E0, 128, F0 // 128 * D)
    a["b1_0"] = I["L0_ffn_b1"].reshape(E0, F0 // 128, 128).transpose(0, 2, 1)
    a["b2_0"] = I["L0_ffn_b2"].reshape(E0, 2, 128).transpose(0, 2, 1)
    gu = np.concatenate([I["L3_ffn_w_gate"], I["L3_ffn_w_up"]], 2)
    a["gu_3"] = gu.reshape(E3, 2, 128, 2 * F3).transpose(0, 2, 1, 3).reshape(E3, 128, 4 * F3)
    a["down_3"] = I["L3_ffn_w_down"].reshape(E3, 2, FH, D).transpose(0, 2, 1, 3).reshape(E3, FH, 2 * D)
    return {n: np.ascontiguousarray(v) for n, v in a.items()}


def kernel(**inputs):
    import concourse.bacc as bacc
    from concourse.bass_utils import run_bass_kernel_spmd

    arrays = lay_out({n: np.asarray(v) for n, v in inputs.items()})
    nc = bacc.Bacc("TRN2", target_bir_lowering=False, num_devices=1)
    dram = {n: nc.dram_tensor("in_" + n, a.shape, F32, kind="ExternalInput").ap() for n, a in arrays.items()}
    dram["out"] = nc.dram_tensor("out", (T, P, D), F32, kind="ExternalOutput").ap()
    for n, shape in (("cw0", (E0, NTOK)), ("cw2", (E2, NTOK)), ("slots_x", (SLOT_ROWS, D)), ("slots_y", (SLOTS, D))):
        dram[n] = nc.dram_tensor(n, shape, F32).ap()
    vit_tower(nc, dram)
    r = run_bass_kernel_spmd(nc, [{"in_" + n: a for n, a in arrays.items()}], core_ids=[0])
    return r.results[0]["out"].reshape(T * SEQS, L, D)[:BATCH]
```
